# Optimizing a Trainium2 kernel written in Bass

```python
import numpy as np
import jax
import jax.numpy as jnp

def _softmax(x, axis=-1):
    return jax.nn.softmax(x, axis=axis)

def _gelu(x):
    return jax.nn.gelu(x, approximate=True)

def _silu(x):
    return jax.nn.silu(x)

def _sigmoid(x):
    return jax.nn.sigmoid(x)

def _layernorm(x, axis=-1, eps=1e-05):
    m = jnp.mean(x, axis=axis, keepdims=True)
    v = jnp.var(x, axis=axis, keepdims=True)
    return (x - m) / jnp.sqrt(v + eps)

def _scatter_add(tgt, idx, src, axis=0):
    return tgt.at[idx].add(src)

def _segment_sum(src, seg, n):
    return jax.ops.segment_sum(src, seg, n)
kernel_name = 'mk_decoder_postln_d2_seqx_r4_d5414b'

def setup_inputs(seed: int=0):
    np.random.seed(seed)
    _w = jnp.asarray

    def _rec_inputs():
        import jax
        import jax.numpy as jnp
        _rk = jax.random.key(seed)
        x = 0.0002417 + 0.9998 * jax.random.normal(jax.random.fold_in(_rk, 1), (8, 256, 256), jnp.float32)
        _lenS = 256 - jax.random.randint(jax.random.fold_in(_rk, 7), (8,), 0, max(1, 256 // 4) + 1, jnp.int32)
        _lenS2 = 256 - jax.random.randint(jax.random.fold_in(_rk, 8), (8,), 0, max(1, 256 // 4) + 1, jnp.int32)
        _ctx_1024P = jax.random.normal(jax.random.fold_in(_rk, 11), (8, 16, 256), jnp.float32)
        _ctx_1024c = jax.random.dirichlet(jax.random.fold_in(_rk, 511), 0.3 * jnp.ones((16,), jnp.float32), (8, 256))
        _ctx_1024t = jnp.einsum('bsk,bkd->bsd', _ctx_1024c, _ctx_1024P)
        _ctx_1024t = _ctx_1024t * jax.lax.rsqrt(jnp.mean(jnp.square(_ctx_1024t)) + 1e-12) * 0.953939
        ctx_1024 = 7.22013e-05 + 1.00017 * (_ctx_1024t + 0.3 * jax.random.normal(jax.random.fold_in(_rk, 611), (8, 256, 256), jnp.float32))
        fside_BxSxS2_0 = jax.random.uniform(jax.random.fold_in(_rk, 12), (8, 256, 256), jnp.float32, 0.0, 0.999998)
        _validS = jnp.arange(256)[None, :] < _lenS[:, None]
        _validS2 = jnp.arange(256)[None, :] < _lenS2[:, None]
        _causal = jnp.tril(jnp.ones((256, 256), dtype=bool))
        mask_Bx1x1xS2_ff0 = jnp.where(jnp.ones((8, 1, 1, 256), dtype=bool), 0.0, -1000000000.0).astype(jnp.float32)
        return (x, ctx_1024, fside_BxSxS2_0, mask_Bx1x1xS2_ff0)
    x, ctx_1024, fside_BxSxS2_0, mask_Bx1x1xS2_ff0 = _rec_inputs()

    def _L0_attn_setup():
        import jax, jax.numpy as jnp
        import numpy as np
        from jax import lax
        H = 256
        E = 2
        INNER = H * E
        N = 16
        K = 4
        R = 64
        B, L = (2, 1024)
        key = jax.random.key(seed)
        ks = jax.random.split(key, 12)
        s = 0.02
        inp = {'hidden': jax.random.normal(ks[0], (B, L, H), dtype=jnp.float32), 'ln_w': jnp.ones((H,), jnp.float32), 'ln_b': jnp.zeros((H,), jnp.float32), 'in_w': jax.random.normal(ks[1], (2 * INNER, H), jnp.float32) * s, 'in_b': jnp.zeros((2 * INNER,), jnp.float32), 'conv_w': jax.random.normal(ks[2], (INNER, 1, K), jnp.float32) * s, 'conv_b': jnp.zeros((INNER,), jnp.float32), 'xp_w': jax.random.normal(ks[3], (R + 2 * N, INNER), jnp.float32) * s, 'dtp_w': jax.random.normal(ks[4], (INNER, R), jnp.float32) * s, 'dtp_b': jax.random.normal(ks[5], (INNER,), jnp.float32) * s, 'A_log': jnp.log(jnp.tile(jnp.arange(1, N + 1, dtype=jnp.float32), (INNER, 1))), 'D': jnp.ones((INNER,), jnp.float32), 'out_w': jax.random.normal(ks[6], (H, INNER), jnp.float32) * s, 'out_b': jnp.zeros((H,), jnp.float32)}
        return inp
    _L0_attn_all = _L0_attn_setup()
    _L0_attn_in = {k: v for k, v in _L0_attn_all.items() if k in ('ln_w', 'ln_b', 'in_w', 'in_b', 'conv_w', 'conv_b', 'xp_w', 'dtp_w', 'dtp_b', 'A_log', 'D', 'out_w', 'out_b')}
    del _L0_attn_all

    def _L0_xattn_setup():
        import jax, jax.numpy as jnp
        import numpy as np
        EMBED = 256
        HEADS = 16
        HEAD_DIM = EMBED // HEADS
        key = jax.random.key(seed)
        ks = jax.random.split(key, 8)
        N, S = (4, 512)
        values = jax.random.normal(ks[0], (N, S, EMBED), dtype=jnp.float32)
        keys_ = jax.random.normal(ks[1], (N, S, EMBED), dtype=jnp.float32)
        query = jax.random.normal(ks[2], (N, S, EMBED), dtype=jnp.float32)
        sd = 1.0 / np.sqrt(HEAD_DIM)
        Wv = jax.random.normal(ks[3], (HEAD_DIM, HEAD_DIM), dtype=jnp.float32) * sd
        Wk = jax.random.normal(ks[4], (HEAD_DIM, HEAD_DIM), dtype=jnp.float32) * sd
        Wq = jax.random.normal(ks[5], (HEAD_DIM, HEAD_DIM), dtype=jnp.float32) * sd
        Wo = jax.random.normal(ks[6], (EMBED, EMBED), dtype=jnp.float32) * (1.0 / np.sqrt(EMBED))
        bo = jnp.zeros((EMBED,), dtype=jnp.float32)
        return {'values': values, 'keys': keys_, 'query': query, 'Wv': Wv, 'Wk': Wk, 'Wq': Wq, 'Wo': Wo, 'bo': bo}
    _L0_xattn_all = _L0_xattn_setup()
    _L0_xattn_in = {k: v for k, v in _L0_xattn_all.items() if k in ('Wv', 'Wk', 'Wq', 'Wo', 'bo')}
    del _L0_xattn_all

    def _L0_ffn_setup():
        import jax, jax.numpy as jnp
        import numpy as np
        EPS = 1e-05

        def _ln(x, g, b):
            mu = jnp.mean(x, axis=-1, keepdims=True)
            var = jnp.mean(jnp.square(x - mu), axis=-1, keepdims=True)
            return (x - mu) * jax.lax.rsqrt(var + EPS) * g + b

        def _forward(x, index_b, index_t, sw1, sb1, sw2, sb2, sw3, sb3, s_ln_g, s_ln_b, sg_w, sg_b, eg_w, eg_b, exp_bias, ew1, eb1, ew2, eb2, ew3, eb3, sel_ln_g, sel_ln_b):
            x1 = jnp.einsum('btd,hd->bth', x, sw1) + sb1
            x2 = jnp.einsum('btd,hd->bth', x, sw2) + sb2
            sh = _ln(jax.nn.silu(x1) * x2, s_ln_g, s_ln_b)
            shared_out = jnp.einsum('bth,dh->btd', sh, sw3) + sb3
            x_moe = x[index_b, index_t]
            shared_scores = jax.nn.sigmoid(x_moe @ sg_w.T + sg_b)
            expert_scores = jax.nn.sigmoid(x_moe @ eg_w.T + eg_b)
            top1_idx = jnp.argmax(expert_scores + exp_bias, axis=-1)
            top1_score = jnp.take_along_axis(expert_scores, top1_idx[:, None], axis=-1)
            weights = jax.nn.softmax(jnp.concatenate([shared_scores, top1_score], axis=-1), axis=-1)
            shared_w, expert_w = (weights[:, 0], weights[:, 1])
            shared_moe_out = shared_out[index_b, index_t] * shared_w[:, None]
            h1 = jnp.einsum('md,ehd->meh', x_moe, ew1) + eb1
            h2 = jnp.einsum('md,ehd->meh', x_moe, ew2) + eb2
            z = _ln(jax.nn.silu(h1) * h2, sel_ln_g, sel_ln_b)
            out_all = jnp.einsum('meh,edh->med', z, ew3) + eb3
            expert_out = jnp.take_along_axis(out_all, top1_idx[:, None, None], axis=1)[:, 0]
            expert_moe_out = expert_out * expert_w[:, None]
            final_out = shared_out.at[index_b, index_t].set(shared_moe_out + expert_moe_out)
            return final_out
        B, T, D, E, H, M = (2, 512, 256, 8, 128, 512)
        key = jax.random.key(seed)
        ks = jax.random.split(key, 24)
        s = 0.02
        inp = {}
        inp['x'] = jax.random.normal(ks[0], (B, T, D), jnp.float32)
        flat = jnp.arange(M, dtype=jnp.int32) * 2
        inp['index_b'] = flat // T
        inp['index_t'] = flat % T
        inp['sw1'] = jax.random.normal(ks[1], (H, D), jnp.float32) * s
        inp['sb1'] = jnp.zeros((H,), jnp.float32)
        inp['sw2'] = jax.random.normal(ks[2], (H, D), jnp.float32) * s
        inp['sb2'] = jnp.zeros((H,), jnp.float32)
        inp['sw3'] = jax.random.normal(ks[3], (D, H), jnp.float32) * s
        inp['sb3'] = jnp.zeros((D,), jnp.float32)
        inp['s_ln_g'] = jnp.ones((H,), jnp.float32)
        inp['s_ln_b'] = jnp.zeros((H,), jnp.float32)
        inp['sg_w'] = jax.random.normal(ks[4], (1, D), jnp.float32) * s
        inp['sg_b'] = jnp.zeros((1,), jnp.float32)
        inp['eg_w'] = jax.random.normal(ks[5], (E, D), jnp.float32) * s
        inp['eg_b'] = jnp.zeros((E,), jnp.float32)
        inp['exp_bias'] = jnp.zeros((E,), jnp.float32)
        inp['ew1'] = jax.random.normal(ks[6], (E, H, D), jnp.float32) * s
        inp['eb1'] = jnp.zeros((E, H), jnp.float32)
        inp['ew2'] = jax.random.normal(ks[7], (E, H, D), jnp.float32) * s
        inp['eb2'] = jnp.zeros((E, H), jnp.float32)
        inp['ew3'] = jax.random.normal(ks[8], (E, D, H), jnp.float32) * s
        inp['eb3'] = jnp.zeros((E, D), jnp.float32)
        inp['sel_ln_g'] = jnp.ones((H,), jnp.float32)
        inp['sel_ln_b'] = jnp.zeros((H,), jnp.float32)
        return inp
    _L0_ffn_all = _L0_ffn_setup()
    _L0_ffn_in = {k: v for k, v in _L0_ffn_all.items() if k in ('index_b', 'index_t', 'sw1', 'sb1', 'sw2', 'sb2', 'sw3', 'sb3', 's_ln_g', 's_ln_b', 'sg_w', 'sg_b', 'eg_w', 'eg_b', 'exp_bias', 'ew1', 'eb1', 'ew2', 'eb2', 'ew3', 'eb3', 'sel_ln_g', 'sel_ln_b')}
    del _L0_ffn_all

    def _L1_attn_setup():
        import jax, jax.numpy as jnp
        import numpy as np

        def _phm(x, A, S, b):
            f = A.shape[0]
            din = f * S.shape[1]
            dout = f * S.shape[2]
            W = jnp.einsum('nij,nkl->ikjl', A, S).reshape(din, dout)
            return x @ W + b

        def _ln(x, g, b, eps=1e-05):
            mu = jnp.mean(x, axis=-1, keepdims=True)
            var = jnp.mean((x - mu) ** 2, axis=-1, keepdims=True)
            return (x - mu) * jax.lax.rsqrt(var + eps) * g + b
        key = jax.random.key(seed)
        ks = jax.random.split(key, 10)
        L, N, E, f = (512, 4, 256, 4)
        p = lambda k, sh: jax.random.normal(k, sh, jnp.float32) * 0.02
        return {'query': jax.random.normal(ks[0], (L, N, E), jnp.float32), 'qA': p(ks[1], (f, f, f)), 'qS': p(ks[2], (f, E // f, E // f)), 'qb': jnp.zeros((E,), jnp.float32), 'kA': p(ks[3], (f, f, f)), 'kS': p(ks[4], (f, E // f, E // f)), 'kb': jnp.zeros((E,), jnp.float32), 'vA': p(ks[5], (f, f, f)), 'vS': p(ks[6], (f, E // f, E // f)), 'vb': jnp.zeros((E,), jnp.float32), 'oA': p(ks[7], (f, f, f)), 'oS': p(ks[8], (f, E // f, E // f)), 'ob': jnp.zeros((E,), jnp.float32), 'g1': jnp.ones((E,), jnp.float32), 'b1': jnp.zeros((E,), jnp.float32), 'g2': jnp.ones((E,), jnp.float32), 'b2': jnp.zeros((E,), jnp.float32)}
    _L1_attn_all = _L1_attn_setup()
    _L1_attn_in = {k: v for k, v in _L1_attn_all.items() if k in ('qA', 'qS', 'qb', 'kA', 'kS', 'kb', 'vA', 'vS', 'vb', 'oA', 'oS', 'ob', 'g1', 'b1', 'g2', 'b2')}
    del _L1_attn_all

    def _L1_xattn_setup():
        import jax, jax.numpy as jnp
        import numpy as np
        B, F, T = (2, 128, 128)
        D, N, H = (256, 16, 64)
        K = 32
        FILT = 1024
        L = 4
        EPS = 1e-06

        def _glorot(key, shape, fan_in, fan_out):
            lim = np.sqrt(6.0 / (fan_in + fan_out)).astype(np.float32)
            return jax.random.uniform(key, shape, jnp.float32, -lim, lim)

        def _norm(x):
            m = jnp.mean(x, axis=-1, keepdims=True)
            s = jnp.sqrt(jnp.mean((x - m) ** 2, axis=-1, keepdims=True))
            return (x - m) / (s + EPS)

        def _attention(x, src, dist, bias, Wq, Wk, Wv, Wo, Wth, bth, Wto, bto):
            q = jnp.einsum('bfd,dnh->bfnh', x, Wq) * H ** (-0.5)
            k = jnp.einsum('btd,dnh->btnh', src, Wk)
            v = jnp.einsum('btd,dnh->btnh', src, Wv)
            hbias = jax.nn.relu(dist[..., None] @ Wth + bth)
            qs_bias = (hbias @ Wto + bto)[..., 0]
            logits = jnp.einsum('btnh,bfnh->bnft', k, q)
            logits = logits + bias + qs_bias[:, None]
            w = jax.nn.softmax(logits, axis=-1)
            out = jnp.einsum('bnft,btnh->bfnh', w, v)
            return jnp.einsum('bfnh,nhd->bfd', out, Wo)
        key = jax.random.key(seed)
        ks = jax.random.split(key, 18)
        inp = {'decoder_inputs': jax.random.normal(ks[0], (B, F, D), jnp.float32), 'encoder_outputs': jax.random.normal(ks[1], (B, T, D), jnp.float32), 'decoder_times_dist': jax.random.uniform(ks[2], (B, F, F), jnp.float32), 'decoder_encoder_times_dist': jax.random.uniform(ks[3], (B, F, T), jnp.float32), 'dec_self_attn_bias': jnp.zeros((B, 1, 1, F), jnp.float32), 'enc_dec_attn_bias': jnp.zeros((B, 1, 1, T), jnp.float32), 'Wq': _glorot(ks[4], (L, D, N, H), D, D), 'Wk': _glorot(ks[5], (L, D, N, H), D, D), 'Wv': _glorot(ks[6], (L, D, N, H), D, D), 'Wo': _glorot(ks[7], (L, N, H, D), D, D), 'Wth': _glorot(ks[8], (L, 1, K), 1, K), 'bth': jnp.zeros((L, K), jnp.float32), 'Wto': _glorot(ks[9], (L, K, 1), K, 1), 'bto': jnp.zeros((L, 1), jnp.float32), 'Wf1': _glorot(ks[10], (L, D, FILT), D, FILT), 'bf1': jnp.zeros((L, FILT), jnp.float32), 'Wf2': _glorot(ks[11], (L, FILT, D), FILT, D), 'bf2': jnp.zeros((L, D), jnp.float32)}
        return inp
    _L1_xattn_all = _L1_xattn_setup()
    _L1_xattn_in = {k: v for k, v in _L1_xattn_all.items() if k in ('Wq', 'Wk', 'Wv', 'Wo', 'Wth', 'bth', 'Wto', 'bto', 'Wf1', 'bf1', 'Wf2', 'bf2')}
    del _L1_xattn_all

    def _L1_ffn_setup():
        import jax, jax.numpy as jnp
        import numpy as np
        B, S, D, E, F = (2, 256, 256, 14, 512)
        key = jax.random.key(seed)
        k0, k1, k2, k3 = jax.random.split(key, 4)
        h = jax.random.normal(k0, (B, S, D), jnp.float32)
        gate_w = jax.random.normal(k1, (E, D), jnp.float32) * 0.02
        w1 = jax.random.normal(k2, (E, D, F), jnp.float32) * (1.0 / np.sqrt(D).astype(np.float32))
        b1 = jnp.zeros((E, F), jnp.float32)
        w2 = jax.random.normal(k3, (E, F, D), jnp.float32) * (1.0 / np.sqrt(F).astype(np.float32))
        b2 = jnp.zeros((E, D), jnp.float32)
        return {'h': h, 'gate_w': gate_w, 'w1': w1, 'b1': b1, 'w2': w2, 'b2': b2}
    _L1_ffn_all = _L1_ffn_setup()
    _L1_ffn_in = {k: v for k, v in _L1_ffn_all.items() if k in ('gate_w', 'w1', 'b1', 'w2', 'b2')}
    del _L1_ffn_all
    return {'x': x, 'ctx_1024': ctx_1024, 'fside_BxSxS2_0': fside_BxSxS2_0, 'mask_Bx1x1xS2_ff0': mask_Bx1x1xS2_ff0, 'L0_attn_ln_w': _L0_attn_in['ln_w'], 'L0_attn_ln_b': _L0_attn_in['ln_b'], 'L0_attn_in_w': _L0_attn_in['in_w'], 'L0_attn_in_b': _L0_attn_in['in_b'], 'L0_attn_conv_w': _L0_attn_in['conv_w'], 'L0_attn_conv_b': _L0_attn_in['conv_b'], 'L0_attn_xp_w': _L0_attn_in['xp_w'], 'L0_attn_dtp_w': _L0_attn_in['dtp_w'], 'L0_attn_dtp_b': _L0_attn_in['dtp_b'], 'L0_attn_A_log': _L0_attn_in['A_log'], 'L0_attn_D': _L0_attn_in['D'], 'L0_attn_out_w': _L0_attn_in['out_w'], 'L0_attn_out_b': _L0_attn_in['out_b'], 'L0_xattn_Wv': _L0_xattn_in['Wv'], 'L0_xattn_Wk': _L0_xattn_in['Wk'], 'L0_xattn_Wq': _L0_xattn_in['Wq'], 'L0_xattn_Wo': _L0_xattn_in['Wo'], 'L0_xattn_bo': _L0_xattn_in['bo'], 'L0_ffn_index_b': _L0_ffn_in['index_b'], 'L0_ffn_index_t': _L0_ffn_in['index_t'], 'L0_ffn_sw1': _L0_ffn_in['sw1'], 'L0_ffn_sb1': _L0_ffn_in['sb1'], 'L0_ffn_sw2': _L0_ffn_in['sw2'], 'L0_ffn_sb2': _L0_ffn_in['sb2'], 'L0_ffn_sw3': _L0_ffn_in['sw3'], 'L0_ffn_sb3': _L0_ffn_in['sb3'], 'L0_ffn_s_ln_g': _L0_ffn_in['s_ln_g'], 'L0_ffn_s_ln_b': _L0_ffn_in['s_ln_b'], 'L0_ffn_sg_w': _L0_ffn_in['sg_w'], 'L0_ffn_sg_b': _L0_ffn_in['sg_b'], 'L0_ffn_eg_w': _L0_ffn_in['eg_w'], 'L0_ffn_eg_b': _L0_ffn_in['eg_b'], 'L0_ffn_exp_bias': _L0_ffn_in['exp_bias'], 'L0_ffn_ew1': _L0_ffn_in['ew1'], 'L0_ffn_eb1': _L0_ffn_in['eb1'], 'L0_ffn_ew2': _L0_ffn_in['ew2'], 'L0_ffn_eb2': _L0_ffn_in['eb2'], 'L0_ffn_ew3': _L0_ffn_in['ew3'], 'L0_ffn_eb3': _L0_ffn_in['eb3'], 'L0_ffn_sel_ln_g': _L0_ffn_in['sel_ln_g'], 'L0_ffn_sel_ln_b': _L0_ffn_in['sel_ln_b'], 'L1_attn_qA': _L1_attn_in['qA'], 'L1_attn_qS': _L1_attn_in['qS'], 'L1_attn_qb': _L1_attn_in['qb'], 'L1_attn_kA': _L1_attn_in['kA'], 'L1_attn_kS': _L1_attn_in['kS'], 'L1_attn_kb': _L1_attn_in['kb'], 'L1_attn_vA': _L1_attn_in['vA'], 'L1_attn_vS': _L1_attn_in['vS'], 'L1_attn_vb': _L1_attn_in['vb'], 'L1_attn_oA': _L1_attn_in['oA'], 'L1_attn_oS': _L1_attn_in['oS'], 'L1_attn_ob': _L1_attn_in['ob'], 'L1_attn_g1': _L1_attn_in['g1'], 'L1_attn_b1': _L1_attn_in['b1'], 'L1_attn_g2': _L1_attn_in['g2'], 'L1_attn_b2': _L1_attn_in['b2'], 'L1_xattn_Wq': _L1_xattn_in['Wq'], 'L1_xattn_Wk': _L1_xattn_in['Wk'], 'L1_xattn_Wv': _L1_xattn_in['Wv'], 'L1_xattn_Wo': _L1_xattn_in['Wo'], 'L1_xattn_Wth': _L1_xattn_in['Wth'], 'L1_xattn_bth': _L1_xattn_in['bth'], 'L1_xattn_Wto': _L1_xattn_in['Wto'], 'L1_xattn_bto': _L1_xattn_in['bto'], 'L1_xattn_Wf1': _L1_xattn_in['Wf1'], 'L1_xattn_bf1': _L1_xattn_in['bf1'], 'L1_xattn_Wf2': _L1_xattn_in['Wf2'], 'L1_xattn_bf2': _L1_xattn_in['bf2'], 'L1_ffn_gate_w': _L1_ffn_in['gate_w'], 'L1_ffn_w1': _L1_ffn_in['w1'], 'L1_ffn_b1': _L1_ffn_in['b1'], 'L1_ffn_w2': _L1_ffn_in['w2'], 'L1_ffn_b2': _L1_ffn_in['b2']}

def reference(x, ctx_1024, fside_BxSxS2_0, mask_Bx1x1xS2_ff0, L0_attn_ln_w, L0_attn_ln_b, L0_attn_in_w, L0_attn_in_b, L0_attn_conv_w, L0_attn_conv_b, L0_attn_xp_w, L0_attn_dtp_w, L0_attn_dtp_b, L0_attn_A_log, L0_attn_D, L0_attn_out_w, L0_attn_out_b, L0_xattn_Wv, L0_xattn_Wk, L0_xattn_Wq, L0_xattn_Wo, L0_xattn_bo, L0_ffn_index_b, L0_ffn_index_t, L0_ffn_sw1, L0_ffn_sb1, L0_ffn_sw2, L0_ffn_sb2, L0_ffn_sw3, L0_ffn_sb3, L0_ffn_s_ln_g, L0_ffn_s_ln_b, L0_ffn_sg_w, L0_ffn_sg_b, L0_ffn_eg_w, L0_ffn_eg_b, L0_ffn_exp_bias, L0_ffn_ew1, L0_ffn_eb1, L0_ffn_ew2, L0_ffn_eb2, L0_ffn_ew3, L0_ffn_eb3, L0_ffn_sel_ln_g, L0_ffn_sel_ln_b, L1_attn_qA, L1_attn_qS, L1_attn_qb, L1_attn_kA, L1_attn_kS, L1_attn_kb, L1_attn_vA, L1_attn_vS, L1_attn_vb, L1_attn_oA, L1_attn_oS, L1_attn_ob, L1_attn_g1, L1_attn_b1, L1_attn_g2, L1_attn_b2, L1_xattn_Wq, L1_xattn_Wk, L1_xattn_Wv, L1_xattn_Wo, L1_xattn_Wth, L1_xattn_bth, L1_xattn_Wto, L1_xattn_bto, L1_xattn_Wf1, L1_xattn_bf1, L1_xattn_Wf2, L1_xattn_bf2, L1_ffn_gate_w, L1_ffn_w1, L1_ffn_b1, L1_ffn_w2, L1_ffn_b2):
    import jax
    import jax.numpy as jnp

    def _L0_attn_ref(hidden, ln_w, ln_b, in_w, in_b, conv_w, conv_b, xp_w, dtp_w, dtp_b, A_log, D, out_w, out_b):
        import jax, jax.numpy as jnp
        import numpy as np
        from jax import lax
        H = 256
        E = 2
        INNER = H * E
        N = 16
        K = 4
        R = 64
        B, L = (2, 1024)
        b_, l_, h_ = hidden.shape
        inner = conv_w.shape[0]
        n = A_log.shape[1]
        r = dtp_w.shape[1]
        k = conv_w.shape[2]
        mu = jnp.mean(hidden, axis=-1, keepdims=True)
        var = jnp.mean((hidden - mu) ** 2, axis=-1, keepdims=True)
        hn = (hidden - mu) / jnp.sqrt(var + 1e-05) * ln_w + ln_b
        proj = hn @ in_w.T + in_b
        x, gate = (proj[..., :inner], proj[..., inner:])
        xc = x.transpose(0, 2, 1)
        xc = lax.conv_general_dilated(xc, conv_w, window_strides=(1,), padding=[(k - 1, 0)], dimension_numbers=('NCH', 'OIH', 'NCH'), feature_group_count=inner) + conv_b[None, :, None]
        x = jax.nn.silu(xc.transpose(0, 2, 1))
        params = x @ xp_w.T
        dt_raw = params[..., :r]
        b_mat = params[..., r:r + n]
        c_mat = params[..., r + n:]
        dt = jax.nn.softplus(dt_raw @ dtp_w.T + dtp_b)
        a = -jnp.exp(A_log)

        def step(state, ins):
            dt_t, x_t, b_t, c_t = ins
            decay = jnp.exp(dt_t[..., None] * a)
            state = decay * state + (dt_t * x_t)[..., None] * b_t[:, None, :]
            y_t = jnp.einsum('bdn,bn->bd', state, c_t) + D * x_t
            return (state, y_t)
        state0 = jnp.zeros((b_, inner, n), dtype=x.dtype)
        xs = (dt.transpose(1, 0, 2), x.transpose(1, 0, 2), b_mat.transpose(1, 0, 2), c_mat.transpose(1, 0, 2))
        _, ys = lax.scan(step, state0, xs)
        y = ys.transpose(1, 0, 2) * jax.nn.silu(gate)
        return hidden + y @ out_w.T + out_b

    def _L0_xattn_ref(values, keys, query, Wv, Wk, Wq, Wo, bo):
        import jax, jax.numpy as jnp
        import numpy as np
        EMBED = 256
        HEADS = 16
        HEAD_DIM = EMBED // HEADS
        N, S, E = query.shape
        H, D = (HEADS, HEAD_DIM)
        v = values.reshape(N, S, H, D)
        k = keys.reshape(N, S, H, D)
        q = query.reshape(N, S, H, D)
        v = jnp.einsum('nshd,ed->nshe', v, Wv)
        k = jnp.einsum('nshd,ed->nshe', k, Wk)
        q = jnp.einsum('nshd,ed->nshe', q, Wq)
        energy = jnp.einsum('nqhd,nkhd->nhqk', q, k)
        attn = jax.nn.softmax(energy / jnp.sqrt(jnp.float32(E)), axis=-1)
        out = jnp.einsum('nhqk,nkhd->nqhd', attn, v).reshape(N, S, E)
        return out @ Wo.T + bo

    def _L0_ffn_ref(x, index_b, index_t, sw1, sb1, sw2, sb2, sw3, sb3, s_ln_g, s_ln_b, sg_w, sg_b, eg_w, eg_b, exp_bias, ew1, eb1, ew2, eb2, ew3, eb3, sel_ln_g, sel_ln_b):
        import jax, jax.numpy as jnp
        import numpy as np
        EPS = 1e-05

        def _ln(x, g, b):
            mu = jnp.mean(x, axis=-1, keepdims=True)
            var = jnp.mean(jnp.square(x - mu), axis=-1, keepdims=True)
            return (x - mu) * jax.lax.rsqrt(var + EPS) * g + b

        def _forward(x, index_b, index_t, sw1, sb1, sw2, sb2, sw3, sb3, s_ln_g, s_ln_b, sg_w, sg_b, eg_w, eg_b, exp_bias, ew1, eb1, ew2, eb2, ew3, eb3, sel_ln_g, sel_ln_b):
            x1 = jnp.einsum('btd,hd->bth', x, sw1) + sb1
            x2 = jnp.einsum('btd,hd->bth', x, sw2) + sb2
            sh = _ln(jax.nn.silu(x1) * x2, s_ln_g, s_ln_b)
            shared_out = jnp.einsum('bth,dh->btd', sh, sw3) + sb3
            x_moe = x[index_b, index_t]
            shared_scores = jax.nn.sigmoid(x_moe @ sg_w.T + sg_b)
            expert_scores = jax.nn.sigmoid(x_moe @ eg_w.T + eg_b)
            top1_idx = jnp.argmax(expert_scores + exp_bias, axis=-1)
            top1_score = jnp.take_along_axis(expert_scores, top1_idx[:, None], axis=-1)
            weights = jax.nn.softmax(jnp.concatenate([shared_scores, top1_score], axis=-1), axis=-1)
            shared_w, expert_w = (weights[:, 0], weights[:, 1])
            shared_moe_out = shared_out[index_b, index_t] * shared_w[:, None]
            h1 = jnp.einsum('md,ehd->meh', x_moe, ew1) + eb1
            h2 = jnp.einsum('md,ehd->meh', x_moe, ew2) + eb2
            z = _ln(jax.nn.silu(h1) * h2, sel_ln_g, sel_ln_b)
            out_all = jnp.einsum('meh,edh->med', z, ew3) + eb3
            expert_out = jnp.take_along_axis(out_all, top1_idx[:, None, None], axis=1)[:, 0]
            expert_moe_out = expert_out * expert_w[:, None]
            final_out = shared_out.at[index_b, index_t].set(shared_moe_out + expert_moe_out)
            return final_out
        return _forward(x, index_b, index_t, sw1, sb1, sw2, sb2, sw3, sb3, s_ln_g, s_ln_b, sg_w, sg_b, eg_w, eg_b, exp_bias, ew1, eb1, ew2, eb2, ew3, eb3, sel_ln_g, sel_ln_b)

    def _L1_attn_ref(query, qA, qS, qb, kA, kS, kb, vA, vS, vb, oA, oS, ob, g1, b1, g2, b2):
        import jax, jax.numpy as jnp
        import numpy as np

        def _phm(x, A, S, b):
            f = A.shape[0]
            din = f * S.shape[1]
            dout = f * S.shape[2]
            W = jnp.einsum('nij,nkl->ikjl', A, S).reshape(din, dout)
            return x @ W + b

        def _ln(x, g, b, eps=1e-05):
            mu = jnp.mean(x, axis=-1, keepdims=True)
            var = jnp.mean((x - mu) ** 2, axis=-1, keepdims=True)
            return (x - mu) * jax.lax.rsqrt(var + eps) * g + b
        L, N, E = query.shape
        H = 16
        D = E // H
        eps = 1e-06
        key_raw = query
        val_raw = query
        qn = _ln(query, g1, b1)
        q = jax.nn.relu(_phm(qn, qA, qS, qb))
        k = jax.nn.relu(_phm(key_raw, kA, kS, kb))
        v = _phm(val_raw, vA, vS, vb)
        resh = lambda t: t.reshape(L, N * H, D).transpose(1, 0, 2)
        q, k, v = (resh(q), resh(k), resh(v))
        idx = np.pi / 2 * jnp.arange(1, L + 1, dtype=query.dtype)[None, :, None] / L
        s, c = (jnp.sin(idx), jnp.cos(idx))
        q_ = jnp.concatenate([q * s, q * c], axis=-1)
        k_ = jnp.concatenate([k * s, k * c], axis=-1)
        kv = jnp.einsum('nld,nlm->ndm', k_, v)
        z = 1.0 / jnp.maximum(jnp.einsum('nld,nd->nl', q_, k_.sum(axis=1)), eps)
        attn = jnp.einsum('nld,ndm->nlm', q_, kv) * z[..., None]
        attn = attn.transpose(1, 0, 2).reshape(L, N, E)
        attn = attn + qn
        out = _ln(attn, g2, b2)
        return _phm(out, oA, oS, ob) + out

    def _L1_xattn_ref(decoder_inputs, encoder_outputs, decoder_times_dist, decoder_encoder_times_dist, dec_self_attn_bias, enc_dec_attn_bias, Wq, Wk, Wv, Wo, Wth, bth, Wto, bto, Wf1, bf1, Wf2, bf2):
        import jax, jax.numpy as jnp
        import numpy as np
        B, F, T = (2, 128, 128)
        D, N, H = (256, 16, 64)
        K = 32
        FILT = 1024
        L = 4
        EPS = 1e-06

        def _glorot(key, shape, fan_in, fan_out):
            lim = np.sqrt(6.0 / (fan_in + fan_out)).astype(np.float32)
            return jax.random.uniform(key, shape, jnp.float32, -lim, lim)

        def _norm(x):
            m = jnp.mean(x, axis=-1, keepdims=True)
            s = jnp.sqrt(jnp.mean((x - m) ** 2, axis=-1, keepdims=True))
            return (x - m) / (s + EPS)

        def _attention(x, src, dist, bias, Wq, Wk, Wv, Wo, Wth, bth, Wto, bto):
            q = jnp.einsum('bfd,dnh->bfnh', x, Wq) * H ** (-0.5)
            k = jnp.einsum('btd,dnh->btnh', src, Wk)
            v = jnp.einsum('btd,dnh->btnh', src, Wv)
            hbias = jax.nn.relu(dist[..., None] @ Wth + bth)
            qs_bias = (hbias @ Wto + bto)[..., 0]
            logits = jnp.einsum('btnh,bfnh->bnft', k, q)
            logits = logits + bias + qs_bias[:, None]
            w = jax.nn.softmax(logits, axis=-1)
            out = jnp.einsum('bnft,btnh->bfnh', w, v)
            return jnp.einsum('bfnh,nhd->bfd', out, Wo)
        x = decoder_inputs
        for i in range(L):
            y = _attention(_norm(x), encoder_outputs, decoder_encoder_times_dist, enc_dec_attn_bias, Wq[i], Wk[i], Wv[i], Wo[i], Wth[i], bth[i], Wto[i], bto[i])
            x = x + y
            y = jax.nn.relu(_norm(x) @ Wf1[i] + bf1[i]) @ Wf2[i] + bf2[i]
            x = x + y
        return _norm(x)

    def _L1_ffn_ref(h, gate_w, w1, b1, w2, b2):
        import jax, jax.numpy as jnp
        import numpy as np
        B, S, D, E, F = (2, 256, 256, 14, 512)
        Bb, Ss, Dd = h.shape
        x = h.reshape(Bb * Ss, Dd)
        logits = x @ gate_w.T
        probs = jax.nn.softmax(logits, axis=-1)
        top2_p, top2_i = jax.lax.top_k(probs, 2)
        w = top2_p / jnp.maximum(top2_p.sum(-1, keepdims=True), 1e-10)
        hh = jnp.einsum('nd,edf->nef', x, w1) + b1
        hh = jax.nn.gelu(hh, approximate=False)
        all_out = jnp.einsum('nef,efd->ned', hh, w2) + b2
        n = jnp.arange(x.shape[0])
        out0 = all_out[n, top2_i[:, 0]]
        out1 = all_out[n, top2_i[:, 1]]
        moe_out = w[:, 0:1] * out0 + w[:, 1:2] * out1
        result = jnp.clip(x + moe_out, -100.0, 100.0).reshape(Bb, Ss, Dd)
        return result
    x = _layernorm(x + _L0_attn_ref(x, L0_attn_ln_w, L0_attn_ln_b, L0_attn_in_w, L0_attn_in_b, L0_attn_conv_w, L0_attn_conv_b, L0_attn_xp_w, L0_attn_dtp_w, L0_attn_dtp_b, L0_attn_A_log, L0_attn_D, L0_attn_out_w, L0_attn_out_b), axis=-1)
    x = _layernorm(x + _L0_xattn_ref(ctx_1024, ctx_1024, x, L0_xattn_Wv, L0_xattn_Wk, L0_xattn_Wq, L0_xattn_Wo, L0_xattn_bo), axis=-1)
    x = _layernorm(x + _L0_ffn_ref(x, L0_ffn_index_b, L0_ffn_index_t, L0_ffn_sw1, L0_ffn_sb1, L0_ffn_sw2, L0_ffn_sb2, L0_ffn_sw3, L0_ffn_sb3, L0_ffn_s_ln_g, L0_ffn_s_ln_b, L0_ffn_sg_w, L0_ffn_sg_b, L0_ffn_eg_w, L0_ffn_eg_b, L0_ffn_exp_bias, L0_ffn_ew1, L0_ffn_eb1, L0_ffn_ew2, L0_ffn_eb2, L0_ffn_ew3, L0_ffn_eb3, L0_ffn_sel_ln_g, L0_ffn_sel_ln_b), axis=-1)
    x = _layernorm(x + _L1_attn_ref(x, L1_attn_qA, L1_attn_qS, L1_attn_qb, L1_attn_kA, L1_attn_kS, L1_attn_kb, L1_attn_vA, L1_attn_vS, L1_attn_vb, L1_attn_oA, L1_attn_oS, L1_attn_ob, L1_attn_g1, L1_attn_b1, L1_attn_g2, L1_attn_b2), axis=-1)
    x = _layernorm(x + _L1_xattn_ref(x, ctx_1024, fside_BxSxS2_0, fside_BxSxS2_0, mask_Bx1x1xS2_ff0, mask_Bx1x1xS2_ff0, L1_xattn_Wq, L1_xattn_Wk, L1_xattn_Wv, L1_xattn_Wo, L1_xattn_Wth, L1_xattn_bth, L1_xattn_Wto, L1_xattn_bto, L1_xattn_Wf1, L1_xattn_bf1, L1_xattn_Wf2, L1_xattn_bf2), axis=-1)
    x = _layernorm(x + _L1_ffn_ref(x, L1_ffn_gate_w, L1_ffn_w1, L1_ffn_b1, L1_ffn_w2, L1_ffn_b2), axis=-1)
    return x

_drawn_inputs = setup_inputs


def setup_inputs(seed=0):
    import zlib

    import numpy as np

    out = dict(_drawn_inputs(seed))
    spreads = {'L0_attn_ln_w': (1.0, 0.6),
     'L0_attn_ln_b': (0.0, 0.8),
     'L0_attn_in_b': (0.0, 0.8),
     'L0_attn_conv_b': (0.0, 0.8),
     'L0_attn_D': (1.0, 0.6),
     'L0_attn_out_b': (0.0, 0.8),
     'L0_xattn_bo': (0.0, 0.1),
     'L0_ffn_sb1': (0.0, 0.1),
     'L0_ffn_sb2': (0.0, 0.1),
     'L0_ffn_sb3': (0.0, 0.1),
     'L0_ffn_s_ln_g': (1.0, 0.2),
     'L0_ffn_s_ln_b': (0.0, 0.1),
     'L0_ffn_eg_b': (0.0, 0.576),
     'L0_ffn_exp_bias': (0.0, 0.1),
     'L0_ffn_eb1': (0.0, 0.341),
     'L0_ffn_eb2': (0.0, 0.373),
     'L0_ffn_eb3': (0.0, 0.343),
     'L0_ffn_sel_ln_g': (1.0, 0.6),
     'L0_ffn_sel_ln_b': (0.0, 0.708),
     'L1_attn_qb': (0.0, 0.8),
     'L1_attn_kb': (0.0, 0.8),
     'L1_attn_vb': (0.0, 0.1),
     'L1_attn_ob': (0.0, 0.1),
     'L1_attn_g1': (1.0, 0.2),
     'L1_attn_b1': (0.0, 0.1),
     'L1_attn_g2': (1.0, 0.2),
     'L1_attn_b2': (0.0, 0.1),
     'L1_xattn_bth': (0.0, 0.8),
     'L1_xattn_bto': (0.0, 2.0),
     'L1_xattn_bf1': (0.0, 0.1),
     'L1_xattn_bf2': (0.0, 0.1),
     'L1_ffn_b1': (0.0, 0.335),
     'L1_ffn_b2': (0.0, 0.1)}
    factors = {'fside_BxSxS2_0': 3.675,
     'L0_attn_in_w': 6.672,
     'L0_attn_conv_w': 8.0,
     'L0_attn_xp_w': 8.0,
     'L0_attn_dtp_w': 8.0,
     'L0_attn_dtp_b': 8.0,
     'L0_attn_A_log': 8.0,
     'L0_attn_out_w': 6.431,
     'L0_ffn_sg_w': 23.743,
     'L1_attn_qA': 8.0,
     'L1_attn_qS': 8.0,
     'L1_attn_kA': 8.0,
     'L1_attn_kS': 8.0,
     'L1_attn_vA': 5.094,
     'L1_attn_vS': 5.27,
     'L1_attn_oA': 3.082,
     'L1_attn_oS': 3.427,
     'L1_xattn_Wth': 4.289,
     'L1_xattn_Wto': 3.324}
    for name, (base, spread) in spreads.items():
        noise = np.random.default_rng([zlib.crc32(name.encode()), seed]).standard_normal(out[name].shape)
        drawn = base * np.exp(spread * noise) if base else spread * noise
        out[name] = jnp.asarray(drawn.astype(out[name].dtype))
    for name, factor in factors.items():
        out[name] = (out[name] * factor).astype(out[name].dtype)
    return out
```

```python
import math
from contextlib import ExitStack

import numpy as np

import concourse.bass as bass
from concourse import mybir

P = 128
F32 = mybir.dt.float32
BF16 = mybir.dt.bfloat16
I32 = mybir.dt.int32
U32 = mybir.dt.uint32
ALU = mybir.AluOpType
ACT = mybir.ActivationFunctionType
AX = mybir.AxisListType.X

B, S, D = 8, 256, 256
TOK = B * S
DT = D // P
ST = S // P
NT = TOK // P
NORM_FLOOR = 1e-19


class Signal:

    def __init__(self, sem, per=0, ahead=0):
        self.sem, self.per, self.ahead = sem, per, ahead

    def open(self, eng):
        eng.sem_inc(self.sem, self.ahead)

    def at(self, n, i=0):
        return self.sem, i * self.per + (n + self.ahead)


class Chain:

    def __init__(self, eng, signal, i=0, started=None):
        self.eng, self.step, self.i, self.n, self.started = eng, signal, i, 0, started

    def __call__(self, instruction, by_itself=False):
        self.n += 1
        instruction.then_inc(self.step.sem, 1)
        if by_itself:
            alone(self.eng, *self.step.at(self.n, self.i), self.started)
        else:
            self.eng.wait_ge(*self.step.at(self.n, self.i))

    def close(self):
        assert self.n == self.step.per, (self.step.sem, self.n)


class Room:

    def __init__(self, nc, ctx, prefix):
        self.nc, self.ctx, self.prefix = nc, ctx, prefix
        self.semaphores = []
        ctx.callback(self.clear)

    def clear(self):
        self.nc.clear_and_free_semaphores(self.semaphores)
        self.nc.all_engine_barrier()

    def sb(self, name, shape, dt=F32):
        return self.ctx.enter_context(self.nc.sbuf_tensor(f"{self.prefix}_{name}", shape, dt))

    def ps(self, name, shape, dt=F32):
        return self.ctx.enter_context(self.nc.psum_tensor(f"{self.prefix}_{name}", shape, dt))

    def counter(self, name, per=0, ahead=0):
        self.semaphores.append(self.nc.alloc_semaphore(f"{self.prefix}_{name}"))
        return Signal(self.semaphores[-1], per, ahead)


def alone(eng, sem, value, started):
    if not isinstance(value, int):
        value = eng.to_reg(value)
        eng.wait_ge(started.sem, 1)
    eng.wait_ge(sem, value)


class Norm:

    def __init__(self, room, name, tiles, per=1):
        self.tiles = tiles
        self.stats = room.sb(name + "_stats", [P, tiles, 6])
        self.mv = room.sb(name + "_mv", [P, tiles, 2])
        self.var = room.sb(name + "_var", [P, tiles])
        self.logv = room.sb(name + "_logv", [P, tiles])
        self.guess = room.sb(name + "_guess", [P, tiles])
        self.work = room.sb(name + "_work", [P, tiles])
        self.rstd = room.sb(name + "_rstd", [P, tiles])
        self.var_ready = room.counter(name + "_var_ready", per)
        self.log_ready = room.counter(name + "_log_ready", per)
        self.guess_ready = room.counter(name + "_guess_ready", per)

    def mean(self, t):
        return self.mv[:, t, 0:1]

    def r(self, t):
        return self.rstd[:, t:t + 1]

    def vector(self, dve, chain, x, eps, n=1, i=0):
        for t in range(self.tiles):
            last = dve.bn_stats(self.stats[:, t, :], x(t))
        chain(last, by_itself=True)
        for t in range(self.tiles):
            last = dve.bn_aggr(self.mv[:, t, :], self.stats[:, t, :])
        chain(last)
        dve.tensor_scalar(self.var[:], self.mv[:, :, 1], eps, NORM_FLOOR, ALU.add, ALU.max).then_inc(
            self.var_ready.sem, 1)
        dve.wait_ge(*self.guess_ready.at(n, i))
        dve.wait_ge(*self.var_ready.at(n, i))
        chain(dve.tensor_tensor(self.work[:], self.var[:], self.guess[:], ALU.mult))
        chain(dve.tensor_tensor(self.work[:], self.work[:], self.guess[:], ALU.mult))
        chain(dve.tensor_scalar(self.work[:], self.work[:], -0.5, 1.5, ALU.mult, ALU.add))
        chain(dve.tensor_tensor(self.rstd[:], self.guess[:], self.work[:], ALU.mult))


    def scalar(self, act, n=1, i=0):
        act.wait_ge(*self.var_ready.at(n, i))
        act.activation(self.logv[:], self.var[:], ACT.Ln).then_inc(self.log_ready.sem, 1)
        act.wait_ge(*self.log_ready.at(n, i))
        act.activation(self.guess[:], self.logv[:], ACT.Exp, scale=-0.5).then_inc(self.guess_ready.sem, 1)


class Attention:

    HEADS, GROUP = 16, 4

    def __init__(self, room, head_rows, depth, value, scale, biased):
        self.head_rows, self.depth, self.value, self.scale, self.biased = head_rows, depth, value, scale, biased
        self.groups = self.HEADS // self.GROUP
        self.mtiles = self.GROUP * head_rows // P
        m = room
        self.qT = m.sb("qT", [P, 2, self.mtiles, S])
        self.kT = m.sb("kT", [P, 2, self.mtiles, S])
        self.v = m.sb("v", [P, 2, ST, self.GROUP * value])
        self.logit = m.sb("logit", [P, 2, ST, S]) if biased else None
        self.neg_max = m.sb("neg_max", [P, 2, ST])
        self.prob = m.sb("prob", [P, 2, ST, S])
        self.row_sum = m.sb("row_sum", [P, ST, self.HEADS])
        self.row_inv = m.sb("row_inv", [P, ST, self.HEADS])
        self.pT = m.sb("pT", [P, 2, ST, S])
        self.o = m.sb("o", [P, ST, self.HEADS * value])
        self.features = self.HEADS * value // P
        self.oT = m.sb("oT", [P, self.features, S])
        self.psS = [m.ps(f"psS{n}", [P, ST, S]) for n in range(2)]
        self.psT = [m.ps(f"psT{n}", [P, ST, S]) for n in range(2)]
        self.psO = [m.ps(f"psO{n}", [P, 512]) for n in range(2)]
        self.psA = m.ps("psA", [P, 512])
        self.psB = m.ps("psB", [P, 512])
        g, h = self.groups, self.HEADS
        self.projected = m.counter("projected", 3 * g, ahead=3 * g)
        self.q_kept = m.counter("q_kept", g)
        self.k_kept = m.counter("k_kept", g)
        self.v_kept = m.counter("v_kept", g)
        self.scored = m.counter("scored", h)
        self.bias_added = m.counter("bias_added", h, ahead=h)
        self.max_ready = m.counter("max_ready", h)
        self.exp_done = m.counter("exp_done", h)
        self.turned = m.counter("turned", h)
        self.pT_kept = m.counter("pT_kept", h)
        self.weighed = m.counter("weighed", h)
        self.inv_ready = m.counter("inv_ready", g)
        self.o_kept = m.counter("o_kept", g)
        self.o_turned = m.counter("o_turned", self.features // 2)
        self.oT_kept = m.counter("oT_kept", self.features // 2)
        self.projected_out = m.counter("projected_out", 1)

    def open(self, pe=None, dve=None):
        if pe is not None:
            self.projected.open(pe)
        if dve is not None:
            self.bias_added.open(dve)

    def head_at(self, h):
        row = (h % self.GROUP) * self.head_rows
        return row // P, row % P

    def tensor(self, pe, ident, project_q, project_k, project_v, w_out, i):
        def project(g):
            if g >= 1:
                pe.wait_ge(*self.v_kept.at(g, i))
            project_q(g, self.psA).then_inc(self.projected.sem, 1)
            if g >= 1:
                pe.wait_ge(*self.k_kept.at(g, i))
            project_k(g, self.psB).then_inc(self.projected.sem, 1)
            pe.wait_ge(*self.q_kept.at(g + 1, i))
            project_v(g, self.psA).then_inc(self.projected.sem, 1)

        def scores(h):
            g = h // self.GROUP
            if h % self.GROUP == 0:
                pe.wait_ge(*self.q_kept.at(g + 1, i))
                pe.wait_ge(*self.k_kept.at(g + 1, i))
            if h >= 2:
                pe.wait_ge(*(self.bias_added if self.biased else self.exp_done).at(h - 1, i))
            mt, row = self.head_at(h)
            for qt in range(ST):
                last = pe.matmul(self.psS[h % 2][:, qt, :],
                                 self.qT[row:row + self.depth, g % 2, mt, qt * P:(qt + 1) * P],
                                 self.kT[row:row + self.depth, g % 2, mt, :], start=True, stop=True)
            last.then_inc(self.scored.sem, 1)

        def turn(h):
            pe.wait_ge(*self.exp_done.at(h + 1, i))
            if h >= 2:
                pe.wait_ge(*self.pT_kept.at(h - 1, i))
            for kt in range(ST):
                for qt in range(ST):
                    last = pe.transpose(self.psT[h % 2][:, kt, qt * P:(qt + 1) * P],
                                        self.prob[:, h % 2, qt, kt * P:(kt + 1) * P], ident[:])
            last.then_inc(self.turned.sem, 1)

        def weigh(h):
            g, j = h // self.GROUP, h % self.GROUP
            if j == 0:
                pe.wait_ge(*self.v_kept.at(g + 1, i))
                if g >= 2:
                    pe.wait_ge(*self.o_kept.at(g - 1, i))
            pe.wait_ge(*self.pT_kept.at(h + 1, i))
            out = self.psO[g % 2][:, 0:ST * self.GROUP * self.value].rearrange("p (t d) -> p t d", t=ST)
            for qt in range(ST):
                for kt in range(ST):
                    last = pe.matmul(out[:, qt, j * self.value:(j + 1) * self.value],
                                     self.pT[:, h % 2, kt, qt * P:(qt + 1) * P],
                                     self.v[:, g % 2, kt, j * self.value:(j + 1) * self.value],
                                     start=(kt == 0), stop=(kt == ST - 1))
            last.then_inc(self.weighed.sem, 1)

        project(0)
        for h in range(self.HEADS + 2):
            if h < self.HEADS:
                scores(h)
            if 1 <= h <= self.HEADS:
                turn(h - 1)
            if h >= 2:
                weigh(h - 2)
            if h % self.GROUP == 1 and h // self.GROUP + 1 < self.groups:
                project(h // self.GROUP + 1)
        for j in range(self.features // 2):
            pe.wait_ge(*self.o_kept.at(-(-self.groups * (2 * j + 2) // self.features), i))
            if j >= 2:
                pe.wait_ge(*self.oT_kept.at(j - 1, i))
            for f in range(2):
                for qt in range(ST):
                    last = pe.transpose(self.psT[j % 2][:, f, qt * P:(qt + 1) * P],
                                        self.o[:, qt, (2 * j + f) * P:(2 * j + f + 1) * P], ident[:])
            last.then_inc(self.o_turned.sem, 1)
        pe.wait_ge(*self.oT_kept.at(self.features // 2, i))
        out = self.psA[:].rearrange("p (t d) -> p t d", t=ST)
        for qt in range(ST):
            for f in range(self.features):
                last = pe.matmul(out[:, qt, :], self.oT[:, f, qt * P:(qt + 1) * P], w_out[:, f, :],
                                 start=(f == 0), stop=(f == self.features - 1))
        last.then_inc(self.projected_out.sem, 1)

    def scalar(self, act, i):
        def keep_qk(g):
            act.wait_ge(*self.projected.at(3 * g + 1, i))
            act.activation(self.qT[:, g % 2], self.psA[:, 0:self.mtiles * S].rearrange("p (m q) -> p m q", q=S),
                           ACT.Copy, scale=self.scale).then_inc(self.q_kept.sem, 1)
            act.wait_ge(*self.projected.at(3 * g + 2, i))
            act.activation(self.kT[:, g % 2], self.psB[:, 0:self.mtiles * S].rearrange("p (m q) -> p m q", q=S),
                           ACT.Copy).then_inc(self.k_kept.sem, 1)

        keep_qk(0)
        for h in range(self.HEADS + 1):
            if h < self.HEADS:
                act.wait_ge(*self.max_ready.at(h + 1, i))
                if h >= 2:
                    act.wait_ge(*self.turned.at(h - 1, i))
                source = self.logit[:, h % 2] if self.biased else self.psS[h % 2]
                for qt in range(ST):
                    last = act.activation(self.prob[:, h % 2, qt, :], source[:, qt, :], ACT.Exp,
                                          bias=self.neg_max[:, h % 2, qt:qt + 1],
                                          accum_out=self.row_sum[:, qt, h:h + 1])
                last.then_inc(self.exp_done.sem, 1)
            if h >= 1:
                act.wait_ge(*self.turned.at(h, i))
                if h >= 3:
                    act.wait_ge(*self.weighed.at(h - 2, i))
                act.activation(self.pT[:, (h - 1) % 2], self.psT[(h - 1) % 2][:], ACT.Copy).then_inc(
                    self.pT_kept.sem, 1)
            if h % self.GROUP == 1 and h // self.GROUP + 1 < self.groups:
                keep_qk(h // self.GROUP + 1)
        for j in range(self.features // 2):
            act.wait_ge(*self.o_turned.at(j + 1, i))
            act.activation(self.oT[:, 2 * j:2 * j + 2, :], self.psT[j % 2][:], ACT.Copy).then_inc(self.oT_kept.sem, 1)

    def vector(self, dve, i, bias=None):
        def keep_v(g):
            dve.wait_ge(*self.projected.at(3 * g + 3, i))
            width = ST * self.GROUP * self.value
            dve.tensor_copy(self.v[:, g % 2], self.psA[:, 0:width].rearrange("p (t d) -> p t d", t=ST)).then_inc(
                self.v_kept.sem, 1)

        def normalise(g):
            dve.wait_ge(*self.exp_done.at(self.GROUP * (g + 1), i))
            heads = slice(self.GROUP * g, self.GROUP * (g + 1))
            dve.reciprocal(self.row_inv[:, :, heads], self.row_sum[:, :, heads]).then_inc(self.inv_ready.sem, 1)
            dve.wait_ge(*self.weighed.at(self.GROUP * (g + 1), i))
            dve.wait_ge(*self.inv_ready.at(g + 1, i))
            width = self.GROUP * self.value
            for qt in range(ST):
                last = dve.tensor_tensor(
                    self.o[:, qt, g * width:(g + 1) * width].rearrange("p (h d) -> p h d", d=self.value),
                    self.psO[g % 2][:, qt * width:(qt + 1) * width].rearrange("p (h d) -> p h d", d=self.value),
                    self.row_inv[:, qt, heads].unsqueeze(2).to_broadcast([P, self.GROUP, self.value]), ALU.mult)
            last.then_inc(self.o_kept.sem, 1)

        keep_v(0)
        for h in range(self.HEADS):
            dve.wait_ge(*self.scored.at(h + 1, i))
            if h >= 2:
                dve.wait_ge(*self.exp_done.at(h - 1, i))
            source = self.psS[h % 2]
            if self.biased:
                dve.tensor_tensor(self.logit[:, h % 2], self.psS[h % 2][:], bias[:], ALU.add).then_inc(
                    self.bias_added.sem, 1)
                dve.wait_ge(*self.bias_added.at(h + 1, i))
                source = self.logit[:, h % 2]
            dve.tensor_reduce(self.neg_max[:, h % 2, :], source[:], AX, ALU.max, negate=True).then_inc(
                self.max_ready.sem, 1)
            if h % self.GROUP == 1 and h // self.GROUP + 1 < self.groups:
                keep_v(h // self.GROUP + 1)
            if h % self.GROUP == self.GROUP - 2 and h > self.GROUP:
                normalise(h // self.GROUP - 1)
        normalise(self.groups - 1)


KD = 32
NL = 4
QUAD = P // KD
UM = 4
UNITS_B = P // QUAD // UM
PARTS = 3
COLS = QUAD * 2 * PARTS


def bias_stage(nc, w, bias_out):
    dT_in = w["distT"].rearrange("b (h p) q -> (b h) p q", p=P)
    dn_in = w["dist"].rearrange("b (t p) (h k) -> b h p t k", p=P, k=P)
    mask_in = w["mask"].rearrange("b (h k) -> (b h) k", k=P)
    out_v = bias_out.rearrange("(l b) (t p) (h k) -> b h p l t k", l=NL, p=P, k=P)
    with ExitStack() as ctx:
        m = Room(nc, ctx, "bias")
        ident = m.sb("ident", [P, P])
        select = m.sb("select", [P, KD, QUAD, KD])
        abw = m.sb("abw", [P, 3, NL])
        neg_b = m.sb("neg_b", [P, NL])
        bto = m.sb("bto", [P, NL])
        coef = m.sb("coef", [P, NL, 2])
        rest = m.sb("rest", [P, NL, 2])
        part = m.sb("part", [P, NL, 2, PARTS], BF16)
        rhs = m.sb("rhs", [P, NL, QUAD, 2, PARTS], BF16)
        ones = m.sb("ones", [P, P], BF16)
        dT = m.sb("dT", [P, S])
        dn = m.sb("dn", [P, ST, P])
        mask = m.sb("mask", [P, P])
        spread = [m.sb(f"spread{n}", [P, UM * S]) for n in range(2)]
        on = [m.sb(f"on{n}", [P, NL, UM * S], BF16) for n in range(2)]
        sums = m.sb("sums", [P, NL * ST, UNITS_B * UM, QUAD, 2])
        t1 = m.sb("t1", [P, NL * ST, P])
        bo = m.sb("bo", [P, NL * ST, P])
        psX = [m.ps(f"psX{n}", [P, UM * S]) for n in range(2)]
        psP = [m.ps(f"psP{n}", [P, 2, 512]) for n in range(2)]
        U = UNITS_B
        const_in = m.counter("const_in")
        prep = m.counter("prep")
        ready = m.counter("ready")
        loaded = m.counter("loaded", 48)
        spread_done = m.counter("spread_done", U)
        copied = m.counter("copied", U, ahead=2)
        on_v = m.counter("on_v", U, ahead=2)
        on_a = m.counter("on_a", U)
        summed = m.counter("summed", U, ahead=U)
        reduced = m.counter("reduced", U, ahead=2)
        combined = m.counter("combined", 1, ahead=1)
        stored = m.counter("stored", 16 * NL, ahead=16 * NL)
        chain = m.counter("chain", 2)

        with nc.Block() as block:
            @block.sync
            def _(sp):
                stored.open(sp)
                sp.dma_start(ident[:], w["ident"]).then_inc(const_in.sem, 16)
                for g in range(QUAD):
                    sp.dma_start(abw[g * KD:(g + 1) * KD], w["abw"]).then_inc(const_in.sem, 16)
                sp.dma_start(bto[:], w["bto"].partition_broadcast(P)).then_inc(const_in.sem, 16)
                with sp.Fori(0, B) as b:
                    for h in range(2):
                        sp.wait_ge(*combined.at(0, b * 2 + h))
                        sp.dma_start(dT[:], dT_in[bass.ds(b * 2 + h, 1)][0]).then_inc(loaded.sem, 16)
                        sp.dma_start(dn[:], dn_in[bass.ds(b, 1)][0][h]).then_inc(loaded.sem, 16)
                        sp.dma_start(mask[:], mask_in[bass.ds(b * 2 + h, 1)][0].partition_broadcast(P)).then_inc(
                            loaded.sem, 16)
                        sp.wait_ge(*combined.at(1, b * 2 + h))
                        for l in range(NL):
                            sp.dma_start(out_v[bass.ds(b, 1)][0][h][:, l], bo[:, 2 * l:2 * l + 2, :]).then_inc(
                                stored.sem, 16)
                sp.wait_ge(*stored.at(0, 2 * B))

            @block.tensor
            def _(pe):
                summed.open(pe)
                pe.wait_ge(*ready.at(1))
                with pe.Fori(0, 2 * B) as i:
                    pe.wait_ge(*loaded.at(48, i))

                    def spread_unit(u):
                        pe.wait_ge(*copied.at(u + 1 - 2, i))
                        for r in range(UM):
                            rows = select[:, u * UM + r].rearrange("p g k -> p (g k)")
                            last = pe.matmul(psX[u % 2][:, r * S:(r + 1) * S], rows, dT[:], start=True, stop=True)
                        last.then_inc(spread_done.sem, 1)

                    def sum_unit(u):
                        pe.wait_ge(*on_v.at(u + 1, i))
                        pe.wait_ge(*on_a.at(u + 1, i))
                        pe.wait_ge(*reduced.at(u + 1 - 2, i))
                        for l in range(NL):
                            for q in range(ST):
                                for r in range(UM):
                                    lq = l * ST + q
                                    col = (lq % 4) * UM * COLS + r * COLS
                                    out = psP[u % 2][:, lq // 4, col:col + COLS]
                                    terms = rhs[:, l].rearrange("p g a c -> p (g a c)")
                                    if l == NL - 1:
                                        pe.matmul(out, ones[:], terms, start=True, stop=False)
                                    last = pe.matmul(out, on[u % 2][:, l, r * S + q * P:r * S + (q + 1) * P], terms,
                                                     start=(l < NL - 1), stop=True)
                        last.then_inc(summed.sem, 1)

                    for u in range(U + 1):
                        if u < U:
                            spread_unit(u)
                        if u > 0:
                            sum_unit(u - 1)

            @block.scalar
            def _(act):
                copied.open(act)
                act.wait_ge(*ready.at(1))
                with act.Fori(0, 2 * B) as i:
                    for u in range(U):
                        act.wait_ge(*spread_done.at(u + 1, i))
                        act.wait_ge(*on_v.at(u + 1 - 2, i))
                        act.activation(spread[u % 2][:], psX[u % 2][:], ACT.Copy).then_inc(copied.sem, 1)
                        act.wait_ge(*copied.at(u + 1, i))
                        act.wait_ge(*summed.at(u + 1 - 2, i))
                        act.activation(on[u % 2][:, NL - 1, :], spread[u % 2][:], ACT.Sign,
                                       scale=abw[:, 0, NL - 1:NL], bias=abw[:, 1, NL - 1:NL]).then_inc(on_a.sem, 1)

            @block.vector
            def _(dve):
                on_v.open(dve)
                reduced.open(dve)
                combined.open(dve)
                link = Chain(dve, prep)
                dve.memset(ones[:], 1.0)
                link(dve.memset(rhs[:], 0.0))
                dve.wait_ge(*const_in.at(16 * 6))
                link(dve.tensor_copy(select[:], ident[:].rearrange("p (g r) -> p r g", g=QUAD).unsqueeze(3).to_broadcast(
                    [P, KD, QUAD, KD])))
                link(dve.tensor_scalar(neg_b[:], abw[:, 1, :], -1.0, None, ALU.mult))
                for n in range(2):
                    link(dve.tensor_tensor(coef[:, :, n], abw[:, n, :], abw[:, 2, :], ALU.mult))
                link(dve.tensor_scalar(coef[:, NL - 1, :], coef[:, NL - 1, :], 0.5, None, ALU.mult))
                link(dve.tensor_copy(rest[:], coef[:]))
                for c in range(PARTS):
                    link(dve.tensor_copy(part[:, :, :, c], rest[:]))
                    if c < PARTS - 1:
                        link(dve.tensor_tensor(rest[:], rest[:], part[:, :, :, c], ALU.subtract))
                for g in range(QUAD):
                    rows = slice(g * KD, (g + 1) * KD)
                    last = dve.tensor_copy(rhs[rows, :, g], part[rows])
                last.then_inc(ready.sem, 1)

                with dve.Fori(0, 2 * B) as i:
                    link = Chain(dve, chain, i)

                    def switch_unit(u):
                        dve.wait_ge(*copied.at(u + 1, i))
                        dve.wait_ge(*summed.at(u + 1 - 2, i))
                        for l in range(NL - 1):
                            last = dve.tensor_scalar(on[u % 2][:, l, :], spread[u % 2][:], abw[:, 0, l:l + 1],
                                                     neg_b[:, l:l + 1], ALU.mult, ALU.is_gt)
                        last.then_inc(on_v.sem, 1)

                    def reduce_unit(u):
                        dve.wait_ge(*summed.at(u + 1, i))
                        src = psP[u % 2][:, :, 0:4 * UM * COLS].rearrange("p n (q x c) -> p n q x c", q=4, c=PARTS)
                        for n in range(2):
                            last = dve.tensor_reduce(
                                sums[:, 4 * n:4 * n + 4, u * UM:(u + 1) * UM].rearrange("p q r g a -> p q (r g a)"),
                                src[:, n], AX, ALU.add)
                        last.then_inc(reduced.sem, 1)

                    for u in range(U + 1):
                        if u < U:
                            switch_unit(u)
                        if u > 0:
                            reduce_unit(u - 1)
                    dve.wait_ge(*reduced.at(U, i))
                    dve.wait_ge(*loaded.at(48, i))
                    dve.wait_ge(*stored.at(0, i))
                    keys = lambda x, lq: x[:, lq].rearrange("p (g r) -> p g r", g=QUAD)
                    for lq in range(NL * ST):
                        last = dve.tensor_tensor(keys(t1, lq), sums[:, lq, :, :, 0].rearrange("p r g -> p g r"),
                                                 dn[:, lq % ST].rearrange("p (g r) -> p g r", g=QUAD), ALU.mult)
                    link(last)
                    for lq in range(NL * ST):
                        last = dve.scalar_tensor_tensor(
                            out=keys(t1, lq), in0=keys(t1, lq), scalar=bto[:, lq // ST:lq // ST + 1],
                            in1=sums[:, lq, :, :, 1].rearrange("p r g -> p g r"), op0=ALU.add, op1=ALU.add)
                    link(last)
                    dve.tensor_tensor(bo[:], t1[:], mask[:].unsqueeze(1).to_broadcast([P, NL * ST, P]),
                                      ALU.add).then_inc(combined.sem, 1)
                    link.close()


INNER, NST, RANK, TAPS = 512, 16, 64, 4
IT = INNER // P
PRM = RANK + 2 * NST
LOG1P = (2.0, 0.6666664033669932, 0.40007560644854595, 0.2823661980652396, 0.26851498016560554)


def scan_stage(nc, x_in, w, x_out):
    batches_in = x_in.rearrange("(b t p) d -> b p t d", p=P, t=ST)
    batches_out = x_out.rearrange("(b t p) d -> b p t d", p=P, t=ST)
    with ExitStack() as ctx:
        m = Room(nc, ctx, "ssm")
        ident = m.sb("ident", [P, P])
        ones = m.sb("ones", [1, P])
        ln_wb = m.sb("ln_wb", [P, DT, 2])
        in_w = m.sb("in_w", [P, DT, 2 * INNER])
        in_b = m.sb("in_b", [P, 2 * IT])
        taps = m.sb("taps", [P, IT, TAPS + 1])
        xp_w = m.sb("xp_w", [P, IT, PRM])
        dtp_w = m.sb("dtp_w", [RANK, INNER])
        dtp_b = m.sb("dtp_b", [P, IT])
        a = m.sb("a", [P, IT, NST])
        skip = m.sb("skip", [P, IT])
        out_w = m.sb("out_w", [P, IT, D])
        out_b = m.sb("out_b", [1, D])
        x = m.sb("x", [P, ST, D])
        hn = m.sb("hn", [P, ST, D])
        hT = m.sb("hT", [P, DT, S])
        line = m.sb("line", [P, IT, TAPS - 1 + S])
        gate = m.sb("gate", [P, IT, S])
        conv = m.sb("conv", [P, IT, S])
        sig_c = m.sb("sig_c", [P, IT, S])
        sig_g = m.sb("sig_g", [P, IT, S])
        u = m.sb("u", [P, IT, S])
        params = m.sb("params", [PRM, S])
        dtr = m.sb("dtr", [P, IT, S])
        soft = m.sb("soft", [P, IT, S])
        ratio = m.sb("ratio", [P, IT, S])
        square = m.sb("square", [P, IT, S])
        dt = m.sb("dt", [P, IT, S])
        dtu = m.sb("dtu", [P, IT, S])
        rowsB = m.sb("rowsB", [P, NST, S])
        rowsC = m.sb("rowsC", [P, NST, S])
        decay = [m.sb(f"decay{n}", [P, NST, S]) for n in range(2)]
        state = [m.sb(f"state{n}", [P, NST, S]) for n in range(2)]
        y = m.sb("y", [P, IT, S])
        xo = m.sb("xo", [P, ST, D])
        bank = [m.ps(f"bank{n}", [P, 2, S]) for n in range(8)]
        norm_in, norm_out = Norm(m, "norm_in", ST), Norm(m, "norm_out", ST)
        started = m.counter("started", ahead=1)
        const_in = m.counter("const_in")
        a_exp = m.counter("a_exp")
        loaded = m.counter("loaded", 16)
        stored = m.counter("stored", 16, ahead=16)
        chain = m.counter("chain", 31)
        setup = m.counter("setup")
        normed = m.counter("normed", 1)
        n_turned = m.counter("n_turned", 1)
        nT_kept = m.counter("nT_kept", 1)
        projected = m.counter("projected", 4)
        proj_kept = m.counter("proj_kept", 4)
        conv_done = m.counter("conv_done", 1)
        gate_exp = m.counter("gate_exp", 1)
        conv_exp = m.counter("conv_exp", 1)
        u_ready = m.counter("u_ready", 1)
        params_done = m.counter("params_done", 1)
        params_kept = m.counter("params_kept", 1)
        dt_done = m.counter("dt_done", 1)
        abs_ready = m.counter("abs_ready", 1)
        soft_exp = m.counter("soft_exp", 1)
        dt_ready = m.counter("dt_ready", 1)
        rows_spread = m.counter("rows_spread", NST)
        rows_kept = m.counter("rows_kept", NST)
        decayed = m.counter("decayed", IT)
        driven = m.counter("driven", IT)
        scanned = m.counter("scanned", IT)
        read_out = m.counter("read_out", IT)
        added = m.counter("added", IT)
        skipped = m.counter("skipped", IT)
        y_ready = m.counter("y_ready", IT)
        out_done = m.counter("out_done", 1)
        x_read = m.counter("x_read", 1, ahead=1)
        done = m.counter("done", 1)

        with nc.Block() as block:
            @block.sync
            def _(sp):
                started.open(sp)
                stored.open(sp)
                for dst, src in ((ident, w["ident"]), (ln_wb, w["ln_wb"]), (in_w, w["in_wT"].rearrange("(k p) n -> p k n", p=P)),
                                 (in_b, w["in_b_cols"]), (taps, w["taps"]),
                                 (xp_w, w["xp_wT"].rearrange("(k p) n -> p k n", p=P)), (dtp_w, w["dtp_wT"]),
                                 (dtp_b, w["dtp_b_cols"]), (a, w["A_log"].rearrange("(k p) n -> p k n", p=P)),
                                 (skip, w["D_cols"]), (out_w, w["out_wT"].rearrange("(k p) n -> p k n", p=P)),
                                 (out_b, w["out_b"].rearrange("(a n) -> a n", a=1))):
                    sp.dma_start(dst[:], src).then_inc(const_in.sem, 16)
                with sp.Fori(0, B) as b:
                    sp.wait_ge(*x_read.at(0, b))
                    sp.dma_start(x[:], batches_in[bass.ds(b, 1)][0]).then_inc(loaded.sem, 16)
                    sp.wait_ge(*done.at(1, b))
                    sp.dma_start(batches_out[bass.ds(b, 1)][0], xo[:]).then_inc(stored.sem, 16)
                sp.wait_ge(*stored.at(0, B))

            @block.tensor
            def _(pe):
                pe.wait_ge(*const_in.at(16 * 12))
                with pe.Fori(0, B) as b:
                    pe.wait_ge(*normed.at(1, b))
                    for k in range(DT):
                        for t in range(ST):
                            last = pe.transpose(bank[0][:, k, t * P:(t + 1) * P], hn[:, t, k * P:(k + 1) * P], ident[:])
                    last.then_inc(n_turned.sem, 1)
                    pe.wait_ge(*nT_kept.at(1, b))
                    for j in range(2 * IT):
                        for k in range(DT):
                            last = pe.matmul(bank[1 + j // 2][:, j % 2, :], in_w[:, k, j * P:(j + 1) * P], hT[:, k, :],
                                             start=(k == 0), stop=(k == DT - 1))
                        if j % 2:
                            last.then_inc(projected.sem, 1)
                    pe.wait_ge(*u_ready.at(1, b))
                    for k in range(IT):
                        last = pe.matmul(bank[5][0:PRM, 0, :], xp_w[:, k, :], u[:, k, :], start=(k == 0), stop=(k == IT - 1))
                    last.then_inc(params_done.sem, 1)
                    pe.wait_ge(*params_kept.at(1, b))
                    for j in range(IT):
                        last = pe.matmul(bank[6 + j // 2][:, j % 2, :], dtp_w[:, j * P:(j + 1) * P], params[0:RANK, :],
                                         start=True, stop=True)
                    last.then_inc(dt_done.sem, 1)
                    for n in range(NST):
                        if n >= 4:
                            pe.wait_ge(*rows_kept.at(n - 3, b))
                        for c in range(2):
                            row = RANK + 2 * n + c
                            last = pe.matmul(bank[1 + n % 4][:, c, :], ident[0:PRM, row:row + 1].to_broadcast([PRM, P]),
                                             params[:], start=True, stop=True)
                        last.then_inc(rows_spread.sem, 1)
                    for j in range(IT):
                        pe.wait_ge(*read_out.at(j + 1, b))
                        if j == 0:
                            pe.wait_ge(*params_kept.at(1, b))
                        if j >= 2:
                            pe.wait_ge(*skipped.at(j - 1, b))
                        out = bank[(5, 0)[j % 2]][:, 0, :]
                        for n in range(NST):
                            last = pe.matmul(out, ident[:], state[j % 2][:, n, :], start=(n == 0), stop=(n == NST - 1))
                        last.then_inc(added.sem, 1)
                    pe.wait_ge(*y_ready.at(IT, b))
                    for t in range(ST):
                        for k in range(IT):
                            pe.matmul(bank[1][:, t, :], y[:, k, t * P:(t + 1) * P], out_w[:, k, :],
                                      start=(k == 0), stop=False)
                        last = pe.matmul(bank[1][:, t, :], ones[:], out_b[:], start=False, stop=True)
                    last.then_inc(out_done.sem, 1)

            @block.scalar
            def _(act):
                act.wait_ge(*const_in.at(16 * 12))
                act.activation(a[:], a[:], ACT.Exp).then_inc(a_exp.sem, 1)
                with act.Fori(0, B) as b:
                    norm_in.scalar(act, 1, b)
                    act.wait_ge(*n_turned.at(1, b))
                    for k in range(DT):
                        last = act.activation(hT[:, k, :], bank[0][:, k, :], ACT.Identity, scale=ln_wb[:, k, 0:1],
                                              bias=ln_wb[:, k, 1:2])
                    last.then_inc(nT_kept.sem, 1)
                    for n in range(4):
                        act.wait_ge(*projected.at(n + 1, b))
                        for c in range(2):
                            j = 2 * n + c
                            out = line[:, j, TAPS - 1:] if j < IT else gate[:, j - IT, :]
                            last = act.activation(out, bank[1 + n][:, c, :], ACT.Identity, bias=in_b[:, j:j + 1])
                        last.then_inc(proj_kept.sem, 1)
                    act.wait_ge(*proj_kept.at(4, b))
                    act.activation(sig_g[:], gate[:], ACT.Exp, scale=-1.0).then_inc(gate_exp.sem, 1)
                    act.wait_ge(*conv_done.at(1, b))
                    act.activation(sig_c[:], conv[:], ACT.Exp, scale=-1.0).then_inc(conv_exp.sem, 1)
                    act.wait_ge(*params_done.at(1, b))
                    act.activation(params[:], bank[5][0:PRM, 0, :], ACT.Copy).then_inc(params_kept.sem, 1)
                    act.wait_ge(*abs_ready.at(1, b))
                    act.activation(soft[:], soft[:], ACT.Exp, scale=-1.0).then_inc(soft_exp.sem, 1)
                    for n in range(NST):
                        act.wait_ge(*rows_spread.at(n + 1, b))
                        rows, r = (rowsB, 2 * n) if n < NST // 2 else (rowsC, 2 * n - NST)
                        act.activation(rows[:, r:r + 2, :], bank[1 + n % 4][:], ACT.Copy).then_inc(rows_kept.sem, 1)
                    act.wait_ge(*dt_ready.at(1, b))
                    for j in range(IT):
                        if j >= 2:
                            act.wait_ge(*scanned.at(j - 1, b))
                        for n in range(NST):
                            last = act.activation(decay[j % 2][:, n, 1:], dt[:, j, 1:], ACT.Exp, scale=a[:, j, n:n + 1])
                        last.then_inc(decayed.sem, 1)
                    norm_out.scalar(act, 1, b)

            @block.gpsimd
            def _(pool):
                with pool.Fori(0, B) as b:
                    for j in range(IT):
                        pool.wait_ge(*scanned.at(j + 1, b))
                        pool.wait_ge(*rows_kept.at(NST, b))
                        pool.tensor_tensor(state[j % 2][:], state[j % 2][:], rowsC[:], ALU.mult).then_inc(
                            read_out.sem, 1)

            @block.vector
            def _(dve):
                link = Chain(dve, setup)
                x_read.open(dve)
                dve.memset(ones[:], 1.0)
                dve.memset(line[:], 0.0)
                for n in range(2):
                    dve.memset(decay[n][:, :, 0:1], 0.0)
                dve.wait_ge(*a_exp.at(1))
                link(dve.tensor_scalar(a[:], a[:], -1.0, None, ALU.mult))
                with dve.Fori(0, B) as b:
                    link = Chain(dve, chain, b, started)
                    dve.wait_ge(*loaded.at(16, b))
                    norm_in.vector(dve, link, lambda t: x[:, t, :], 1e-5, 1, b)
                    for t in range(ST):
                        last = dve.tensor_scalar(hn[:, t, :], x[:, t, :], norm_in.mean(t), norm_in.r(t),
                                                 ALU.subtract, ALU.mult)
                    last.then_inc(normed.sem, 1)
                    dve.wait_ge(*proj_kept.at(2, b))
                    for j in range(IT):
                        last = dve.tensor_scalar(conv[:, j, :], line[:, j, 0:S], taps[:, j, 0:1], taps[:, j, TAPS:TAPS + 1],
                                                 ALU.mult, ALU.add)
                    link(last)
                    for k in range(1, TAPS):
                        for j in range(IT):
                            last = dve.scalar_tensor_tensor(out=conv[:, j, :], in0=line[:, j, k:k + S],
                                                            scalar=taps[:, j, k:k + 1], in1=conv[:, j, :],
                                                            op0=ALU.mult, op1=ALU.add)
                        if k < TAPS - 1:
                            link(last)
                        else:
                            last.then_inc(conv_done.sem, 1)
                    for src, sig, exp_done in ((conv, sig_c, conv_exp), (gate, sig_g, gate_exp)):
                        dve.wait_ge(*exp_done.at(1, b))
                        link(dve.tensor_scalar(sig[:], sig[:], 1.0, None, ALU.add))
                        link(dve.reciprocal(sig[:], sig[:]))
                        if src is conv:
                            dve.tensor_tensor(u[:], conv[:], sig[:], ALU.mult).then_inc(u_ready.sem, 1)
                        else:
                            link(dve.tensor_tensor(sig[:], gate[:], sig[:], ALU.mult))
                    dve.wait_ge(*dt_done.at(1, b))
                    for j in range(IT):
                        last = dve.tensor_scalar(dtr[:, j, :], bank[6 + j // 2][:, j % 2, :], dtp_b[:, j:j + 1], None, ALU.add)
                    link(last)
                    dve.scalar_tensor_tensor(out=soft[:], in0=dtr[:], scalar=-1.0, in1=dtr[:], op0=ALU.mult,
                                             op1=ALU.max).then_inc(abs_ready.sem, 1)
                    dve.wait_ge(*soft_exp.at(1, b))
                    link(dve.tensor_scalar(ratio[:], soft[:], 2.0, None, ALU.add))
                    link(dve.reciprocal(ratio[:], ratio[:]))
                    link(dve.tensor_tensor(ratio[:], ratio[:], soft[:], ALU.mult))
                    link(dve.tensor_tensor(square[:], ratio[:], ratio[:], ALU.mult))
                    link(dve.tensor_scalar(soft[:], square[:], LOG1P[-1], None, ALU.mult))
                    for c in reversed(LOG1P[1:-1]):
                        link(dve.scalar_tensor_tensor(out=soft[:], in0=soft[:], scalar=c, in1=square[:],
                                                      op0=ALU.add, op1=ALU.mult))
                    link(dve.scalar_tensor_tensor(out=soft[:], in0=soft[:], scalar=LOG1P[0], in1=ratio[:],
                                                  op0=ALU.add, op1=ALU.mult))
                    dve.scalar_tensor_tensor(out=dt[:], in0=dtr[:], scalar=0.0, in1=soft[:], op0=ALU.max,
                                             op1=ALU.add).then_inc(dt_ready.sem, 1)
                    dve.wait_ge(*dt_ready.at(1, b))
                    link(dve.tensor_tensor(dtu[:], dt[:], u[:], ALU.mult))
                    dve.wait_ge(*rows_kept.at(NST // 2, b))

                    def finish(j):
                        dve.wait_ge(*added.at(j + 1, b))
                        dve.scalar_tensor_tensor(out=y[:, j, :], in0=u[:, j, :], scalar=skip[:, j:j + 1],
                                                 in1=bank[(5, 0)[j % 2]][:, 0, :], op0=ALU.mult, op1=ALU.add).then_inc(
                            skipped.sem, 1)
                        dve.wait_ge(*skipped.at(j + 1, b))
                        dve.tensor_tensor(y[:, j, :], y[:, j, :], sig_g[:, j, :], ALU.mult).then_inc(y_ready.sem, 1)

                    for j in range(IT):
                        if j >= 2:
                            dve.wait_ge(*added.at(j - 1, b))
                        dve.tensor_tensor(state[j % 2][:], rowsB[:], dtu[:, j, :].unsqueeze(1).to_broadcast([P, NST, S]),
                                          ALU.mult).then_inc(driven.sem, 1)
                        dve.wait_ge(*decayed.at(j + 1, b))
                        dve.wait_ge(*driven.at(j + 1, b))
                        flat = lambda t: t[j % 2][:].rearrange("p n s -> p (n s)")
                        dve.tensor_tensor_scan(flat(state), flat(decay), flat(state), 0.0, ALU.mult, ALU.add).then_inc(
                            scanned.sem, 1)
                        if j >= 1:
                            finish(j - 1)
                    finish(IT - 1)
                    dve.wait_ge(*out_done.at(1, b))
                    dve.wait_ge(*stored.at(0, b))
                    dve.scalar_tensor_tensor(out=xo[:], in0=x[:], scalar=2.0, in1=bank[1][:], op0=ALU.mult,
                                             op1=ALU.add).then_inc(x_read.sem, 1)
                    dve.wait_ge(*x_read.at(1, b))
                    norm_out.vector(dve, link, lambda t: xo[:, t, :], 1e-5, 1, b)
                    for t in range(ST):
                        last = dve.tensor_scalar(xo[:, t, :], xo[:, t, :], norm_out.mean(t), norm_out.r(t),
                                                 ALU.subtract, ALU.mult)
                    last.then_inc(done.sem, 1)
                    link.close()


XD = 16
XP = 32


def cross_stage(nc, x_in, w, x_out):
    batches_in = x_in.rearrange("(b t p) d -> b p t d", p=P, t=ST)
    batches_out = x_out.rearrange("(b t p) d -> b p t d", p=P, t=ST)
    with ExitStack() as ctx:
        m = Room(nc, ctx, "xat")
        ident = m.sb("ident", [P, P])
        ones = m.sb("ones", [1, P])
        wqk = m.sb("wqk", [P, 2, 2, P])
        wv = m.sb("wv", [P, P])
        wo = m.sb("wo", [P, DT, D])
        bo = m.sb("bo", [P, D])
        x = m.sb("x", [P, ST, D])
        xT = m.sb("xT", [P, DT, S])
        ctxT = m.sb("ctxT", [P, DT, S])
        xo = m.sb("xo", [P, ST, D])
        at = Attention(m, XP, XD, XD, D ** -0.5, False)
        norm = Norm(m, "norm", ST)
        started = m.counter("started", ahead=1)
        zeroed = m.counter("zeroed")
        const_in = m.counter("const_in")
        x_loaded = m.counter("x_loaded", 16)
        ctx_loaded = m.counter("ctx_loaded", 16)
        x_turned = m.counter("x_turned", 1)
        xT_kept = m.counter("xT_kept", 1)
        summed = m.counter("summed", 1, ahead=1)
        chain = m.counter("chain", 7)
        done = m.counter("done", 1)
        stored = m.counter("stored", 16, ahead=16)

        with nc.Block() as block:
            @block.sync
            def _(sp):
                started.open(sp)
                stored.open(sp)
                sp.dma_start(ident[:], w["ident"]).then_inc(const_in.sem, 16)
                sp.dma_start(wo[:], w["WoT"].rearrange("(k p) n -> p k n", p=P)).then_inc(const_in.sem, 16)
                sp.dma_start(bo[:], w["bo"].partition_broadcast(P)).then_inc(const_in.sem, 16)
                sp.wait_ge(*zeroed.at(1))
                for h in range(P // XD):
                    rows = slice(h * XD, (h + 1) * XD)
                    for n, name in enumerate(("WqT", "WkT")):
                        col = (h % 4) * XP
                        sp.dma_start(wqk[rows, n, h // 4, col:col + XD], w[name]).then_inc(const_in.sem, 16)
                    sp.dma_start(wv[rows, h * XD:(h + 1) * XD], w["WvT"]).then_inc(const_in.sem, 16)
                with sp.Fori(0, B) as b:
                    sp.wait_ge(*summed.at(0, b))
                    sp.dma_start(x[:], batches_in[bass.ds(b, 1)][0]).then_inc(x_loaded.sem, 16)
                    sp.wait_ge(*at.projected.at(0, b))
                    sp.dma_start(ctxT[:], w["ctxT"].rearrange("b (k p) s -> b p k s", p=P)[bass.ds(b, 1)][0]).then_inc(
                        ctx_loaded.sem, 16)
                    sp.wait_ge(*done.at(1, b))
                    sp.dma_start(batches_out[bass.ds(b, 1)][0], xo[:]).then_inc(stored.sem, 16)
                sp.wait_ge(*stored.at(0, B))

            @block.tensor
            def _(pe):
                at.open(pe=pe)
                pe.wait_ge(*const_in.at(16 * (3 + 3 * (P // XD))))
                with pe.Fori(0, B) as b:
                    pe.wait_ge(*x_loaded.at(16, b))
                    for k in range(DT):
                        for t in range(ST):
                            last = pe.transpose(at.psT[0][:, k, t * P:(t + 1) * P], x[:, t, k * P:(k + 1) * P], ident[:])
                    last.then_inc(x_turned.sem, 1)
                    pe.wait_ge(*xT_kept.at(1, b))
                    pe.wait_ge(*ctx_loaded.at(16, b))

                    def rows(n, source):
                        return lambda g, bank: pe.matmul(bank[:, 0:S], wqk[:, n, g % 2, :], source[:, g // 2, :],
                                                         start=True, stop=True)

                    def values(g, bank):
                        width = 4 * XD
                        for t in range(ST):
                            last = pe.matmul(bank[:, t * width:(t + 1) * width], ctxT[:, g // 2, t * P:(t + 1) * P],
                                             wv[:, (g % 2) * width:(g % 2 + 1) * width], start=True, stop=True)
                        return last

                    at.tensor(pe, ident, rows(0, xT), rows(1, ctxT), values, wo, b)

            @block.scalar
            def _(act):
                with act.Fori(0, B) as b:
                    act.wait_ge(*x_turned.at(1, b))
                    act.activation(xT[:], at.psT[0][:], ACT.Copy).then_inc(xT_kept.sem, 1)
                    at.scalar(act, b)
                    norm.scalar(act, 1, b)

            @block.vector
            def _(dve):
                summed.open(dve)
                dve.memset(wv[:], 0.0)
                dve.memset(wqk[:], 0.0).then_inc(zeroed.sem, 1)
                dve.wait_ge(*const_in.at(16 * (3 + 3 * (P // XD))))
                with dve.Fori(0, B) as b:
                    link = Chain(dve, chain, b, started)
                    at.vector(dve, b)
                    dve.wait_ge(*at.projected_out.at(1, b))
                    dve.wait_ge(*stored.at(0, b))
                    dve.tensor_tensor(xo[:], x[:], at.psA[:].rearrange("p (t d) -> p t d", t=ST), ALU.add).then_inc(
                        summed.sem, 1)
                    dve.wait_ge(*summed.at(1, b))
                    link(dve.tensor_tensor(xo[:], xo[:], bo[:].unsqueeze(1).to_broadcast([P, ST, D]), ALU.add))
                    norm.vector(dve, link, lambda t: xo[:, t, :], 1e-5, 1, b)
                    for t in range(ST):
                        last = dve.tensor_scalar(xo[:, t, :], xo[:, t, :], norm.mean(t), norm.r(t),
                                                 ALU.subtract, ALU.mult)
                    last.then_inc(done.sem, 1)
                    link.close()


E8, HID = 8, 128
IDX = 512
GATES = 1 + E8


def moe8_stage(nc, x_in, w, x_out):
    tiles_in = x_in.rearrange("(t p) d -> t p d", p=P)
    tiles_out = x_out.rearrange("(t p) d -> t p d", p=P)
    SL = range(2)
    with ExitStack() as ctx:
        m = Room(nc, ctx, "m8")
        ident = m.sb("ident", [P, P])
        ones = m.sb("ones", [1, P])
        ones_col = m.sb("ones_col", [P, 1], BF16)
        iota = m.sb("iota", [P, TOK])
        named = m.sb("named", [P, IDX // P, TOK], BF16)
        idx = m.sb("idx", [P, 2, IDX // P], I32)
        at_bt = m.sb("at_bt", [P, 2, IDX // P])
        test = m.sb("test", [P, 2, IDX // P])
        inside = m.sb("inside", [P, 2, IDX // P])
        key = m.sb("key", [P, IDX // P])
        hit = m.sb("hit", [P, NT])
        sw12 = m.sb("sw12", [P, DT, 2 * HID])
        sb12 = m.sb("sb12", [1, 2 * HID])
        gates_w = m.sb("gates_w", [P, DT, GATES])
        gates_b = m.sb("gates_b", [1, GATES])
        exp_bias = m.sb("exp_bias", [P, E8])
        ew12 = m.sb("ew12", [P, DT, E8, 2 * HID])
        eb12 = m.sb("eb12", [E8, 2 * HID])
        sw3 = m.sb("sw3", [P, D])
        sb3 = m.sb("sb3", [1, D])
        ew3 = m.sb("ew3", [P, E8, D])
        eb3 = m.sb("eb3", [E8, D])
        gain = m.sb("gain", [P, 2])
        shift = m.sb("shift", [P, 2])
        A = [m.ps(f"A{s}", [P, 512]) for s in SL]
        Bk = [m.ps(f"B{s}", [P, 512]) for s in SL]
        R = [m.ps(f"R{s}", [P, 2, 4, P]) for s in SL]
        const_in = m.counter("const_in")
        idx_in = m.counter("idx_in")
        iota_in = m.counter("iota_in")
        keyed = m.counter("keyed")
        marked = m.counter("marked")
        counted = m.counter("counted")

        with nc.Block() as block:
            @block.sync
            def _(sp):
                for n, name in enumerate(("index_b", "index_t")):
                    sp.dma_start(idx[:, n, :], w[name].rearrange("(p c) -> p c", p=P)).then_inc(idx_in.sem, 16)
                sp.dma_start(iota[:], w["iota_tok"].partition_broadcast(P)).then_inc(iota_in.sem, 16)
                halves = lambda a, b, n: ((slice(0, n), w[a]), (slice(n, 2 * n), w[b]))
                for cols, src in halves("sw1T", "sw2T", HID):
                    sp.dma_start(sw12[:, :, cols], src.rearrange("(k p) h -> p k h", p=P)).then_inc(const_in.sem, 16)
                for cols, src in halves("sb1", "sb2", HID):
                    sp.dma_start(sb12[:, cols], src.rearrange("(a h) -> a h", a=1)).then_inc(const_in.sem, 16)
                sp.dma_start(gates_w[:], w["gates_wT"].rearrange("(k p) h -> p k h", p=P)).then_inc(const_in.sem, 16)
                sp.dma_start(gates_b[:], w["gates_b"].rearrange("(a h) -> a h", a=1)).then_inc(const_in.sem, 16)
                sp.dma_start(exp_bias[:], w["exp_bias"].partition_broadcast(P)).then_inc(const_in.sem, 16)
                for cols, src in halves("ew1T", "ew2T", HID):
                    for k in range(DT):
                        sp.dma_start(ew12[:, k, :, cols], src[:, k * P:(k + 1) * P, :].rearrange("e p h -> p e h")).then_inc(
                            const_in.sem, 16)
                for cols, src in halves("eb1", "eb2", HID):
                    sp.dma_start(eb12[:, cols], src).then_inc(const_in.sem, 16)
                sp.dma_start(sw3[:], w["sw3T"]).then_inc(const_in.sem, 16)
                sp.dma_start(sb3[:], w["sb3"].rearrange("(a h) -> a h", a=1)).then_inc(const_in.sem, 16)
                sp.dma_start(ew3[:], w["ew3T"].rearrange("e h d -> h e d")).then_inc(const_in.sem, 16)
                sp.dma_start(eb3[:], w["eb3"]).then_inc(const_in.sem, 16)
                sp.dma_start(ident[:], w["ident"]).then_inc(const_in.sem, 16)
                sp.dma_start(gain[:], w["gains"]).then_inc(const_in.sem, 16)
                sp.dma_start(shift[:], w["shifts"]).then_inc(const_in.sem, 16)
                sp.wait_ge(*const_in.at(16 * 20))

            @block.vector
            def _(dve):
                link = Chain(dve, keyed)
                dve.memset(ones[:], 1.0)
                dve.memset(ones_col[:], 1.0)
                dve.wait_ge(*idx_in.at(32))
                link(dve.tensor_copy(at_bt[:], idx[:]))
                link(dve.tensor_scalar(test[:], at_bt[:], 0.0, None, ALU.is_lt))
                link(dve.tensor_scalar(test[:, 0], test[:, 0], float(B), None, ALU.mult))
                link(dve.tensor_scalar(test[:, 1], test[:, 1], float(S), None, ALU.mult))
                link(dve.tensor_tensor(at_bt[:], at_bt[:], test[:], ALU.add))
                link(dve.tensor_scalar(inside[:], at_bt[:], 0.0, None, ALU.is_ge))
                link(dve.tensor_scalar(test[:, 0], at_bt[:, 0], float(B), None, ALU.is_lt))
                link(dve.tensor_scalar(test[:, 1], at_bt[:, 1], float(S), None, ALU.is_lt))
                link(dve.tensor_tensor(inside[:], inside[:], test[:], ALU.mult))
                link(dve.tensor_tensor(inside[:, 0], inside[:, 0], inside[:, 1], ALU.mult))
                link(dve.scalar_tensor_tensor(out=key[:], in0=at_bt[:, 0], scalar=float(S), in1=at_bt[:, 1],
                                              op0=ALU.mult, op1=ALU.add))
                link(dve.scalar_tensor_tensor(out=key[:], in0=key[:], scalar=1.0, in1=inside[:, 0],
                                              op0=ALU.add, op1=ALU.mult))
                link(dve.tensor_scalar(key[:], key[:], -1.0, None, ALU.add))
                dve.wait_ge(*iota_in.at(16))
                for c in range(IDX // P):
                    last = dve.tensor_scalar(named[:, c, :], iota[:], key[:, c:c + 1], None, ALU.is_equal)
                last.then_inc(marked.sem, 1)
                dve.wait_ge(*counted.at(1))
                dve.tensor_scalar(hit[:], A[0][:, 0:NT], 0.5, None, ALU.is_gt)

            @block.tensor
            def _(pe):
                pe.wait_ge(*marked.at(1))
                for t in range(NT):
                    for c in range(IDX // P):
                        last = pe.matmul(A[0][:, t:t + 1], named[:, c, t * P:(t + 1) * P], ones_col[:],
                                         start=(c == 0), stop=(c == IDX // P - 1))
                last.then_inc(counted.sem, 1)

        sb = lambda n, shape, dt=F32: [m.sb(f"{n}{s}", shape, dt) for s in SL]
        sig = lambda n, per, ahead=0: [m.counter(f"{n}{s}", per, ahead) for s in SL]
        x, fT, gate_e, gate = sb("x", [P, D]), sb("fT", [P, DT, P]), sb("gate_e", [P, GATES]), sb("gate", [P, GATES])
        biased, best, best_i = sb("biased", [P, E8]), sb("best", [P, 8]), sb("best_i", [P, 8], U32)
        best_f, onehot, chosen = sb("best_f", [P, 8]), sb("onehot", [P, E8]), sb("chosen", [P, E8])
        pair, pair_m, mix = sb("pair", [P, 2]), sb("pair_m", [P, 1]), sb("mix", [P, 2])
        ohT, xTe, u, ue = sb("ohT", [E8, P]), sb("xTe", [P, DT, E8, P]), sb("u", [P, 2, 2 * HID]), sb("ue", [P, 2, HID])
        z, zT, zTe, y = sb("z", [P, 2, HID]), sb("zT", [P, 2, P]), sb("zTe", [P, E8, P]), sb("y", [P, D])
        inner = [Norm(m, f"inner{s}", 2, 1) for s in SL]
        outer = [Norm(m, f"outer{s}", 1, 1) for s in SL]
        started = m.counter("started", ahead=1)
        loaded, stored = sig("loaded", 16), sig("stored", 16, 16)
        x_read, done = sig("x_read", 1, 1), sig("done", 1)
        turned, turned_kept = sig("turned", 2), sig("turned_kept", 2)
        first, gates_kept, gate_exp = sig("first", 1), sig("gates_kept", 1), sig("gate_exp", 1)
        pair_ready, pair_exp = sig("pair_ready", 1), sig("pair_exp", 1)
        routed, rows_done, masked = sig("routed", 1), sig("rows_done", 1), sig("masked", 1)
        hidden, u_ready, u_exp = sig("hidden", 1), sig("u_ready", 1), sig("u_exp", 1)
        z_ready, z_masked, outs = sig("z_ready", 1), sig("z_masked", 1), sig("outs", 1)
        chains = sig("chain", 35)

        with nc.Block() as block:
            @block.sync
            def _(sp):
                started.open(sp)
                for s in SL:
                    stored[s].open(sp)
                with sp.Fori(0, NT // 2) as i:
                    for s in SL:
                        sp.wait_ge(*x_read[s].at(0, i))
                        sp.dma_start(x[s][:], tiles_in[bass.ds(i * 2 + s, 1)][0]).then_inc(loaded[s].sem, 16)
                    for s in SL:
                        sp.wait_ge(*done[s].at(1, i))
                        sp.dma_start(tiles_out[bass.ds(i * 2 + s, 1)][0], y[s][:]).then_inc(stored[s].sem, 16)
                for s in SL:
                    sp.wait_ge(*stored[s].at(0, NT // 2))

            @block.tensor
            def _(pe):
                with pe.Fori(0, NT // 2) as i:
                    for s in SL:
                        pe.wait_ge(*loaded[s].at(16, i))
                        for k in range(DT):
                            last = pe.transpose(A[s][:, k * P:(k + 1) * P], x[s][:, k * P:(k + 1) * P], ident[:])
                        last.then_inc(turned[s].sem, 1)
                    for s in SL:
                        pe.wait_ge(*turned_kept[s].at(1, i))
                        for cols, weight, row in ((slice(0, 2 * HID), sw12, sb12),
                                                  (slice(2 * HID, 2 * HID + GATES), gates_w, gates_b)):
                            for k in range(DT):
                                pe.matmul(Bk[s][:, cols], fT[s][:, k, :], weight[:, k, :], start=(k == 0), stop=False)
                            last = pe.matmul(Bk[s][:, cols], ones[:], row[:], start=False, stop=True)
                        last.then_inc(first[s].sem, 1)
                    for s in SL:
                        pe.wait_ge(*routed[s].at(1, i))
                        for e in range(E8):
                            pe.matmul(R[s][:, e // 4, e % 4, :], onehot[s][:, e:e + 1].to_broadcast([P, P]), ident[:],
                                      start=True, stop=True)
                        pe.transpose(Bk[s][0:E8, 3 * P:4 * P], onehot[s][:], ident[:]).then_inc(rows_done[s].sem, 1)
                    for s in SL:
                        pe.wait_ge(*masked[s].at(1, i))
                        for e in range(E8):
                            for k in range(DT):
                                pe.matmul(A[s][:, 0:2 * HID], xTe[s][:, k, e, :], ew12[:, k, e, :],
                                          start=(e == 0 and k == 0), stop=False)
                        pe.matmul(A[s][:, 0:2 * HID], ohT[s][:], eb12[:], start=False, stop=True).then_inc(
                            hidden[s].sem, 1)
                    for s in SL:
                        pe.wait_ge(*z_ready[s].at(1, i))
                        for n in range(2):
                            last = pe.transpose(A[s][:, (2 + n) * P:(3 + n) * P], z[s][:, n, :], ident[:])
                        last.then_inc(turned[s].sem, 1)
                    for s in SL:
                        pe.wait_ge(*z_masked[s].at(1, i))
                        pe.matmul(Bk[s][:, 0:D], zT[s][:, 0, :], sw3[:], start=True, stop=False)
                        pe.matmul(Bk[s][:, 0:D], ones[:], sb3[:], start=False, stop=True)
                        for e in range(E8):
                            pe.matmul(Bk[s][:, D:2 * D], zTe[s][:, e, :], ew3[:, e, :], start=(e == 0), stop=False)
                        pe.matmul(Bk[s][:, D:2 * D], ohT[s][:], eb3[:], start=False, stop=True).then_inc(outs[s].sem, 1)

            @block.scalar
            def _(act):
                with act.Fori(0, NT // 2) as i:
                    for s in SL:
                        act.wait_ge(*turned[s].at(1, i))
                        act.activation(fT[s][:].rearrange("p k t -> p (k t)"), A[s][:, 0:DT * P], ACT.Copy).then_inc(
                            turned_kept[s].sem, 1)
                    for s in SL:
                        act.wait_ge(*gates_kept[s].at(1, i))
                        act.activation(gate_e[s][:], gate[s][:], ACT.Exp, scale=-1.0).then_inc(gate_exp[s].sem, 1)
                    for s in SL:
                        act.wait_ge(*pair_ready[s].at(1, i))
                        act.activation(pair[s][:], pair[s][:], ACT.Exp).then_inc(pair_exp[s].sem, 1)
                    for s in SL:
                        act.wait_ge(*u_ready[s].at(1, i))
                        act.activation(ue[s][:], u[s][:, :, 0:HID], ACT.Exp, scale=-1.0).then_inc(u_exp[s].sem, 1)
                    for s in SL:
                        inner[s].scalar(act, 1, i)
                    for s in SL:
                        act.wait_ge(*turned[s].at(2, i))
                        for n in range(2):
                            last = act.activation(zT[s][:, n, :], A[s][:, (2 + n) * P:(3 + n) * P], ACT.Identity,
                                                  scale=gain[:, n:n + 1], bias=shift[:, n:n + 1])
                        last.then_inc(turned_kept[s].sem, 1)
                    for s in SL:
                        outer[s].scalar(act, 1, i)

            @block.vector
            def _(dve):
                for s in SL:
                    x_read[s].open(dve)
                with dve.Fori(0, NT // 2) as i:
                    link = [Chain(dve, chains[s], i, started) for s in SL]
                    for s in SL:
                        dve.wait_ge(*first[s].at(1, i))
                        link[s](dve.tensor_copy(u[s][:, 0, :], Bk[s][:, 0:2 * HID]))
                        dve.tensor_copy(gate[s][:], Bk[s][:, 2 * HID:2 * HID + GATES]).then_inc(gates_kept[s].sem, 1)
                    for s in SL:
                        dve.wait_ge(*gate_exp[s].at(1, i))
                        link[s](dve.tensor_scalar(gate_e[s][:], gate_e[s][:], 1.0, None, ALU.add))
                        link[s](dve.reciprocal(gate[s][:], gate_e[s][:]))
                        link[s](dve.tensor_tensor(biased[s][:], gate[s][:, 1:GATES], exp_bias[:], ALU.add), True)
                        link[s](dve.max(best[s][:], biased[s][:]), True)
                        link[s](dve.max_index(best_i[s][:], best[s][:], biased[s][:]))
                        link[s](dve.tensor_copy(best_f[s][:], best_i[s][:]))
                        dve.tensor_scalar(onehot[s][:], iota[:, 0:E8], best_f[s][:, 0:1], None, ALU.is_equal).then_inc(
                            routed[s].sem, 1)
                        dve.wait_ge(*routed[s].at(1, i))
                        link[s](dve.tensor_tensor(chosen[s][:], gate[s][:, 1:GATES], onehot[s][:], ALU.mult))
                        link[s](dve.tensor_copy(pair[s][:, 0:1], gate[s][:, 0:1]))
                        link[s](dve.tensor_reduce(pair[s][:, 1:2], chosen[s][:], AX, ALU.add))
                        link[s](dve.tensor_reduce(pair_m[s][:], pair[s][:], AX, ALU.max))
                        dve.tensor_scalar(pair[s][:], pair[s][:], pair_m[s][:], None, ALU.subtract).then_inc(
                            pair_ready[s].sem, 1)
                    for s in SL:
                        dve.wait_ge(*rows_done[s].at(1, i))
                        link[s](dve.tensor_copy(ohT[s][:], Bk[s][0:E8, 3 * P:4 * P]))
                        for k in range(DT):
                            for half in range(2):
                                last = dve.tensor_tensor(xTe[s][:, k, 4 * half:4 * half + 4, :], R[s][:, half],
                                                         fT[s][:, k, :].unsqueeze(1).to_broadcast([P, 4, P]), ALU.mult)
                        last.then_inc(masked[s].sem, 1)
                    for s in SL:
                        dve.wait_ge(*pair_exp[s].at(1, i))
                        link[s](dve.tensor_reduce(pair_m[s][:], pair[s][:], AX, ALU.add))
                        link[s](dve.reciprocal(pair_m[s][:], pair_m[s][:]))
                        link[s](dve.tensor_scalar(mix[s][:], pair[s][:], pair_m[s][:], None, ALU.mult))
                        link[s](dve.tensor_scalar(mix[s][:, 0:1], mix[s][:, 0:1], -1.0, None, ALU.add))
                        link[s](dve.tensor_tensor(mix[s][:], mix[s][:], hit[:, bass.ds(i * 2 + s, 1)].to_broadcast([P, 2]),
                                                  ALU.mult))
                        link[s](dve.tensor_scalar(mix[s][:, 0:1], mix[s][:, 0:1], 1.0, None, ALU.add))
                    for s in SL:
                        dve.wait_ge(*hidden[s].at(1, i))
                        dve.tensor_copy(u[s][:, 1, :], A[s][:, 0:2 * HID]).then_inc(u_ready[s].sem, 1)
                    for s in SL:
                        dve.wait_ge(*u_exp[s].at(1, i))
                        link[s](dve.tensor_scalar(ue[s][:], ue[s][:], 1.0, None, ALU.add))
                        link[s](dve.reciprocal(ue[s][:], ue[s][:]))
                        link[s](dve.tensor_tensor(ue[s][:], ue[s][:], u[s][:, :, 0:HID], ALU.mult))
                        link[s](dve.tensor_tensor(z[s][:], ue[s][:], u[s][:, :, HID:2 * HID], ALU.mult))
                        inner[s].vector(dve, link[s], lambda t: z[s][:, t, :], 1e-5, 1, i)
                        for n in range(2):
                            last = dve.tensor_scalar(z[s][:, n, :], z[s][:, n, :], inner[s].mean(n), inner[s].r(n),
                                                     ALU.subtract, ALU.mult)
                        last.then_inc(z_ready[s].sem, 1)
                    for s in SL:
                        dve.wait_ge(*turned_kept[s].at(2, i))
                        for half in range(2):
                            last = dve.tensor_tensor(zTe[s][:, 4 * half:4 * half + 4, :], R[s][:, half],
                                                     zT[s][:, 1, :].unsqueeze(1).to_broadcast([P, 4, P]), ALU.mult)
                        last.then_inc(z_masked[s].sem, 1)
                    for s in SL:
                        dve.wait_ge(*outs[s].at(1, i))
                        dve.wait_ge(*stored[s].at(0, i))
                        link[s](dve.scalar_tensor_tensor(out=y[s][:], in0=Bk[s][:, 0:D], scalar=mix[s][:, 0:1],
                                                         in1=x[s][:], op0=ALU.mult, op1=ALU.add))
                        dve.scalar_tensor_tensor(out=y[s][:], in0=Bk[s][:, D:2 * D], scalar=mix[s][:, 1:2],
                                                 in1=y[s][:], op0=ALU.mult, op1=ALU.add).then_inc(x_read[s].sem, 1)
                        dve.wait_ge(*x_read[s].at(1, i))
                        outer[s].vector(dve, link[s], lambda t: y[s][:], 1e-5, 1, i)
                        dve.tensor_scalar(y[s][:], y[s][:], outer[s].mean(0), outer[s].r(0), ALU.subtract,
                                          ALU.mult).then_inc(done[s].sem, 1)
                        link[s].close()


PF = 4
PB = D // PF
LH, LD = 16, 16
ROWS = P // B
LG = S // ROWS
HP = 32


def linear_constants():
    angle = np.pi / 2 * np.arange(1, B + 1, dtype=np.float32) / B
    s, c = np.sin(angle, dtype=np.float32), np.cos(angle, dtype=np.float32)
    pair = np.outer(s, s) + np.outer(c, c)
    return np.kron(pair, np.eye(ROWS)).astype(np.float32)


def linear_stage(nc, x_in, w, x_out):
    rows_in = x_in.rearrange("(l g r) d -> g l r d", l=B, r=ROWS)
    rows_out = x_out.rearrange("(l g r) d -> g l r d", l=B, r=ROWS)
    with ExitStack() as ctx:
        m = Room(nc, ctx, "lin")
        ident = m.sb("ident", [P, P])
        ones = m.sb("ones", [1, P])
        pair = m.sb("pair", [P, P])
        s2 = m.sb("s2", [P, PF, PB])
        a2 = m.sb("a2", [P, DT, PF, PF])
        term = m.sb("term", [P, PF, PB])
        weights = {n: m.sb("w" + n, [P, DT, PF, PB]) for n in "qkvo"}
        padded = {n: m.sb("wp" + n, [P, DT, PF, 4, HP]) for n in "qk"}
        row_bias = {n: m.sb("b" + n, [1, 4 * P]) for n in "qk"}
        row_bias.update({n: m.sb("b" + n, [1, D]) for n in "vo"})
        affine = {n: m.sb(n, [P, D]) for n in ("g1", "b1", "g2", "b2")}
        w_in = m.counter("w_in")
        b_in = m.counter("b_in")
        built = m.counter("built")
        w_free = m.counter("w_free")

        with nc.Block() as block:
            @block.sync
            def _(sp):
                sp.dma_start(ident[:], w["ident"]).then_inc(b_in.sem, 16)
                sp.dma_start(pair[:], w["pair"]).then_inc(b_in.sem, 16)
                for n in "qkvo":
                    sp.dma_start(row_bias[n][:], w[n + "b_row"]).then_inc(b_in.sem, 16)
                for n in affine:
                    sp.dma_start(affine[n][:], w[n].partition_broadcast(P)).then_inc(b_in.sem, 16)
                for j, n in enumerate("qkvo"):
                    if j:
                        sp.wait_ge(*w_free.at(j))
                    for half in range(2):
                        rows = slice(half * PB, (half + 1) * PB)
                        sp.dma_start(s2[rows], w[n + "S"].rearrange("n k l -> k n l")).then_inc(w_in.sem, 16)
                        sp.dma_start(a2[rows], w[n + "A_halves"][half].rearrange("k n j -> (k n j)").partition_broadcast(
                            PB).rearrange("p (k n j) -> p k n j", k=DT, n=PF)).then_inc(w_in.sem, 16)
                sp.wait_ge(*b_in.at(16 * 10))

            @block.vector
            def _(dve):
                dve.memset(ones[:], 1.0)
                for n in "qk":
                    dve.memset(padded[n][:], 0.0)
                link = Chain(dve, built)
                for j, n in enumerate("qkvo"):
                    dve.wait_ge(*w_in.at(64 * (j + 1)))
                    for k in range(DT):
                        for c in range(PF):
                            out = weights[n][:, k] if c == 0 else term[:]
                            link(dve.tensor_tensor(out, a2[:, k, c, :].unsqueeze(2).to_broadcast([P, PF, PB]),
                                                   s2[:, c, :].unsqueeze(1).to_broadcast([P, PF, PB]), ALU.mult))
                            if c:
                                link(dve.tensor_tensor(weights[n][:, k], weights[n][:, k], term[:], ALU.add))
                    if n in "qk":
                        for k in range(DT):
                            for c in range(PF):
                                last = dve.tensor_copy(padded[n][:, k, c, :, 0:LD],
                                                       weights[n][:, k, c, :].rearrange("p (h m) -> p h m", m=LD))
                        link(last)
                    dve.sem_inc(w_free.sem, 1)

        SL = range(2)
        x = [m.sb(f"x{s}", [P, D]) for s in SL]
        qn = [m.sb(f"qn{s}", [P, D]) for s in SL]
        fT = [m.sb(f"fT{s}", [P, 2 * DT, P]) for s in SL]
        qT = [m.sb(f"qT{s}", [P, 4, P]) for s in SL]
        kT = [m.sb(f"kT{s}", [P, 4, P]) for s in SL]
        v = [m.sb(f"v{s}", [P, LH, LD + 1]) for s in SL]
        masked = [m.sb(f"masked{s}", [P, 4, 4, P]) for s in SL]
        z = [m.sb(f"z{s}", [P, LH]) for s in SL]
        o = [m.sb(f"o{s}", [P, D]) for s in SL]
        oT = [m.sb(f"oT{s}", [P, DT, P]) for s in SL]
        y = [m.sb(f"y{s}", [P, D]) for s in SL]
        bT = [m.ps(f"bT{s}", [P, 4, P]) for s in SL]
        bQ = [m.ps(f"bQ{s}", [P, 4, P]) for s in SL]
        bK = [m.ps(f"bK{s}", [P, 4, P]) for s in SL]
        bV = [m.ps(f"bV{s}", [P, 512]) for s in SL]
        norms = [[Norm(m, f"n{k}{s}", 1, 1) for k in range(3)] for s in SL]
        started = m.counter("started", ahead=1)
        loaded = [m.counter(f"loaded{s}", 16 * B) for s in SL]
        stored = [m.counter(f"stored{s}", 16 * B, ahead=16 * B) for s in SL]
        q_normed = [m.counter(f"q_normed{s}", 1) for s in SL]
        turned = [m.counter(f"turned{s}", 2) for s in SL]
        turned_kept = [m.counter(f"turned_kept{s}", 2) for s in SL]
        projected = [m.counter(f"projected{s}", 3) for s in SL]
        qk_kept = [m.counter(f"qk_kept{s}", 2) for s in SL]
        v_kept = [m.counter(f"v_kept{s}", 1) for s in SL]
        scored = [m.counter(f"scored{s}", 4) for s in SL]
        mask_done = [m.counter(f"mask_done{s}", 4) for s in SL]
        weighed = [m.counter(f"weighed{s}", 1) for s in SL]
        o_normed = [m.counter(f"o_normed{s}", 1) for s in SL]
        final = [m.counter(f"final{s}", 1) for s in SL]
        x_read = [m.counter(f"x_read{s}", 1, ahead=1) for s in SL]
        done = [m.counter(f"done{s}", 1) for s in SL]
        chains = [m.counter(f"chain{s}", 27) for s in SL]

        with nc.Block() as block:
            @block.sync
            def _(sp):
                started.open(sp)
                for s in SL:
                    stored[s].open(sp)
                with sp.Fori(0, LG // 2) as i:
                    for s in SL:
                        sp.wait_ge(*x_read[s].at(0, i))
                        for l in range(B):
                            sp.dma_start(x[s][l * ROWS:(l + 1) * ROWS, :], rows_in[bass.ds(i * 2 + s, 1)][0][l]).then_inc(
                                loaded[s].sem, 16)
                    for s in SL:
                        sp.wait_ge(*done[s].at(1, i))
                        for l in range(B):
                            sp.dma_start(rows_out[bass.ds(i * 2 + s, 1)][0][l], y[s][l * ROWS:(l + 1) * ROWS, :]).then_inc(
                                stored[s].sem, 16)
                for s in SL:
                    sp.wait_ge(*stored[s].at(0, LG // 2))

            @block.tensor
            def _(pe):
                with pe.Fori(0, LG // 2) as i:
                    for s in SL:
                        pe.wait_ge(*q_normed[s].at(1, i))
                        for n, src in enumerate((x[s], qn[s])):
                            for k in range(DT):
                                last = pe.transpose(bT[s][:, n * DT + k, :], src[:, k * P:(k + 1) * P], ident[:])
                        last.then_inc(turned[s].sem, 1)
                    for s in SL:
                        pe.wait_ge(*turned_kept[s].at(1, i))
                        for n, bank, first in (("q", bQ[s], DT), ("k", bK[s], 0)):
                            for g in range(4):
                                for k in range(DT):
                                    pe.matmul(bank[:, g, :], padded[n][:, k, g].rearrange("p h m -> p (h m)"),
                                              fT[s][:, first + k, :], start=(k == 0), stop=False)
                                last = pe.matmul(bank[:, g, :], row_bias[n][:, g * P:(g + 1) * P], ones[:],
                                                 start=False, stop=True)
                            last.then_inc(projected[s].sem, 1)
                        for k in range(DT):
                            pe.matmul(bV[s][:, 0:D], fT[s][:, k, :], weights["v"][:, k].rearrange("p j l -> p (j l)"),
                                      start=(k == 0), stop=False)
                        pe.matmul(bV[s][:, 0:D], ones[:], row_bias["v"][:], start=False, stop=True).then_inc(
                            projected[s].sem, 1)
                    for h in range(4):
                        for s in SL:
                            if h == 0:
                                pe.wait_ge(*qk_kept[s].at(2, i))
                            if h >= 2:
                                pe.wait_ge(*mask_done[s].at(h - 1, i))
                            for g in range(4):
                                rows = slice(HP * h, HP * h + LD)
                                last = pe.matmul((bQ, bK)[h % 2][s][:, g, :], kT[s][rows, g, :], qT[s][rows, g, :],
                                                 start=True, stop=True)
                            last.then_inc(scored[s].sem, 1)
                    for s in SL:
                        pe.wait_ge(*v_kept[s].at(1, i))
                        pe.wait_ge(*mask_done[s].at(4, i))
                        for h in range(LH):
                            last = pe.matmul(bV[s][:, h * (LD + 1):(h + 1) * (LD + 1)], masked[s][:, h % 4, h // 4, :],
                                             v[s][:, h, :], start=True, stop=True)
                        last.then_inc(weighed[s].sem, 1)
                    for s in SL:
                        pe.wait_ge(*o_normed[s].at(1, i))
                        for k in range(DT):
                            last = pe.transpose(bT[s][:, k, :], o[s][:, k * P:(k + 1) * P], ident[:])
                        last.then_inc(turned[s].sem, 1)
                    for s in SL:
                        pe.wait_ge(*turned_kept[s].at(2, i))
                        for k in range(DT):
                            pe.matmul(bV[s][:, 0:D], oT[s][:, k, :], weights["o"][:, k].rearrange("p j l -> p (j l)"),
                                      start=(k == 0), stop=False)
                        pe.matmul(bV[s][:, 0:D], ones[:], row_bias["o"][:], start=False, stop=True).then_inc(
                            final[s].sem, 1)

            @block.scalar
            def _(act):
                with act.Fori(0, LG // 2) as i:
                    for s in SL:
                        norms[s][0].scalar(act, 1, i)
                    for s in SL:
                        act.wait_ge(*turned[s].at(1, i))
                        act.activation(fT[s][:], bT[s][:], ACT.Copy).then_inc(turned_kept[s].sem, 1)
                    for s in SL:
                        for n, (dst, bank) in enumerate(((qT[s], bQ[s]), (kT[s], bK[s]))):
                            act.wait_ge(*projected[s].at(n + 1, i))
                            act.activation(dst[:], bank[:], ACT.Relu).then_inc(qk_kept[s].sem, 1)
                    for s in SL:
                        norms[s][1].scalar(act, 1, i)
                    for s in SL:
                        act.wait_ge(*turned[s].at(2, i))
                        act.activation(oT[s][:], bT[s][:, 0:DT, :], ACT.Copy).then_inc(turned_kept[s].sem, 1)
                    for s in SL:
                        norms[s][2].scalar(act, 1, i)

            @block.vector
            def _(dve):
                for s in SL:
                    x_read[s].open(dve)
                    dve.memset(v[s][:], 1.0)
                with dve.Fori(0, LG // 2) as i:
                    link = [Chain(dve, chains[s], i, started) for s in SL]

                    def normalise(s, n, src, dst):
                        norms[s][n].vector(dve, link[s], lambda t: src[:], 1e-5, 1, i)
                        return dve.tensor_scalar(dst[:], src[:], norms[s][n].mean(0), norms[s][n].r(0),
                                                 ALU.subtract, ALU.mult)

                    for s in SL:
                        dve.wait_ge(*loaded[s].at(16 * B, i))
                        link[s](normalise(s, 0, x[s], qn[s]))
                        link[s](dve.tensor_tensor(qn[s][:], qn[s][:], affine["g1"][:], ALU.mult))
                        dve.tensor_tensor(qn[s][:], qn[s][:], affine["b1"][:], ALU.add).then_inc(q_normed[s].sem, 1)
                    for s in SL:
                        dve.wait_ge(*projected[s].at(3, i))
                        dve.tensor_copy(v[s][:, :, 0:LD], bV[s][:, 0:D].rearrange("p (h m) -> p h m", m=LD)).then_inc(
                            v_kept[s].sem, 1)
                    for h in range(4):
                        for s in SL:
                            dve.wait_ge(*scored[s].at(h + 1, i))
                            dve.tensor_tensor(masked[s][:, h], (bQ, bK)[h % 2][s][:],
                                              pair[:].unsqueeze(1).to_broadcast([P, 4, P]), ALU.mult).then_inc(
                                mask_done[s].sem, 1)
                    for s in SL:
                        dve.wait_ge(*weighed[s].at(1, i))
                        ov = bV[s][:, 0:LH * (LD + 1)].rearrange("p (h m) -> p h m", m=LD + 1)
                        link[s](dve.tensor_scalar(z[s][:], ov[:, :, LD], 1e-6, None, ALU.max))
                        link[s](dve.reciprocal(z[s][:], z[s][:]))
                        link[s](dve.tensor_tensor(o[s][:].rearrange("p (h m) -> p h m", m=LD), ov[:, :, 0:LD],
                                                  z[s][:].unsqueeze(2).to_broadcast([P, LH, LD]), ALU.mult))
                        dve.wait_ge(*q_normed[s].at(1, i))
                        link[s](dve.tensor_tensor(o[s][:], o[s][:], qn[s][:], ALU.add))
                        link[s](normalise(s, 1, o[s], o[s]))
                        link[s](dve.tensor_tensor(o[s][:], o[s][:], affine["g2"][:], ALU.mult))
                        dve.tensor_tensor(o[s][:], o[s][:], affine["b2"][:], ALU.add).then_inc(o_normed[s].sem, 1)
                    for s in SL:
                        dve.wait_ge(*o_normed[s].at(1, i))
                        dve.wait_ge(*stored[s].at(0, i))
                        dve.tensor_tensor(y[s][:], x[s][:], o[s][:], ALU.add).then_inc(x_read[s].sem, 1)
                        dve.wait_ge(*final[s].at(1, i))
                        dve.wait_ge(*x_read[s].at(1, i))
                        link[s](dve.tensor_tensor(y[s][:], y[s][:], bV[s][:, 0:D], ALU.add))
                        normalise(s, 2, y[s], y[s]).then_inc(done[s].sem, 1)
                        link[s].close()


LAYERS, HD = 4, 64
QW = 16 * HD
FF = 1024
FFT = FF // P


def decoder_stage(nc, x_in, bias_in, w, x_out):
    tiles_in = x_in.rearrange("(t p) d -> p t d", p=P)
    tiles_out = x_out.rearrange("(t p) d -> p t d", p=P)
    with ExitStack() as ctx:
        m = Room(nc, ctx, "dec")
        ident = m.sb("ident", [P, P])
        ones = m.sb("ones", [1, P])
        x = m.sb("x", [P, NT, D])
        xn = m.sb("xn", [P, ST, D])
        xnT = m.sb("xnT", [P, DT, S])
        ctxT = m.sb("ctxT", [P, DT, S])
        bias = m.sb("bias", [P, ST, S])
        wq = m.sb("wq", [P, DT, QW])
        wk = m.sb("wk", [P, DT, QW])
        wv = m.sb("wv", [P, DT, QW])
        wo = m.sb("wo", [P, QW // P, D])
        wf1 = m.sb("wf1", [P, DT, FF])
        wf2 = m.sb("wf2", [P, FFT, D])
        bf1 = m.sb("bf1", [P, FFT])
        bf2 = m.sb("bf2", [1, D])
        hid = m.sb("hid", [P, FFT, S])
        at = Attention(m, HD, HD, HD, HD ** -0.5, True)
        norm = Norm(m, "norm", ST, 2)
        started = m.counter("started", ahead=1)
        const_in = m.counter("const_in")
        w_loaded = m.counter("w_loaded", 16 * 8)
        ctx_loaded = m.counter("ctx_loaded", 16)
        bias_loaded = m.counter("bias_loaded", 16)
        chain = m.counter("chain", 20)
        normed = m.counter("normed", 2)
        n_turned = m.counter("n_turned", 2)
        nT_kept = m.counter("nT_kept", 2)
        up = m.counter("up", FFT // 2)
        up_kept_a = m.counter("up_kept_a", FFT // 4)
        up_kept_v = m.counter("up_kept_v", FFT // 4)
        down = m.counter("down", 1, ahead=1)

        with nc.Block() as block:
            @block.sync
            def _(sp):
                started.open(sp)
                sp.dma_start(ident[:], w["ident"]).then_inc(const_in.sem, 16)
                sp.dma_start(x[:], tiles_in).then_inc(const_in.sem, 16)
                with sp.Fori(0, LAYERS) as l:
                    sp.wait_ge(*down.at(0, l * B))
                    for dst, name in ((wq, "wq"), (wk, "wk"), (wv, "wv"), (wo, "wo"), (wf1, "wf1"), (wf2, "wf2")):
                        src = w[name].rearrange("l (k p) n -> l p k n", p=P)
                        sp.dma_start(dst[:], src[bass.ds(l, 1)][0]).then_inc(w_loaded.sem, 16)
                    sp.dma_start(bf1[:], w["bf1_cols"][bass.ds(l, 1)][0]).then_inc(w_loaded.sem, 16)
                    sp.dma_start(bf2[:], w["bf2"][bass.ds(l, 1)]).then_inc(w_loaded.sem, 16)
                    with sp.Fori(0, B) as b:
                        i = l * B + b
                        sp.wait_ge(*at.projected.at(0, i))
                        sp.dma_start(ctxT[:], w["ctxT"].rearrange("b (k p) s -> b p k s", p=P)[bass.ds(b, 1)][0]).then_inc(
                            ctx_loaded.sem, 16)
                        sp.wait_ge(*at.bias_added.at(0, i))
                        sp.dma_start(bias[:], bias_in.rearrange("n (t p) s -> n p t s", p=P)[bass.ds(i, 1)][0]).then_inc(
                            bias_loaded.sem, 16)

            @block.tensor
            def _(pe):
                pe.wait_ge(*const_in.at(32))
                down.open(pe)
                at.open(pe=pe)
                with pe.Fori(0, LAYERS) as l:
                    with pe.Fori(0, B) as b:
                        i = l * B + b
                        pe.wait_ge(*w_loaded.at(16 * 8, l))

                        def turn_normed(n):
                            pe.wait_ge(*normed.at(n, i))
                            for k in range(DT):
                                for t in range(ST):
                                    last = pe.transpose(at.psT[0][:, k, t * P:(t + 1) * P],
                                                        xn[:, t, k * P:(k + 1) * P], ident[:])
                            last.then_inc(n_turned.sem, 1)
                            pe.wait_ge(*nT_kept.at(n, i))

                        def rows(weight, source):
                            def project(g, bank):
                                for mt in range(at.mtiles):
                                    col = (g * at.mtiles + mt) * P
                                    for k in range(DT):
                                        last = pe.matmul(bank[:, mt * S:(mt + 1) * S], weight[:, k, col:col + P],
                                                         source[:, k, :], start=(k == 0), stop=(k == DT - 1))
                                return last
                            return project

                        def values(g, bank):
                            width = 4 * HD
                            for t in range(ST):
                                for k in range(DT):
                                    last = pe.matmul(bank[:, t * width:(t + 1) * width], ctxT[:, k, t * P:(t + 1) * P],
                                                     wv[:, k, g * width:(g + 1) * width],
                                                     start=(k == 0), stop=(k == DT - 1))
                            return last

                        turn_normed(1)
                        pe.wait_ge(*ctx_loaded.at(16, i))
                        at.tensor(pe, ident, rows(wq, xnT), rows(wk, ctxT), values, wo, i)
                        turn_normed(2)
                        for j in range(FFT // 2):
                            if j >= 2:
                                pe.wait_ge(*(up_kept_a, up_kept_v)[j % 2].at(j // 2, i))
                            for f in range(2):
                                for k in range(DT):
                                    last = pe.matmul(at.psS[j % 2][:, f, :],
                                                     wf1[:, k, (2 * j + f) * P:(2 * j + f + 1) * P], xnT[:, k, :],
                                                     start=(k == 0), stop=(k == DT - 1))
                            last.then_inc(up.sem, 1)
                        pe.wait_ge(*up_kept_a.at(FFT // 4, i))
                        pe.wait_ge(*up_kept_v.at(FFT // 4, i))
                        out = at.psB[:].rearrange("p (t d) -> p t d", t=ST)
                        for t in range(ST):
                            for f in range(FFT):
                                pe.matmul(out[:, t, :], hid[:, f, t * P:(t + 1) * P], wf2[:, f, :],
                                          start=(f == 0), stop=False)
                            last = pe.matmul(out[:, t, :], ones[:], bf2[:], start=False, stop=True)
                        last.then_inc(down.sem, 1)

            @block.scalar
            def _(act):
                with act.Fori(0, LAYERS) as l:
                    with act.Fori(0, B) as b:
                        i = l * B + b

                        def keep_normed(n):
                            act.wait_ge(*n_turned.at(n, i))
                            act.activation(xnT[:], at.psT[0][:], ACT.Copy).then_inc(nT_kept.sem, 1)

                        norm.scalar(act, 1, i)
                        keep_normed(1)
                        at.scalar(act, i)
                        norm.scalar(act, 2, i)
                        keep_normed(2)
                        for j in range(0, FFT // 2, 2):
                            act.wait_ge(*up.at(j + 1, i))
                            for f in range(2):
                                last = act.activation(hid[:, 2 * j + f, :], at.psS[0][:, f, :], ACT.Relu,
                                                      bias=bf1[:, 2 * j + f:2 * j + f + 1])
                            last.then_inc(up_kept_a.sem, 1)

            @block.vector
            def _(dve):
                at.open(dve=dve)
                dve.memset(ones[:], 1.0)
                dve.wait_ge(*const_in.at(32))
                with dve.Fori(0, LAYERS) as l:
                    with dve.Fori(0, B) as b:
                        i = l * B + b
                        link = Chain(dve, chain, i, started)
                        xb = x[:, bass.ds(b * ST, ST)]

                        def normalise(n):
                            norm.vector(dve, link, lambda t: xb[:, t, :], 0.0, n, i)
                            link(dve.tensor_tensor(norm.work[:], norm.mv[:, :, 1], norm.rstd[:], ALU.mult))
                            link(dve.tensor_scalar(norm.work[:], norm.work[:], 1e-6, None, ALU.add))
                            link(dve.reciprocal(norm.rstd[:], norm.work[:]))
                            for t in range(ST):
                                last = dve.tensor_scalar(xn[:, t, :], xb[:, t, :], norm.mean(t), norm.r(t),
                                                         ALU.subtract, ALU.mult)
                            last.then_inc(normed.sem, 1)

                        normalise(1)
                        dve.wait_ge(*bias_loaded.at(16, i))
                        at.vector(dve, i, bias)
                        dve.wait_ge(*at.projected_out.at(1, i))
                        link(dve.tensor_tensor(xb, xb, at.psA[:].rearrange("p (t d) -> p t d", t=ST), ALU.add), True)
                        normalise(2)
                        for j in range(1, FFT // 2, 2):
                            dve.wait_ge(*up.at(j + 1, i))
                            for f in range(2):
                                last = dve.tensor_scalar(hid[:, 2 * j + f, :], at.psS[1][:, f, :],
                                                         bf1[:, 2 * j + f:2 * j + f + 1], 0.0, ALU.add, ALU.max)
                            last.then_inc(up_kept_v.sem, 1)
                        dve.wait_ge(*down.at(1, i))
                        link(dve.tensor_tensor(xb, xb, at.psB[:].rearrange("p (t d) -> p t d", t=ST), ALU.add))
                        link.close()

        xs = m.sb("xs", [P, ST, D])
        again = m.counter("again", 16)
        xs_free = m.counter("xs_free", 1, ahead=1)
        done = m.counter("done", 1)
        stored = m.counter("stored", 16, ahead=16)
        fin = m.counter("fin", 17)
        norm1 = Norm(m, "norm1", ST, 1)
        norm2 = Norm(m, "norm2", ST, 1)
        batches_in = x_in.rearrange("(b t p) d -> b p t d", p=P, t=ST)
        batches_out = x_out.rearrange("(b t p) d -> b p t d", p=P, t=ST)
        with nc.Block() as block:
            @block.sync
            def _(sp):
                stored.open(sp)
                with sp.Fori(0, B) as b:
                    sp.wait_ge(*xs_free.at(0, b))
                    sp.dma_start(xs[:], batches_in[bass.ds(b, 1)][0]).then_inc(again.sem, 16)
                    sp.wait_ge(*done.at(1, b))
                    sp.dma_start(batches_out[bass.ds(b, 1)][0], xn[:]).then_inc(stored.sem, 16)
                sp.wait_ge(*stored.at(0, B))

            @block.scalar
            def _(act):
                with act.Fori(0, B) as b:
                    norm1.scalar(act, 1, b)
                    norm2.scalar(act, 1, b)

            @block.vector
            def _(dve):
                xs_free.open(dve)
                with dve.Fori(0, B) as b:
                    link = Chain(dve, fin, b, started)
                    xb = x[:, bass.ds(b * ST, ST)]
                    norm1.vector(dve, link, lambda t: xb[:, t, :], 0.0, 1, b)
                    link(dve.tensor_tensor(norm1.work[:], norm1.mv[:, :, 1], norm1.rstd[:], ALU.mult))
                    link(dve.tensor_scalar(norm1.work[:], norm1.work[:], 1e-6, None, ALU.add))
                    link(dve.reciprocal(norm1.rstd[:], norm1.work[:]))
                    dve.wait_ge(*stored.at(0, b))
                    for t in range(ST):
                        last = dve.tensor_scalar(xn[:, t, :], xb[:, t, :], norm1.mean(t), norm1.r(t),
                                                 ALU.subtract, ALU.mult)
                    link(last)
                    dve.wait_ge(*again.at(16, b))
                    dve.tensor_tensor(xn[:], xn[:], xs[:], ALU.add).then_inc(xs_free.sem, 1)
                    dve.wait_ge(*xs_free.at(1, b))
                    norm2.vector(dve, link, lambda t: xn[:, t, :], 1e-5, 1, b)
                    for t in range(ST):
                        last = dve.tensor_scalar(xn[:, t, :], xn[:, t, :], norm2.mean(t), norm2.r(t),
                                                 ALU.subtract, ALU.mult)
                    last.then_inc(done.sem, 1)
                    link(dve.tensor_copy(norm2.work[:, 0:1], norm2.rstd[:, 0:1]))
                    link.close()


E14, FE = 14, 512
FT = FE // P
CH = 512
NC4 = TOK // CH
CT = CH // P


def moe14_stage(nc, x_in, w, out):
    xin_c = x_in.rearrange("(c t p) d -> c p t d", p=P, t=CT)
    out_c = out.rearrange("(c t p) d -> c p t d", p=P, t=CT)
    w1_e = w["w1"].rearrange("e (k p) f -> e p k f", p=P)
    w2_e = w["w2"].rearrange("e (k p) d -> e p k d", p=P)
    with ExitStack() as ctx:
        m = Room(nc, ctx, "m14")
        ident = m.sb("ident", [P, P])
        gate_w = m.sb("gate_w", [P, DT, E14])
        b2 = m.sb("b2", [E14, D])
        b1 = m.sb("b1", [P, E14, FT])
        iota = m.sb("iota", [P, E14])
        xT = m.sb("xT", [P, DT, TOK])
        acc = m.sb("acc", [P, NT, D])
        wt = m.sb("wt", [P, NT, E14])
        xs = m.sb("xs", [P, CT, D])
        xTs = m.sb("xTs", [P, DT, CH])
        top = m.sb("top", [P, CT, 1])
        prob = m.sb("prob", [P, CT, E14])
        psumr = m.sb("psumr", [P, CT, 1])
        best = m.sb("best", [P, CT, 8])
        best_i = m.sb("best_i", [P, CT, 8], U32)
        best_f = m.sb("best_f", [P, CT, 8])
        mask = m.sb("mask", [P, CT, E14])
        mask2 = m.sb("mask2", [P, CT, E14])
        den = m.sb("den", [P, CT, 1])
        wc = m.sb("wc", [P, CT, E14])
        wT = m.sb("wT", [E14, CH])
        w1s = m.sb("w1s", [P, 2, DT, FE])
        w2s = m.sb("w2s", [P, 2, FT, D])
        hid = m.sb("hid", [P, 2, FT, CH])
        xo = m.sb("xo", [P, CT, D])
        psT = m.ps("psT", [P, DT, CH])
        psL = m.ps("psL", [P, 512])
        psW = m.ps("psW", [P, 512])
        psB = m.ps("psB", [P, CT, D])
        norm = Norm(m, "norm", CT)

        started = m.counter("started", ahead=1)
        const_in = m.counter("const_in")
        x_loaded = m.counter("x_loaded", 16)
        xs_free = m.counter("xs_free", 1, ahead=1)
        xT_done = m.counter("xT_done", 1)
        xT_stored = m.counter("xT_stored", 1)
        xT_kept = m.counter("xT_kept", 1, ahead=1)
        logits = m.counter("logits", 1)
        shifted = m.counter("shifted", 1)
        exps = m.counter("exps", 1)
        w_ready = m.counter("w_ready", 1)
        wT_done = m.counter("wT_done", 1)
        wT_stored = m.counter("wT_stored", 1)
        bias_done = m.counter("bias_done", 1)
        chain = m.counter("chain", 15)

        with nc.Block() as block:
            @block.sync
            def _(sp):
                started.open(sp)
                sp.dma_start(ident[:], w["ident"]).then_inc(const_in.sem, 16)
                sp.dma_start(gate_w[:], w["gate_wT"].rearrange("(k p) e -> p k e", p=P)).then_inc(const_in.sem, 16)
                sp.dma_start(b2[:], w["b2"]).then_inc(const_in.sem, 16)
                sp.dma_start(b1[:], w["b1_cols"]).then_inc(const_in.sem, 16)
                sp.dma_start(iota[:], w["iota14"].partition_broadcast(P)).then_inc(const_in.sem, 16)
                with sp.Fori(0, NC4) as c:
                    sp.wait_ge(*xs_free.at(1 - 1, c))
                    sp.dma_start(xs[:], xin_c[bass.ds(c, 1)][0]).then_inc(x_loaded.sem, 16)

            @block.tensor
            def _(pe):
                pe.wait_ge(*const_in.at(80))
                with pe.Fori(0, NC4) as c:
                    pe.wait_ge(*x_loaded.at(16, c))
                    for k in range(DT):
                        for t in range(CT):
                            last = pe.transpose(psT[:, k, t * P:(t + 1) * P], xs[:, t, k * P:(k + 1) * P], ident[:])
                    last.then_inc(xT_done.sem, 1)
                    pe.wait_ge(*xT_stored.at(1, c))
                    for t in range(CT):
                        for k in range(DT):
                            last = pe.matmul(psL[:, t * E14:(t + 1) * E14], xTs[:, k, t * P:(t + 1) * P],
                                             gate_w[:, k, :], start=(k == 0), stop=(k == DT - 1))
                    last.then_inc(logits.sem, 1)
                    pe.wait_ge(*w_ready.at(1, c))
                    for t in range(CT):
                        last = pe.transpose(psW[0:E14, t * P:(t + 1) * P], wc[:, t, :], ident[:])
                    last.then_inc(wT_done.sem, 1)
                    pe.wait_ge(*wT_stored.at(1, c))
                    for t in range(CT):
                        last = pe.matmul(psB[:, t, :], wT[:, t * P:(t + 1) * P], b2[:], start=True, stop=True)
                    last.then_inc(bias_done.sem, 1)

            @block.scalar
            def _(act):
                xT_kept.open(act)
                with act.Fori(0, NC4) as c:
                    alone(act, *xT_stored.at(1, c), started)
                    act.activation(xT[:, :, bass.ds(c * CH, CH)], xTs[:], ACT.Copy).then_inc(xT_kept.sem, 1)
                    act.wait_ge(*shifted.at(1, c))
                    act.activation(prob[:], prob[:], ACT.Exp).then_inc(exps.sem, 1)

            @block.vector
            def _(dve):
                xs_free.open(dve)
                dve.wait_ge(*const_in.at(80))
                with dve.Fori(0, NC4) as c:
                    link = Chain(dve, chain, c, started)
                    dve.wait_ge(*xT_done.at(1, c))
                    dve.wait_ge(*xT_kept.at(0, c))
                    dve.tensor_copy(xTs[:], psT[:]).then_inc(xT_stored.sem, 1)
                    dve.wait_ge(*logits.at(1, c))
                    lg = psL[:, 0:CT * E14].rearrange("p (t e) -> p t e", e=E14)
                    link(dve.tensor_reduce(top[:, :, 0], lg, AX, ALU.max))
                    dve.tensor_tensor(prob[:], lg, top[:].to_broadcast([P, CT, E14]), ALU.subtract).then_inc(
                        shifted.sem, 1)
                    dve.wait_ge(*exps.at(1, c))
                    link(dve.tensor_reduce(psumr[:, :, 0], prob[:], AX, ALU.add))
                    link(dve.reciprocal(psumr[:], psumr[:]))
                    link(dve.tensor_tensor(prob[:], prob[:], psumr[:].to_broadcast([P, CT, E14]), ALU.mult), by_itself=True)
                    for t in range(CT):
                        last = dve.max(best[:, t, :], prob[:, t, :])
                    link(last, by_itself=True)
                    for t in range(CT):
                        last = dve.max_index(best_i[:, t, :], best[:, t, :], prob[:, t, :])
                    link(last)
                    link(dve.tensor_copy(best_f[:], best_i[:]))
                    places = iota[:].unsqueeze(1).to_broadcast([P, CT, E14])
                    dve.tensor_tensor(mask[:], places, best_f[:, :, 0:1].to_broadcast([P, CT, E14]), ALU.is_equal)
                    link(dve.tensor_tensor(mask2[:], places, best_f[:, :, 1:2].to_broadcast([P, CT, E14]),
                                           ALU.is_equal))
                    link(dve.tensor_tensor(mask[:], mask[:], mask2[:], ALU.add))
                    link(dve.tensor_tensor(den[:], best[:, :, 0:1], best[:, :, 1:2], ALU.add))
                    link(dve.tensor_scalar(den[:], den[:], 1e-10, None, ALU.max))
                    link(dve.reciprocal(den[:], den[:]))
                    link(dve.tensor_tensor(mask[:], mask[:], prob[:], ALU.mult))
                    link(dve.tensor_tensor(wc[:], mask[:], den[:].to_broadcast([P, CT, E14]), ALU.mult))
                    dve.tensor_copy(wt[:, bass.ds(c * CT, CT)], wc[:]).then_inc(w_ready.sem, 1)
                    dve.wait_ge(*wT_done.at(1, c))
                    dve.tensor_copy(wT[:], psW[0:E14, :]).then_inc(wT_stored.sem, 1)
                    dve.wait_ge(*bias_done.at(1, c))
                    link(dve.tensor_tensor(acc[:, bass.ds(c * CT, CT)], xs[:], psB[:], ALU.add))
                    dve.sem_inc(xs_free.sem, 1)
                    link.close()

        UNITS = 2 * NC4
        w_loaded = [m.counter(f"w_loaded{s}", 32) for s in range(2)]
        up = m.counter("up", UNITS * FT)
        gelu = m.counter("gelu", UNITS * FT, ahead=2)
        down = m.counter("down", UNITS * 2, ahead=UNITS * 2)
        summed = m.counter("summed", UNITS * 2, ahead=8)
        psU = [psL, psW]

        def down_bank(n):
            if n % 4 < 2:
                return psB[:, 2 * (n % 2):2 * (n % 2) + 2, :]
            return psT[:, n % 2, :].rearrange("p (t d) -> p t d", d=D)

        with nc.Block() as block:
            @block.sync
            def _(sp):
                with sp.Fori(0, E14 // 2) as i:
                    for s in range(2):
                        sp.wait_ge(*down.at((s + 1) * NC4 * 2 - UNITS * 2, i))
                        sp.dma_start(w1s[:, s], w1_e[bass.ds(i * 2 + s, 1)][0]).then_inc(w_loaded[s].sem, 16)
                        sp.dma_start(w2s[:, s], w2_e[bass.ds(i * 2 + s, 1)][0]).then_inc(w_loaded[s].sem, 16)

            @block.tensor
            def _(pe):
                down.open(pe)
                with pe.Fori(0, E14 // 2) as i:
                    for u in range(UNITS + 1):
                        if u < UNITS:
                            s, c = u // NC4, u % NC4
                            if c == 0:
                                pe.wait_ge(*w_loaded[s].at(32, i))
                            for f in range(FT):
                                pe.wait_ge(*gelu.at(u * FT + f + 1 - 2, i))
                                for k in range(DT):
                                    last = pe.matmul(psU[f % 2][:], w1s[:, s, k, f * P:(f + 1) * P],
                                                     xT[:, k, c * CH:(c + 1) * CH], start=(k == 0), stop=(k == DT - 1))
                                last.then_inc(up.sem, 1)
                        if u > 0:
                            v = u - 1
                            s = v // NC4
                            pe.wait_ge(*gelu.at(v * FT + FT, i))
                            for h in range(2):
                                n = v * 2 + h
                                pe.wait_ge(*summed.at(n + 1 - 4, i))
                                for t in range(2):
                                    for f in range(FT):
                                        last = pe.matmul(down_bank(n)[:, t, :],
                                                         hid[:, v % 2, f, (2 * h + t) * P:(2 * h + t + 1) * P],
                                                         w2s[:, s, f, :], start=(f == 0), stop=(f == FT - 1))
                                last.then_inc(down.sem, 1)

            @block.scalar
            def _(act):
                gelu.open(act)
                with act.Fori(0, E14 // 2) as i:
                    for u in range(UNITS):
                        act.wait_ge(*down.at(2 * (u + 1) - 4, i))
                        for f in range(FT):
                            alone(act, *up.at(u * FT + f + 1, i), started)
                            act.activation(hid[:, u % 2, f, :], psU[f % 2][:], ACT.Gelu,
                                           bias=b1[:, bass.ds(i * 2 + u // NC4, 1), f]).then_inc(gelu.sem, 1)

            @block.vector
            def _(dve):
                summed.open(dve)
                with dve.Fori(0, E14 // 2) as i:
                    for u in range(UNITS):
                        s, c = u // NC4, u % NC4
                        for h in range(2):
                            n = u * 2 + h
                            dve.wait_ge(*down.at(n + 1, i))
                            dve.wait_ge(*summed.at(n + 1 - 8, i))
                            for t in range(2):
                                tile = c * CT + 2 * h + t
                                last = dve.scalar_tensor_tensor(
                                    out=acc[:, tile, :], in0=down_bank(n)[:, t, :],
                                    scalar=wt[:, tile, bass.ds(i * 2 + s, 1)], in1=acc[:, tile, :],
                                    op0=ALU.mult, op1=ALU.add)
                            last.then_inc(summed.sem, 1)

        x_again = m.counter("x_again", 16)
        xs_read = m.counter("xs_read", 1, ahead=1)
        normed = m.counter("normed", 1)
        stored = m.counter("stored", 16, ahead=16)
        fin = m.counter("fin", 8)

        with nc.Block() as block:
            @block.sync
            def _(sp):
                stored.open(sp)
                with sp.Fori(0, NC4) as c:
                    sp.wait_ge(*xs_read.at(1 - 1, c))
                    sp.dma_start(xs[:], xin_c[bass.ds(c, 1)][0]).then_inc(x_again.sem, 16)
                    sp.wait_ge(*normed.at(1, c))
                    sp.dma_start(out_c[bass.ds(c, 1)][0], xo[:]).then_inc(stored.sem, 16)
                sp.wait_ge(*stored.at(0, NC4))

            @block.scalar
            def _(act):
                with act.Fori(0, NC4) as c:
                    norm.scalar(act, 1, c)

            @block.vector
            def _(dve):
                xs_read.open(dve)
                with dve.Fori(0, NC4) as c:
                    link = Chain(dve, fin, c, started)
                    part = acc[:, bass.ds(c * CT, CT)]
                    link(dve.tensor_scalar(part, part, 100.0, -100.0, ALU.min, ALU.max))
                    dve.wait_ge(*x_again.at(16, c))
                    dve.wait_ge(*stored.at(0, c))
                    dve.tensor_tensor(xo[:], xs[:], part, ALU.add).then_inc(xs_read.sem, 1)
                    dve.wait_ge(*xs_read.at(1, c))
                    norm.vector(dve, link, lambda t: xo[:, t, :], 1e-5, 1, c)
                    for t in range(CT):
                        last = dve.tensor_scalar(xo[:, t, :], xo[:, t, :], norm.mean(t), norm.r(t),
                                                 ALU.subtract, ALU.mult)
                    last.then_inc(normed.sem, 1)
                    link(dve.tensor_copy(norm.work[:, 0:1], norm.rstd[:, 0:1]))
                    link.close()


def build(nc, a, out):
    def of(stage):
        named = {k.split(".", 1)[1]: v for k, v in a.items() if k.startswith(stage + ".")}
        named.update(ident=a["ident"], ctxT=a["ctxT"])
        return named

    between = [nc.dram_tensor(f"x_after_{n}", (TOK, D), F32, kind="Internal").ap() for n in range(1, 6)]
    bias = nc.dram_tensor("distance_bias", (NL * B, S, S), F32, kind="Internal").ap()
    bias_stage(nc, of("bias"), bias)
    scan_stage(nc, a["x"], of("ssm"), between[0])
    cross_stage(nc, between[0], of("xat"), between[1])
    moe8_stage(nc, between[1], of("m8"), between[2])
    linear_stage(nc, between[2], of("lin"), between[3])
    decoder_stage(nc, between[3], bias, of("dec"), between[4])
    moe14_stage(nc, between[4], of("m14"), out)


def layouts(i):
    def turned(v):
        return np.swapaxes(v, -1, -2)

    def cols(v):
        return turned(v.reshape(*v.shape[:-1], -1, P))

    def padded_heads(v):
        wide = np.zeros((LH, HP), v.dtype)
        wide[:, :LD] = v.reshape(LH, LD)
        return wide.reshape(1, LH * HP)

    s, x0, f0 = (lambda n: i["L0_attn_" + n]), (lambda n: i["L0_xattn_" + n]), (lambda n: i["L0_ffn_" + n])
    l1, x1, f1 = (lambda n: i["L1_attn_" + n]), (lambda n: i["L1_xattn_" + n]), (lambda n: i["L1_ffn_" + n])
    dist = i["fside_BxSxS2_0"]
    a = {
        "ident": np.eye(P, dtype=np.float32),
        "x": i["x"].reshape(TOK, D),
        "ctxT": turned(i["ctx_1024"]),
        "bias.distT": turned(dist),
        "bias.dist": dist,
        "bias.mask": i["mask_Bx1x1xS2_ff0"].reshape(B, S),
        "bias.abw": np.stack([x1("Wth")[:, 0].T, x1("bth").T, x1("Wto")[:, :, 0].T], 1),
        "bias.bto": x1("bto")[:, 0],
        "ssm.ln_wb": np.stack([cols(s("ln_w")), cols(s("ln_b"))], -1),
        "ssm.in_wT": turned(s("in_w")),
        "ssm.in_b_cols": cols(s("in_b")),
        "ssm.taps": np.concatenate([s("conv_w")[:, 0], s("conv_b")[:, None]], 1).reshape(IT, P, TAPS + 1).transpose(1, 0, 2),
        "ssm.xp_wT": turned(s("xp_w")),
        "ssm.dtp_wT": turned(s("dtp_w")),
        "ssm.dtp_b_cols": cols(s("dtp_b")),
        "ssm.A_log": s("A_log"),
        "ssm.D_cols": cols(s("D")),
        "ssm.out_wT": turned(s("out_w")),
        "ssm.out_b": s("out_b"),
        "xat.bo": x0("bo"),
        "m8.iota_tok": np.arange(TOK, dtype=np.float32),
        "m8.gates_wT": np.concatenate([turned(f0("sg_w")), turned(f0("eg_w"))], 1),
        "m8.gates_b": np.concatenate([f0("sg_b"), f0("eg_b")]),
        "m8.gains": np.stack([f0("s_ln_g"), f0("sel_ln_g")], 1),
        "m8.shifts": np.stack([f0("s_ln_b"), f0("sel_ln_b")], 1),
        "lin.pair": linear_constants(),
        "lin.qb_row": padded_heads(l1("qb")),
        "lin.kb_row": padded_heads(l1("kb")),
        "lin.vb_row": l1("vb")[None],
        "lin.ob_row": l1("ob")[None],
        "dec.bf1_cols": cols(x1("bf1")),
        "m14.gate_wT": turned(f1("gate_w")),
        "m14.b1_cols": f1("b1").reshape(E14, FT, P).transpose(2, 0, 1),
        "m14.iota14": np.arange(E14, dtype=np.float32),
        "dec.bf2": x1("bf2"),
        "dec.wq": x1("Wq").reshape(LAYERS, D, QW),
        "dec.wk": x1("Wk").reshape(LAYERS, D, QW),
        "dec.wv": x1("Wv").reshape(LAYERS, D, QW),
        "dec.wo": x1("Wo").reshape(LAYERS, QW, D),
        "dec.wf1": x1("Wf1"),
        "dec.wf2": x1("Wf2"),
    }
    for n in ("Wq", "Wk", "Wv", "Wo"):
        a[f"xat.{n}T"] = turned(x0(n))
    for n in ("sw1", "sw2", "sw3", "ew1", "ew2", "ew3"):
        a[f"m8.{n}T"] = turned(f0(n))
    for n in ("index_b", "index_t", "sb1", "sb2", "sb3", "eb1", "eb2", "eb3", "exp_bias"):
        a[f"m8.{n}"] = f0(n)
    for n in ("g1", "b1", "g2", "b2"):
        a[f"lin.{n}"] = l1(n)
    for n in "qkvo":
        a[f"lin.{n}S"] = l1(n + "S")
        a[f"lin.{n}A_halves"] = l1(n + "A").reshape(PF, DT, 2, PF).transpose(2, 1, 0, 3)
    for n in ("w1", "w2", "b2"):
        a[f"m14.{n}"] = f1(n)
    return {k: np.ascontiguousarray(v) for k, v in a.items()}


def kernel(**inputs):
    import concourse.bacc as bacc
    from concourse.bass_utils import run_bass_kernel_spmd

    nc = bacc.Bacc("TRN2", target_bir_lowering=False, num_devices=1)
    arrays = layouts({k: np.asarray(v) for k, v in inputs.items()})
    dram = {k.replace(".", "_"): v for k, v in arrays.items()}
    aps = {k: nc.dram_tensor(k.replace(".", "_") + "_in", v.shape, mybir.dt.from_np(v.dtype), kind="ExternalInput").ap()
           for k, v in arrays.items()}
    out = nc.dram_tensor("out_0", (TOK, D), F32, kind="ExternalOutput").ap()
    build(nc, aps, out)
    r = run_bass_kernel_spmd(nc, [{k + "_in": v for k, v in dram.items()}], core_ids=[0])
    return r.results[0]["out_0"].reshape(B, S, D)
```

```python
import math
from contextlib import ExitStack

import numpy as np

import concourse.bass as bass
from concourse import mybir

P = 128
F32 = mybir.dt.float32
BF16 = mybir.dt.bfloat16
I32 = mybir.dt.int32
U32 = mybir.dt.uint32
ALU = mybir.AluOpType
ACT = mybir.ActivationFunctionType
AX = mybir.AxisListType.X

B, S, D = 8, 256, 256
TOK = B * S
DT = D // P
ST = S // P
NT = TOK // P


class Signal:

    def __init__(self, sem, per=0, ahead=0):
        self.sem, self.per, self.ahead = sem, per, ahead

    def open(self, eng):
        eng.sem_inc(self.sem, self.ahead)

    def at(self, n, i=0):
        return self.sem, i * self.per + (n + self.ahead)


class Chain:

    def __init__(self, eng, signal, i=0, started=None):
        self.eng, self.step, self.i, self.n, self.started = eng, signal, i, 0, started

    def __call__(self, instruction, by_itself=False):
        self.n += 1
        instruction.then_inc(self.step.sem, 1)
        if by_itself:
            alone(self.eng, *self.step.at(self.n, self.i), self.started)
        else:
            self.eng.wait_ge(*self.step.at(self.n, self.i))

    def close(self):
        assert self.n == self.step.per, (self.step.sem, self.n)


class Room:

    def __init__(self, nc, ctx, prefix):
        self.nc, self.ctx, self.prefix = nc, ctx, prefix
        self.semaphores = []
        ctx.callback(self.clear)

    def clear(self):
        self.nc.clear_and_free_semaphores(self.semaphores)
        self.nc.all_engine_barrier()

    def sb(self, name, shape, dt=F32):
        return self.ctx.enter_context(self.nc.sbuf_tensor(f"{self.prefix}_{name}", shape, dt))

    def ps(self, name, shape, dt=F32):
        return self.ctx.enter_context(self.nc.psum_tensor(f"{self.prefix}_{name}", shape, dt))

    def counter(self, name, per=0, ahead=0):
        self.semaphores.append(self.nc.alloc_semaphore(f"{self.prefix}_{name}"))
        return Signal(self.semaphores[-1], per, ahead)


def alone(eng, sem, value, started):
    if not isinstance(value, int):
        value = eng.to_reg(value)
        eng.wait_ge(started.sem, 1)
    eng.wait_ge(sem, value)


class Norm:

    MAGIC, NEWTON = float(0x5F3759DF), 3

    def __init__(self, room, name, tiles):
        self.tiles = tiles
        self.stats = room.sb(name + "_stats", [P, tiles, 6])
        self.mv = room.sb(name + "_mv", [P, tiles, 2])
        self.var = room.sb(name + "_var", [P, tiles])
        self.half = room.sb(name + "_half", [P, tiles])
        self.work = room.sb(name + "_work", [P, tiles])
        self.rstd = room.sb(name + "_rstd", [P, tiles])

    def mean(self, t):
        return self.mv[:, t, 0:1]

    def r(self, t):
        return self.rstd[:, t:t + 1]

    def vector(self, dve, chain, x, eps):
        for t in range(self.tiles):
            last = dve.bn_stats(self.stats[:, t, :], x(t))
        chain(last, by_itself=True)
        for t in range(self.tiles):
            last = dve.bn_aggr(self.mv[:, t, :], self.stats[:, t, :])
        chain(last)
        if eps:
            chain(dve.tensor_scalar(self.var[:], self.mv[:, :, 1], eps, None, ALU.add))
        else:
            chain(dve.tensor_copy(self.var[:], self.mv[:, :, 1]))
        dve.tensor_scalar(self.half[:], self.var[:], -0.5, None, ALU.mult)
        chain(dve.tensor_scalar(self.rstd[:].bitcast(I32), self.var[:].bitcast(I32), -0.5, self.MAGIC,
                                ALU.mult, ALU.add))
        for _ in range(self.NEWTON):
            chain(dve.tensor_tensor(self.work[:], self.half[:], self.rstd[:], ALU.mult))
            chain(dve.tensor_tensor(self.work[:], self.work[:], self.rstd[:], ALU.mult))
            chain(dve.scalar_tensor_tensor(self.rstd[:], self.work[:], 1.5, self.rstd[:], ALU.add, ALU.mult))


class Attention:

    HEADS, GROUP = 16, 4

    def __init__(self, room, head_rows, depth, value, scale, biased):
        self.head_rows, self.depth, self.value, self.scale, self.biased = head_rows, depth, value, scale, biased
        self.groups = self.HEADS // self.GROUP
        self.mtiles = self.GROUP * head_rows // P
        m = room
        self.qT = m.sb("qT", [P, 2, self.mtiles, S])
        self.kT = m.sb("kT", [P, 2, self.mtiles, S])
        self.v = m.sb("v", [P, 2, ST, self.GROUP * value])
        self.logit = m.sb("logit", [P, 2, ST, S]) if biased else None
        self.neg_max = m.sb("neg_max", [P, 2, ST])
        self.prob = m.sb("prob", [P, 2, ST, S])
        self.row_sum = m.sb("row_sum", [P, ST, self.HEADS])
        self.row_inv = m.sb("row_inv", [P, ST, self.HEADS])
        self.pT = m.sb("pT", [P, 2, ST, S])
        self.o = m.sb("o", [P, ST, self.HEADS * value])
        self.features = self.HEADS * value // P
        self.oT = m.sb("oT", [P, self.features, S])
        self.psS = [m.ps(f"psS{n}", [P, ST, S]) for n in range(2)]
        self.psT = [m.ps(f"psT{n}", [P, ST, S]) for n in range(2)]
        self.psO = [m.ps(f"psO{n}", [P, 512]) for n in range(2)]
        self.psA = m.ps("psA", [P, 512])
        self.psB = m.ps("psB", [P, 512])
        g, h = self.groups, self.HEADS
        self.projected = m.counter("projected", 3 * g, ahead=3 * g)
        self.q_kept = m.counter("q_kept", g)
        self.k_kept = m.counter("k_kept", g)
        self.v_kept = m.counter("v_kept", g)
        self.scored = m.counter("scored", h)
        self.bias_added = m.counter("bias_added", h, ahead=h)
        self.max_ready = m.counter("max_ready", h)
        self.exp_done = m.counter("exp_done", h)
        self.turned = m.counter("turned", h)
        self.pT_kept = m.counter("pT_kept", h)
        self.weighed = m.counter("weighed", h)
        self.inv_ready = m.counter("inv_ready", g)
        self.o_kept = m.counter("o_kept", g)
        self.o_turned = m.counter("o_turned", self.features // 2)
        self.oT_kept = m.counter("oT_kept", self.features // 2)
        self.projected_out = m.counter("projected_out", 1)

    def open(self, pe=None, dve=None):
        if pe is not None:
            self.projected.open(pe)
        if dve is not None:
            self.bias_added.open(dve)

    def head_at(self, h):
        row = (h % self.GROUP) * self.head_rows
        return row // P, row % P

    def tensor(self, pe, ident, project_q, project_k, project_v, w_out, i):
        def project(g):
            if g >= 1:
                pe.wait_ge(*self.v_kept.at(g, i))
            project_q(g, self.psA).then_inc(self.projected.sem, 1)
            if g >= 1:
                pe.wait_ge(*self.k_kept.at(g, i))
            project_k(g, self.psB).then_inc(self.projected.sem, 1)
            pe.wait_ge(*self.q_kept.at(g + 1, i))
            project_v(g, self.psA).then_inc(self.projected.sem, 1)

        def scores(h):
            g = h // self.GROUP
            if h % self.GROUP == 0:
                pe.wait_ge(*self.q_kept.at(g + 1, i))
                pe.wait_ge(*self.k_kept.at(g + 1, i))
            if h >= 2:
                pe.wait_ge(*(self.bias_added if self.biased else self.exp_done).at(h - 1, i))
            mt, row = self.head_at(h)
            for qt in range(ST):
                last = pe.matmul(self.psS[h % 2][:, qt, :],
                                 self.qT[row:row + self.depth, g % 2, mt, qt * P:(qt + 1) * P],
                                 self.kT[row:row + self.depth, g % 2, mt, :], start=True, stop=True)
            last.then_inc(self.scored.sem, 1)

        def turn(h):
            pe.wait_ge(*self.exp_done.at(h + 1, i))
            if h >= 2:
                pe.wait_ge(*self.pT_kept.at(h - 1, i))
            for kt in range(ST):
                for qt in range(ST):
                    last = pe.transpose(self.psT[h % 2][:, kt, qt * P:(qt + 1) * P],
                                        self.prob[:, h % 2, qt, kt * P:(kt + 1) * P], ident[:])
            last.then_inc(self.turned.sem, 1)

        def weigh(h):
            g, j = h // self.GROUP, h % self.GROUP
            if j == 0:
                pe.wait_ge(*self.v_kept.at(g + 1, i))
                if g >= 2:
                    pe.wait_ge(*self.o_kept.at(g - 1, i))
            pe.wait_ge(*self.pT_kept.at(h + 1, i))
            out = self.psO[g % 2][:, 0:ST * self.GROUP * self.value].rearrange("p (t d) -> p t d", t=ST)
            for qt in range(ST):
                for kt in range(ST):
                    last = pe.matmul(out[:, qt, j * self.value:(j + 1) * self.value],
                                     self.pT[:, h % 2, kt, qt * P:(qt + 1) * P],
                                     self.v[:, g % 2, kt, j * self.value:(j + 1) * self.value],
                                     start=(kt == 0), stop=(kt == ST - 1))
            last.then_inc(self.weighed.sem, 1)

        project(0)
        for h in range(self.HEADS + 2):
            if h < self.HEADS:
                scores(h)
            if 1 <= h <= self.HEADS:
                turn(h - 1)
            if h >= 2:
                weigh(h - 2)
            if h % self.GROUP == 1 and h // self.GROUP + 1 < self.groups:
                project(h // self.GROUP + 1)
        for j in range(self.features // 2):
            pe.wait_ge(*self.o_kept.at(-(-self.groups * (2 * j + 2) // self.features), i))
            if j >= 2:
                pe.wait_ge(*self.oT_kept.at(j - 1, i))
            for f in range(2):
                for qt in range(ST):
                    last = pe.transpose(self.psT[j % 2][:, f, qt * P:(qt + 1) * P],
                                        self.o[:, qt, (2 * j + f) * P:(2 * j + f + 1) * P], ident[:])
            last.then_inc(self.o_turned.sem, 1)
        pe.wait_ge(*self.oT_kept.at(self.features // 2, i))
        out = self.psA[:].rearrange("p (t d) -> p t d", t=ST)
        for qt in range(ST):
            for f in range(self.features):
                last = pe.matmul(out[:, qt, :], self.oT[:, f, qt * P:(qt + 1) * P], w_out[:, f, :],
                                 start=(f == 0), stop=(f == self.features - 1))
        last.then_inc(self.projected_out.sem, 1)

    def scalar(self, act, i):
        def keep_qk(g):
            act.wait_ge(*self.projected.at(3 * g + 1, i))
            act.activation(self.qT[:, g % 2], self.psA[:, 0:self.mtiles * S].rearrange("p (m q) -> p m q", q=S),
                           ACT.Copy, scale=self.scale).then_inc(self.q_kept.sem, 1)
            act.wait_ge(*self.projected.at(3 * g + 2, i))
            act.activation(self.kT[:, g % 2], self.psB[:, 0:self.mtiles * S].rearrange("p (m q) -> p m q", q=S),
                           ACT.Copy).then_inc(self.k_kept.sem, 1)

        keep_qk(0)
        for h in range(self.HEADS + 1):
            if h < self.HEADS:
                act.wait_ge(*self.max_ready.at(h + 1, i))
                if h >= 2:
                    act.wait_ge(*self.turned.at(h - 1, i))
                source = self.logit[:, h % 2] if self.biased else self.psS[h % 2]
                for qt in range(ST):
                    last = act.activation(self.prob[:, h % 2, qt, :], source[:, qt, :], ACT.Exp,
                                          bias=self.neg_max[:, h % 2, qt:qt + 1],
                                          accum_out=self.row_sum[:, qt, h:h + 1])
                last.then_inc(self.exp_done.sem, 1)
            if h >= 1:
                act.wait_ge(*self.turned.at(h, i))
                if h >= 3:
                    act.wait_ge(*self.weighed.at(h - 2, i))
                act.activation(self.pT[:, (h - 1) % 2], self.psT[(h - 1) % 2][:], ACT.Copy).then_inc(
                    self.pT_kept.sem, 1)
            if h % self.GROUP == 1 and h // self.GROUP + 1 < self.groups:
                keep_qk(h // self.GROUP + 1)
        for j in range(self.features // 2):
            act.wait_ge(*self.o_turned.at(j + 1, i))
            act.activation(self.oT[:, 2 * j:2 * j + 2, :], self.psT[j % 2][:], ACT.Copy).then_inc(self.oT_kept.sem, 1)

    def vector(self, dve, i, bias=None):
        def keep_v(g):
            dve.wait_ge(*self.projected.at(3 * g + 3, i))
            width = ST * self.GROUP * self.value
            dve.tensor_copy(self.v[:, g % 2], self.psA[:, 0:width].rearrange("p (t d) -> p t d", t=ST)).then_inc(
                self.v_kept.sem, 1)

        def normalise(g):
            dve.wait_ge(*self.exp_done.at(self.GROUP * (g + 1), i))
            heads = slice(self.GROUP * g, self.GROUP * (g + 1))
            dve.reciprocal(self.row_inv[:, :, heads], self.row_sum[:, :, heads]).then_inc(self.inv_ready.sem, 1)
            dve.wait_ge(*self.weighed.at(self.GROUP * (g + 1), i))
            dve.wait_ge(*self.inv_ready.at(g + 1, i))
            width = self.GROUP * self.value
            for qt in range(ST):
                last = dve.tensor_tensor(
                    self.o[:, qt, g * width:(g + 1) * width].rearrange("p (h d) -> p h d", d=self.value),
                    self.psO[g % 2][:, qt * width:(qt + 1) * width].rearrange("p (h d) -> p h d", d=self.value),
                    self.row_inv[:, qt, heads].unsqueeze(2).to_broadcast([P, self.GROUP, self.value]), ALU.mult)
            last.then_inc(self.o_kept.sem, 1)

        keep_v(0)
        for h in range(self.HEADS):
            dve.wait_ge(*self.scored.at(h + 1, i))
            if h >= 2:
                dve.wait_ge(*self.exp_done.at(h - 1, i))
            source = self.psS[h % 2]
            if self.biased:
                dve.tensor_tensor(self.logit[:, h % 2], self.psS[h % 2][:], bias[:], ALU.add).then_inc(
                    self.bias_added.sem, 1)
                dve.wait_ge(*self.bias_added.at(h + 1, i))
                source = self.logit[:, h % 2]
            dve.tensor_reduce(self.neg_max[:, h % 2, :], source[:], AX, ALU.max, negate=True).then_inc(
                self.max_ready.sem, 1)
            if h % self.GROUP == 1 and h // self.GROUP + 1 < self.groups:
                keep_v(h // self.GROUP + 1)
            if h % self.GROUP == self.GROUP - 2 and h > self.GROUP:
                normalise(h // self.GROUP - 1)
        normalise(self.groups - 1)


KD = 32
NL = 4
QUAD = P // KD
UM = 4
UNITS_B = P // QUAD // UM
PARTS = 3
COLS = QUAD * 2 * PARTS


def bias_stage(nc, w, bias_out):
    dT_in = w["distT"].rearrange("b (h p) q -> (b h) p q", p=P)
    dn_in = w["dist"].rearrange("b (t p) (h k) -> b h p t k", p=P, k=P)
    mask_in = w["mask"].rearrange("b (h k) -> (b h) k", k=P)
    out_v = bias_out.rearrange("(l b) (t p) (h k) -> b h p l t k", l=NL, p=P, k=P)
    with ExitStack() as ctx:
        m = Room(nc, ctx, "bias")
        ident = m.sb("ident", [P, P])
        select = m.sb("select", [P, KD, QUAD, KD])
        abw = m.sb("abw", [P, 3, NL])
        neg_b = m.sb("neg_b", [P, NL])
        bto = m.sb("bto", [P, NL])
        coef = m.sb("coef", [P, NL, 2])
        rest = m.sb("rest", [P, NL, 2])
        part = m.sb("part", [P, NL, 2, PARTS], BF16)
        rhs = m.sb("rhs", [P, NL, QUAD, 2, PARTS], BF16)
        ones = m.sb("ones", [P, P], BF16)
        dT = m.sb("dT", [P, S])
        dn = m.sb("dn", [P, ST, P])
        mask = m.sb("mask", [P, P])
        spread = [m.sb(f"spread{n}", [P, UM * S]) for n in range(2)]
        on = [m.sb(f"on{n}", [P, NL, UM * S], BF16) for n in range(2)]
        sums = m.sb("sums", [P, NL * ST, UNITS_B * UM, QUAD, 2])
        t1 = m.sb("t1", [P, NL * ST, P])
        bo = m.sb("bo", [P, NL * ST, P])
        psX = [m.ps(f"psX{n}", [P, UM * S]) for n in range(2)]
        psP = [m.ps(f"psP{n}", [P, 2, 512]) for n in range(2)]
        U = UNITS_B
        const_in = m.counter("const_in")
        prep = m.counter("prep")
        ready = m.counter("ready")
        loaded = m.counter("loaded", 48)
        spread_done = m.counter("spread_done", U)
        copied = m.counter("copied", U, ahead=2)
        on_v = m.counter("on_v", U, ahead=2)
        on_a = m.counter("on_a", U)
        summed = m.counter("summed", U, ahead=U)
        reduced = m.counter("reduced", U, ahead=2)
        combined = m.counter("combined", 1, ahead=1)
        stored = m.counter("stored", 16 * NL, ahead=16 * NL)
        chain = m.counter("chain", 2)

        with nc.Block() as block:
            @block.sync
            def _(sp):
                stored.open(sp)
                sp.dma_start(ident[:], w["ident"]).then_inc(const_in.sem, 16)
                for g in range(QUAD):
                    sp.dma_start(abw[g * KD:(g + 1) * KD], w["abw"]).then_inc(const_in.sem, 16)
                sp.dma_start(bto[:], w["bto"].partition_broadcast(P)).then_inc(const_in.sem, 16)
                with sp.Fori(0, B) as b:
                    for h in range(2):
                        sp.wait_ge(*combined.at(0, b * 2 + h))
                        sp.dma_start(dT[:], dT_in[bass.ds(b * 2 + h, 1)][0]).then_inc(loaded.sem, 16)
                        sp.dma_start(dn[:], dn_in[bass.ds(b, 1)][0][h]).then_inc(loaded.sem, 16)
                        sp.dma_start(mask[:], mask_in[bass.ds(b * 2 + h, 1)][0].partition_broadcast(P)).then_inc(
                            loaded.sem, 16)
                        sp.wait_ge(*combined.at(1, b * 2 + h))
                        for l in range(NL):
                            sp.dma_start(out_v[bass.ds(b, 1)][0][h][:, l], bo[:, 2 * l:2 * l + 2, :]).then_inc(
                                stored.sem, 16)
                sp.wait_ge(*stored.at(0, 2 * B))

            @block.tensor
            def _(pe):
                summed.open(pe)
                pe.wait_ge(*ready.at(1))
                with pe.Fori(0, 2 * B) as i:
                    pe.wait_ge(*loaded.at(48, i))

                    def spread_unit(u):
                        pe.wait_ge(*copied.at(u + 1 - 2, i))
                        for r in range(UM):
                            rows = select[:, u * UM + r].rearrange("p g k -> p (g k)")
                            last = pe.matmul(psX[u % 2][:, r * S:(r + 1) * S], rows, dT[:], start=True, stop=True)
                        last.then_inc(spread_done.sem, 1)

                    def sum_unit(u):
                        pe.wait_ge(*on_v.at(u + 1, i))
                        pe.wait_ge(*on_a.at(u + 1, i))
                        pe.wait_ge(*reduced.at(u + 1 - 2, i))
                        for l in range(NL):
                            for q in range(ST):
                                for r in range(UM):
                                    lq = l * ST + q
                                    col = (lq % 4) * UM * COLS + r * COLS
                                    out = psP[u % 2][:, lq // 4, col:col + COLS]
                                    terms = rhs[:, l].rearrange("p g a c -> p (g a c)")
                                    if l == NL - 1:
                                        pe.matmul(out, ones[:], terms, start=True, stop=False)
                                    last = pe.matmul(out, on[u % 2][:, l, r * S + q * P:r * S + (q + 1) * P], terms,
                                                     start=(l < NL - 1), stop=True)
                        last.then_inc(summed.sem, 1)

                    for u in range(U + 1):
                        if u < U:
                            spread_unit(u)
                        if u > 0:
                            sum_unit(u - 1)

            @block.scalar
            def _(act):
                copied.open(act)
                act.wait_ge(*ready.at(1))
                with act.Fori(0, 2 * B) as i:
                    for u in range(U):
                        act.wait_ge(*spread_done.at(u + 1, i))
                        act.wait_ge(*on_v.at(u + 1 - 2, i))
                        act.activation(spread[u % 2][:], psX[u % 2][:], ACT.Copy).then_inc(copied.sem, 1)
                        act.wait_ge(*copied.at(u + 1, i))
                        act.wait_ge(*summed.at(u + 1 - 2, i))
                        act.activation(on[u % 2][:, NL - 1, :], spread[u % 2][:], ACT.Sign,
                                       scale=abw[:, 0, NL - 1:NL], bias=abw[:, 1, NL - 1:NL]).then_inc(on_a.sem, 1)

            @block.vector
            def _(dve):
                on_v.open(dve)
                reduced.open(dve)
                combined.open(dve)
                link = Chain(dve, prep)
                dve.memset(ones[:], 1.0)
                link(dve.memset(rhs[:], 0.0))
                dve.wait_ge(*const_in.at(16 * 6))
                link(dve.tensor_copy(select[:], ident[:].rearrange("p (g r) -> p r g", g=QUAD).unsqueeze(3).to_broadcast(
                    [P, KD, QUAD, KD])))
                link(dve.tensor_scalar(neg_b[:], abw[:, 1, :], -1.0, None, ALU.mult))
                for n in range(2):
                    link(dve.tensor_tensor(coef[:, :, n], abw[:, n, :], abw[:, 2, :], ALU.mult))
                link(dve.tensor_scalar(coef[:, NL - 1, :], coef[:, NL - 1, :], 0.5, None, ALU.mult))
                link(dve.tensor_copy(rest[:], coef[:]))
                for c in range(PARTS):
                    link(dve.tensor_copy(part[:, :, :, c], rest[:]))
                    if c < PARTS - 1:
                        link(dve.tensor_tensor(rest[:], rest[:], part[:, :, :, c], ALU.subtract))
                for g in range(QUAD):
                    rows = slice(g * KD, (g + 1) * KD)
                    last = dve.tensor_copy(rhs[rows, :, g], part[rows])
                last.then_inc(ready.sem, 1)

                with dve.Fori(0, 2 * B) as i:
                    link = Chain(dve, chain, i)

                    def switch_unit(u):
                        dve.wait_ge(*copied.at(u + 1, i))
                        dve.wait_ge(*summed.at(u + 1 - 2, i))
                        for l in range(NL - 1):
                            last = dve.tensor_scalar(on[u % 2][:, l, :], spread[u % 2][:], abw[:, 0, l:l + 1],
                                                     neg_b[:, l:l + 1], ALU.mult, ALU.is_gt)
                        last.then_inc(on_v.sem, 1)

                    def reduce_unit(u):
                        dve.wait_ge(*summed.at(u + 1, i))
                        src = psP[u % 2][:, :, 0:4 * UM * COLS].rearrange("p n (q x c) -> p n q x c", q=4, c=PARTS)
                        for n in range(2):
                            last = dve.tensor_reduce(
                                sums[:, 4 * n:4 * n + 4, u * UM:(u + 1) * UM].rearrange("p q r g a -> p q (r g a)"),
                                src[:, n], AX, ALU.add)
                        last.then_inc(reduced.sem, 1)

                    for u in range(U + 1):
                        if u < U:
                            switch_unit(u)
                        if u > 0:
                            reduce_unit(u - 1)
                    dve.wait_ge(*reduced.at(U, i))
                    dve.wait_ge(*loaded.at(48, i))
                    dve.wait_ge(*stored.at(0, i))
                    keys = lambda x, lq: x[:, lq].rearrange("p (g r) -> p g r", g=QUAD)
                    for lq in range(NL * ST):
                        last = dve.tensor_tensor(keys(t1, lq), sums[:, lq, :, :, 0].rearrange("p r g -> p g r"),
                                                 dn[:, lq % ST].rearrange("p (g r) -> p g r", g=QUAD), ALU.mult)
                    link(last)
                    for lq in range(NL * ST):
                        last = dve.scalar_tensor_tensor(
                            out=keys(t1, lq), in0=keys(t1, lq), scalar=bto[:, lq // ST:lq // ST + 1],
                            in1=sums[:, lq, :, :, 1].rearrange("p r g -> p g r"), op0=ALU.add, op1=ALU.add)
                    link(last)
                    dve.tensor_tensor(bo[:], t1[:], mask[:].unsqueeze(1).to_broadcast([P, NL * ST, P]),
                                      ALU.add).then_inc(combined.sem, 1)
                    link.close()


INNER, NST, RANK, TAPS = 512, 16, 64, 4
IT = INNER // P
PRM = RANK + 2 * NST
LOG1P = (2.0, 0.6666664033669932, 0.40007560644854595, 0.2823661980652396, 0.26851498016560554)


def scan_stage(nc, x_in, w, x_out):
    batches_in = x_in.rearrange("(b t p) d -> b p t d", p=P, t=ST)
    batches_out = x_out.rearrange("(b t p) d -> b p t d", p=P, t=ST)
    with ExitStack() as ctx:
        m = Room(nc, ctx, "ssm")
        ident = m.sb("ident", [P, P])
        ones = m.sb("ones", [1, P])
        two = m.sb("two", [P, 1])
        ln_wb = m.sb("ln_wb", [P, DT, 2])
        in_w = m.sb("in_w", [P, DT, 2 * INNER])
        in_b = m.sb("in_b", [P, 2 * IT])
        taps = m.sb("taps", [P, IT, TAPS + 1])
        xp_w = m.sb("xp_w", [P, IT, PRM])
        dtp_w = m.sb("dtp_w", [RANK, INNER])
        dtp_b = m.sb("dtp_b", [P, IT])
        a = m.sb("a", [P, IT, NST])
        skip = m.sb("skip", [P, IT])
        out_w = m.sb("out_w", [P, IT, D])
        out_b = m.sb("out_b", [1, D])
        x = m.sb("x", [P, 3, ST, D])
        hn = m.sb("hn", [P, ST, D])
        hT = m.sb("hT", [P, DT, S])
        line = m.sb("line", [P, IT, TAPS - 1 + S])
        gate = m.sb("gate", [P, IT, S])
        conv = m.sb("conv", [P, IT, S])
        sig_c = m.sb("sig_c", [P, IT, S])
        sig_g = m.sb("sig_g", [P, IT, S])
        gated = m.sb("gated", [P, 2, IT, S])
        u = m.sb("u", [P, 2, IT, S])
        params = m.sb("params", [PRM, S])
        soft = m.sb("soft", [P, IT, S])
        dt = m.sb("dt", [P, IT, S])
        dtu = m.sb("dtu", [P, IT, S])
        dtr, ratio, square = conv, sig_c, gate
        rowsB = m.sb("rowsB", [P, NST, S])
        rowsC = m.sb("rowsC", [P, NST, S])
        decay = [m.sb(f"decay{n}", [P, NST, S]) for n in range(2)]
        state = [m.sb(f"state{n}", [P, NST, S]) for n in range(2)]
        y = m.sb("y", [P, IT, S])
        xo = m.sb("xo", [P, ST, D])
        psSum = [m.ps(f"psSum{n}", [P, S]) for n in range(2)]
        psOut = m.ps("psOut", [P, ST, D])
        psTurn = m.ps("psTurn", [P, 2, S])
        psP = [m.ps(f"psP{n}", [P, 2, S]) for n in range(4)]
        norm_in, norm_out = Norm(m, "norm_in", ST), Norm(m, "norm_out", ST)
        started = m.counter("started", ahead=1)
        const_in = m.counter("const_in")
        a_exp = m.counter("a_exp")
        loaded = m.counter("loaded", 16)
        stored = m.counter("stored", 16, ahead=16)
        chain = m.counter("chain", 26)
        last_chain = m.counter("last_chain", 14)
        setup = m.counter("setup")
        normed = m.counter("normed", 1)
        n_turned = m.counter("n_turned", 1)
        nT_kept = m.counter("nT_kept", 1)
        projected = m.counter("projected", 4)
        proj_kept = m.counter("proj_kept", 4)
        conv_done = m.counter("conv_done", 1)
        gate_tanh = m.counter("gate_tanh", 1)
        conv_tanh = m.counter("conv_tanh", 1)
        u_ready = m.counter("u_ready", 1)
        params_done = m.counter("params_done", 1)
        params_kept = m.counter("params_kept", 1)
        dt_done = m.counter("dt_done", 1)
        abs_ready = m.counter("abs_ready", 1)
        soft_exp = m.counter("soft_exp", 3)
        dt_ready = m.counter("dt_ready", 1)
        rows_spread = m.counter("rows_spread", NST)
        rows_kept = m.counter("rows_kept", NST)
        decayed = m.counter("decayed", IT)
        driven = m.counter("driven", IT)
        scanned = m.counter("scanned", IT)
        read_out = m.counter("read_out", IT)
        added = m.counter("added", IT)
        skipped = m.counter("skipped", IT)
        y_ready = m.counter("y_ready", IT)
        out_done = m.counter("out_done", 1)
        x_read = m.counter("x_read", 1, ahead=3)
        done = m.counter("done", 1)

        with nc.Block() as block:
            @block.sync
            def _(sp):
                started.open(sp)
                stored.open(sp)
                for dst, src in ((ident, w["ident"]), (ln_wb, w["ln_wb"]), (in_w, w["in_wT"].rearrange("(k p) n -> p k n", p=P)),
                                 (in_b, w["in_b_cols"]), (taps, w["taps"]),
                                 (xp_w, w["xp_wT"].rearrange("(k p) n -> p k n", p=P)), (dtp_w, w["dtp_wT"]),
                                 (dtp_b, w["dtp_b_cols"]), (a, w["A_log"].rearrange("(k p) n -> p k n", p=P)),
                                 (skip, w["D_cols"]), (out_w, w["out_wT"].rearrange("(k p) n -> p k n", p=P)),
                                 (out_b, w["out_b"].rearrange("(a n) -> a n", a=1))):
                    sp.dma_start(dst[:], src).then_inc(const_in.sem, 16)
                def load(b, before=True):
                    if before:
                        read, there = (sp.to_reg(v[1]) for v in (x_read.at(0, b - 2), loaded.at(16, b - 1)))
                        sp.wait_ge(x_read.sem, read)
                        sp.wait_ge(loaded.sem, there)
                    sp.dma_start(x[:, bass.ds(b % 3, 1)][:, 0], batches_in[bass.ds(b, 1)][0]).then_inc(loaded.sem, 16)

                def store(b):
                    sp.wait_ge(*done.at(1, b))
                    sp.dma_start(batches_out[bass.ds(b, 1)][0], xo[:]).then_inc(stored.sem, 16)

                load(0, False)
                load(1)
                with sp.Fori(0, B - 2) as b:
                    load(b + 2)
                    store(b)
                store(B - 2)
                store(B - 1)
                sp.wait_ge(*stored.at(0, B))

            @block.tensor
            def _(pe):
                def project_in(b):
                    pe.wait_ge(*normed.at(1, b))
                    for k in range(DT):
                        for t in range(ST):
                            last = pe.transpose(psTurn[:, k, t * P:(t + 1) * P], hn[:, t, k * P:(k + 1) * P], ident[:])
                    last.then_inc(n_turned.sem, 1)
                    pe.wait_ge(*nT_kept.at(1, b))
                    for j in range(2 * IT):
                        for k in range(DT):
                            last = pe.matmul(psP[j // 2][:, j % 2, :], in_w[:, k, j * P:(j + 1) * P], hT[:, k, :],
                                             start=(k == 0), stop=(k == DT - 1))
                        if j % 2:
                            last.then_inc(projected.sem, 1)

                def project_params(b):
                    pe.wait_ge(*u_ready.at(1, b))
                    for k in range(IT):
                        last = pe.matmul(psTurn[0:PRM, 0, :], xp_w[:, k, :], u[:, bass.ds(b % 2, 1), k, :][:, 0],
                                         start=(k == 0), stop=(k == IT - 1))
                    last.then_inc(params_done.sem, 1)
                    pe.wait_ge(*params_kept.at(1, b))
                    pe.wait_ge(*proj_kept.at(4, b))
                    for j in range(IT):
                        last = pe.matmul(psP[2 + j // 2][:, j % 2, :], dtp_w[:, j * P:(j + 1) * P], params[0:RANK, :],
                                         start=True, stop=True)
                    last.then_inc(dt_done.sem, 1)

                def spread(b, first):
                    for n in range(0, NST // 2) if first else range(NST // 2, NST):
                        if n == 0:
                            pe.wait_ge(*abs_ready.at(1, b))
                        if n >= 4:
                            pe.wait_ge(*rows_kept.at(n - 3, b))
                        for c in range(2):
                            row = RANK + 2 * n + c
                            last = pe.matmul(psP[n % 4][:, c, :], ident[0:PRM, row:row + 1].to_broadcast([PRM, P]),
                                             params[:], start=True, stop=True)
                        last.then_inc(rows_spread.sem, 1)

                def sum_states(j, b):
                    pe.wait_ge(*read_out.at(j + 1, b))
                    if j >= 2:
                        pe.wait_ge(*skipped.at(j - 1, b))
                    for n in range(NST):
                        last = pe.matmul(psSum[j % 2][:], ident[:], state[j % 2][:, n, :], start=(n == 0),
                                         stop=(n == NST - 1))
                    last.then_inc(added.sem, 1)

                def project_out(b):
                    pe.wait_ge(*y_ready.at(IT, b))
                    for t in range(ST):
                        for k in range(IT):
                            pe.matmul(psOut[:, t, :], y[:, k, t * P:(t + 1) * P], out_w[:, k, :],
                                      start=(k == 0), stop=False)
                        last = pe.matmul(psOut[:, t, :], ones[:], out_b[:], start=False, stop=True)
                    last.then_inc(out_done.sem, 1)

                def step(b, after):
                    if after:
                        project_in(b + 1)
                    sum_states(0, b)
                    sum_states(1, b)
                    if after:
                        project_params(b + 1)
                    sum_states(2, b)
                    if after:
                        spread(b + 1, True)
                    sum_states(3, b)
                    project_out(b)
                    if after:
                        spread(b + 1, False)

                pe.wait_ge(*const_in.at(16 * 12))
                project_in(0)
                project_params(0)
                spread(0, True)
                spread(0, False)
                with pe.Fori(0, B - 1) as b:
                    step(b, True)
                step(B - 1, False)

            @block.scalar
            def _(act):
                def keep_projected(b):
                    for n in range(4):
                        act.wait_ge(*projected.at(n + 1, b))
                        for c in range(2):
                            j = 2 * n + c
                            out = line[:, j, TAPS - 1:] if j < IT else gate[:, j - IT, :]
                            last = act.activation(out, psP[n][:, c, :], ACT.Identity, bias=in_b[:, j:j + 1],
                                                  scale=1.0 if j < IT else 0.5)
                        last.then_inc(proj_kept.sem, 1)
                    act.wait_ge(*proj_kept.at(4, b))
                    act.activation(sig_g[:], gate[:], ACT.Tanh).then_inc(gate_tanh.sem, 1)

                def keep_normed(b):
                    act.wait_ge(*n_turned.at(1, b))
                    for k in range(DT):
                        last = act.activation(hT[:, k, :], psTurn[:, k, :], ACT.Identity, scale=ln_wb[:, k, 0:1],
                                              bias=ln_wb[:, k, 1:2])
                    last.then_inc(nT_kept.sem, 1)

                def tanh_conv(b):
                    act.wait_ge(*conv_done.at(1, b))
                    act.activation(sig_c[:], conv[:], ACT.Tanh).then_inc(conv_tanh.sem, 1)

                def keep_params(b):
                    act.wait_ge(*params_done.at(1, b))
                    act.activation(params[:], psTurn[0:PRM, 0, :], ACT.Copy).then_inc(params_kept.sem, 1)

                def exp_steps(b):
                    act.wait_ge(*abs_ready.at(1, b))
                    act.activation(soft[:], soft[:], ACT.Exp, scale=-1.0).then_inc(soft_exp.sem, 1)
                    act.wait_ge(*soft_exp.at(1, b))
                    act.activation(ratio[:], soft[:], ACT.Ln, bias=two[:]).then_inc(soft_exp.sem, 1)
                    act.wait_ge(*soft_exp.at(2, b))
                    act.activation(ratio[:], ratio[:], ACT.Exp, scale=-1.0).then_inc(soft_exp.sem, 1)

                def keep_rows(b, first, before):
                    if before:
                        act.wait_ge(*(driven if first else read_out).at(IT, b - 1))
                    for n in range(0, NST // 2) if first else range(NST // 2, NST):
                        act.wait_ge(*rows_spread.at(n + 1, b))
                        rows, r = (rowsB, 2 * n) if first else (rowsC, 2 * n - NST)
                        act.activation(rows[:, r:r + 2, :], psP[n % 4][:], ACT.Copy).then_inc(rows_kept.sem, 1)

                def decays(j, b, before=True):
                    if j == 0:
                        act.wait_ge(*dt_ready.at(1, b))
                    if j >= 2:
                        act.wait_ge(*scanned.at(j - 1, b))
                    elif before:
                        act.wait_ge(*scanned.at(IT + j - 1, b - 1))
                    for n in range(NST):
                        last = act.activation(decay[j % 2][:, n, 1:], dt[:, j, 1:], ACT.Exp, scale=a[:, j, n:n + 1])
                    last.then_inc(decayed.sem, 1)

                def step(b, before, after):
                    if after:
                        keep_normed(b + 1)
                    decays(1, b, before)
                    if after:
                        keep_projected(b + 1)
                    decays(2, b)
                    if after:
                        tanh_conv(b + 1)
                    decays(3, b)
                    if after:
                        keep_params(b + 1)
                        exp_steps(b + 1)
                        keep_rows(b + 1, True, True)
                        decays(0, b + 1)
                        keep_rows(b + 1, False, True)

                act.wait_ge(*const_in.at(16 * 12))
                act.activation(a[:], a[:], ACT.Exp).then_inc(a_exp.sem, 1)
                act.wait_ge(*setup.at(1))
                keep_normed(0)
                keep_projected(0)
                tanh_conv(0)
                keep_params(0)
                exp_steps(0)
                keep_rows(0, True, False)
                keep_rows(0, False, False)
                decays(0, 0, False)
                step(0, False, True)
                with act.Fori(1, B - 1) as b:
                    step(b, True, True)
                step(B - 1, True, False)

            @block.gpsimd
            def _(pool):
                with pool.Fori(0, B) as b:
                    for j in range(IT):
                        pool.wait_ge(*scanned.at(j + 1, b))
                        pool.wait_ge(*rows_kept.at(NST, b))
                        pool.tensor_tensor(state[j % 2][:], state[j % 2][:], rowsC[:], ALU.mult).then_inc(
                            read_out.sem, 1)

            @block.vector
            def _(dve):
                def norm_first(b, link):
                    xb = x[:, bass.ds(b % 3, 1)][:, 0]
                    alone(dve, *loaded.at(16, b), started)
                    norm_in.vector(dve, link, lambda t: xb[:, t, :], 1e-5)
                    for t in range(ST):
                        last = dve.tensor_scalar(hn[:, t, :], xb[:, t, :], norm_in.mean(t), norm_in.r(t),
                                                 ALU.subtract, ALU.mult)
                    last.then_inc(normed.sem, 1)

                def convolve(b, link):
                    dve.wait_ge(*proj_kept.at(2, b))
                    for j in range(IT):
                        last = dve.tensor_scalar(conv[:, j, :], line[:, j, 0:S], taps[:, j, 0:1], taps[:, j, TAPS:TAPS + 1],
                                                 ALU.mult, ALU.add)
                    link(last)
                    for k in range(1, TAPS):
                        for j in range(IT):
                            last = dve.scalar_tensor_tensor(out=conv[:, j, :], in0=line[:, j, k:k + S],
                                                            scalar=taps[:, j, k:k + 1], in1=conv[:, j, :],
                                                            op0=ALU.mult, op1=ALU.add)
                        if k < TAPS - 1:
                            link(last)
                        else:
                            last.then_inc(conv_done.sem, 1)

                def silus(b, link):
                    slot = bass.ds(b % 2, 1)
                    dve.wait_ge(*conv_tanh.at(1, b))
                    dve.scalar_tensor_tensor(out=u[:, slot][:, 0], in0=sig_c[:], scalar=1.0, in1=conv[:], op0=ALU.add,
                                             op1=ALU.mult).then_inc(u_ready.sem, 1)
                    dve.wait_ge(*gate_tanh.at(1, b))
                    link(dve.scalar_tensor_tensor(out=gated[:, slot][:, 0], in0=sig_g[:], scalar=1.0, in1=gate[:],
                                                  op0=ALU.add, op1=ALU.mult))

                def start_steps(b, link):
                    dve.wait_ge(*u_ready.at(1, b))
                    dve.wait_ge(*dt_done.at(1, b))
                    for j in range(IT):
                        last = dve.tensor_scalar(dtr[:, j, :], psP[2 + j // 2][:, j % 2, :], dtp_b[:, j:j + 1], None,
                                                 ALU.add)
                    link(last)
                    dve.scalar_tensor_tensor(out=soft[:], in0=dtr[:], scalar=-1.0, in1=dtr[:], op0=ALU.mult,
                                             op1=ALU.max).then_inc(abs_ready.sem, 1)

                def finish_steps(b, link):
                    dve.wait_ge(*soft_exp.at(3, b))
                    link(dve.tensor_tensor(ratio[:], ratio[:], soft[:], ALU.mult))
                    link(dve.tensor_tensor(square[:], ratio[:], ratio[:], ALU.mult))
                    link(dve.tensor_scalar(soft[:], square[:], LOG1P[-1], None, ALU.mult))
                    for c in reversed(LOG1P[1:-1]):
                        link(dve.scalar_tensor_tensor(out=soft[:], in0=soft[:], scalar=c, in1=square[:],
                                                      op0=ALU.add, op1=ALU.mult))
                    link(dve.scalar_tensor_tensor(out=soft[:], in0=soft[:], scalar=LOG1P[0], in1=ratio[:],
                                                  op0=ALU.add, op1=ALU.mult))
                    dve.scalar_tensor_tensor(out=dt[:], in0=dtr[:], scalar=0.0, in1=soft[:], op0=ALU.max,
                                             op1=ALU.add).then_inc(dt_ready.sem, 1)
                    dve.wait_ge(*dt_ready.at(1, b))
                    link(dve.tensor_tensor(dtu[:], dt[:], u[:, bass.ds(b % 2, 1)][:, 0], ALU.mult))
                    link.close()

                def scan(j, b, before=True):
                    if j == 0:
                        dve.wait_ge(*rows_kept.at(NST // 2, b))
                    if j >= 2:
                        dve.wait_ge(*added.at(j - 1, b))
                    elif before:
                        dve.wait_ge(*added.at(IT + j - 1, b - 1))
                    dve.tensor_tensor(state[j % 2][:], rowsB[:], dtu[:, j, :].unsqueeze(1).to_broadcast([P, NST, S]),
                                      ALU.mult).then_inc(driven.sem, 1)
                    dve.wait_ge(*decayed.at(j + 1, b))
                    dve.wait_ge(*driven.at(j + 1, b))
                    flat = lambda t: t[j % 2][:].rearrange("p n s -> p (n s)")
                    dve.tensor_tensor_scan(flat(state), flat(decay), flat(state), 0.0, ALU.mult, ALU.add).then_inc(
                        scanned.sem, 1)

                def finish(j, b):
                    slot = bass.ds(b % 2, 1)
                    alone(dve, *added.at(j + 1, b), started)
                    dve.scalar_tensor_tensor(out=y[:, j, :], in0=u[:, slot, j, :][:, 0], scalar=skip[:, j:j + 1],
                                             in1=psSum[j % 2][:], op0=ALU.mult, op1=ALU.add).then_inc(skipped.sem, 1)
                    dve.wait_ge(*skipped.at(j + 1, b))
                    dve.tensor_tensor(y[:, j, :], y[:, j, :], gated[:, slot, j, :][:, 0], ALU.mult).then_inc(
                        y_ready.sem, 1)

                def output(b):
                    link = Chain(dve, last_chain, b, started)
                    dve.wait_ge(*out_done.at(1, b))
                    dve.wait_ge(*stored.at(0, b))
                    dve.scalar_tensor_tensor(out=xo[:], in0=x[:, bass.ds(b % 3, 1)][:, 0], scalar=2.0, in1=psOut[:],
                                             op0=ALU.mult, op1=ALU.add).then_inc(x_read.sem, 1)
                    alone(dve, *x_read.at(1, b), started)
                    norm_out.vector(dve, link, lambda t: xo[:, t, :], 1e-5)
                    for t in range(ST):
                        last = dve.tensor_scalar(xo[:, t, :], xo[:, t, :], norm_out.mean(t), norm_out.r(t),
                                                 ALU.subtract, ALU.mult)
                    last.then_inc(done.sem, 1)
                    dve.wait_ge(*done.at(1, b))
                    link(dve.tensor_copy(norm_out.work[:, 0:1], norm_out.rstd[:, 0:1]))
                    link.close()

                def step(b, before, after):
                    link = Chain(dve, chain, b + 1, started)
                    if after:
                        norm_first(b + 1, link)
                    scan(0, b, before)
                    if before:
                        output(b - 1)
                    scan(1, b, before)
                    if after:
                        convolve(b + 1, link)
                    finish(0, b)
                    scan(2, b)
                    if after:
                        silus(b + 1, link)
                    finish(1, b)
                    scan(3, b)
                    if after:
                        start_steps(b + 1, link)
                    finish(2, b)
                    if after:
                        finish_steps(b + 1, link)
                    finish(3, b)

                x_read.open(dve)
                dve.memset(ones[:], 1.0)
                dve.memset(two[:], 2.0)
                dve.memset(line[:], 0.0)
                for n in range(2):
                    dve.memset(decay[n][:, :, 0:1], 0.0)
                dve.wait_ge(*a_exp.at(1))
                dve.tensor_scalar(a[:], a[:], -1.0, None, ALU.mult)
                dve.tensor_scalar(taps[:], taps[:], 0.5, None, ALU.mult)
                dve.tensor_scalar(in_b[:, IT:], in_b[:, IT:], 0.5, None, ALU.mult).then_inc(setup.sem, 1)
                dve.wait_ge(*setup.at(1))
                link = Chain(dve, chain, 0, started)
                norm_first(0, link)
                convolve(0, link)
                silus(0, link)
                start_steps(0, link)
                finish_steps(0, link)
                step(0, False, True)
                with dve.Fori(1, B - 1) as b:
                    step(b, True, True)
                step(B - 1, True, False)
                output(B - 1)


XD = 16
XP = 32


def cross_stage(nc, x_in, w, x_out):
    batches_in = x_in.rearrange("(b t p) d -> b p t d", p=P, t=ST)
    batches_out = x_out.rearrange("(b t p) d -> b p t d", p=P, t=ST)
    with ExitStack() as ctx:
        m = Room(nc, ctx, "xat")
        ident = m.sb("ident", [P, P])
        ones = m.sb("ones", [1, P])
        wqk = m.sb("wqk", [P, 2, 2, P])
        wv = m.sb("wv", [P, P])
        wo = m.sb("wo", [P, DT, D])
        bo = m.sb("bo", [P, D])
        x = m.sb("x", [P, ST, D])
        xT = m.sb("xT", [P, DT, S])
        ctxT = m.sb("ctxT", [P, DT, S])
        xo = m.sb("xo", [P, ST, D])
        at = Attention(m, XP, XD, XD, D ** -0.5, False)
        norm = Norm(m, "norm", ST)
        started = m.counter("started", ahead=1)
        zeroed = m.counter("zeroed")
        const_in = m.counter("const_in")
        x_loaded = m.counter("x_loaded", 16)
        ctx_loaded = m.counter("ctx_loaded", 16)
        x_turned = m.counter("x_turned", 1)
        xT_kept = m.counter("xT_kept", 1)
        summed = m.counter("summed", 1, ahead=1)
        chain = m.counter("chain", 14)
        done = m.counter("done", 1)
        stored = m.counter("stored", 16, ahead=16)

        with nc.Block() as block:
            @block.sync
            def _(sp):
                started.open(sp)
                stored.open(sp)
                sp.dma_start(ident[:], w["ident"]).then_inc(const_in.sem, 16)
                sp.dma_start(wo[:], w["WoT"].rearrange("(k p) n -> p k n", p=P)).then_inc(const_in.sem, 16)
                sp.dma_start(bo[:], w["bo"].partition_broadcast(P)).then_inc(const_in.sem, 16)
                sp.wait_ge(*zeroed.at(1))
                for h in range(P // XD):
                    rows = slice(h * XD, (h + 1) * XD)
                    for n, name in enumerate(("WqT", "WkT")):
                        col = (h % 4) * XP
                        sp.dma_start(wqk[rows, n, h // 4, col:col + XD], w[name]).then_inc(const_in.sem, 16)
                    sp.dma_start(wv[rows, h * XD:(h + 1) * XD], w["WvT"]).then_inc(const_in.sem, 16)
                with sp.Fori(0, B) as b:
                    sp.wait_ge(*summed.at(0, b))
                    sp.dma_start(x[:], batches_in[bass.ds(b, 1)][0]).then_inc(x_loaded.sem, 16)
                    sp.wait_ge(*at.projected.at(0, b))
                    sp.dma_start(ctxT[:], w["ctxT"].rearrange("b (k p) s -> b p k s", p=P)[bass.ds(b, 1)][0]).then_inc(
                        ctx_loaded.sem, 16)
                    sp.wait_ge(*done.at(1, b))
                    sp.dma_start(batches_out[bass.ds(b, 1)][0], xo[:]).then_inc(stored.sem, 16)
                sp.wait_ge(*stored.at(0, B))

            @block.tensor
            def _(pe):
                at.open(pe=pe)
                pe.wait_ge(*const_in.at(16 * (3 + 3 * (P // XD))))
                with pe.Fori(0, B) as b:
                    pe.wait_ge(*x_loaded.at(16, b))
                    for k in range(DT):
                        for t in range(ST):
                            last = pe.transpose(at.psT[0][:, k, t * P:(t + 1) * P], x[:, t, k * P:(k + 1) * P], ident[:])
                    last.then_inc(x_turned.sem, 1)
                    pe.wait_ge(*xT_kept.at(1, b))
                    pe.wait_ge(*ctx_loaded.at(16, b))

                    def rows(n, source):
                        return lambda g, bank: pe.matmul(bank[:, 0:S], wqk[:, n, g % 2, :], source[:, g // 2, :],
                                                         start=True, stop=True)

                    def values(g, bank):
                        width = 4 * XD
                        for t in range(ST):
                            last = pe.matmul(bank[:, t * width:(t + 1) * width], ctxT[:, g // 2, t * P:(t + 1) * P],
                                             wv[:, (g % 2) * width:(g % 2 + 1) * width], start=True, stop=True)
                        return last

                    at.tensor(pe, ident, rows(0, xT), rows(1, ctxT), values, wo, b)

            @block.scalar
            def _(act):
                with act.Fori(0, B) as b:
                    act.wait_ge(*x_turned.at(1, b))
                    act.activation(xT[:], at.psT[0][:], ACT.Copy).then_inc(xT_kept.sem, 1)
                    at.scalar(act, b)

            @block.vector
            def _(dve):
                summed.open(dve)
                dve.memset(wv[:], 0.0)
                dve.memset(wqk[:], 0.0).then_inc(zeroed.sem, 1)
                dve.wait_ge(*const_in.at(16 * (3 + 3 * (P // XD))))
                with dve.Fori(0, B) as b:
                    link = Chain(dve, chain, b, started)
                    at.vector(dve, b)
                    dve.wait_ge(*at.projected_out.at(1, b))
                    dve.wait_ge(*stored.at(0, b))
                    dve.tensor_tensor(xo[:], x[:], at.psA[:].rearrange("p (t d) -> p t d", t=ST), ALU.add).then_inc(
                        summed.sem, 1)
                    dve.wait_ge(*summed.at(1, b))
                    link(dve.tensor_tensor(xo[:], xo[:], bo[:].unsqueeze(1).to_broadcast([P, ST, D]), ALU.add))
                    norm.vector(dve, link, lambda t: xo[:, t, :], 1e-5)
                    for t in range(ST):
                        last = dve.tensor_scalar(xo[:, t, :], xo[:, t, :], norm.mean(t), norm.r(t),
                                                 ALU.subtract, ALU.mult)
                    last.then_inc(done.sem, 1)
                    link.close()


E8, HID = 8, 128
IDX = 512
GATES = 1 + E8


def moe8_stage(nc, x_in, w, x_out):
    tiles_in = x_in.rearrange("(t p) d -> t p d", p=P)
    tiles_out = x_out.rearrange("(t p) d -> t p d", p=P)
    SL = range(2)
    with ExitStack() as ctx:
        m = Room(nc, ctx, "m8")
        ident = m.sb("ident", [P, P])
        ones = m.sb("ones", [1, P])
        ones_col = m.sb("ones_col", [P, 1], BF16)
        iota = m.sb("iota", [P, TOK])
        named = m.sb("named", [P, IDX // P, TOK], BF16)
        idx = m.sb("idx", [P, 2, IDX // P], I32)
        at_bt = m.sb("at_bt", [P, 2, IDX // P])
        test = m.sb("test", [P, 2, IDX // P])
        inside = m.sb("inside", [P, 2, IDX // P])
        key = m.sb("key", [P, IDX // P])
        hit = m.sb("hit", [P, NT])
        sw12 = m.sb("sw12", [P, DT, 2 * HID])
        sb12 = m.sb("sb12", [1, 2 * HID])
        gates_w = m.sb("gates_w", [P, DT, GATES])
        gates_b = m.sb("gates_b", [1, GATES])
        exp_bias = m.sb("exp_bias", [P, E8])
        ew12 = m.sb("ew12", [P, DT, E8, 2 * HID])
        eb12 = m.sb("eb12", [E8, 2 * HID])
        sw3 = m.sb("sw3", [P, D])
        sb3 = m.sb("sb3", [1, D])
        ew3 = m.sb("ew3", [P, E8, D])
        eb3 = m.sb("eb3", [E8, D])
        gain = m.sb("gain", [P, 2])
        shift = m.sb("shift", [P, 2])
        A = [m.ps(f"A{s}", [P, 512]) for s in SL]
        Bk = [m.ps(f"B{s}", [P, 512]) for s in SL]
        R = [m.ps(f"R{s}", [P, 2, 4, P]) for s in SL]
        const_in = m.counter("const_in")
        idx_in = m.counter("idx_in")
        iota_in = m.counter("iota_in")
        keyed = m.counter("keyed")
        marked = m.counter("marked")
        counted = m.counter("counted")

        with nc.Block() as block:
            @block.sync
            def _(sp):
                for n, name in enumerate(("index_b", "index_t")):
                    sp.dma_start(idx[:, n, :], w[name].rearrange("(p c) -> p c", p=P)).then_inc(idx_in.sem, 16)
                sp.dma_start(iota[:], w["iota_tok"].partition_broadcast(P)).then_inc(iota_in.sem, 16)
                halves = lambda a, b, n: ((slice(0, n), w[a]), (slice(n, 2 * n), w[b]))
                for cols, src in halves("sw1T", "sw2T", HID):
                    sp.dma_start(sw12[:, :, cols], src.rearrange("(k p) h -> p k h", p=P)).then_inc(const_in.sem, 16)
                for cols, src in halves("sb1", "sb2", HID):
                    sp.dma_start(sb12[:, cols], src.rearrange("(a h) -> a h", a=1)).then_inc(const_in.sem, 16)
                sp.dma_start(gates_w[:], w["gates_wT"].rearrange("(k p) h -> p k h", p=P)).then_inc(const_in.sem, 16)
                sp.dma_start(gates_b[:], w["gates_b"].rearrange("(a h) -> a h", a=1)).then_inc(const_in.sem, 16)
                sp.dma_start(exp_bias[:], w["exp_bias"].partition_broadcast(P)).then_inc(const_in.sem, 16)
                for cols, src in halves("ew1T", "ew2T", HID):
                    for k in range(DT):
                        sp.dma_start(ew12[:, k, :, cols], src[:, k * P:(k + 1) * P, :].rearrange("e p h -> p e h")).then_inc(
                            const_in.sem, 16)
                for cols, src in halves("eb1", "eb2", HID):
                    sp.dma_start(eb12[:, cols], src).then_inc(const_in.sem, 16)
                sp.dma_start(sw3[:], w["sw3T"]).then_inc(const_in.sem, 16)
                sp.dma_start(sb3[:], w["sb3"].rearrange("(a h) -> a h", a=1)).then_inc(const_in.sem, 16)
                sp.dma_start(ew3[:], w["ew3T"].rearrange("e h d -> h e d")).then_inc(const_in.sem, 16)
                sp.dma_start(eb3[:], w["eb3"]).then_inc(const_in.sem, 16)
                sp.dma_start(ident[:], w["ident"]).then_inc(const_in.sem, 16)
                sp.dma_start(gain[:], w["gains"]).then_inc(const_in.sem, 16)
                sp.dma_start(shift[:], w["shifts"]).then_inc(const_in.sem, 16)
                sp.wait_ge(*const_in.at(16 * 20))

            @block.vector
            def _(dve):
                link = Chain(dve, keyed)
                dve.memset(ones[:], 1.0)
                dve.memset(ones_col[:], 1.0)
                dve.wait_ge(*idx_in.at(32))
                link(dve.tensor_copy(at_bt[:], idx[:]))
                link(dve.tensor_scalar(test[:], at_bt[:], 0.0, None, ALU.is_lt))
                link(dve.tensor_scalar(test[:, 0], test[:, 0], float(B), None, ALU.mult))
                link(dve.tensor_scalar(test[:, 1], test[:, 1], float(S), None, ALU.mult))
                link(dve.tensor_tensor(at_bt[:], at_bt[:], test[:], ALU.add))
                link(dve.tensor_scalar(inside[:], at_bt[:], 0.0, None, ALU.is_ge))
                link(dve.tensor_scalar(test[:, 0], at_bt[:, 0], float(B), None, ALU.is_lt))
                link(dve.tensor_scalar(test[:, 1], at_bt[:, 1], float(S), None, ALU.is_lt))
                link(dve.tensor_tensor(inside[:], inside[:], test[:], ALU.mult))
                link(dve.tensor_tensor(inside[:, 0], inside[:, 0], inside[:, 1], ALU.mult))
                link(dve.scalar_tensor_tensor(out=key[:], in0=at_bt[:, 0], scalar=float(S), in1=at_bt[:, 1],
                                              op0=ALU.mult, op1=ALU.add))
                link(dve.scalar_tensor_tensor(out=key[:], in0=key[:], scalar=1.0, in1=inside[:, 0],
                                              op0=ALU.add, op1=ALU.mult))
                link(dve.tensor_scalar(key[:], key[:], -1.0, None, ALU.add))
                dve.wait_ge(*iota_in.at(16))
                for c in range(IDX // P):
                    last = dve.tensor_scalar(named[:, c, :], iota[:], key[:, c:c + 1], None, ALU.is_equal)
                last.then_inc(marked.sem, 1)
                dve.wait_ge(*counted.at(1))
                dve.tensor_scalar(hit[:], A[0][:, 0:NT], 0.5, None, ALU.is_gt)

            @block.tensor
            def _(pe):
                pe.wait_ge(*marked.at(1))
                for t in range(NT):
                    for c in range(IDX // P):
                        last = pe.matmul(A[0][:, t:t + 1], named[:, c, t * P:(t + 1) * P], ones_col[:],
                                         start=(c == 0), stop=(c == IDX // P - 1))
                last.then_inc(counted.sem, 1)

        sb = lambda n, shape, dt=F32: [m.sb(f"{n}{s}", shape, dt) for s in SL]
        sig = lambda n, per, ahead=0: [m.counter(f"{n}{s}", per, ahead) for s in SL]
        x, fT, gate_e, gate = sb("x", [P, D]), sb("fT", [P, DT, P]), sb("gate_e", [P, GATES]), sb("gate", [P, GATES])
        biased, best, best_i = sb("biased", [P, E8]), sb("best", [P, 8]), sb("best_i", [P, 8], U32)
        best_f, onehot, chosen = sb("best_f", [P, 8]), sb("onehot", [P, E8]), sb("chosen", [P, E8])
        pair, pair_m, mix = sb("pair", [P, 2]), sb("pair_m", [P, 1]), sb("mix", [P, 2])
        ohT, xTe, u, ue = sb("ohT", [E8, P]), sb("xTe", [P, DT, E8, P]), sb("u", [P, 2, 2 * HID]), sb("ue", [P, 2, HID])
        z, zT, zTe, y = sb("z", [P, 2, HID]), sb("zT", [P, 2, P]), sb("zTe", [P, E8, P]), sb("y", [P, D])
        inner = [Norm(m, f"inner{s}", 2) for s in SL]
        outer = [Norm(m, f"outer{s}", 1) for s in SL]
        started = m.counter("started", ahead=1)
        loaded, stored = sig("loaded", 16), sig("stored", 16, 16)
        x_read, done = sig("x_read", 1, 1), sig("done", 1)
        turned, turned_kept = sig("turned", 2), sig("turned_kept", 2)
        first, gates_kept, gate_exp = sig("first", 1), sig("gates_kept", 1), sig("gate_exp", 1)
        pair_ready, pair_exp = sig("pair_ready", 1), sig("pair_exp", 1)
        routed, rows_done, masked = sig("routed", 1), sig("rows_done", 1), sig("masked", 1)
        hidden, u_ready, u_exp = sig("hidden", 1), sig("u_ready", 1), sig("u_exp", 1)
        z_ready, z_masked, outs = sig("z_ready", 1), sig("z_masked", 1), sig("outs", 1)
        chains = sig("chain", 49)

        with nc.Block() as block:
            @block.sync
            def _(sp):
                started.open(sp)
                for s in SL:
                    stored[s].open(sp)
                with sp.Fori(0, NT // 2) as i:
                    for s in SL:
                        sp.wait_ge(*x_read[s].at(0, i))
                        sp.dma_start(x[s][:], tiles_in[bass.ds(i * 2 + s, 1)][0]).then_inc(loaded[s].sem, 16)
                    for s in SL:
                        sp.wait_ge(*done[s].at(1, i))
                        sp.dma_start(tiles_out[bass.ds(i * 2 + s, 1)][0], y[s][:]).then_inc(stored[s].sem, 16)
                for s in SL:
                    sp.wait_ge(*stored[s].at(0, NT // 2))

            @block.tensor
            def _(pe):
                with pe.Fori(0, NT // 2) as i:
                    for s in SL:
                        pe.wait_ge(*loaded[s].at(16, i))
                        for k in range(DT):
                            last = pe.transpose(A[s][:, k * P:(k + 1) * P], x[s][:, k * P:(k + 1) * P], ident[:])
                        last.then_inc(turned[s].sem, 1)
                    for s in SL:
                        pe.wait_ge(*turned_kept[s].at(1, i))
                        for cols, weight, row in ((slice(0, 2 * HID), sw12, sb12),
                                                  (slice(2 * HID, 2 * HID + GATES), gates_w, gates_b)):
                            for k in range(DT):
                                pe.matmul(Bk[s][:, cols], fT[s][:, k, :], weight[:, k, :], start=(k == 0), stop=False)
                            last = pe.matmul(Bk[s][:, cols], ones[:], row[:], start=False, stop=True)
                        last.then_inc(first[s].sem, 1)
                    for s in SL:
                        pe.wait_ge(*routed[s].at(1, i))
                        for e in range(E8):
                            pe.matmul(R[s][:, e // 4, e % 4, :], onehot[s][:, e:e + 1].to_broadcast([P, P]), ident[:],
                                      start=True, stop=True)
                        pe.transpose(Bk[s][0:E8, 3 * P:4 * P], onehot[s][:], ident[:]).then_inc(rows_done[s].sem, 1)
                    for s in SL:
                        pe.wait_ge(*masked[s].at(1, i))
                        for e in range(E8):
                            for k in range(DT):
                                pe.matmul(A[s][:, 0:2 * HID], xTe[s][:, k, e, :], ew12[:, k, e, :],
                                          start=(e == 0 and k == 0), stop=False)
                        pe.matmul(A[s][:, 0:2 * HID], ohT[s][:], eb12[:], start=False, stop=True).then_inc(
                            hidden[s].sem, 1)
                    for s in SL:
                        pe.wait_ge(*z_ready[s].at(1, i))
                        for n in range(2):
                            last = pe.transpose(A[s][:, (2 + n) * P:(3 + n) * P], z[s][:, n, :], ident[:])
                        last.then_inc(turned[s].sem, 1)
                    for s in SL:
                        pe.wait_ge(*z_masked[s].at(1, i))
                        pe.matmul(Bk[s][:, 0:D], zT[s][:, 0, :], sw3[:], start=True, stop=False)
                        pe.matmul(Bk[s][:, 0:D], ones[:], sb3[:], start=False, stop=True)
                        for e in range(E8):
                            pe.matmul(Bk[s][:, D:2 * D], zTe[s][:, e, :], ew3[:, e, :], start=(e == 0), stop=False)
                        pe.matmul(Bk[s][:, D:2 * D], ohT[s][:], eb3[:], start=False, stop=True).then_inc(outs[s].sem, 1)

            @block.scalar
            def _(act):
                with act.Fori(0, NT // 2) as i:
                    for s in SL:
                        act.wait_ge(*turned[s].at(1, i))
                        act.activation(fT[s][:].rearrange("p k t -> p (k t)"), A[s][:, 0:DT * P], ACT.Copy).then_inc(
                            turned_kept[s].sem, 1)
                    for s in SL:
                        act.wait_ge(*gates_kept[s].at(1, i))
                        act.activation(gate_e[s][:], gate[s][:], ACT.Exp, scale=-1.0).then_inc(gate_exp[s].sem, 1)
                    for s in SL:
                        act.wait_ge(*pair_ready[s].at(1, i))
                        act.activation(pair[s][:], pair[s][:], ACT.Exp).then_inc(pair_exp[s].sem, 1)
                    for s in SL:
                        act.wait_ge(*u_ready[s].at(1, i))
                        act.activation(ue[s][:], u[s][:, :, 0:HID], ACT.Exp, scale=-1.0).then_inc(u_exp[s].sem, 1)
                    for s in SL:
                        act.wait_ge(*turned[s].at(2, i))
                        for n in range(2):
                            last = act.activation(zT[s][:, n, :], A[s][:, (2 + n) * P:(3 + n) * P], ACT.Identity,
                                                  scale=gain[:, n:n + 1], bias=shift[:, n:n + 1])
                        last.then_inc(turned_kept[s].sem, 1)

            @block.vector
            def _(dve):
                for s in SL:
                    x_read[s].open(dve)
                with dve.Fori(0, NT // 2) as i:
                    link = [Chain(dve, chains[s], i, started) for s in SL]
                    for s in SL:
                        dve.wait_ge(*first[s].at(1, i))
                        link[s](dve.tensor_copy(u[s][:, 0, :], Bk[s][:, 0:2 * HID]))
                        dve.tensor_copy(gate[s][:], Bk[s][:, 2 * HID:2 * HID + GATES]).then_inc(gates_kept[s].sem, 1)
                    for s in SL:
                        dve.wait_ge(*gate_exp[s].at(1, i))
                        link[s](dve.tensor_scalar(gate_e[s][:], gate_e[s][:], 1.0, None, ALU.add))
                        link[s](dve.reciprocal(gate[s][:], gate_e[s][:]))
                        link[s](dve.tensor_tensor(biased[s][:], gate[s][:, 1:GATES], exp_bias[:], ALU.add), True)
                        link[s](dve.max(best[s][:], biased[s][:]), True)
                        link[s](dve.max_index(best_i[s][:], best[s][:], biased[s][:]))
                        link[s](dve.tensor_copy(best_f[s][:], best_i[s][:]))
                        dve.tensor_scalar(onehot[s][:], iota[:, 0:E8], best_f[s][:, 0:1], None, ALU.is_equal).then_inc(
                            routed[s].sem, 1)
                        dve.wait_ge(*routed[s].at(1, i))
                        link[s](dve.tensor_tensor(chosen[s][:], gate[s][:, 1:GATES], onehot[s][:], ALU.mult))
                        link[s](dve.tensor_copy(pair[s][:, 0:1], gate[s][:, 0:1]))
                        link[s](dve.tensor_reduce(pair[s][:, 1:2], chosen[s][:], AX, ALU.add))
                        link[s](dve.tensor_reduce(pair_m[s][:], pair[s][:], AX, ALU.max))
                        dve.tensor_scalar(pair[s][:], pair[s][:], pair_m[s][:], None, ALU.subtract).then_inc(
                            pair_ready[s].sem, 1)
                    for s in SL:
                        dve.wait_ge(*rows_done[s].at(1, i))
                        link[s](dve.tensor_copy(ohT[s][:], Bk[s][0:E8, 3 * P:4 * P]))
                        for k in range(DT):
                            for half in range(2):
                                last = dve.tensor_tensor(xTe[s][:, k, 4 * half:4 * half + 4, :], R[s][:, half],
                                                         fT[s][:, k, :].unsqueeze(1).to_broadcast([P, 4, P]), ALU.mult)
                        last.then_inc(masked[s].sem, 1)
                    for s in SL:
                        dve.wait_ge(*pair_exp[s].at(1, i))
                        link[s](dve.tensor_reduce(pair_m[s][:], pair[s][:], AX, ALU.add))
                        link[s](dve.reciprocal(pair_m[s][:], pair_m[s][:]))
                        link[s](dve.tensor_scalar(mix[s][:], pair[s][:], pair_m[s][:], None, ALU.mult))
                        link[s](dve.tensor_scalar(mix[s][:, 0:1], mix[s][:, 0:1], -1.0, None, ALU.add))
                        link[s](dve.tensor_tensor(mix[s][:], mix[s][:], hit[:, bass.ds(i * 2 + s, 1)].to_broadcast([P, 2]),
                                                  ALU.mult))
                        link[s](dve.tensor_scalar(mix[s][:, 0:1], mix[s][:, 0:1], 1.0, None, ALU.add))
                    for s in SL:
                        dve.wait_ge(*hidden[s].at(1, i))
                        dve.tensor_copy(u[s][:, 1, :], A[s][:, 0:2 * HID]).then_inc(u_ready[s].sem, 1)
                    for s in SL:
                        dve.wait_ge(*u_exp[s].at(1, i))
                        link[s](dve.tensor_scalar(ue[s][:], ue[s][:], 1.0, None, ALU.add))
                        link[s](dve.reciprocal(ue[s][:], ue[s][:]))
                        link[s](dve.tensor_tensor(ue[s][:], ue[s][:], u[s][:, :, 0:HID], ALU.mult))
                        link[s](dve.tensor_tensor(z[s][:], ue[s][:], u[s][:, :, HID:2 * HID], ALU.mult))
                        inner[s].vector(dve, link[s], lambda t: z[s][:, t, :], 1e-5)
                        for n in range(2):
                            last = dve.tensor_scalar(z[s][:, n, :], z[s][:, n, :], inner[s].mean(n), inner[s].r(n),
                                                     ALU.subtract, ALU.mult)
                        last.then_inc(z_ready[s].sem, 1)
                    for s in SL:
                        dve.wait_ge(*turned_kept[s].at(2, i))
                        for half in range(2):
                            last = dve.tensor_tensor(zTe[s][:, 4 * half:4 * half + 4, :], R[s][:, half],
                                                     zT[s][:, 1, :].unsqueeze(1).to_broadcast([P, 4, P]), ALU.mult)
                        last.then_inc(z_masked[s].sem, 1)
                    for s in SL:
                        dve.wait_ge(*outs[s].at(1, i))
                        dve.wait_ge(*stored[s].at(0, i))
                        link[s](dve.scalar_tensor_tensor(out=y[s][:], in0=Bk[s][:, 0:D], scalar=mix[s][:, 0:1],
                                                         in1=x[s][:], op0=ALU.mult, op1=ALU.add))
                        dve.scalar_tensor_tensor(out=y[s][:], in0=Bk[s][:, D:2 * D], scalar=mix[s][:, 1:2],
                                                 in1=y[s][:], op0=ALU.mult, op1=ALU.add).then_inc(x_read[s].sem, 1)
                        dve.wait_ge(*x_read[s].at(1, i))
                        outer[s].vector(dve, link[s], lambda t: y[s][:], 1e-5)
                        dve.tensor_scalar(y[s][:], y[s][:], outer[s].mean(0), outer[s].r(0), ALU.subtract,
                                          ALU.mult).then_inc(done[s].sem, 1)
                        link[s].close()


PF = 4
PB = D // PF
LH, LD = 16, 16
ROWS = P // B
LG = S // ROWS
HP = 32


def linear_constants():
    angle = np.pi / 2 * np.arange(1, B + 1, dtype=np.float32) / B
    s, c = np.sin(angle, dtype=np.float32), np.cos(angle, dtype=np.float32)
    pair = np.outer(s, s) + np.outer(c, c)
    return np.kron(pair, np.eye(ROWS)).astype(np.float32)


def linear_stage(nc, x_in, w, x_out):
    rows_in = x_in.rearrange("(l g r) d -> g l r d", l=B, r=ROWS)
    rows_out = x_out.rearrange("(l g r) d -> g l r d", l=B, r=ROWS)
    with ExitStack() as ctx:
        m = Room(nc, ctx, "lin")
        ident = m.sb("ident", [P, P])
        ones = m.sb("ones", [1, P])
        pair = m.sb("pair", [P, P])
        s2 = m.sb("s2", [P, PF, PB])
        a2 = m.sb("a2", [P, DT, PF, PF])
        term = m.sb("term", [P, PF, PB])
        weights = {n: m.sb("w" + n, [P, DT, PF, PB]) for n in "qkvo"}
        padded = {n: m.sb("wp" + n, [P, DT, PF, 4, HP]) for n in "qk"}
        row_bias = {n: m.sb("b" + n, [1, 4 * P]) for n in "qk"}
        row_bias.update({n: m.sb("b" + n, [1, D]) for n in "vo"})
        affine = {n: m.sb(n, [P, D]) for n in ("g1", "b1", "g2", "b2")}
        w_in = m.counter("w_in")
        b_in = m.counter("b_in")
        built = m.counter("built")
        w_free = m.counter("w_free")

        with nc.Block() as block:
            @block.sync
            def _(sp):
                sp.dma_start(ident[:], w["ident"]).then_inc(b_in.sem, 16)
                sp.dma_start(pair[:], w["pair"]).then_inc(b_in.sem, 16)
                for n in "qkvo":
                    sp.dma_start(row_bias[n][:], w[n + "b_row"]).then_inc(b_in.sem, 16)
                for n in affine:
                    sp.dma_start(affine[n][:], w[n].partition_broadcast(P)).then_inc(b_in.sem, 16)
                for j, n in enumerate("qkvo"):
                    if j:
                        sp.wait_ge(*w_free.at(j))
                    for half in range(2):
                        rows = slice(half * PB, (half + 1) * PB)
                        sp.dma_start(s2[rows], w[n + "S"].rearrange("n k l -> k n l")).then_inc(w_in.sem, 16)
                        sp.dma_start(a2[rows], w[n + "A_halves"][half].rearrange("k n j -> (k n j)").partition_broadcast(
                            PB).rearrange("p (k n j) -> p k n j", k=DT, n=PF)).then_inc(w_in.sem, 16)
                sp.wait_ge(*b_in.at(16 * 10))

            @block.vector
            def _(dve):
                dve.memset(ones[:], 1.0)
                for n in "qk":
                    dve.memset(padded[n][:], 0.0)
                link = Chain(dve, built)
                for j, n in enumerate("qkvo"):
                    dve.wait_ge(*w_in.at(64 * (j + 1)))
                    for k in range(DT):
                        for c in range(PF):
                            out = weights[n][:, k] if c == 0 else term[:]
                            link(dve.tensor_tensor(out, a2[:, k, c, :].unsqueeze(2).to_broadcast([P, PF, PB]),
                                                   s2[:, c, :].unsqueeze(1).to_broadcast([P, PF, PB]), ALU.mult))
                            if c:
                                link(dve.tensor_tensor(weights[n][:, k], weights[n][:, k], term[:], ALU.add))
                    if n in "qk":
                        for k in range(DT):
                            for c in range(PF):
                                last = dve.tensor_copy(padded[n][:, k, c, :, 0:LD],
                                                       weights[n][:, k, c, :].rearrange("p (h m) -> p h m", m=LD))
                        link(last)
                    dve.sem_inc(w_free.sem, 1)

        SL = range(2)
        x = [m.sb(f"x{s}", [P, D]) for s in SL]
        qn = [m.sb(f"qn{s}", [P, D]) for s in SL]
        fT = [m.sb(f"fT{s}", [P, 2 * DT, P]) for s in SL]
        qT = [m.sb(f"qT{s}", [P, 4, P]) for s in SL]
        kT = [m.sb(f"kT{s}", [P, 4, P]) for s in SL]
        v = [m.sb(f"v{s}", [P, LH, LD + 1]) for s in SL]
        masked = [m.sb(f"masked{s}", [P, 4, 4, P]) for s in SL]
        z = [m.sb(f"z{s}", [P, LH]) for s in SL]
        o = [m.sb(f"o{s}", [P, D]) for s in SL]
        oT = [m.sb(f"oT{s}", [P, DT, P]) for s in SL]
        y = [m.sb(f"y{s}", [P, D]) for s in SL]
        bT = [m.ps(f"bT{s}", [P, 4, P]) for s in SL]
        bQ = [m.ps(f"bQ{s}", [P, 4, P]) for s in SL]
        bK = [m.ps(f"bK{s}", [P, 4, P]) for s in SL]
        bV = [m.ps(f"bV{s}", [P, 512]) for s in SL]
        norms = [[Norm(m, f"n{k}{s}", 1) for k in range(3)] for s in SL]
        started = m.counter("started", ahead=1)
        loaded = [m.counter(f"loaded{s}", 16 * B) for s in SL]
        stored = [m.counter(f"stored{s}", 16 * B, ahead=16 * B) for s in SL]
        q_normed = [m.counter(f"q_normed{s}", 1) for s in SL]
        turned = [m.counter(f"turned{s}", 2) for s in SL]
        turned_kept = [m.counter(f"turned_kept{s}", 2) for s in SL]
        projected = [m.counter(f"projected{s}", 3) for s in SL]
        qk_kept = [m.counter(f"qk_kept{s}", 2) for s in SL]
        v_kept = [m.counter(f"v_kept{s}", 1) for s in SL]
        scored = [m.counter(f"scored{s}", 4) for s in SL]
        mask_done = [m.counter(f"mask_done{s}", 4) for s in SL]
        weighed = [m.counter(f"weighed{s}", 1) for s in SL]
        o_normed = [m.counter(f"o_normed{s}", 1) for s in SL]
        final = [m.counter(f"final{s}", 1) for s in SL]
        x_read = [m.counter(f"x_read{s}", 1, ahead=1) for s in SL]
        done = [m.counter(f"done{s}", 1) for s in SL]
        chains = [m.counter(f"chain{s}", 48) for s in SL]

        with nc.Block() as block:
            @block.sync
            def _(sp):
                started.open(sp)
                for s in SL:
                    stored[s].open(sp)
                with sp.Fori(0, LG // 2) as i:
                    for s in SL:
                        sp.wait_ge(*x_read[s].at(0, i))
                        for l in range(B):
                            sp.dma_start(x[s][l * ROWS:(l + 1) * ROWS, :], rows_in[bass.ds(i * 2 + s, 1)][0][l]).then_inc(
                                loaded[s].sem, 16)
                    for s in SL:
                        sp.wait_ge(*done[s].at(1, i))
                        for l in range(B):
                            sp.dma_start(rows_out[bass.ds(i * 2 + s, 1)][0][l], y[s][l * ROWS:(l + 1) * ROWS, :]).then_inc(
                                stored[s].sem, 16)
                for s in SL:
                    sp.wait_ge(*stored[s].at(0, LG // 2))

            @block.tensor
            def _(pe):
                with pe.Fori(0, LG // 2) as i:
                    for s in SL:
                        pe.wait_ge(*q_normed[s].at(1, i))
                        for n, src in enumerate((x[s], qn[s])):
                            for k in range(DT):
                                last = pe.transpose(bT[s][:, n * DT + k, :], src[:, k * P:(k + 1) * P], ident[:])
                        last.then_inc(turned[s].sem, 1)
                    for s in SL:
                        pe.wait_ge(*turned_kept[s].at(1, i))
                        for n, bank, first in (("q", bQ[s], DT), ("k", bK[s], 0)):
                            for g in range(4):
                                for k in range(DT):
                                    pe.matmul(bank[:, g, :], padded[n][:, k, g].rearrange("p h m -> p (h m)"),
                                              fT[s][:, first + k, :], start=(k == 0), stop=False)
                                last = pe.matmul(bank[:, g, :], row_bias[n][:, g * P:(g + 1) * P], ones[:],
                                                 start=False, stop=True)
                            last.then_inc(projected[s].sem, 1)
                        for k in range(DT):
                            pe.matmul(bV[s][:, 0:D], fT[s][:, k, :], weights["v"][:, k].rearrange("p j l -> p (j l)"),
                                      start=(k == 0), stop=False)
                        pe.matmul(bV[s][:, 0:D], ones[:], row_bias["v"][:], start=False, stop=True).then_inc(
                            projected[s].sem, 1)
                    for h in range(4):
                        for s in SL:
                            if h == 0:
                                pe.wait_ge(*qk_kept[s].at(2, i))
                            if h >= 2:
                                pe.wait_ge(*mask_done[s].at(h - 1, i))
                            for g in range(4):
                                rows = slice(HP * h, HP * h + LD)
                                last = pe.matmul((bQ, bK)[h % 2][s][:, g, :], kT[s][rows, g, :], qT[s][rows, g, :],
                                                 start=True, stop=True)
                            last.then_inc(scored[s].sem, 1)
                    for s in SL:
                        pe.wait_ge(*v_kept[s].at(1, i))
                        pe.wait_ge(*mask_done[s].at(4, i))
                        for h in range(LH):
                            last = pe.matmul(bV[s][:, h * (LD + 1):(h + 1) * (LD + 1)], masked[s][:, h % 4, h // 4, :],
                                             v[s][:, h, :], start=True, stop=True)
                        last.then_inc(weighed[s].sem, 1)
                    for s in SL:
                        pe.wait_ge(*o_normed[s].at(1, i))
                        for k in range(DT):
                            last = pe.transpose(bT[s][:, k, :], o[s][:, k * P:(k + 1) * P], ident[:])
                        last.then_inc(turned[s].sem, 1)
                    for s in SL:
                        pe.wait_ge(*turned_kept[s].at(2, i))
                        for k in range(DT):
                            pe.matmul(bV[s][:, 0:D], oT[s][:, k, :], weights["o"][:, k].rearrange("p j l -> p (j l)"),
                                      start=(k == 0), stop=False)
                        pe.matmul(bV[s][:, 0:D], ones[:], row_bias["o"][:], start=False, stop=True).then_inc(
                            final[s].sem, 1)

            @block.scalar
            def _(act):
                with act.Fori(0, LG // 2) as i:
                    for s in SL:
                        act.wait_ge(*turned[s].at(1, i))
                        act.activation(fT[s][:], bT[s][:], ACT.Copy).then_inc(turned_kept[s].sem, 1)
                    for s in SL:
                        for n, (dst, bank) in enumerate(((qT[s], bQ[s]), (kT[s], bK[s]))):
                            act.wait_ge(*projected[s].at(n + 1, i))
                            act.activation(dst[:], bank[:], ACT.Relu).then_inc(qk_kept[s].sem, 1)
                    for s in SL:
                        act.wait_ge(*turned[s].at(2, i))
                        act.activation(oT[s][:], bT[s][:, 0:DT, :], ACT.Copy).then_inc(turned_kept[s].sem, 1)

            @block.vector
            def _(dve):
                for s in SL:
                    x_read[s].open(dve)
                    dve.memset(v[s][:], 1.0)
                with dve.Fori(0, LG // 2) as i:
                    link = [Chain(dve, chains[s], i, started) for s in SL]

                    def normalise(s, n, src, dst):
                        norms[s][n].vector(dve, link[s], lambda t: src[:], 1e-5)
                        return dve.tensor_scalar(dst[:], src[:], norms[s][n].mean(0), norms[s][n].r(0),
                                                 ALU.subtract, ALU.mult)

                    for s in SL:
                        dve.wait_ge(*loaded[s].at(16 * B, i))
                        link[s](normalise(s, 0, x[s], qn[s]))
                        link[s](dve.tensor_tensor(qn[s][:], qn[s][:], affine["g1"][:], ALU.mult))
                        dve.tensor_tensor(qn[s][:], qn[s][:], affine["b1"][:], ALU.add).then_inc(q_normed[s].sem, 1)
                    for s in SL:
                        dve.wait_ge(*projected[s].at(3, i))
                        dve.tensor_copy(v[s][:, :, 0:LD], bV[s][:, 0:D].rearrange("p (h m) -> p h m", m=LD)).then_inc(
                            v_kept[s].sem, 1)
                    for h in range(4):
                        for s in SL:
                            dve.wait_ge(*scored[s].at(h + 1, i))
                            dve.tensor_tensor(masked[s][:, h], (bQ, bK)[h % 2][s][:],
                                              pair[:].unsqueeze(1).to_broadcast([P, 4, P]), ALU.mult).then_inc(
                                mask_done[s].sem, 1)
                    for s in SL:
                        dve.wait_ge(*weighed[s].at(1, i))
                        ov = bV[s][:, 0:LH * (LD + 1)].rearrange("p (h m) -> p h m", m=LD + 1)
                        link[s](dve.tensor_scalar(z[s][:], ov[:, :, LD], 1e-6, None, ALU.max))
                        link[s](dve.reciprocal(z[s][:], z[s][:]))
                        link[s](dve.tensor_tensor(o[s][:].rearrange("p (h m) -> p h m", m=LD), ov[:, :, 0:LD],
                                                  z[s][:].unsqueeze(2).to_broadcast([P, LH, LD]), ALU.mult))
                        dve.wait_ge(*q_normed[s].at(1, i))
                        link[s](dve.tensor_tensor(o[s][:], o[s][:], qn[s][:], ALU.add))
                        link[s](normalise(s, 1, o[s], o[s]))
                        link[s](dve.tensor_tensor(o[s][:], o[s][:], affine["g2"][:], ALU.mult))
                        dve.tensor_tensor(o[s][:], o[s][:], affine["b2"][:], ALU.add).then_inc(o_normed[s].sem, 1)
                    for s in SL:
                        dve.wait_ge(*o_normed[s].at(1, i))
                        dve.wait_ge(*stored[s].at(0, i))
                        dve.tensor_tensor(y[s][:], x[s][:], o[s][:], ALU.add).then_inc(x_read[s].sem, 1)
                        dve.wait_ge(*final[s].at(1, i))
                        dve.wait_ge(*x_read[s].at(1, i))
                        link[s](dve.tensor_tensor(y[s][:], y[s][:], bV[s][:, 0:D], ALU.add))
                        normalise(s, 2, y[s], y[s]).then_inc(done[s].sem, 1)
                        link[s].close()


LAYERS, HD = 4, 64
QW = 16 * HD
FF = 1024
FFT = FF // P


class DecoderHeads:

    HEADS, GROUP = 16, 4
    GROUPS, MT = HEADS // GROUP, GROUP * HD // P
    FEATURES = HEADS * HD // P

    def __init__(self, m):
        self.qT = m.sb("qT", [P, 2, self.MT, S])
        self.kT = m.sb("kT", [P, 2, self.MT, S])
        self.v = m.sb("v", [P, 2, ST, self.GROUP * HD])
        self.logit = m.sb("logit", [P, 2, ST, S])
        self.neg_max = m.sb("neg_max", [P, 2, ST])
        self.prob = m.sb("prob", [P, 2, ST, S])
        self.row_sum = m.sb("row_sum", [P, ST, self.HEADS])
        self.row_inv = m.sb("row_inv", [P, ST, self.HEADS])
        self.pT = m.sb("pT", [P, 2, ST, S])
        self.o = m.sb("o", [P, ST, QW])
        self.oT = m.sb("oT", [P, self.FEATURES, S])
        self.psS = [m.ps(f"psS{n}", [P, ST, S]) for n in range(2)]
        self.psT = [m.ps(f"psT{n}", [P, ST, S]) for n in range(2)]
        self.psO = [m.ps(f"psO{n}", [P, ST, self.GROUP * HD]) for n in range(2)]
        self.psA = m.ps("psA", [P, ST, S])
        self.psB = m.ps("psB", [P, ST, S])
        g, h = self.GROUPS, self.HEADS
        self.projected = m.counter("projected", 3 * g, ahead=3 * g)
        self.q_kept = m.counter("q_kept", g)
        self.k_kept = m.counter("k_kept", g)
        self.v_kept = m.counter("v_kept", g)
        self.scored = m.counter("scored", h)
        self.bias_added = m.counter("bias_added", h, ahead=2 * h)
        self.max_ready = m.counter("max_ready", h)
        self.exp_done = m.counter("exp_done", h)
        self.turned = m.counter("turned", h)
        self.pT_kept = m.counter("pT_kept", h)
        self.weighed = m.counter("weighed", h)
        self.inv_ready = m.counter("inv_ready", g)
        self.o_kept = m.counter("o_kept", g)
        self.o_turned = m.counter("o_turned", self.FEATURES // 2)
        self.oT_kept = m.counter("oT_kept", self.FEATURES // 2)
        self.projected_out = m.counter("projected_out", 1, ahead=1)

    def project(self, pe, g, wq, wk, wv, xT, cT, i):
        for weight, source, bank in ((wk, cT, self.psB), (wq, xT, self.psA)):
            for mt in range(self.MT):
                col = (g * self.MT + mt) * P
                for k in range(DT):
                    last = pe.matmul(bank[:, mt, :], weight[:, k, col:col + P], source[:, k, :],
                                     start=(k == 0), stop=(k == DT - 1))
            last.then_inc(self.projected.sem, 1)
        pe.wait_ge(*self.k_kept.at(g + 1, i))
        width = self.GROUP * HD
        for t in range(ST):
            for k in range(DT):
                last = pe.matmul(self.psB[:, t, :], cT[:, k, t * P:(t + 1) * P],
                                 wv[:, k, g * width:(g + 1) * width], start=(k == 0), stop=(k == DT - 1))
        last.then_inc(self.projected.sem, 1)

    def turn_out(self, pe, ident, j, i):
        bank = (self.psA, self.psB)[j % 2]
        for f in range(2):
            for qt in range(ST):
                last = pe.transpose(bank[:, f, qt * P:(qt + 1) * P],
                                    self.o[:, qt, (2 * j + f) * P:(2 * j + f + 1) * P], ident[:])
        last.then_inc(self.o_turned.sem, 1)

    def project_out(self, pe, wo, i):
        pe.wait_ge(*self.oT_kept.at(self.FEATURES // 2, i))
        for qt in range(ST):
            for f in range(self.FEATURES):
                last = pe.matmul(self.psA[:, qt, :], self.oT[:, f, qt * P:(qt + 1) * P], wo[:, f, :],
                                 start=(f == 0), stop=(f == self.FEATURES - 1))
        last.then_inc(self.projected_out.sem, 1)

    def tensor(self, pe, ident, i, extra):
        def scores(h):
            g = h // self.GROUP
            if h % self.GROUP == 0:
                pe.wait_ge(*self.q_kept.at(g + 1, i))
            pe.wait_ge(*self.bias_added.at(h - 1, i))
            mt, row = h % self.GROUP * HD // P, h * HD % P
            for qt in range(ST):
                last = pe.matmul(self.psS[h % 2][:, qt, :], self.qT[row:row + HD, g % 2, mt, qt * P:(qt + 1) * P],
                                 self.kT[row:row + HD, g % 2, mt, :], start=True, stop=True)
            last.then_inc(self.scored.sem, 1)

        def turn(h):
            pe.wait_ge(*self.exp_done.at(h + 1, i))
            if h >= 2:
                pe.wait_ge(*self.pT_kept.at(h - 1, i))
            for kt in range(ST):
                for qt in range(ST):
                    last = pe.transpose(self.psT[h % 2][:, kt, qt * P:(qt + 1) * P],
                                        self.prob[:, h % 2, qt, kt * P:(kt + 1) * P], ident[:])
            last.then_inc(self.turned.sem, 1)

        def weigh(h):
            g, j = h // self.GROUP, h % self.GROUP
            if j == 0:
                pe.wait_ge(*self.v_kept.at(g + 1, i))
                if g >= 2:
                    pe.wait_ge(*self.o_kept.at(g - 1, i))
            pe.wait_ge(*self.pT_kept.at(h + 1, i))
            for qt in range(ST):
                for kt in range(ST):
                    last = pe.matmul(self.psO[g % 2][:, qt, j * HD:(j + 1) * HD],
                                     self.pT[:, h % 2, kt, qt * P:(qt + 1) * P],
                                     self.v[:, g % 2, kt, j * HD:(j + 1) * HD], start=(kt == 0), stop=(kt == ST - 1))
            last.then_inc(self.weighed.sem, 1)

        for h in range(self.HEADS + 2):
            if h < self.HEADS:
                scores(h)
            if 1 <= h <= self.HEADS:
                turn(h - 1)
            if h >= 2:
                weigh(h - 2)
            if h in extra:
                extra[h]()

    def keep_qk(self, act, g, i):
        act.wait_ge(*self.projected.at(3 * g + 1, i))
        act.activation(self.kT[:, g % 2], self.psB[:], ACT.Copy).then_inc(self.k_kept.sem, 1)
        act.wait_ge(*self.projected.at(3 * g + 2, i))
        act.activation(self.qT[:, g % 2], self.psA[:], ACT.Copy, scale=HD ** -0.5).then_inc(self.q_kept.sem, 1)

    def keep_turned_out(self, act, j, i):
        act.wait_ge(*self.o_turned.at(j + 1, i))
        act.activation(self.oT[:, 2 * j:2 * j + 2, :], (self.psA, self.psB)[j % 2][:], ACT.Copy).then_inc(
            self.oT_kept.sem, 1)

    def scalar(self, act, i, extra):
        for h in range(self.HEADS + 2):
            if h < self.HEADS:
                act.wait_ge(*self.max_ready.at(h + 1, i))
                if h >= 2:
                    act.wait_ge(*self.turned.at(h - 1, i))
                for qt in range(ST):
                    last = act.activation(self.prob[:, h % 2, qt, :], self.logit[:, h % 2, qt, :], ACT.Exp,
                                          bias=self.neg_max[:, h % 2, qt:qt + 1],
                                          accum_out=self.row_sum[:, qt, h:h + 1])
                last.then_inc(self.exp_done.sem, 1)
            if 1 <= h <= self.HEADS:
                act.wait_ge(*self.turned.at(h, i))
                if h >= 3:
                    act.wait_ge(*self.weighed.at(h - 2, i))
                act.activation(self.pT[:, (h - 1) % 2], self.psT[(h - 1) % 2][:], ACT.Copy).then_inc(
                    self.pT_kept.sem, 1)
            if h in extra:
                extra[h]()

    def keep_v(self, dve, g, i):
        dve.wait_ge(*self.projected.at(3 * g + 3, i))
        dve.tensor_copy(self.v[:, g % 2], self.psB[:]).then_inc(self.v_kept.sem, 1)

    def normalise(self, dve, g, i):
        dve.wait_ge(*self.exp_done.at(self.GROUP * (g + 1), i))
        heads = slice(self.GROUP * g, self.GROUP * (g + 1))
        dve.reciprocal(self.row_inv[:, :, heads], self.row_sum[:, :, heads]).then_inc(self.inv_ready.sem, 1)
        dve.wait_ge(*self.weighed.at(self.GROUP * (g + 1), i))
        dve.wait_ge(*self.inv_ready.at(g + 1, i))
        width = self.GROUP * HD
        for qt in range(ST):
            last = dve.tensor_tensor(
                self.o[:, qt, g * width:(g + 1) * width].rearrange("p (h d) -> p h d", d=HD),
                self.psO[g % 2][:, qt, :].rearrange("p (h d) -> p h d", d=HD),
                self.row_inv[:, qt, heads].unsqueeze(2).to_broadcast([P, self.GROUP, HD]), ALU.mult)
        last.then_inc(self.o_kept.sem, 1)

    def vector(self, dve, bias, i, extra):
        for h in range(self.HEADS + 2):
            if h < self.HEADS:
                dve.wait_ge(*self.scored.at(h + 1, i))
                if h >= 2:
                    dve.wait_ge(*self.exp_done.at(h - 1, i))
                dve.tensor_tensor(self.logit[:, h % 2], self.psS[h % 2][:], bias, ALU.add).then_inc(
                    self.bias_added.sem, 1)
                dve.wait_ge(*self.bias_added.at(h + 1, i))
                dve.tensor_reduce(self.neg_max[:, h % 2, :], self.logit[:, h % 2], AX, ALU.max, negate=True).then_inc(
                    self.max_ready.sem, 1)
            if h in extra:
                extra[h]()


def decoder_stage(nc, x_in, bias_in, w, x_out):
    tiles_in = x_in.rearrange("(t p) d -> p t d", p=P)
    tiles_out = x_out.rearrange("(t p) d -> p t d", p=P)
    STEPS = LAYERS * B
    with ExitStack() as ctx:
        m = Room(nc, ctx, "dec")
        ident = m.sb("ident", [P, P])
        ones = m.sb("ones", [1, P])
        x = m.sb("x", [P, NT, D])
        xn = m.sb("xn", [P, 2, ST, D])
        xnT = m.sb("xnT", [P, 2, DT, S])
        ctxT = m.sb("ctxT", [P, DT, S])
        bias = m.sb("bias", [P, 2, ST, S])
        wq = m.sb("wq", [P, DT, QW])
        wk = m.sb("wk", [P, DT, QW])
        wv = m.sb("wv", [P, DT, QW])
        wo = m.sb("wo", [P, QW // P, D])
        wf1 = m.sb("wf1", [P, DT, FF])
        wf2 = m.sb("wf2", [P, FFT, D])
        bf1 = m.sb("bf1", [P, FFT])
        bf2 = m.sb("bf2", [1, D])
        hid = m.sb("hid", [P, FFT, S])
        at = DecoderHeads(m)
        norm = Norm(m, "norm", ST)
        started = m.counter("started", ahead=1)
        const_in = m.counter("const_in")
        qkv_loaded = m.counter("qkv_loaded", 16 * 3)
        wo_loaded = m.counter("wo_loaded", 16)
        ff_loaded = m.counter("ff_loaded", 16 * 4)
        ctx_loaded = m.counter("ctx_loaded", 16)
        bias_loaded = m.counter("bias_loaded", 16)
        chain = [m.counter(f"chain{n}", 17) for n in range(2)]
        added = m.counter("added", 1)
        normed = [m.counter(f"normed{n}", 1) for n in range(2)]
        n_turned = [m.counter(f"n_turned{n}", 1) for n in range(2)]
        nT_kept = [m.counter(f"nT_kept{n}", 1) for n in range(2)]
        up = m.counter("up", FFT // 2)
        up_kept_a = m.counter("up_kept_a", FFT // 4)
        up_kept_v = m.counter("up_kept_v", FFT // 4)
        down = m.counter("down", 1, ahead=1)
        step_done = m.counter("step_done", 1)

        with nc.Block() as block:
            @block.sync
            def _(sp):
                started.open(sp)

                def load_step(i):
                    sp.wait_ge(*at.projected.at(0, i))
                    sp.dma_start(ctxT[:], w["ctxT"].rearrange("b (k p) s -> b p k s", p=P)[
                        bass.ds(i % B, 1)][0]).then_inc(ctx_loaded.sem, 16)
                    sp.wait_ge(*at.bias_added.at(0, i - 1))
                    sp.dma_start(bias[:, bass.ds(i % 2, 1)][:, 0], bias_in.rearrange("n (t p) s -> n p t s", p=P)[
                        bass.ds(i, 1)][0]).then_inc(bias_loaded.sem, 16)

                def load(names, l, signal):
                    for dst, name in names:
                        src = w[name].rearrange("l (k p) n -> l p k n", p=P)
                        sp.dma_start(dst[:], src[bass.ds(l, 1)][0]).then_inc(signal.sem, 16)

                sp.dma_start(ident[:], w["ident"]).then_inc(const_in.sem, 16)
                sp.dma_start(x[:], tiles_in).then_inc(const_in.sem, 16)
                with sp.Fori(0, LAYERS) as l:
                    sp.wait_ge(*at.projected.at(0, l * B))
                    load(((wk, "wk"), (wq, "wq"), (wv, "wv")), l, qkv_loaded)
                    load_step(l * B)
                    sp.wait_ge(*at.projected_out.at(0, l * B))
                    load(((wo, "wo"),), l, wo_loaded)
                    load_step(l * B + 1)
                    sp.wait_ge(*down.at(0, l * B))
                    load(((wf1, "wf1"), (wf2, "wf2")), l, ff_loaded)
                    sp.dma_start(bf1[:], w["bf1_cols"][bass.ds(l, 1)][0]).then_inc(ff_loaded.sem, 16)
                    sp.dma_start(bf2[:], w["bf2"][bass.ds(l, 1)]).then_inc(ff_loaded.sem, 16)
                    with sp.Fori(2, B) as b:
                        load_step(l * B + b)

            @block.tensor
            def _(pe):
                def turn_normed(n, bank, i):
                    pe.wait_ge(*normed[n].at(1, i))
                    for k in range(DT):
                        for t in range(ST):
                            last = pe.transpose(bank[:, k, t * P:(t + 1) * P], xn[:, n, t, k * P:(k + 1) * P], ident[:])
                    last.then_inc(n_turned[n].sem, 1)

                def first_projection(i):
                    pe.wait_ge(*qkv_loaded.at(16 * 3, i // B))
                    pe.wait_ge(*ctx_loaded.at(16, i))
                    pe.wait_ge(*nT_kept[0].at(1, i))
                    at.project(pe, 0, wq, wk, wv, xnT[:, 0], ctxT, i)

                def up_rows(j, i):
                    for f in range(2):
                        for k in range(DT):
                            last = pe.matmul((at.psA, at.psB)[j % 2][:, f, :],
                                             wf1[:, k, (2 * j + f) * P:(2 * j + f + 1) * P], xnT[:, 1, k, :],
                                             start=(k == 0), stop=(k == DT - 1))
                    last.then_inc(up.sem, 1)

                def down_rows(i):
                    pe.wait_ge(*up_kept_a.at(FFT // 4, i))
                    pe.wait_ge(*up_kept_v.at(FFT // 4, i))
                    for t in range(ST):
                        for f in range(FFT):
                            pe.matmul(at.psA[:, t, :], hid[:, f, t * P:(t + 1) * P], wf2[:, f, :],
                                      start=(f == 0), stop=False)
                        last = pe.matmul(at.psA[:, t, :], ones[:], bf2[:], start=False, stop=True)
                    last.then_inc(down.sem, 1)

                def out_0(i):
                    pe.wait_ge(*at.o_kept.at(at.GROUPS, i))
                    at.turn_out(pe, ident, 0, i)
                    at.turn_out(pe, ident, 1, i)

                def out_1(i):
                    pe.wait_ge(*at.oT_kept.at(1, i))
                    at.turn_out(pe, ident, 2, i)
                    pe.wait_ge(*at.oT_kept.at(2, i))
                    at.turn_out(pe, ident, 3, i)

                def out_2(i):
                    pe.wait_ge(*wo_loaded.at(16, i // B))
                    at.project_out(pe, wo, i)

                def step(i, before, after):
                    p = i - 1

                    def e0():
                        pe.wait_ge(*at.v_kept.at(1, i))
                        out_0(p)

                    def e3():
                        if before:
                            pe.wait_ge(*added.at(1, p))
                        else:
                            pe.wait_ge(*at.v_kept.at(1, i))
                        at.project(pe, 1, wq, wk, wv, xnT[:, 0], ctxT, i)

                    def e5():
                        pe.wait_ge(*at.q_kept.at(2, i))
                        turn_normed(1, at.psA, p)

                    def e6():
                        if before:
                            pe.wait_ge(*nT_kept[1].at(1, p))
                        pe.wait_ge(*at.v_kept.at(2, i))
                        pe.wait_ge(*at.q_kept.at(2, i))
                        at.project(pe, 2, wq, wk, wv, xnT[:, 0], ctxT, i)

                    def e7():
                        pe.wait_ge(*ff_loaded.at(16 * 4, p // B))
                        pe.wait_ge(*at.q_kept.at(3, i))
                        up_rows(0, p)

                    def e8():
                        pe.wait_ge(*at.v_kept.at(3, i))
                        up_rows(1, p)

                    def e9():
                        pe.wait_ge(*up_kept_a.at(1, p))
                        up_rows(2, p)

                    def e10():
                        if before:
                            pe.wait_ge(*up_kept_a.at(2, p))
                            pe.wait_ge(*up_kept_v.at(1, p))
                        pe.wait_ge(*at.v_kept.at(3, i))
                        pe.wait_ge(*at.q_kept.at(3, i))
                        at.project(pe, 3, wq, wk, wv, xnT[:, 0], ctxT, i)

                    def e11():
                        pe.wait_ge(*at.v_kept.at(4, i))
                        up_rows(3, p)

                    def e13():
                        pe.wait_ge(*at.q_kept.at(4, i))
                        down_rows(p)

                    def e14():
                        if before:
                            pe.wait_ge(*up_kept_v.at(2, p))
                        pe.wait_ge(*at.v_kept.at(4, i))
                        turn_normed(0, at.psB, i + 1)

                    def e17():
                        if before:
                            pe.wait_ge(*step_done.at(1, p))
                        pe.wait_ge(*at.q_kept.at(4, i))
                        first_projection(i + 1)

                    extra = {3: e3, 6: e6, 10: e10}
                    if before:
                        extra.update({0: e0, 1: lambda: out_1(p), 2: lambda: out_2(p), 5: e5, 7: e7, 8: e8, 9: e9,
                                      11: e11, 13: e13})
                    if after:
                        extra.update({14: e14, at.HEADS + 1: e17})
                    at.tensor(pe, ident, i, extra)

                pe.wait_ge(*const_in.at(32))
                down.open(pe)
                at.projected.open(pe)
                at.projected_out.open(pe)
                turn_normed(0, at.psB, 0)
                first_projection(0)
                step(0, False, True)
                with pe.Fori(1, STEPS - 1) as i:
                    step(i, True, True)
                step(STEPS - 1, True, False)
                last = STEPS - 1
                pe.wait_ge(*step_done.at(1, last - 1))
                pe.wait_ge(*at.v_kept.at(4, last))
                out_0(last)
                out_1(last)
                out_2(last)
                pe.wait_ge(*added.at(1, last))
                turn_normed(1, at.psA, last)
                pe.wait_ge(*nT_kept[1].at(1, last))
                up_rows(0, last)
                up_rows(1, last)
                pe.wait_ge(*up_kept_a.at(1, last))
                up_rows(2, last)
                pe.wait_ge(*up_kept_v.at(1, last))
                up_rows(3, last)
                down_rows(last)

            @block.scalar
            def _(act):
                def keep_normed(n, bank, i):
                    act.wait_ge(*n_turned[n].at(1, i))
                    act.activation(xnT[:, n], bank[:], ACT.Copy).then_inc(nT_kept[n].sem, 1)

                def keep_up(j, i):
                    act.wait_ge(*up.at(j + 1, i))
                    for f in range(2):
                        last = act.activation(hid[:, 2 * j + f, :], at.psA[:, f, :], ACT.Relu,
                                              bias=bf1[:, 2 * j + f:2 * j + f + 1])
                    last.then_inc(up_kept_a.sem, 1)

                def keep_out(j, i):
                    at.keep_turned_out(act, j, i)
                    at.keep_turned_out(act, j + 1, i)

                def step(i, before, after):
                    p = i - 1
                    extra = {3: lambda: at.keep_qk(act, 1, i), 6: lambda: at.keep_qk(act, 2, i),
                             10: lambda: at.keep_qk(act, 3, i)}
                    if before:
                        extra.update({0: lambda: keep_out(0, p), 1: lambda: keep_out(2, p),
                                      5: lambda: keep_normed(1, at.psA, p), 7: lambda: keep_up(0, p),
                                      9: lambda: keep_up(2, p)})
                    if after:
                        extra.update({14: lambda: keep_normed(0, at.psB, i + 1),
                                      at.HEADS + 1: lambda: at.keep_qk(act, 0, i + 1)})
                    at.scalar(act, i, extra)

                keep_normed(0, at.psB, 0)
                at.keep_qk(act, 0, 0)
                step(0, False, True)
                with act.Fori(1, STEPS - 1) as i:
                    step(i, True, True)
                step(STEPS - 1, True, False)
                last = STEPS - 1
                keep_out(0, last)
                keep_out(2, last)
                keep_normed(1, at.psA, last)
                keep_up(0, last)
                keep_up(2, last)

            @block.vector
            def _(dve):
                def rows(i):
                    return x[:, bass.ds(i % B * ST, ST)]

                def normalise(n, i):
                    link = Chain(dve, chain[n], i, started)
                    xb = rows(i)
                    norm.vector(dve, link, lambda t: xb[:, t, :], 0.0)
                    link(dve.tensor_tensor(norm.work[:], norm.mv[:, :, 1], norm.rstd[:], ALU.mult))
                    link(dve.tensor_scalar(norm.work[:], norm.work[:], 1e-6, None, ALU.add))
                    link(dve.reciprocal(norm.rstd[:], norm.work[:]))
                    for t in range(ST):
                        last = dve.tensor_scalar(xn[:, n, t, :], xb[:, t, :], norm.mean(t), norm.r(t),
                                                 ALU.subtract, ALU.mult)
                    last.then_inc(normed[n].sem, 1)
                    dve.wait_ge(*normed[n].at(1, i))
                    link(dve.tensor_copy(norm.work[:, 0:1], norm.rstd[:, 0:1]))
                    link.close()

                def add_out(i):
                    dve.wait_ge(*at.projected_out.at(1, i))
                    xb = rows(i)
                    dve.tensor_tensor(xb, xb, at.psA[:], ALU.add).then_inc(added.sem, 1)

                def add_down(i):
                    dve.wait_ge(*down.at(1, i))
                    xb = rows(i)
                    dve.tensor_tensor(xb, xb, at.psA[:], ALU.add).then_inc(step_done.sem, 1)

                def keep_up(j, i):
                    dve.wait_ge(*up.at(j + 1, i))
                    for f in range(2):
                        last = dve.tensor_scalar(hid[:, 2 * j + f, :], at.psB[:, f, :],
                                                 bf1[:, 2 * j + f:2 * j + f + 1], 0.0, ALU.add, ALU.max)
                    last.then_inc(up_kept_v.sem, 1)

                def norm_out(i):
                    alone(dve, *added.at(1, i), started)
                    normalise(1, i)

                def norm_next(i):
                    normalise(0, i)

                def step(i, before, after):
                    p = i - 1

                    def e3():
                        if before:
                            norm_out(p)
                        at.keep_v(dve, 1, i)

                    def e6():
                        at.normalise(dve, 0, i)
                        at.keep_v(dve, 2, i)

                    def e10():
                        at.normalise(dve, 1, i)
                        at.keep_v(dve, 3, i)

                    def e17():
                        at.normalise(dve, 3, i)
                        if after:
                            at.keep_v(dve, 0, i + 1)

                    extra = {3: e3, 6: e6, 10: e10, 14: lambda: at.normalise(dve, 2, i), at.HEADS + 1: e17}
                    if before:
                        extra.update({2: lambda: add_out(p), 8: lambda: keep_up(1, p), 11: lambda: keep_up(3, p),
                                      13: lambda: add_down(p)})
                    if after:
                        extra[12] = lambda: norm_next(i + 1)
                    dve.wait_ge(*bias_loaded.at(16, i))
                    at.vector(dve, bias[:, bass.ds(i % 2, 1)][:, 0], i, extra)

                at.bias_added.open(dve)
                dve.memset(ones[:], 1.0)
                dve.wait_ge(*const_in.at(32))
                normalise(0, 0)
                at.keep_v(dve, 0, 0)
                step(0, False, True)
                with dve.Fori(1, STEPS - 1) as i:
                    step(i, True, True)
                step(STEPS - 1, True, False)
                last = STEPS - 1
                add_out(last)
                norm_out(last)
                keep_up(1, last)
                keep_up(3, last)
                add_down(last)
                dve.wait_ge(*step_done.at(1, last))

        xs = m.sb("xs", [P, ST, D])
        again = m.counter("again", 16)
        xs_free = m.counter("xs_free", 1, ahead=1)
        done = m.counter("done", 1)
        stored = m.counter("stored", 16, ahead=16)
        fin = m.counter("fin", 31)
        norm1 = Norm(m, "norm1", ST)
        norm2 = Norm(m, "norm2", ST)
        batches_in = x_in.rearrange("(b t p) d -> b p t d", p=P, t=ST)
        batches_out = x_out.rearrange("(b t p) d -> b p t d", p=P, t=ST)
        with nc.Block() as block:
            @block.sync
            def _(sp):
                stored.open(sp)
                with sp.Fori(0, B) as b:
                    sp.wait_ge(*xs_free.at(0, b))
                    sp.dma_start(xs[:], batches_in[bass.ds(b, 1)][0]).then_inc(again.sem, 16)
                    sp.wait_ge(*done.at(1, b))
                    sp.dma_start(batches_out[bass.ds(b, 1)][0], xn[:, 0]).then_inc(stored.sem, 16)
                sp.wait_ge(*stored.at(0, B))

            @block.vector
            def _(dve):
                xs_free.open(dve)
                with dve.Fori(0, B) as b:
                    link = Chain(dve, fin, b, started)
                    xb = x[:, bass.ds(b * ST, ST)]
                    norm1.vector(dve, link, lambda t: xb[:, t, :], 0.0)
                    link(dve.tensor_tensor(norm1.work[:], norm1.mv[:, :, 1], norm1.rstd[:], ALU.mult))
                    link(dve.tensor_scalar(norm1.work[:], norm1.work[:], 1e-6, None, ALU.add))
                    link(dve.reciprocal(norm1.rstd[:], norm1.work[:]))
                    dve.wait_ge(*stored.at(0, b))
                    for t in range(ST):
                        last = dve.tensor_scalar(xn[:, 0, t, :], xb[:, t, :], norm1.mean(t), norm1.r(t),
                                                 ALU.subtract, ALU.mult)
                    link(last)
                    dve.wait_ge(*again.at(16, b))
                    dve.tensor_tensor(xn[:, 0], xn[:, 0], xs[:], ALU.add).then_inc(xs_free.sem, 1)
                    dve.wait_ge(*xs_free.at(1, b))
                    norm2.vector(dve, link, lambda t: xn[:, 0, t, :], 1e-5)
                    for t in range(ST):
                        last = dve.tensor_scalar(xn[:, 0, t, :], xn[:, 0, t, :], norm2.mean(t), norm2.r(t),
                                                 ALU.subtract, ALU.mult)
                    last.then_inc(done.sem, 1)
                    link(dve.tensor_copy(norm2.work[:, 0:1], norm2.rstd[:, 0:1]))
                    link.close()


E14, FE = 14, 512
FT = FE // P
CH = 512
NC4 = TOK // CH
CT = CH // P


def moe14_stage(nc, x_in, w, out):
    xin_c = x_in.rearrange("(c t p) d -> c p t d", p=P, t=CT)
    out_c = out.rearrange("(c t p) d -> c p t d", p=P, t=CT)
    w1_e = w["w1"].rearrange("e (k p) f -> e p k f", p=P)
    w2_e = w["w2"].rearrange("e (k p) d -> e p k d", p=P)
    with ExitStack() as ctx:
        m = Room(nc, ctx, "m14")
        ident = m.sb("ident", [P, P])
        gate_w = m.sb("gate_w", [P, DT, E14])
        b2 = m.sb("b2", [E14, D])
        b1 = m.sb("b1", [P, E14, FT])
        iota = m.sb("iota", [P, E14])
        xT = m.sb("xT", [P, DT, TOK])
        acc = m.sb("acc", [P, NT, D])
        wt = m.sb("wt", [P, NT, E14])
        xs = m.sb("xs", [P, CT, D])
        xTs = m.sb("xTs", [P, DT, CH])
        top = m.sb("top", [P, CT, 1])
        prob = m.sb("prob", [P, CT, E14])
        psumr = m.sb("psumr", [P, CT, 1])
        best = m.sb("best", [P, CT, 8])
        best_i = m.sb("best_i", [P, CT, 8], U32)
        best_f = m.sb("best_f", [P, CT, 8])
        mask = m.sb("mask", [P, CT, E14])
        mask2 = m.sb("mask2", [P, CT, E14])
        den = m.sb("den", [P, CT, 1])
        wc = m.sb("wc", [P, CT, E14])
        wT = m.sb("wT", [E14, CH])
        w1s = m.sb("w1s", [P, 2, DT, FE])
        w2s = m.sb("w2s", [P, 2, FT, D])
        hid = m.sb("hid", [P, 2, FT, CH])
        xo = m.sb("xo", [P, CT, D])
        psT = m.ps("psT", [P, DT, CH])
        psL = m.ps("psL", [P, 512])
        psW = m.ps("psW", [P, 512])
        psB = m.ps("psB", [P, CT, D])
        norm = Norm(m, "norm", CT)

        started = m.counter("started", ahead=1)
        const_in = m.counter("const_in")
        x_loaded = m.counter("x_loaded", 16)
        xs_free = m.counter("xs_free", 1, ahead=1)
        xT_done = m.counter("xT_done", 1)
        xT_stored = m.counter("xT_stored", 1)
        xT_kept = m.counter("xT_kept", 1, ahead=1)
        logits = m.counter("logits", 1)
        shifted = m.counter("shifted", 1)
        exps = m.counter("exps", 1)
        w_ready = m.counter("w_ready", 1)
        wT_done = m.counter("wT_done", 1)
        wT_stored = m.counter("wT_stored", 1)
        bias_done = m.counter("bias_done", 1)
        chain = m.counter("chain", 15)

        with nc.Block() as block:
            @block.sync
            def _(sp):
                started.open(sp)
                sp.dma_start(ident[:], w["ident"]).then_inc(const_in.sem, 16)
                sp.dma_start(gate_w[:], w["gate_wT"].rearrange("(k p) e -> p k e", p=P)).then_inc(const_in.sem, 16)
                sp.dma_start(b2[:], w["b2"]).then_inc(const_in.sem, 16)
                sp.dma_start(b1[:], w["b1_cols"]).then_inc(const_in.sem, 16)
                sp.dma_start(iota[:], w["iota14"].partition_broadcast(P)).then_inc(const_in.sem, 16)
                with sp.Fori(0, NC4) as c:
                    sp.wait_ge(*xs_free.at(1 - 1, c))
                    sp.dma_start(xs[:], xin_c[bass.ds(c, 1)][0]).then_inc(x_loaded.sem, 16)

            @block.tensor
            def _(pe):
                pe.wait_ge(*const_in.at(80))
                with pe.Fori(0, NC4) as c:
                    pe.wait_ge(*x_loaded.at(16, c))
                    for k in range(DT):
                        for t in range(CT):
                            last = pe.transpose(psT[:, k, t * P:(t + 1) * P], xs[:, t, k * P:(k + 1) * P], ident[:])
                    last.then_inc(xT_done.sem, 1)
                    pe.wait_ge(*xT_stored.at(1, c))
                    for t in range(CT):
                        for k in range(DT):
                            last = pe.matmul(psL[:, t * E14:(t + 1) * E14], xTs[:, k, t * P:(t + 1) * P],
                                             gate_w[:, k, :], start=(k == 0), stop=(k == DT - 1))
                    last.then_inc(logits.sem, 1)
                    pe.wait_ge(*w_ready.at(1, c))
                    for t in range(CT):
                        last = pe.transpose(psW[0:E14, t * P:(t + 1) * P], wc[:, t, :], ident[:])
                    last.then_inc(wT_done.sem, 1)
                    pe.wait_ge(*wT_stored.at(1, c))
                    for t in range(CT):
                        last = pe.matmul(psB[:, t, :], wT[:, t * P:(t + 1) * P], b2[:], start=True, stop=True)
                    last.then_inc(bias_done.sem, 1)

            @block.scalar
            def _(act):
                xT_kept.open(act)
                with act.Fori(0, NC4) as c:
                    alone(act, *xT_stored.at(1, c), started)
                    act.activation(xT[:, :, bass.ds(c * CH, CH)], xTs[:], ACT.Copy).then_inc(xT_kept.sem, 1)
                    act.wait_ge(*shifted.at(1, c))
                    act.activation(prob[:], prob[:], ACT.Exp).then_inc(exps.sem, 1)

            @block.vector
            def _(dve):
                xs_free.open(dve)
                dve.wait_ge(*const_in.at(80))
                with dve.Fori(0, NC4) as c:
                    link = Chain(dve, chain, c, started)
                    dve.wait_ge(*xT_done.at(1, c))
                    dve.wait_ge(*xT_kept.at(0, c))
                    dve.tensor_copy(xTs[:], psT[:]).then_inc(xT_stored.sem, 1)
                    dve.wait_ge(*logits.at(1, c))
                    lg = psL[:, 0:CT * E14].rearrange("p (t e) -> p t e", e=E14)
                    link(dve.tensor_reduce(top[:, :, 0], lg, AX, ALU.max))
                    dve.tensor_tensor(prob[:], lg, top[:].to_broadcast([P, CT, E14]), ALU.subtract).then_inc(
                        shifted.sem, 1)
                    dve.wait_ge(*exps.at(1, c))
                    link(dve.tensor_reduce(psumr[:, :, 0], prob[:], AX, ALU.add))
                    link(dve.reciprocal(psumr[:], psumr[:]))
                    link(dve.tensor_tensor(prob[:], prob[:], psumr[:].to_broadcast([P, CT, E14]), ALU.mult), by_itself=True)
                    for t in range(CT):
                        last = dve.max(best[:, t, :], prob[:, t, :])
                    link(last, by_itself=True)
                    for t in range(CT):
                        last = dve.max_index(best_i[:, t, :], best[:, t, :], prob[:, t, :])
                    link(last)
                    link(dve.tensor_copy(best_f[:], best_i[:]))
                    places = iota[:].unsqueeze(1).to_broadcast([P, CT, E14])
                    dve.tensor_tensor(mask[:], places, best_f[:, :, 0:1].to_broadcast([P, CT, E14]), ALU.is_equal)
                    link(dve.tensor_tensor(mask2[:], places, best_f[:, :, 1:2].to_broadcast([P, CT, E14]),
                                           ALU.is_equal))
                    link(dve.tensor_tensor(mask[:], mask[:], mask2[:], ALU.add))
                    link(dve.tensor_tensor(den[:], best[:, :, 0:1], best[:, :, 1:2], ALU.add))
                    link(dve.tensor_scalar(den[:], den[:], 1e-10, None, ALU.max))
                    link(dve.reciprocal(den[:], den[:]))
                    link(dve.tensor_tensor(mask[:], mask[:], prob[:], ALU.mult))
                    link(dve.tensor_tensor(wc[:], mask[:], den[:].to_broadcast([P, CT, E14]), ALU.mult))
                    dve.tensor_copy(wt[:, bass.ds(c * CT, CT)], wc[:]).then_inc(w_ready.sem, 1)
                    dve.wait_ge(*wT_done.at(1, c))
                    dve.tensor_copy(wT[:], psW[0:E14, :]).then_inc(wT_stored.sem, 1)
                    dve.wait_ge(*bias_done.at(1, c))
                    link(dve.tensor_tensor(acc[:, bass.ds(c * CT, CT)], xs[:], psB[:], ALU.add))
                    dve.sem_inc(xs_free.sem, 1)
                    link.close()

        UNITS = 2 * NC4
        w_loaded = [m.counter(f"w_loaded{s}", 32) for s in range(2)]
        up = m.counter("up", UNITS * FT)
        gelu = m.counter("gelu", UNITS * FT, ahead=2)
        down = m.counter("down", UNITS * 2, ahead=UNITS * 2)
        summed = m.counter("summed", UNITS * 2, ahead=8)
        psU = [psL, psW]

        def down_bank(n):
            if n % 4 < 2:
                return psB[:, 2 * (n % 2):2 * (n % 2) + 2, :]
            return psT[:, n % 2, :].rearrange("p (t d) -> p t d", d=D)

        with nc.Block() as block:
            @block.sync
            def _(sp):
                with sp.Fori(0, E14 // 2) as i:
                    for s in range(2):
                        sp.wait_ge(*down.at((s + 1) * NC4 * 2 - UNITS * 2, i))
                        sp.dma_start(w1s[:, s], w1_e[bass.ds(i * 2 + s, 1)][0]).then_inc(w_loaded[s].sem, 16)
                        sp.dma_start(w2s[:, s], w2_e[bass.ds(i * 2 + s, 1)][0]).then_inc(w_loaded[s].sem, 16)

            @block.tensor
            def _(pe):
                down.open(pe)
                with pe.Fori(0, E14 // 2) as i:
                    for u in range(UNITS + 1):
                        if u < UNITS:
                            s, c = u // NC4, u % NC4
                            if c == 0:
                                pe.wait_ge(*w_loaded[s].at(32, i))
                            for f in range(FT):
                                pe.wait_ge(*gelu.at(u * FT + f + 1 - 2, i))
                                for k in range(DT):
                                    last = pe.matmul(psU[f % 2][:], w1s[:, s, k, f * P:(f + 1) * P],
                                                     xT[:, k, c * CH:(c + 1) * CH], start=(k == 0), stop=(k == DT - 1))
                                last.then_inc(up.sem, 1)
                        if u > 0:
                            v = u - 1
                            s = v // NC4
                            pe.wait_ge(*gelu.at(v * FT + FT, i))
                            for h in range(2):
                                n = v * 2 + h
                                pe.wait_ge(*summed.at(n + 1 - 4, i))
                                for t in range(2):
                                    for f in range(FT):
                                        last = pe.matmul(down_bank(n)[:, t, :],
                                                         hid[:, v % 2, f, (2 * h + t) * P:(2 * h + t + 1) * P],
                                                         w2s[:, s, f, :], start=(f == 0), stop=(f == FT - 1))
                                last.then_inc(down.sem, 1)

            @block.scalar
            def _(act):
                gelu.open(act)
                with act.Fori(0, E14 // 2) as i:
                    for u in range(UNITS):
                        act.wait_ge(*down.at(2 * (u + 1) - 4, i))
                        for f in range(FT):
                            alone(act, *up.at(u * FT + f + 1, i), started)
                            act.activation(hid[:, u % 2, f, :], psU[f % 2][:], ACT.Gelu,
                                           bias=b1[:, bass.ds(i * 2 + u // NC4, 1), f]).then_inc(gelu.sem, 1)

            @block.vector
            def _(dve):
                summed.open(dve)
                with dve.Fori(0, E14 // 2) as i:
                    for u in range(UNITS):
                        s, c = u // NC4, u % NC4
                        for h in range(2):
                            n = u * 2 + h
                            dve.wait_ge(*down.at(n + 1, i))
                            dve.wait_ge(*summed.at(n + 1 - 8, i))
                            for t in range(2):
                                tile = c * CT + 2 * h + t
                                last = dve.scalar_tensor_tensor(
                                    out=acc[:, tile, :], in0=down_bank(n)[:, t, :],
                                    scalar=wt[:, tile, bass.ds(i * 2 + s, 1)], in1=acc[:, tile, :],
                                    op0=ALU.mult, op1=ALU.add)
                            last.then_inc(summed.sem, 1)

        x_again = m.counter("x_again", 16)
        xs_read = m.counter("xs_read", 1, ahead=1)
        normed = m.counter("normed", 1)
        stored = m.counter("stored", 16, ahead=16)
        fin = m.counter("fin", 15)

        with nc.Block() as block:
            @block.sync
            def _(sp):
                stored.open(sp)
                with sp.Fori(0, NC4) as c:
                    sp.wait_ge(*xs_read.at(1 - 1, c))
                    sp.dma_start(xs[:], xin_c[bass.ds(c, 1)][0]).then_inc(x_again.sem, 16)
                    sp.wait_ge(*normed.at(1, c))
                    sp.dma_start(out_c[bass.ds(c, 1)][0], xo[:]).then_inc(stored.sem, 16)
                sp.wait_ge(*stored.at(0, NC4))

            @block.vector
            def _(dve):
                xs_read.open(dve)
                with dve.Fori(0, NC4) as c:
                    link = Chain(dve, fin, c, started)
                    part = acc[:, bass.ds(c * CT, CT)]
                    link(dve.tensor_scalar(part, part, 100.0, -100.0, ALU.min, ALU.max))
                    dve.wait_ge(*x_again.at(16, c))
                    dve.wait_ge(*stored.at(0, c))
                    dve.tensor_tensor(xo[:], xs[:], part, ALU.add).then_inc(xs_read.sem, 1)
                    dve.wait_ge(*xs_read.at(1, c))
                    norm.vector(dve, link, lambda t: xo[:, t, :], 1e-5)
                    for t in range(CT):
                        last = dve.tensor_scalar(xo[:, t, :], xo[:, t, :], norm.mean(t), norm.r(t),
                                                 ALU.subtract, ALU.mult)
                    last.then_inc(normed.sem, 1)
                    link(dve.tensor_copy(norm.work[:, 0:1], norm.rstd[:, 0:1]))
                    link.close()


def build(nc, a, out):
    def of(stage):
        named = {k.split(".", 1)[1]: v for k, v in a.items() if k.startswith(stage + ".")}
        named.update(ident=a["ident"], ctxT=a["ctxT"])
        return named

    between = [nc.dram_tensor(f"x_after_{n}", (TOK, D), F32, kind="Internal").ap() for n in range(1, 6)]
    bias = nc.dram_tensor("distance_bias", (NL * B, S, S), F32, kind="Internal").ap()
    bias_stage(nc, of("bias"), bias)
    scan_stage(nc, a["x"], of("ssm"), between[0])
    cross_stage(nc, between[0], of("xat"), between[1])
    moe8_stage(nc, between[1], of("m8"), between[2])
    linear_stage(nc, between[2], of("lin"), between[3])
    decoder_stage(nc, between[3], bias, of("dec"), between[4])
    moe14_stage(nc, between[4], of("m14"), out)


def layouts(i):
    def turned(v):
        return np.swapaxes(v, -1, -2)

    def cols(v):
        return turned(v.reshape(*v.shape[:-1], -1, P))

    def padded_heads(v):
        wide = np.zeros((LH, HP), v.dtype)
        wide[:, :LD] = v.reshape(LH, LD)
        return wide.reshape(1, LH * HP)

    s, x0, f0 = (lambda n: i["L0_attn_" + n]), (lambda n: i["L0_xattn_" + n]), (lambda n: i["L0_ffn_" + n])
    l1, x1, f1 = (lambda n: i["L1_attn_" + n]), (lambda n: i["L1_xattn_" + n]), (lambda n: i["L1_ffn_" + n])
    dist = i["fside_BxSxS2_0"]
    a = {
        "ident": np.eye(P, dtype=np.float32),
        "x": i["x"].reshape(TOK, D),
        "ctxT": turned(i["ctx_1024"]),
        "bias.distT": turned(dist),
        "bias.dist": dist,
        "bias.mask": i["mask_Bx1x1xS2_ff0"].reshape(B, S),
        "bias.abw": np.stack([x1("Wth")[:, 0].T, x1("bth").T, x1("Wto")[:, :, 0].T], 1),
        "bias.bto": x1("bto")[:, 0],
        "ssm.ln_wb": np.stack([cols(s("ln_w")), cols(s("ln_b"))], -1),
        "ssm.in_wT": turned(s("in_w")),
        "ssm.in_b_cols": cols(s("in_b")),
        "ssm.taps": np.concatenate([s("conv_w")[:, 0], s("conv_b")[:, None]], 1).reshape(IT, P, TAPS + 1).transpose(1, 0, 2),
        "ssm.xp_wT": turned(s("xp_w")),
        "ssm.dtp_wT": turned(s("dtp_w")),
        "ssm.dtp_b_cols": cols(s("dtp_b")),
        "ssm.A_log": s("A_log"),
        "ssm.D_cols": cols(s("D")),
        "ssm.out_wT": turned(s("out_w")),
        "ssm.out_b": s("out_b"),
        "xat.bo": x0("bo"),
        "m8.iota_tok": np.arange(TOK, dtype=np.float32),
        "m8.gates_wT": np.concatenate([turned(f0("sg_w")), turned(f0("eg_w"))], 1),
        "m8.gates_b": np.concatenate([f0("sg_b"), f0("eg_b")]),
        "m8.gains": np.stack([f0("s_ln_g"), f0("sel_ln_g")], 1),
        "m8.shifts": np.stack([f0("s_ln_b"), f0("sel_ln_b")], 1),
        "lin.pair": linear_constants(),
        "lin.qb_row": padded_heads(l1("qb")),
        "lin.kb_row": padded_heads(l1("kb")),
        "lin.vb_row": l1("vb")[None],
        "lin.ob_row": l1("ob")[None],
        "dec.bf1_cols": cols(x1("bf1")),
        "m14.gate_wT": turned(f1("gate_w")),
        "m14.b1_cols": f1("b1").reshape(E14, FT, P).transpose(2, 0, 1),
        "m14.iota14": np.arange(E14, dtype=np.float32),
        "dec.bf2": x1("bf2"),
        "dec.wq": x1("Wq").reshape(LAYERS, D, QW),
        "dec.wk": x1("Wk").reshape(LAYERS, D, QW),
        "dec.wv": x1("Wv").reshape(LAYERS, D, QW),
        "dec.wo": x1("Wo").reshape(LAYERS, QW, D),
        "dec.wf1": x1("Wf1"),
        "dec.wf2": x1("Wf2"),
    }
    for n in ("Wq", "Wk", "Wv", "Wo"):
        a[f"xat.{n}T"] = turned(x0(n))
    for n in ("sw1", "sw2", "sw3", "ew1", "ew2", "ew3"):
        a[f"m8.{n}T"] = turned(f0(n))
    for n in ("index_b", "index_t", "sb1", "sb2", "sb3", "eb1", "eb2", "eb3", "exp_bias"):
        a[f"m8.{n}"] = f0(n)
    for n in ("g1", "b1", "g2", "b2"):
        a[f"lin.{n}"] = l1(n)
    for n in "qkvo":
        a[f"lin.{n}S"] = l1(n + "S")
        a[f"lin.{n}A_halves"] = l1(n + "A").reshape(PF, DT, 2, PF).transpose(2, 1, 0, 3)
    for n in ("w1", "w2", "b2"):
        a[f"m14.{n}"] = f1(n)
    return {k: np.ascontiguousarray(v) for k, v in a.items()}


def kernel(**inputs):
    import concourse.bacc as bacc
    from concourse.bass_utils import run_bass_kernel_spmd

    nc = bacc.Bacc("TRN2", target_bir_lowering=False, num_devices=1)
    arrays = layouts({k: np.asarray(v) for k, v in inputs.items()})
    dram = {k.replace(".", "_"): v for k, v in arrays.items()}
    aps = {k: nc.dram_tensor(k.replace(".", "_") + "_in", v.shape, mybir.dt.from_np(v.dtype), kind="ExternalInput").ap()
           for k, v in arrays.items()}
    out = nc.dram_tensor("out_0", (TOK, D), F32, kind="ExternalOutput").ap()
    build(nc, aps, out)
    r = run_bass_kernel_spmd(nc, [{k + "_in": v for k, v in dram.items()}], core_ids=[0])
    return r.results[0]["out_0"].reshape(B, S, D)
```

```python
import math
from contextlib import ExitStack

import numpy as np

import concourse.bass as bass
from concourse import mybir

P = 128
F32 = mybir.dt.float32
F32R = mybir.dt.float32r
BF16 = mybir.dt.bfloat16
I32 = mybir.dt.int32
U32 = mybir.dt.uint32
ALU = mybir.AluOpType
ACT = mybir.ActivationFunctionType
AX = mybir.AxisListType.X

B, S, D = 8, 256, 256
TOK = B * S
DT = D // P
ST = S // P
NT = TOK // P


class Signal:

    def __init__(self, sem, per=0, ahead=0):
        self.sem, self.per, self.ahead = sem, per, ahead

    def open(self, eng):
        eng.sem_inc(self.sem, self.ahead)

    def at(self, n, i=0):
        return self.sem, i * self.per + (n + self.ahead)


class Chain:

    def __init__(self, eng, signal, i=0, started=None):
        self.eng, self.step, self.i, self.n, self.started = eng, signal, i, 0, started

    def __call__(self, instruction, by_itself=False):
        self.n += 1
        instruction.then_inc(self.step.sem, 1)
        if by_itself:
            alone(self.eng, *self.step.at(self.n, self.i), self.started)
        else:
            self.eng.wait_ge(*self.step.at(self.n, self.i))

    def close(self):
        assert self.n == self.step.per, (self.step.sem, self.n)


class Room:

    def __init__(self, nc, ctx, prefix):
        self.nc, self.ctx, self.prefix = nc, ctx, prefix
        self.semaphores = []
        ctx.callback(self.clear)

    def clear(self):
        self.nc.clear_and_free_semaphores(self.semaphores)
        self.nc.all_engine_barrier()

    def sb(self, name, shape, dt=F32):
        return self.ctx.enter_context(self.nc.sbuf_tensor(f"{self.prefix}_{name}", shape, dt))

    def ps(self, name, shape, dt=F32):
        return self.ctx.enter_context(self.nc.psum_tensor(f"{self.prefix}_{name}", shape, dt))

    def counter(self, name, per=0, ahead=0):
        self.semaphores.append(self.nc.alloc_semaphore(f"{self.prefix}_{name}"))
        return Signal(self.semaphores[-1], per, ahead)


def alone(eng, sem, value, started):
    if not isinstance(value, int):
        value = eng.to_reg(value)
        eng.wait_ge(started.sem, 1)
    eng.wait_ge(sem, value)


class Norm:

    MAGIC, NEWTON = float(0x5F3759DF), 3

    def __init__(self, room, name, tiles):
        self.tiles = tiles
        self.stats = room.sb(name + "_stats", [P, tiles, 6])
        self.mv = room.sb(name + "_mv", [P, tiles, 2])
        self.var = room.sb(name + "_var", [P, tiles])
        self.half = room.sb(name + "_half", [P, tiles])
        self.work = room.sb(name + "_work", [P, tiles])
        self.rstd = room.sb(name + "_rstd", [P, tiles])

    def mean(self, t):
        return self.mv[:, t, 0:1]

    def r(self, t):
        return self.rstd[:, t:t + 1]

    def vector(self, dve, chain, x, eps):
        for t in range(self.tiles):
            last = dve.bn_stats(self.stats[:, t, :], x(t))
        self.finish(dve, chain, last, eps)

    def finish(self, dve, chain, last, eps):
        chain(last, by_itself=True)
        for t in range(self.tiles):
            last = dve.bn_aggr(self.mv[:, t, :], self.stats[:, t, :])
        chain(last)
        if eps:
            chain(dve.tensor_scalar(self.var[:], self.mv[:, :, 1], eps, None, ALU.add))
        else:
            chain(dve.tensor_copy(self.var[:], self.mv[:, :, 1]))
        dve.tensor_scalar(self.half[:], self.var[:], -0.5, None, ALU.mult)
        chain(dve.tensor_scalar(self.rstd[:].bitcast(I32), self.var[:].bitcast(I32), -0.5, self.MAGIC,
                                ALU.mult, ALU.add))
        for _ in range(self.NEWTON):
            chain(dve.tensor_tensor(self.work[:], self.half[:], self.rstd[:], ALU.mult))
            chain(dve.tensor_tensor(self.work[:], self.work[:], self.rstd[:], ALU.mult))
            chain(dve.scalar_tensor_tensor(self.rstd[:], self.work[:], 1.5, self.rstd[:], ALU.add, ALU.mult))


def split_product(pe, out, weights, moving, start, stop):
    pe.matmul(out, weights[0], moving[0], start=start, stop=False)
    pe.matmul(out, weights[0], moving[1], start=False, stop=False)
    return pe.matmul(out, weights[1], moving[0], start=False, stop=stop)


class Heads:

    HEADS, GROUP = 16, 4
    GROUPS = HEADS // GROUP

    def __init__(self, m, rows, depth, value, scale, biased):
        self.rows, self.depth, self.value, self.scale, self.biased = rows, depth, value, scale, biased
        self.MT, self.WIDTH = self.GROUP * rows // P, self.GROUP * value
        self.FEATURES = self.HEADS * value // P
        self.qT = m.sb("qT", [P, 2, self.MT, S])
        self.kT = m.sb("kT", [P, 2, self.MT, S])
        self.v = m.sb("v", [P, 2, ST, self.WIDTH])
        self.logit = m.sb("logit", [P, 2, ST, S]) if biased else None
        self.neg_max = m.sb("neg_max", [P, 2, ST])
        self.prob = m.sb("prob", [P, 2, ST, S])
        self.row_sum = m.sb("row_sum", [P, ST, self.HEADS])
        self.row_inv = m.sb("row_inv", [P, ST, self.HEADS])
        self.pT = m.sb("pT", [P, 2, ST, S])
        self.o = m.sb("o", [P, ST, self.HEADS * value])
        self.oT = m.sb("oT", [P, self.FEATURES, S])
        self.psS = [m.ps(f"psS{n}", [P, ST, S]) for n in range(2)]
        self.psT = [m.ps(f"psT{n}", [P, ST, S]) for n in range(2)]
        psO = [m.ps(f"psO{n}", [P, ST * S]) for n in range(2)]
        self.psO = [bank[:, 0:ST * self.WIDTH].rearrange("p (t d) -> p t d", t=ST) for bank in psO]
        self.psA = m.ps("psA", [P, ST, S])
        self.psB = m.ps("psB", [P, ST, S])
        self.psV = self.psB[:].rearrange("p t s -> p (t s)")[:, 0:ST * self.WIDTH].rearrange("p (t d) -> p t d", t=ST)
        g, h = self.GROUPS, self.HEADS
        self.projected = m.counter("projected", 3 * g, ahead=3 * g)
        self.q_kept = m.counter("q_kept", g)
        self.k_kept = m.counter("k_kept", g)
        self.v_kept = m.counter("v_kept", g)
        self.scored = m.counter("scored", h)
        self.bias_added = m.counter("bias_added", h, ahead=2 * h)
        self.max_ready = m.counter("max_ready", h)
        self.exp_done = m.counter("exp_done", h)
        self.turned = m.counter("turned", h)
        self.pT_kept = m.counter("pT_kept", h)
        self.weighed = m.counter("weighed", h)
        self.inv_ready = m.counter("inv_ready", g)
        self.o_kept = m.counter("o_kept", g)
        self.o_turned = m.counter("o_turned", self.FEATURES // 2)
        self.oT_kept = m.counter("oT_kept", self.FEATURES // 2)
        self.projected_out = m.counter("projected_out", 1, ahead=1)

    def project(self, pe, g, keys, queries, values, i):
        keys(g, self.psB).then_inc(self.projected.sem, 1)
        queries(g, self.psA).then_inc(self.projected.sem, 1)
        pe.wait_ge(*self.k_kept.at(g + 1, i))
        values(g, self.psV).then_inc(self.projected.sem, 1)

    def turn_out(self, pe, ident, j, i):
        bank = (self.psA, self.psB)[j % 2]
        for f in range(2):
            for qt in range(ST):
                last = pe.transpose(bank[:, f, qt * P:(qt + 1) * P],
                                    self.o[:, qt, (2 * j + f) * P:(2 * j + f + 1) * P], ident[:])
        last.then_inc(self.o_turned.sem, 1)

    def project_out(self, pe, wo, i):
        pe.wait_ge(*self.oT_kept.at(self.FEATURES // 2, i))
        for qt in range(ST):
            for f in range(self.FEATURES):
                last = pe.matmul(self.psA[:, qt, :], self.oT[:, f, qt * P:(qt + 1) * P], wo[:, f, :],
                                 start=(f == 0), stop=(f == self.FEATURES - 1))
        last.then_inc(self.projected_out.sem, 1)

    def tensor(self, pe, ident, i, extra):
        def scores(h):
            g = h // self.GROUP
            if h % self.GROUP == 0:
                pe.wait_ge(*self.q_kept.at(g + 1, i))
            if self.biased:
                pe.wait_ge(*self.bias_added.at(h - 1, i))
            elif h >= 2:
                pe.wait_ge(*self.exp_done.at(h - 1, i))
            mt, row = h % self.GROUP * self.rows // P, h % self.GROUP * self.rows % P
            for qt in range(ST):
                last = pe.matmul(self.psS[h % 2][:, qt, :], self.qT[row:row + self.depth, g % 2, mt, qt * P:(qt + 1) * P],
                                 self.kT[row:row + self.depth, g % 2, mt, :], start=True, stop=True)
            last.then_inc(self.scored.sem, 1)

        def turn(h):
            pe.wait_ge(*self.exp_done.at(h + 1, i))
            if h >= 2:
                pe.wait_ge(*self.pT_kept.at(h - 1, i))
            for kt in range(ST):
                for qt in range(ST):
                    last = pe.transpose(self.psT[h % 2][:, kt, qt * P:(qt + 1) * P],
                                        self.prob[:, h % 2, qt, kt * P:(kt + 1) * P], ident[:])
            last.then_inc(self.turned.sem, 1)

        def weigh(h):
            g, j = h // self.GROUP, h % self.GROUP
            if j == 0:
                pe.wait_ge(*self.v_kept.at(g + 1, i))
                if g >= 2:
                    pe.wait_ge(*self.o_kept.at(g - 1, i))
            pe.wait_ge(*self.pT_kept.at(h + 1, i))
            columns = slice(j * self.value, (j + 1) * self.value)
            for qt in range(ST):
                for kt in range(ST):
                    last = pe.matmul(self.psO[g % 2][:, qt, columns], self.pT[:, h % 2, kt, qt * P:(qt + 1) * P],
                                     self.v[:, g % 2, kt, columns], start=(kt == 0), stop=(kt == ST - 1))
            last.then_inc(self.weighed.sem, 1)

        for h in range(self.HEADS + 2):
            if h < self.HEADS:
                scores(h)
            if 1 <= h <= self.HEADS:
                turn(h - 1)
            if h >= 2:
                weigh(h - 2)
            if h in extra:
                extra[h]()

    def keep_qk(self, act, g, i):
        act.wait_ge(*self.projected.at(3 * g + 1, i))
        act.activation(self.kT[:, g % 2], self.psB[:, 0:self.MT], ACT.Copy).then_inc(self.k_kept.sem, 1)
        act.wait_ge(*self.projected.at(3 * g + 2, i))
        act.activation(self.qT[:, g % 2], self.psA[:, 0:self.MT], ACT.Copy, scale=self.scale).then_inc(self.q_kept.sem, 1)

    def keep_turned_out(self, act, j, i):
        act.wait_ge(*self.o_turned.at(j + 1, i))
        act.activation(self.oT[:, 2 * j:2 * j + 2, :], (self.psA, self.psB)[j % 2][:], ACT.Copy).then_inc(
            self.oT_kept.sem, 1)

    def scalar(self, act, i, extra):
        for h in range(self.HEADS + 2):
            if h < self.HEADS:
                act.wait_ge(*self.max_ready.at(h + 1, i))
                if h >= 2:
                    act.wait_ge(*self.turned.at(h - 1, i))
                source = self.logit[:, h % 2] if self.biased else self.psS[h % 2]
                for qt in range(ST):
                    last = act.activation(self.prob[:, h % 2, qt, :], source[:, qt, :], ACT.Exp,
                                          bias=self.neg_max[:, h % 2, qt:qt + 1],
                                          accum_out=self.row_sum[:, qt, h:h + 1])
                last.then_inc(self.exp_done.sem, 1)
            if 1 <= h <= self.HEADS:
                act.wait_ge(*self.turned.at(h, i))
                if h >= 3:
                    act.wait_ge(*self.weighed.at(h - 2, i))
                act.activation(self.pT[:, (h - 1) % 2], self.psT[(h - 1) % 2][:], ACT.Copy).then_inc(
                    self.pT_kept.sem, 1)
            if h in extra:
                extra[h]()

    def keep_v(self, dve, g, i):
        dve.wait_ge(*self.projected.at(3 * g + 3, i))
        dve.tensor_copy(self.v[:, g % 2], self.psV).then_inc(self.v_kept.sem, 1)

    def normalise(self, dve, g, i):
        dve.wait_ge(*self.exp_done.at(self.GROUP * (g + 1), i))
        heads = slice(self.GROUP * g, self.GROUP * (g + 1))
        dve.reciprocal(self.row_inv[:, :, heads], self.row_sum[:, :, heads]).then_inc(self.inv_ready.sem, 1)
        dve.wait_ge(*self.weighed.at(self.GROUP * (g + 1), i))
        dve.wait_ge(*self.inv_ready.at(g + 1, i))
        for qt in range(ST):
            last = dve.tensor_tensor(
                self.o[:, qt, g * self.WIDTH:(g + 1) * self.WIDTH].rearrange("p (h d) -> p h d", d=self.value),
                self.psO[g % 2][:, qt, :].rearrange("p (h d) -> p h d", d=self.value),
                self.row_inv[:, qt, heads].unsqueeze(2).to_broadcast([P, self.GROUP, self.value]), ALU.mult)
        last.then_inc(self.o_kept.sem, 1)

    def vector(self, dve, bias, i, extra):
        for h in range(self.HEADS + 2):
            if h < self.HEADS:
                dve.wait_ge(*self.scored.at(h + 1, i))
                if h >= 2:
                    dve.wait_ge(*self.exp_done.at(h - 1, i))
                source = self.psS[h % 2]
                if self.biased:
                    dve.tensor_tensor(self.logit[:, h % 2], self.psS[h % 2][:], bias, ALU.add).then_inc(
                        self.bias_added.sem, 1)
                    dve.wait_ge(*self.bias_added.at(h + 1, i))
                    source = self.logit[:, h % 2]
                dve.tensor_reduce(self.neg_max[:, h % 2, :], source[:], AX, ALU.max, negate=True).then_inc(
                    self.max_ready.sem, 1)
            if h in extra:
                extra[h]()


KD = 32
NL = 4
QUAD = P // KD
UM = 4
UNITS_B = P // QUAD // UM
PARTS = 3
COLS = QUAD * 2 * PARTS


def bias_stage(nc, w, bias_out):
    dT_in = w["distT"].rearrange("b (h p) q -> (b h) p q", p=P)
    dn_in = w["dist"].rearrange("b (t p) (h k) -> b h p t k", p=P, k=P)
    mask_in = w["mask"].rearrange("b (h k) -> (b h) k", k=P)
    out_v = bias_out.rearrange("(l b) (t p) (h k) -> b h p l t k", l=NL, p=P, k=P)
    with ExitStack() as ctx:
        m = Room(nc, ctx, "bias")
        ident = m.sb("ident", [P, P])
        select = m.sb("select", [P, KD, QUAD, KD])
        abw = m.sb("abw", [P, 3, NL])
        neg_b = m.sb("neg_b", [P, NL])
        bto = m.sb("bto", [P, NL])
        coef = m.sb("coef", [P, NL, 2])
        rest = m.sb("rest", [P, NL, 2])
        part = m.sb("part", [P, NL, 2, PARTS], BF16)
        rhs = m.sb("rhs", [P, NL, QUAD, 2, PARTS], BF16)
        ones = m.sb("ones", [P, P], BF16)
        dT = m.sb("dT", [P, 2, S])
        dn = m.sb("dn", [P, 2, ST, P])
        mask = m.sb("mask", [P, 2, P])
        spread = [m.sb(f"spread{n}", [P, UM * S]) for n in range(2)]
        on = [m.sb(f"on{n}", [P, NL, UM * S], BF16) for n in range(2)]
        sums = m.sb("sums", [P, 2, NL * ST, UNITS_B * UM, QUAD, 2])
        t1 = m.sb("t1", [P, NL * ST, P])
        bo = m.sb("bo", [P, NL * ST, P])
        psX = [m.ps(f"psX{n}", [P, UM * S]) for n in range(2)]
        psP = [m.ps(f"psP{n}", [P, 2, 512]) for n in range(2)]
        U = UNITS_B
        const_in = m.counter("const_in")
        prep = m.counter("prep")
        ready = m.counter("ready")
        loaded = m.counter("loaded", 48)
        spread_done = m.counter("spread_done", U)
        copied = m.counter("copied", U, ahead=2)
        on_v = m.counter("on_v", U, ahead=2)
        on_a = m.counter("on_a", U)
        summed = m.counter("summed", U, ahead=U)
        reduced = m.counter("reduced", U, ahead=2)
        combined = m.counter("combined", 1, ahead=2)
        stored = m.counter("stored", 16 * NL, ahead=16 * NL)
        slopes_used = m.counter("slopes_used", 1)
        joined = m.counter("joined", 1, ahead=2)
        started = m.counter("started", ahead=1)

        with nc.Block() as block:
            @block.sync
            def _(sp):
                started.open(sp)
                stored.open(sp)
                sp.dma_start(ident[:], w["ident"]).then_inc(const_in.sem, 16)
                for g in range(QUAD):
                    sp.dma_start(abw[g * KD:(g + 1) * KD], w["abw"]).then_inc(const_in.sem, 16)
                sp.dma_start(bto[:], w["bto"].partition_broadcast(P)).then_inc(const_in.sem, 16)

                def load(b, h, before=True):
                    i = b * 2 + h
                    if before:
                        through, there = (sp.to_reg(v[1]) for v in (combined.at(0, i - 1), loaded.at(48, i - 1)))
                        sp.wait_ge(started.sem, 1)
                        sp.wait_ge(combined.sem, through)
                        sp.wait_ge(loaded.sem, there)
                    sp.dma_start(dT[:, h], dT_in[bass.ds(i, 1)][0]).then_inc(loaded.sem, 16)
                    sp.dma_start(dn[:, h], dn_in[bass.ds(b, 1)][0][h]).then_inc(loaded.sem, 16)
                    sp.dma_start(mask[:, h], mask_in[bass.ds(i, 1)][0].partition_broadcast(P)).then_inc(loaded.sem, 16)

                def store(b, h):
                    alone(sp, *combined.at(1, b * 2 + h), started)
                    for l in range(NL):
                        sp.dma_start(out_v[bass.ds(b, 1)][0][h][:, l], bo[:, 2 * l:2 * l + 2, :]).then_inc(
                            stored.sem, 16)

                load(0, 0, False)
                with sp.Fori(0, B - 1) as b:
                    load(b, 1)
                    store(b, 0)
                    load(b + 1, 0)
                    store(b, 1)
                load(B - 1, 1)
                store(B - 1, 0)
                store(B - 1, 1)
                sp.wait_ge(*stored.at(0, 2 * B))

            @block.tensor
            def _(pe):
                summed.open(pe)
                pe.wait_ge(*ready.at(1))

                def spread_unit(u, i):
                    if u == 0:
                        pe.wait_ge(*loaded.at(48, i))
                    pe.wait_ge(*copied.at(u + 1 - 2, i))
                    for r in range(UM):
                        rows = select[:, u * UM + r].rearrange("p g k -> p (g k)")
                        last = pe.matmul(psX[u % 2][:, r * S:(r + 1) * S], rows, dT[:, bass.ds(i % 2, 1), :][:, 0],
                                         start=True, stop=True)
                    last.then_inc(spread_done.sem, 1)

                def sum_unit(u, i):
                    pe.wait_ge(*on_v.at(u + 1, i))
                    pe.wait_ge(*on_a.at(u + 1, i))
                    pe.wait_ge(*reduced.at(u + 1 - 2, i))
                    for l in range(NL):
                        for q in range(ST):
                            for r in range(UM):
                                lq = l * ST + q
                                col = (lq % 4) * UM * COLS + r * COLS
                                out = psP[u % 2][:, lq // 4, col:col + COLS]
                                terms = rhs[:, l].rearrange("p g a c -> p (g a c)")
                                if l == NL - 1:
                                    pe.matmul(out, ones[:], terms, start=True, stop=False)
                                last = pe.matmul(out, on[u % 2][:, l, r * S + q * P:r * S + (q + 1) * P], terms,
                                                 start=(l < NL - 1), stop=True)
                    last.then_inc(summed.sem, 1)

                def half(i, before):
                    for u in range(U):
                        spread_unit(u, i)
                        if u >= 2:
                            sum_unit(u - 2, i)
                        elif before:
                            sum_unit(U - 2 + u, i - 1)

                half(0, False)
                with pe.Fori(1, 2 * B) as i:
                    half(i, True)
                for u in (U - 2, U - 1):
                    sum_unit(u, 2 * B - 1)

            @block.scalar
            def _(act):
                copied.open(act)
                act.wait_ge(*ready.at(1))
                with act.Fori(0, 2 * B) as i:
                    for u in range(U):
                        act.wait_ge(*spread_done.at(u + 1, i))
                        act.wait_ge(*on_v.at(u + 1 - 2, i))
                        act.activation(spread[u % 2][:], psX[u % 2][:], ACT.Copy).then_inc(copied.sem, 1)
                        act.wait_ge(*copied.at(u + 1, i))
                        act.wait_ge(*summed.at(u + 1 - 2, i))
                        act.activation(on[u % 2][:, NL - 1, :], spread[u % 2][:], ACT.Sign,
                                       scale=abw[:, 0, NL - 1:NL], bias=abw[:, 1, NL - 1:NL]).then_inc(on_a.sem, 1)

            @block.gpsimd
            def _(pool):
                joined.open(pool)
                with pool.Fori(0, 2 * B) as i:
                    slot = bass.ds(i % 2, 1)
                    alone(pool, *reduced.at(U, i), started)
                    alone(pool, *loaded.at(48, i), started)
                    alone(pool, *combined.at(0, i), started)
                    keys = lambda x: x.rearrange("p (g r) -> p g r", g=QUAD)
                    term = lambda lq, n: sums[:, slot, lq, :, :, n][:, 0].rearrange("p r g -> p g r")
                    for lq in range(NL * ST):
                        last = pool.tensor_tensor(keys(t1[:, lq]), term(lq, 0), keys(dn[:, slot, lq % ST, :][:, 0]),
                                                  ALU.mult)
                    last.then_inc(slopes_used.sem, 1)
                    alone(pool, *slopes_used.at(1, i), started)
                    for lq in range(NL * ST):
                        last = pool.tensor_tensor(keys(t1[:, lq]), keys(t1[:, lq]), term(lq, 1), ALU.add)
                    last.then_inc(joined.sem, 1)

            @block.vector
            def _(dve):
                on_v.open(dve)
                reduced.open(dve)
                combined.open(dve)
                link = Chain(dve, prep)
                dve.memset(ones[:], 1.0)
                link(dve.memset(rhs[:], 0.0))
                dve.wait_ge(*const_in.at(16 * 6))
                link(dve.tensor_copy(select[:], ident[:].rearrange("p (g r) -> p r g", g=QUAD).unsqueeze(3).to_broadcast(
                    [P, KD, QUAD, KD])))
                link(dve.tensor_scalar(neg_b[:], abw[:, 1, :], -1.0, None, ALU.mult))
                for n in range(2):
                    link(dve.tensor_tensor(coef[:, :, n], abw[:, n, :], abw[:, 2, :], ALU.mult))
                link(dve.tensor_scalar(coef[:, NL - 1, :], coef[:, NL - 1, :], 0.5, None, ALU.mult))
                link(dve.tensor_copy(rest[:], coef[:]))
                for c in range(PARTS):
                    link(dve.tensor_copy(part[:, :, :, c], rest[:]))
                    if c < PARTS - 1:
                        link(dve.tensor_tensor(rest[:], rest[:], part[:, :, :, c], ALU.subtract))
                for g in range(QUAD):
                    rows = slice(g * KD, (g + 1) * KD)
                    last = dve.tensor_copy(rhs[rows, :, g], part[rows])
                last.then_inc(ready.sem, 1)

                def switch_unit(u, i):
                    dve.wait_ge(*copied.at(u + 1, i))
                    dve.wait_ge(*summed.at(u + 1 - 2, i))
                    for l in range(NL - 1):
                        last = dve.tensor_scalar(on[u % 2][:, l, :], spread[u % 2][:], abw[:, 0, l:l + 1],
                                                 neg_b[:, l:l + 1], ALU.mult, ALU.is_gt)
                    last.then_inc(on_v.sem, 1)

                def reduce_unit(u, i):
                    alone(dve, *summed.at(u + 1, i), started)
                    slot = bass.ds(i % 2, 1)
                    src = psP[u % 2][:, :, 0:4 * UM * COLS].rearrange("p n (q x c) -> p n q x c", q=4, c=PARTS)
                    for n in range(2):
                        last = dve.tensor_reduce(
                            sums[:, slot, 4 * n:4 * n + 4, u * UM:(u + 1) * UM][:, 0].rearrange("p q r g a -> p q (r g a)"),
                            src[:, n], AX, ALU.add)
                    last.then_inc(reduced.sem, 1)

                def half(i, before):
                    for u in range(U):
                        switch_unit(u, i)
                        if u >= 2:
                            if u == 2 and before:
                                alone(dve, *joined.at(1 - 2, i), started)
                            reduce_unit(u - 2, i)
                        elif before:
                            reduce_unit(U - 2 + u, i - 1)
                        if u == 5 and before:
                            finish(i - 1)

                def finish(i):
                    alone(dve, *joined.at(1, i), started)
                    alone(dve, *stored.at(0, i), started)
                    row = mask[:, bass.ds(i % 2, 1), :][:, 0].unsqueeze(1).to_broadcast([P, ST, P])
                    for l in range(NL):
                        tiles = slice(l * ST, (l + 1) * ST)
                        last = dve.scalar_tensor_tensor(out=bo[:, tiles], in0=t1[:, tiles], scalar=bto[:, l:l + 1],
                                                        in1=row, op0=ALU.add, op1=ALU.add)
                    last.then_inc(combined.sem, 1)

                half(0, False)
                with dve.Fori(1, 2 * B) as i:
                    half(i, True)
                reduce_unit(U - 2, 2 * B - 1)
                reduce_unit(U - 1, 2 * B - 1)
                finish(2 * B - 1)


INNER, NST, RANK, TAPS = 512, 16, 64, 4
IT = INNER // P
PRM = RANK + 2 * NST
LOG1P = (2.0, 0.6666664033669932, 0.40007560644854595, 0.2823661980652396, 0.26851498016560554)


def scan_stage(nc, x_in, w, x_out):
    batches_in = x_in.rearrange("(b t p) d -> b p t d", p=P, t=ST)
    batches_out = x_out.rearrange("(b t p) d -> b p t d", p=P, t=ST)
    with ExitStack() as ctx:
        m = Room(nc, ctx, "ssm")
        ident = m.sb("ident", [P, P])
        ones = m.sb("ones", [1, P])
        two = m.sb("two", [P, 1])
        ln_wb = m.sb("ln_wb", [P, DT, 2])
        in_w = m.sb("in_w", [P, DT, 2 * INNER])
        in_b = m.sb("in_b", [P, 2 * IT])
        taps = m.sb("taps", [P, IT, TAPS + 1])
        xp_w = m.sb("xp_w", [P, IT, PRM])
        dtp_w = m.sb("dtp_w", [RANK, INNER])
        dtp_b = m.sb("dtp_b", [P, IT])
        a = m.sb("a", [P, IT, NST])
        skip = m.sb("skip", [P, IT])
        out_w = m.sb("out_w", [P, IT, D])
        out_b = m.sb("out_b", [1, D])
        x = m.sb("x", [P, 3, ST, D])
        hn = m.sb("hn", [P, ST, D])
        hT = m.sb("hT", [P, DT, S])
        line = m.sb("line", [P, IT, TAPS - 1 + S])
        gate = m.sb("gate", [P, IT, S])
        conv = m.sb("conv", [P, IT, S])
        sig_c = m.sb("sig_c", [P, IT, S])
        sig_g = m.sb("sig_g", [P, IT, S])
        gated = m.sb("gated", [P, 2, IT, S])
        u = m.sb("u", [P, 2, IT, S])
        params = m.sb("params", [PRM, S])
        soft = m.sb("soft", [P, IT, S])
        dt = m.sb("dt", [P, IT, S])
        dtu = m.sb("dtu", [P, IT, S])
        dtr, ratio, square = conv, sig_c, gate
        rowsB = m.sb("rowsB", [P, NST, S])
        rowsC = m.sb("rowsC", [P, NST, S])
        decay = [m.sb(f"decay{n}", [P, NST, S]) for n in range(2)]
        state = [m.sb(f"state{n}", [P, NST, S]) for n in range(2)]
        y = m.sb("y", [P, IT, S])
        xo = m.sb("xo", [P, ST, D])
        psSum = [m.ps(f"psSum{n}", [P, S]) for n in range(2)]
        psOut = m.ps("psOut", [P, ST, D])
        psTurn = m.ps("psTurn", [P, 2, S])
        psP = [m.ps(f"psP{n}", [P, 2, S]) for n in range(4)]
        norm_in, norm_out = Norm(m, "norm_in", ST), Norm(m, "norm_out", ST)
        started = m.counter("started", ahead=1)
        const_in = m.counter("const_in")
        a_exp = m.counter("a_exp")
        loaded = m.counter("loaded", 16)
        stored = m.counter("stored", 16, ahead=16)
        chain = m.counter("chain", 26)
        last_chain = m.counter("last_chain", 14)
        setup = m.counter("setup")
        normed = m.counter("normed", 1)
        n_turned = m.counter("n_turned", 1)
        nT_kept = m.counter("nT_kept", 1)
        projected = m.counter("projected", 4)
        proj_kept = m.counter("proj_kept", 4)
        conv_done = m.counter("conv_done", 1)
        gate_tanh = m.counter("gate_tanh", 1)
        conv_tanh = m.counter("conv_tanh", 1)
        u_ready = m.counter("u_ready", 1)
        params_done = m.counter("params_done", 1)
        params_kept = m.counter("params_kept", 1)
        dt_done = m.counter("dt_done", 1)
        abs_ready = m.counter("abs_ready", 1)
        soft_exp = m.counter("soft_exp", 3)
        dt_ready = m.counter("dt_ready", 1)
        rows_spread = m.counter("rows_spread", NST)
        rows_kept = m.counter("rows_kept", NST)
        decayed = m.counter("decayed", IT)
        driven = m.counter("driven", IT)
        scanned = m.counter("scanned", IT)
        read_out = m.counter("read_out", IT)
        added = m.counter("added", IT)
        skipped = m.counter("skipped", IT)
        y_ready = m.counter("y_ready", IT)
        out_done = m.counter("out_done", 1)
        x_read = m.counter("x_read", 1, ahead=3)
        done = m.counter("done", 1)

        with nc.Block() as block:
            @block.sync
            def _(sp):
                started.open(sp)
                stored.open(sp)
                for dst, src in ((ident, w["ident"]), (ln_wb, w["ln_wb"]), (in_w, w["in_wT"].rearrange("(k p) n -> p k n", p=P)),
                                 (in_b, w["in_b_cols"]), (taps, w["taps"]),
                                 (xp_w, w["xp_wT"].rearrange("(k p) n -> p k n", p=P)), (dtp_w, w["dtp_wT"]),
                                 (dtp_b, w["dtp_b_cols"]), (a, w["A_log"].rearrange("(k p) n -> p k n", p=P)),
                                 (skip, w["D_cols"]), (out_w, w["out_wT"].rearrange("(k p) n -> p k n", p=P)),
                                 (out_b, w["out_b"].rearrange("(a n) -> a n", a=1))):
                    sp.dma_start(dst[:], src).then_inc(const_in.sem, 16)
                def load(b, before=True):
                    if before:
                        read, there = (sp.to_reg(v[1]) for v in (x_read.at(0, b - 2), loaded.at(16, b - 1)))
                        sp.wait_ge(x_read.sem, read)
                        sp.wait_ge(loaded.sem, there)
                    sp.dma_start(x[:, bass.ds(b % 3, 1)][:, 0], batches_in[bass.ds(b, 1)][0]).then_inc(loaded.sem, 16)

                def store(b):
                    sp.wait_ge(*done.at(1, b))
                    sp.dma_start(batches_out[bass.ds(b, 1)][0], xo[:]).then_inc(stored.sem, 16)

                load(0, False)
                load(1)
                with sp.Fori(0, B - 2) as b:
                    load(b + 2)
                    store(b)
                store(B - 2)
                store(B - 1)
                sp.wait_ge(*stored.at(0, B))

            @block.tensor
            def _(pe):
                def project_in(b):
                    pe.wait_ge(*normed.at(1, b))
                    for k in range(DT):
                        for t in range(ST):
                            last = pe.transpose(psTurn[:, k, t * P:(t + 1) * P], hn[:, t, k * P:(k + 1) * P], ident[:])
                    last.then_inc(n_turned.sem, 1)
                    pe.wait_ge(*nT_kept.at(1, b))
                    for j in range(2 * IT):
                        for k in range(DT):
                            last = pe.matmul(psP[j // 2][:, j % 2, :], in_w[:, k, j * P:(j + 1) * P], hT[:, k, :],
                                             start=(k == 0), stop=(k == DT - 1))
                        if j % 2:
                            last.then_inc(projected.sem, 1)

                def project_params(b):
                    pe.wait_ge(*u_ready.at(1, b))
                    for k in range(IT):
                        last = pe.matmul(psTurn[0:PRM, 0, :], xp_w[:, k, :], u[:, bass.ds(b % 2, 1), k, :][:, 0],
                                         start=(k == 0), stop=(k == IT - 1))
                    last.then_inc(params_done.sem, 1)
                    pe.wait_ge(*params_kept.at(1, b))
                    pe.wait_ge(*proj_kept.at(4, b))
                    for j in range(IT):
                        last = pe.matmul(psP[2 + j // 2][:, j % 2, :], dtp_w[:, j * P:(j + 1) * P], params[0:RANK, :],
                                         start=True, stop=True)
                    last.then_inc(dt_done.sem, 1)

                def spread(b, first):
                    for n in range(0, NST // 2) if first else range(NST // 2, NST):
                        if n == 0:
                            pe.wait_ge(*abs_ready.at(1, b))
                        if n >= 4:
                            pe.wait_ge(*rows_kept.at(n - 3, b))
                        for c in range(2):
                            row = RANK + 2 * n + c
                            last = pe.matmul(psP[n % 4][:, c, :], ident[0:PRM, row:row + 1].to_broadcast([PRM, P]),
                                             params[:], start=True, stop=True)
                        last.then_inc(rows_spread.sem, 1)

                def sum_states(j, b):
                    pe.wait_ge(*read_out.at(j + 1, b))
                    if j >= 2:
                        pe.wait_ge(*skipped.at(j - 1, b))
                    for n in range(NST):
                        last = pe.matmul(psSum[j % 2][:], ident[:], state[j % 2][:, n, :], start=(n == 0),
                                         stop=(n == NST - 1))
                    last.then_inc(added.sem, 1)

                def project_out(b):
                    pe.wait_ge(*y_ready.at(IT, b))
                    for t in range(ST):
                        for k in range(IT):
                            pe.matmul(psOut[:, t, :], y[:, k, t * P:(t + 1) * P], out_w[:, k, :],
                                      start=(k == 0), stop=False)
                        last = pe.matmul(psOut[:, t, :], ones[:], out_b[:], start=False, stop=True)
                    last.then_inc(out_done.sem, 1)

                def step(b, after):
                    if after:
                        project_in(b + 1)
                    sum_states(0, b)
                    sum_states(1, b)
                    if after:
                        project_params(b + 1)
                    sum_states(2, b)
                    if after:
                        spread(b + 1, True)
                    sum_states(3, b)
                    project_out(b)
                    if after:
                        spread(b + 1, False)

                pe.wait_ge(*const_in.at(16 * 12))
                project_in(0)
                project_params(0)
                spread(0, True)
                spread(0, False)
                with pe.Fori(0, B - 1) as b:
                    step(b, True)
                step(B - 1, False)

            @block.scalar
            def _(act):
                def keep_projected(b):
                    for n in range(4):
                        act.wait_ge(*projected.at(n + 1, b))
                        for c in range(2):
                            j = 2 * n + c
                            out = line[:, j, TAPS - 1:] if j < IT else gate[:, j - IT, :]
                            last = act.activation(out, psP[n][:, c, :], ACT.Identity, bias=in_b[:, j:j + 1],
                                                  scale=1.0 if j < IT else 0.5)
                        last.then_inc(proj_kept.sem, 1)
                    act.wait_ge(*proj_kept.at(4, b))
                    act.activation(sig_g[:], gate[:], ACT.Tanh).then_inc(gate_tanh.sem, 1)

                def keep_normed(b):
                    act.wait_ge(*n_turned.at(1, b))
                    for k in range(DT):
                        last = act.activation(hT[:, k, :], psTurn[:, k, :], ACT.Identity, scale=ln_wb[:, k, 0:1],
                                              bias=ln_wb[:, k, 1:2])
                    last.then_inc(nT_kept.sem, 1)

                def tanh_conv(b):
                    act.wait_ge(*conv_done.at(1, b))
                    act.activation(sig_c[:], conv[:], ACT.Tanh).then_inc(conv_tanh.sem, 1)

                def keep_params(b):
                    act.wait_ge(*params_done.at(1, b))
                    act.activation(params[:], psTurn[0:PRM, 0, :], ACT.Copy).then_inc(params_kept.sem, 1)

                def exp_steps(b):
                    act.wait_ge(*abs_ready.at(1, b))
                    act.activation(soft[:], soft[:], ACT.Exp, scale=-1.0).then_inc(soft_exp.sem, 1)
                    act.wait_ge(*soft_exp.at(1, b))
                    act.activation(ratio[:], soft[:], ACT.Ln, bias=two[:]).then_inc(soft_exp.sem, 1)
                    act.wait_ge(*soft_exp.at(2, b))
                    act.activation(ratio[:], ratio[:], ACT.Exp, scale=-1.0).then_inc(soft_exp.sem, 1)

                def keep_rows(b, first, before):
                    if before:
                        act.wait_ge(*(driven if first else read_out).at(IT, b - 1))
                    for n in range(0, NST // 2) if first else range(NST // 2, NST):
                        act.wait_ge(*rows_spread.at(n + 1, b))
                        rows, r = (rowsB, 2 * n) if first else (rowsC, 2 * n - NST)
                        act.activation(rows[:, r:r + 2, :], psP[n % 4][:], ACT.Copy).then_inc(rows_kept.sem, 1)

                def decays(j, b, before=True):
                    if j == 0:
                        act.wait_ge(*dt_ready.at(1, b))
                    if j >= 2:
                        act.wait_ge(*scanned.at(j - 1, b))
                    elif before:
                        act.wait_ge(*scanned.at(IT + j - 1, b - 1))
                    for n in range(NST):
                        last = act.activation(decay[j % 2][:, n, 1:], dt[:, j, 1:], ACT.Exp, scale=a[:, j, n:n + 1])
                    last.then_inc(decayed.sem, 1)

                def step(b, before, after):
                    if after:
                        keep_normed(b + 1)
                    decays(1, b, before)
                    if after:
                        keep_projected(b + 1)
                    decays(2, b)
                    if after:
                        tanh_conv(b + 1)
                    decays(3, b)
                    if after:
                        keep_params(b + 1)
                        exp_steps(b + 1)
                        keep_rows(b + 1, True, True)
                        decays(0, b + 1)
                        keep_rows(b + 1, False, True)

                act.wait_ge(*const_in.at(16 * 12))
                act.activation(a[:], a[:], ACT.Exp).then_inc(a_exp.sem, 1)
                act.wait_ge(*setup.at(1))
                keep_normed(0)
                keep_projected(0)
                tanh_conv(0)
                keep_params(0)
                exp_steps(0)
                keep_rows(0, True, False)
                keep_rows(0, False, False)
                decays(0, 0, False)
                step(0, False, True)
                with act.Fori(1, B - 1) as b:
                    step(b, True, True)
                step(B - 1, True, False)

            @block.gpsimd
            def _(pool):
                with pool.Fori(0, B) as b:
                    for j in range(IT):
                        pool.wait_ge(*scanned.at(j + 1, b))
                        pool.wait_ge(*rows_kept.at(NST, b))
                        pool.tensor_tensor(state[j % 2][:], state[j % 2][:], rowsC[:], ALU.mult).then_inc(
                            read_out.sem, 1)

            @block.vector
            def _(dve):
                def norm_first(b, link):
                    xb = x[:, bass.ds(b % 3, 1)][:, 0]
                    alone(dve, *loaded.at(16, b), started)
                    norm_in.vector(dve, link, lambda t: xb[:, t, :], 1e-5)
                    for t in range(ST):
                        last = dve.tensor_scalar(hn[:, t, :], xb[:, t, :], norm_in.mean(t), norm_in.r(t),
                                                 ALU.subtract, ALU.mult)
                    last.then_inc(normed.sem, 1)

                def convolve(b, link):
                    dve.wait_ge(*proj_kept.at(2, b))
                    for j in range(IT):
                        last = dve.tensor_scalar(conv[:, j, :], line[:, j, 0:S], taps[:, j, 0:1], taps[:, j, TAPS:TAPS + 1],
                                                 ALU.mult, ALU.add)
                    link(last)
                    for k in range(1, TAPS):
                        for j in range(IT):
                            last = dve.scalar_tensor_tensor(out=conv[:, j, :], in0=line[:, j, k:k + S],
                                                            scalar=taps[:, j, k:k + 1], in1=conv[:, j, :],
                                                            op0=ALU.mult, op1=ALU.add)
                        if k < TAPS - 1:
                            link(last)
                        else:
                            last.then_inc(conv_done.sem, 1)

                def silus(b, link):
                    slot = bass.ds(b % 2, 1)
                    dve.wait_ge(*conv_tanh.at(1, b))
                    dve.scalar_tensor_tensor(out=u[:, slot][:, 0], in0=sig_c[:], scalar=1.0, in1=conv[:], op0=ALU.add,
                                             op1=ALU.mult).then_inc(u_ready.sem, 1)
                    dve.wait_ge(*gate_tanh.at(1, b))
                    link(dve.scalar_tensor_tensor(out=gated[:, slot][:, 0], in0=sig_g[:], scalar=1.0, in1=gate[:],
                                                  op0=ALU.add, op1=ALU.mult))

                def start_steps(b, link):
                    dve.wait_ge(*u_ready.at(1, b))
                    dve.wait_ge(*dt_done.at(1, b))
                    for j in range(IT):
                        last = dve.tensor_scalar(dtr[:, j, :], psP[2 + j // 2][:, j % 2, :], dtp_b[:, j:j + 1], None,
                                                 ALU.add)
                    link(last)
                    dve.scalar_tensor_tensor(out=soft[:], in0=dtr[:], scalar=-1.0, in1=dtr[:], op0=ALU.mult,
                                             op1=ALU.max).then_inc(abs_ready.sem, 1)

                def finish_steps(b, link):
                    dve.wait_ge(*soft_exp.at(3, b))
                    link(dve.tensor_tensor(ratio[:], ratio[:], soft[:], ALU.mult))
                    link(dve.tensor_tensor(square[:], ratio[:], ratio[:], ALU.mult))
                    link(dve.tensor_scalar(soft[:], square[:], LOG1P[-1], None, ALU.mult))
                    for c in reversed(LOG1P[1:-1]):
                        link(dve.scalar_tensor_tensor(out=soft[:], in0=soft[:], scalar=c, in1=square[:],
                                                      op0=ALU.add, op1=ALU.mult))
                    link(dve.scalar_tensor_tensor(out=soft[:], in0=soft[:], scalar=LOG1P[0], in1=ratio[:],
                                                  op0=ALU.add, op1=ALU.mult))
                    dve.scalar_tensor_tensor(out=dt[:], in0=dtr[:], scalar=0.0, in1=soft[:], op0=ALU.max,
                                             op1=ALU.add).then_inc(dt_ready.sem, 1)
                    dve.wait_ge(*dt_ready.at(1, b))
                    link(dve.tensor_tensor(dtu[:], dt[:], u[:, bass.ds(b % 2, 1)][:, 0], ALU.mult))
                    link.close()

                def scan(j, b, before=True):
                    if j == 0:
                        dve.wait_ge(*rows_kept.at(NST // 2, b))
                    if j >= 2:
                        dve.wait_ge(*added.at(j - 1, b))
                    elif before:
                        dve.wait_ge(*added.at(IT + j - 1, b - 1))
                    dve.tensor_tensor(state[j % 2][:], rowsB[:], dtu[:, j, :].unsqueeze(1).to_broadcast([P, NST, S]),
                                      ALU.mult).then_inc(driven.sem, 1)
                    dve.wait_ge(*decayed.at(j + 1, b))
                    dve.wait_ge(*driven.at(j + 1, b))
                    flat = lambda t: t[j % 2][:].rearrange("p n s -> p (n s)")
                    dve.tensor_tensor_scan(flat(state), flat(decay), flat(state), 0.0, ALU.mult, ALU.add).then_inc(
                        scanned.sem, 1)

                def finish(j, b):
                    slot = bass.ds(b % 2, 1)
                    alone(dve, *added.at(j + 1, b), started)
                    dve.scalar_tensor_tensor(out=y[:, j, :], in0=u[:, slot, j, :][:, 0], scalar=skip[:, j:j + 1],
                                             in1=psSum[j % 2][:], op0=ALU.mult, op1=ALU.add).then_inc(skipped.sem, 1)
                    dve.wait_ge(*skipped.at(j + 1, b))
                    dve.tensor_tensor(y[:, j, :], y[:, j, :], gated[:, slot, j, :][:, 0], ALU.mult).then_inc(
                        y_ready.sem, 1)

                def output(b):
                    link = Chain(dve, last_chain, b, started)
                    dve.wait_ge(*out_done.at(1, b))
                    dve.wait_ge(*stored.at(0, b))
                    dve.scalar_tensor_tensor(out=xo[:], in0=x[:, bass.ds(b % 3, 1)][:, 0], scalar=2.0, in1=psOut[:],
                                             op0=ALU.mult, op1=ALU.add).then_inc(x_read.sem, 1)
                    alone(dve, *x_read.at(1, b), started)
                    norm_out.vector(dve, link, lambda t: xo[:, t, :], 1e-5)
                    for t in range(ST):
                        last = dve.tensor_scalar(xo[:, t, :], xo[:, t, :], norm_out.mean(t), norm_out.r(t),
                                                 ALU.subtract, ALU.mult)
                    last.then_inc(done.sem, 1)
                    dve.wait_ge(*done.at(1, b))
                    link(dve.tensor_copy(norm_out.work[:, 0:1], norm_out.rstd[:, 0:1]))
                    link.close()

                def step(b, before, after):
                    link = Chain(dve, chain, b + 1, started)
                    if after:
                        norm_first(b + 1, link)
                    scan(0, b, before)
                    if before:
                        output(b - 1)
                    scan(1, b, before)
                    if after:
                        convolve(b + 1, link)
                    finish(0, b)
                    scan(2, b)
                    if after:
                        silus(b + 1, link)
                    finish(1, b)
                    scan(3, b)
                    if after:
                        start_steps(b + 1, link)
                    finish(2, b)
                    if after:
                        finish_steps(b + 1, link)
                    finish(3, b)

                x_read.open(dve)
                dve.memset(ones[:], 1.0)
                dve.memset(two[:], 2.0)
                dve.memset(line[:], 0.0)
                for n in range(2):
                    dve.memset(decay[n][:, :, 0:1], 0.0)
                dve.wait_ge(*a_exp.at(1))
                dve.tensor_scalar(a[:], a[:], -1.0, None, ALU.mult)
                dve.tensor_scalar(taps[:], taps[:], 0.5, None, ALU.mult)
                dve.tensor_scalar(in_b[:, IT:], in_b[:, IT:], 0.5, None, ALU.mult).then_inc(setup.sem, 1)
                dve.wait_ge(*setup.at(1))
                link = Chain(dve, chain, 0, started)
                norm_first(0, link)
                convolve(0, link)
                silus(0, link)
                start_steps(0, link)
                finish_steps(0, link)
                step(0, False, True)
                with dve.Fori(1, B - 1) as b:
                    step(b, True, True)
                step(B - 1, True, False)
                output(B - 1)


XD = 16
XP = 32


def cross_stage(nc, x_in, w, x_out):
    batches_in = x_in.rearrange("(b t p) d -> b p t d", p=P, t=ST)
    batches_out = x_out.rearrange("(b t p) d -> b p t d", p=P, t=ST)
    with ExitStack() as ctx:
        m = Room(nc, ctx, "xat")
        ident = m.sb("ident", [P, P])
        ones = m.sb("ones", [1, P])
        wqk = m.sb("wqk", [P, 2, 2, P])
        wv = m.sb("wv", [P, P])
        wo = m.sb("wo", [P, DT, D])
        bo = m.sb("bo", [P, D])
        x = m.sb("x", [P, ST, D])
        x_ahead = m.sb("x_ahead", [P, ST, D])
        xT = m.sb("xT", [P, DT, S])
        ctxT = m.sb("ctxT", [P, DT, S])
        xo = m.sb("xo", [P, ST, D])
        at = Heads(m, XP, XP, XD, D ** -0.5, False)
        norm = Norm(m, "norm", ST)
        started = m.counter("started", ahead=1)
        zeroed = m.counter("zeroed")
        const_in = m.counter("const_in")
        x_loaded = m.counter("x_loaded", 16)
        ctx_loaded = m.counter("ctx_loaded", 16)
        x_turned = m.counter("x_turned", 1)
        ahead_loaded = m.counter("ahead_loaded", 16)
        xT_kept = m.counter("xT_kept", 1)
        summed = m.counter("summed", 1, ahead=1)
        chain = m.counter("chain", 14)
        done = m.counter("done", 1)
        stored = m.counter("stored", 16, ahead=16)

        with nc.Block() as block:
            @block.sync
            def _(sp):
                started.open(sp)
                stored.open(sp)
                sp.dma_start(ident[:], w["ident"]).then_inc(const_in.sem, 16)
                sp.dma_start(wo[:], w["WoT"].rearrange("(k p) n -> p k n", p=P)).then_inc(const_in.sem, 16)
                sp.dma_start(bo[:], w["bo"].partition_broadcast(P)).then_inc(const_in.sem, 16)
                sp.wait_ge(*zeroed.at(1))
                for h in range(P // XD):
                    rows = slice(h * XD, (h + 1) * XD)
                    for n, name in enumerate(("WqT", "WkT")):
                        col = (h % 4) * XP
                        sp.dma_start(wqk[rows, n, h // 4, col:col + XD], w[name]).then_inc(const_in.sem, 16)
                    sp.dma_start(wv[rows, h * XD:(h + 1) * XD], w["WvT"]).then_inc(const_in.sem, 16)

                def load_ahead(b, before=True):
                    if before:
                        sp.wait_ge(*x_turned.at(0, b))
                    sp.dma_start(x_ahead[:], batches_in[bass.ds(b, 1)][0]).then_inc(ahead_loaded.sem, 16)

                def load_ctx(b):
                    sp.wait_ge(*at.projected.at(0, b))
                    sp.dma_start(ctxT[:], w["ctxT"].rearrange("b (k p) s -> b p k s", p=P)[bass.ds(b, 1)][0]).then_inc(
                        ctx_loaded.sem, 16)

                def load(b):
                    sp.wait_ge(*summed.at(0, b))
                    sp.dma_start(x[:], batches_in[bass.ds(b, 1)][0]).then_inc(x_loaded.sem, 16)

                def store(b):
                    sp.wait_ge(*done.at(1, b))
                    sp.dma_start(batches_out[bass.ds(b, 1)][0], xo[:]).then_inc(stored.sem, 16)

                load_ahead(0, False)
                load_ctx(0)
                load(0)
                load_ahead(1)
                load_ctx(1)
                with sp.Fori(1, B - 1) as b:
                    load_ahead(b + 1)
                    store(b - 1)
                    load(b)
                    load_ctx(b + 1)
                store(B - 2)
                load(B - 1)
                store(B - 1)
                sp.wait_ge(*stored.at(0, B))

            @block.tensor
            def _(pe):
                def rows(n, source):
                    return lambda g, bank: pe.matmul(bank[:, 0, :], wqk[:, n, g % 2, :], source[:, g // 2, :],
                                                     start=True, stop=True)

                def values(g, bank):
                    for t in range(ST):
                        last = pe.matmul(bank[:, t, :], ctxT[:, g // 2, t * P:(t + 1) * P],
                                         wv[:, (g % 2) * at.WIDTH:(g % 2 + 1) * at.WIDTH], start=True, stop=True)
                    return last

                def project(g, i):
                    at.project(pe, g, rows(1, ctxT), rows(0, xT), values, i)

                def turn_x(i):
                    pe.wait_ge(*ahead_loaded.at(16, i))
                    for k in range(DT):
                        for t in range(ST):
                            last = pe.transpose(at.psA[:, k, t * P:(t + 1) * P],
                                                x_ahead[:, t, k * P:(k + 1) * P], ident[:])
                    last.then_inc(x_turned.sem, 1)

                def first_projection(i):
                    pe.wait_ge(*xT_kept.at(1, i))
                    pe.wait_ge(*ctx_loaded.at(16, i))
                    project(0, i)

                def turn_out(i):
                    pe.wait_ge(*at.o_kept.at(at.GROUPS, i))
                    at.turn_out(pe, ident, 0, i)

                def step(i, before, after):
                    p = i - 1

                    def e0():
                        pe.wait_ge(*at.q_kept.at(1, i))
                        turn_out(p)

                    def e1():
                        if before:
                            pe.wait_ge(*at.oT_kept.at(1, p))
                        pe.wait_ge(*at.q_kept.at(1, i))
                        pe.wait_ge(*at.v_kept.at(1, i))
                        project(1, i)

                    def e2():
                        pe.wait_ge(*at.q_kept.at(2, i))
                        at.project_out(pe, wo, p)

                    def e5():
                        if before:
                            pe.wait_ge(*summed.at(1, p))
                        pe.wait_ge(*at.q_kept.at(2, i))
                        pe.wait_ge(*at.v_kept.at(2, i))
                        project(2, i)

                    def e9():
                        pe.wait_ge(*at.q_kept.at(3, i))
                        pe.wait_ge(*at.v_kept.at(3, i))
                        project(3, i)

                    def e12():
                        pe.wait_ge(*at.q_kept.at(4, i))
                        turn_x(i + 1)

                    def e17():
                        pe.wait_ge(*at.v_kept.at(4, i))
                        first_projection(i + 1)

                    extra = {1: e1, 5: e5, 9: e9}
                    if before:
                        extra.update({0: e0, 2: e2})
                    if after:
                        extra.update({12: e12, at.HEADS + 1: e17})
                    at.tensor(pe, ident, i, extra)

                at.projected.open(pe)
                at.projected_out.open(pe)
                pe.wait_ge(*const_in.at(16 * (3 + 3 * (P // XD))))
                turn_x(0)
                first_projection(0)
                step(0, False, True)
                with pe.Fori(1, B - 1) as i:
                    step(i, True, True)
                step(B - 1, True, False)
                pe.wait_ge(*at.q_kept.at(4, B - 1))
                turn_out(B - 1)
                at.project_out(pe, wo, B - 1)

            @block.scalar
            def _(act):
                def keep_x(i):
                    act.wait_ge(*x_turned.at(1, i))
                    act.activation(xT[:], at.psA[:], ACT.Copy).then_inc(xT_kept.sem, 1)

                def step(i, before, after):
                    extra = {1: lambda: at.keep_qk(act, 1, i), 5: lambda: at.keep_qk(act, 2, i),
                             9: lambda: at.keep_qk(act, 3, i)}
                    if before:
                        extra[0] = lambda: at.keep_turned_out(act, 0, i - 1)
                    if after:
                        extra[12] = lambda: keep_x(i + 1)
                        extra[at.HEADS + 1] = lambda: at.keep_qk(act, 0, i + 1)
                    at.scalar(act, i, extra)

                keep_x(0)
                at.keep_qk(act, 0, 0)
                step(0, False, True)
                with act.Fori(1, B - 1) as i:
                    step(i, True, True)
                step(B - 1, True, False)
                at.keep_turned_out(act, 0, B - 1)

            @block.vector
            def _(dve):
                def output(b):
                    link = Chain(dve, chain, b, started)
                    dve.wait_ge(*at.projected_out.at(1, b))
                    dve.wait_ge(*x_loaded.at(16, b))
                    dve.wait_ge(*stored.at(0, b))
                    dve.tensor_tensor(xo[:], x[:], at.psA[:], ALU.add).then_inc(summed.sem, 1)
                    dve.wait_ge(*summed.at(1, b))
                    link(dve.tensor_tensor(xo[:], xo[:], bo[:].unsqueeze(1).to_broadcast([P, ST, D]), ALU.add), True)
                    norm.vector(dve, link, lambda t: xo[:, t, :], 1e-5)
                    for t in range(ST):
                        last = dve.tensor_scalar(xo[:, t, :], xo[:, t, :], norm.mean(t), norm.r(t),
                                                 ALU.subtract, ALU.mult)
                    last.then_inc(done.sem, 1)
                    link.close()

                def step(i, before, after):
                    def group(g):
                        def do():
                            if g < at.GROUPS:
                                at.keep_v(dve, g, i)
                        return do

                    def e6():
                        at.normalise(dve, 0, i)

                    def e17():
                        at.normalise(dve, 3, i)
                        if after:
                            at.keep_v(dve, 0, i + 1)

                    extra = {1: group(1), 5: group(2), 6: e6, 9: group(3), 10: lambda: at.normalise(dve, 1, i),
                             14: lambda: at.normalise(dve, 2, i), at.HEADS + 1: e17}
                    if before:
                        extra[3] = lambda: output(i - 1)
                    at.vector(dve, None, i, extra)

                summed.open(dve)
                dve.memset(wv[:], 0.0)
                dve.memset(wqk[:], 0.0).then_inc(zeroed.sem, 1)
                dve.wait_ge(*const_in.at(16 * (3 + 3 * (P // XD))))
                at.keep_v(dve, 0, 0)
                step(0, False, True)
                with dve.Fori(1, B - 1) as i:
                    step(i, True, True)
                step(B - 1, True, False)
                output(B - 1)


E8, HID = 8, 128
IDX = 512
GATES = 1 + E8


def moe8_stage(nc, x_in, w, x_out):
    tiles_in = x_in.rearrange("(t p) d -> t p d", p=P)
    tiles_out = x_out.rearrange("(t p) d -> t p d", p=P)
    SL = range(2)
    with ExitStack() as ctx:
        m = Room(nc, ctx, "m8")
        ident = m.sb("ident", [P, P])
        ones = m.sb("ones", [1, P])
        ones_col = m.sb("ones_col", [P, 1], BF16)
        iota = m.sb("iota", [P, TOK])
        named = m.sb("named", [P, IDX // P, TOK], BF16)
        idx = m.sb("idx", [P, 2, IDX // P], I32)
        at_bt = m.sb("at_bt", [P, 2, IDX // P])
        test = m.sb("test", [P, 2, IDX // P])
        inside = m.sb("inside", [P, 2, IDX // P])
        key = m.sb("key", [P, IDX // P])
        hit = m.sb("hit", [P, NT])
        sw12 = m.sb("sw12", [P, DT, 2 * HID])
        sb12 = m.sb("sb12", [1, 2 * HID])
        gates_w = m.sb("gates_w", [P, DT, GATES])
        gates_b = m.sb("gates_b", [1, GATES])
        exp_bias = m.sb("exp_bias", [P, E8])
        ew12 = m.sb("ew12", [P, DT, E8, 2 * HID])
        eb12 = m.sb("eb12", [E8, 2 * HID])
        sw3 = m.sb("sw3", [P, D])
        sb3 = m.sb("sb3", [1, D])
        ew3 = m.sb("ew3", [P, E8, D])
        eb3 = m.sb("eb3", [E8, D])
        gain = m.sb("gain", [P, 2])
        shift = m.sb("shift", [P, 2])
        A = [m.ps(f"A{s}", [P, 512]) for s in SL]
        Bk = [m.ps(f"B{s}", [P, 512]) for s in SL]
        R = [m.ps(f"R{s}", [P, 2, 4, P]) for s in SL]
        const_in = m.counter("const_in")
        idx_in = m.counter("idx_in")
        iota_in = m.counter("iota_in")
        keyed = m.counter("keyed")
        marked = m.counter("marked")
        counted = m.counter("counted")

        with nc.Block() as block:
            @block.sync
            def _(sp):
                for n, name in enumerate(("index_b", "index_t")):
                    sp.dma_start(idx[:, n, :], w[name].rearrange("(p c) -> p c", p=P)).then_inc(idx_in.sem, 16)
                sp.dma_start(iota[:], w["iota_tok"].partition_broadcast(P)).then_inc(iota_in.sem, 16)
                halves = lambda a, b, n: ((slice(0, n), w[a]), (slice(n, 2 * n), w[b]))
                for cols, src in halves("sw1T", "sw2T", HID):
                    sp.dma_start(sw12[:, :, cols], src.rearrange("(k p) h -> p k h", p=P)).then_inc(const_in.sem, 16)
                for cols, src in halves("sb1", "sb2", HID):
                    sp.dma_start(sb12[:, cols], src.rearrange("(a h) -> a h", a=1)).then_inc(const_in.sem, 16)
                sp.dma_start(gates_w[:], w["gates_wT"].rearrange("(k p) h -> p k h", p=P)).then_inc(const_in.sem, 16)
                sp.dma_start(gates_b[:], w["gates_b"].rearrange("(a h) -> a h", a=1)).then_inc(const_in.sem, 16)
                sp.dma_start(exp_bias[:], w["exp_bias"].partition_broadcast(P)).then_inc(const_in.sem, 16)
                for cols, src in halves("ew1T", "ew2T", HID):
                    for k in range(DT):
                        sp.dma_start(ew12[:, k, :, cols], src[:, k * P:(k + 1) * P, :].rearrange("e p h -> p e h")).then_inc(
                            const_in.sem, 16)
                for cols, src in halves("eb1", "eb2", HID):
                    sp.dma_start(eb12[:, cols], src).then_inc(const_in.sem, 16)
                sp.dma_start(sw3[:], w["sw3T"]).then_inc(const_in.sem, 16)
                sp.dma_start(sb3[:], w["sb3"].rearrange("(a h) -> a h", a=1)).then_inc(const_in.sem, 16)
                sp.dma_start(ew3[:], w["ew3T"].rearrange("e h d -> h e d")).then_inc(const_in.sem, 16)
                sp.dma_start(eb3[:], w["eb3"]).then_inc(const_in.sem, 16)
                sp.dma_start(ident[:], w["ident"]).then_inc(const_in.sem, 16)
                sp.dma_start(gain[:], w["gains"]).then_inc(const_in.sem, 16)
                sp.dma_start(shift[:], w["shifts"]).then_inc(const_in.sem, 16)
                sp.wait_ge(*const_in.at(16 * 20))

            @block.vector
            def _(dve):
                link = Chain(dve, keyed)
                dve.memset(ones[:], 1.0)
                dve.memset(ones_col[:], 1.0)
                dve.wait_ge(*idx_in.at(32))
                link(dve.tensor_copy(at_bt[:], idx[:]))
                link(dve.tensor_scalar(test[:], at_bt[:], 0.0, None, ALU.is_lt))
                link(dve.tensor_scalar(test[:, 0], test[:, 0], float(B), None, ALU.mult))
                link(dve.tensor_scalar(test[:, 1], test[:, 1], float(S), None, ALU.mult))
                link(dve.tensor_tensor(at_bt[:], at_bt[:], test[:], ALU.add))
                link(dve.tensor_scalar(inside[:], at_bt[:], 0.0, None, ALU.is_ge))
                link(dve.tensor_scalar(test[:, 0], at_bt[:, 0], float(B), None, ALU.is_lt))
                link(dve.tensor_scalar(test[:, 1], at_bt[:, 1], float(S), None, ALU.is_lt))
                link(dve.tensor_tensor(inside[:], inside[:], test[:], ALU.mult))
                link(dve.tensor_tensor(inside[:, 0], inside[:, 0], inside[:, 1], ALU.mult))
                link(dve.scalar_tensor_tensor(out=key[:], in0=at_bt[:, 0], scalar=float(S), in1=at_bt[:, 1],
                                              op0=ALU.mult, op1=ALU.add))
                link(dve.scalar_tensor_tensor(out=key[:], in0=key[:], scalar=1.0, in1=inside[:, 0],
                                              op0=ALU.add, op1=ALU.mult))
                link(dve.tensor_scalar(key[:], key[:], -1.0, None, ALU.add))
                dve.wait_ge(*iota_in.at(16))
                for c in range(IDX // P):
                    last = dve.tensor_scalar(named[:, c, :], iota[:], key[:, c:c + 1], None, ALU.is_equal)
                last.then_inc(marked.sem, 1)
                dve.wait_ge(*counted.at(1))
                dve.tensor_scalar(hit[:], A[0][:, 0:NT], 0.5, None, ALU.is_gt)

            @block.tensor
            def _(pe):
                pe.wait_ge(*marked.at(1))
                for t in range(NT):
                    for c in range(IDX // P):
                        last = pe.matmul(A[0][:, t:t + 1], named[:, c, t * P:(t + 1) * P], ones_col[:],
                                         start=(c == 0), stop=(c == IDX // P - 1))
                last.then_inc(counted.sem, 1)

        sb = lambda n, shape, dt=F32: [m.sb(f"{n}{s}", shape, dt) for s in SL]
        sig = lambda n, per, ahead=0: [m.counter(f"{n}{s}", per, ahead) for s in SL]
        x, fT, gate_e, gate = sb("x", [P, D]), sb("fT", [P, DT, P]), sb("gate_e", [P, GATES]), sb("gate", [P, GATES])
        biased, best, best_i = sb("biased", [P, E8]), sb("best", [P, 8]), sb("best_i", [P, 8], U32)
        best_f, onehot, chosen = sb("best_f", [P, 8]), sb("onehot", [P, E8]), sb("chosen", [P, E8])
        pair, pair_m, mix = sb("pair", [P, 2]), sb("pair_m", [P, 1]), sb("mix", [P, 2])
        ohT, xTe, u, ue = sb("ohT", [E8, P]), sb("xTe", [P, DT, E8, P]), sb("u", [P, 2, 2 * HID]), sb("ue", [P, 2, HID])
        z, zT, zTe, y = sb("z", [P, 2, HID]), sb("zT", [P, 2, P]), sb("zTe", [P, E8, P]), sb("y", [P, D])
        inner = [Norm(m, f"inner{s}", 2) for s in SL]
        outer = [Norm(m, f"outer{s}", 1) for s in SL]
        started = m.counter("started", ahead=1)
        loaded, stored = sig("loaded", 16), sig("stored", 16, 16)
        x_read, done = sig("x_read", 1, 1), sig("done", 1)
        turned, turned_kept = sig("turned", 2), sig("turned_kept", 2)
        first, gates_kept, gate_exp = sig("first", 1), sig("gates_kept", 1), sig("gate_exp", 1)
        pair_ready, pair_exp = sig("pair_ready", 1), sig("pair_exp", 1)
        routed, rows_done, masked = sig("routed", 1), sig("rows_done", 1), sig("masked", 1)
        hidden, u_ready, u_tanh = sig("hidden", 1), sig("u_ready", 1), sig("u_tanh", 1)
        z_ready, z_masked, outs = sig("z_ready", 1), sig("z_masked", 1), sig("outs", 1)
        chains = sig("chain", 47)

        STEPS, LAG, PAIRS = 6, 4, NT // 2

        def body(step, i, before=True, after=True):
            for k in range(STEPS):
                if k < STEPS - LAG and before:
                    step(k + LAG, 1, i - 1)
                if k >= STEPS - LAG and after:
                    step(k + LAG - STEPS, 1, i)
                if after:
                    step(k, 0, i)

        with nc.Block() as block:
            @block.sync
            def _(sp):
                def load(s, i):
                    sp.wait_ge(*x_read[s].at(0, i))
                    sp.dma_start(x[s][:], tiles_in[bass.ds(i * 2 + s, 1)][0]).then_inc(loaded[s].sem, 16)

                def store(s, i):
                    sp.wait_ge(*done[s].at(1, i))
                    sp.dma_start(tiles_out[bass.ds(i * 2 + s, 1)][0], y[s][:]).then_inc(stored[s].sem, 16)

                started.open(sp)
                for s in SL:
                    stored[s].open(sp)
                load(0, 0)
                load(1, 0)
                store(0, 0)
                with sp.Fori(1, PAIRS) as i:
                    load(0, i)
                    store(1, i - 1)
                    load(1, i)
                    store(0, i)
                store(1, PAIRS - 1)
                for s in SL:
                    sp.wait_ge(*stored[s].at(0, PAIRS))

            @block.tensor
            def _(pe):
                def step(k, s, i):
                    if k == 0:
                        pe.wait_ge(*loaded[s].at(16, i))
                        for t in range(DT):
                            last = pe.transpose(A[s][:, t * P:(t + 1) * P], x[s][:, t * P:(t + 1) * P], ident[:])
                        last.then_inc(turned[s].sem, 1)
                    if k == 1:
                        pe.wait_ge(*turned_kept[s].at(1, i))
                        for cols, weight, row in ((slice(0, 2 * HID), sw12, sb12),
                                                  (slice(2 * HID, 2 * HID + GATES), gates_w, gates_b)):
                            for t in range(DT):
                                pe.matmul(Bk[s][:, cols], fT[s][:, t, :], weight[:, t, :], start=(t == 0), stop=False)
                            last = pe.matmul(Bk[s][:, cols], ones[:], row[:], start=False, stop=True)
                        last.then_inc(first[s].sem, 1)
                    if k == 2:
                        pe.wait_ge(*routed[s].at(1, i))
                        for e in range(E8):
                            pe.matmul(R[s][:, e // 4, e % 4, :], onehot[s][:, e:e + 1].to_broadcast([P, P]), ident[:],
                                      start=True, stop=True)
                        pe.transpose(Bk[s][0:E8, 3 * P:4 * P], onehot[s][:], ident[:]).then_inc(rows_done[s].sem, 1)
                    if k == 3:
                        pe.wait_ge(*masked[s].at(1, i))
                        for e in range(E8):
                            for t in range(DT):
                                pe.matmul(A[s][:, 0:2 * HID], xTe[s][:, t, e, :], ew12[:, t, e, :],
                                          start=(e == 0 and t == 0), stop=False)
                        pe.matmul(A[s][:, 0:2 * HID], ohT[s][:], eb12[:], start=False, stop=True).then_inc(
                            hidden[s].sem, 1)
                    if k == 4:
                        pe.wait_ge(*z_ready[s].at(1, i))
                        for n in range(2):
                            last = pe.transpose(A[s][:, (2 + n) * P:(3 + n) * P], z[s][:, n, :], ident[:])
                        last.then_inc(turned[s].sem, 1)
                    if k == 5:
                        pe.wait_ge(*z_masked[s].at(1, i))
                        pe.matmul(Bk[s][:, 0:D], zT[s][:, 0, :], sw3[:], start=True, stop=False)
                        pe.matmul(Bk[s][:, 0:D], ones[:], sb3[:], start=False, stop=True)
                        for e in range(E8):
                            pe.matmul(Bk[s][:, D:2 * D], zTe[s][:, e, :], ew3[:, e, :], start=(e == 0), stop=False)
                        pe.matmul(Bk[s][:, D:2 * D], ohT[s][:], eb3[:], start=False, stop=True).then_inc(outs[s].sem, 1)

                body(step, 0, before=False)
                with pe.Fori(1, PAIRS) as i:
                    body(step, i)
                body(step, PAIRS, after=False)

            @block.scalar
            def _(act):
                def step(k, s, i):
                    if k == 0:
                        act.wait_ge(*turned[s].at(1, i))
                        act.activation(fT[s][:].rearrange("p k t -> p (k t)"), A[s][:, 0:DT * P], ACT.Copy).then_inc(
                            turned_kept[s].sem, 1)
                    if k == 1:
                        act.wait_ge(*gates_kept[s].at(1, i))
                        act.activation(gate_e[s][:], gate[s][:], ACT.Exp, scale=-1.0).then_inc(gate_exp[s].sem, 1)
                        act.wait_ge(*pair_ready[s].at(1, i))
                        act.activation(pair[s][:], pair[s][:], ACT.Exp).then_inc(pair_exp[s].sem, 1)
                    if k == 3:
                        act.wait_ge(*u_ready[s].at(1, i))
                        act.activation(ue[s][:], u[s][:, :, 0:HID], ACT.Tanh, scale=0.5).then_inc(u_tanh[s].sem, 1)
                    if k == 4:
                        act.wait_ge(*turned[s].at(2, i))
                        for n in range(2):
                            last = act.activation(zT[s][:, n, :], A[s][:, (2 + n) * P:(3 + n) * P], ACT.Identity,
                                                  scale=gain[:, n:n + 1], bias=shift[:, n:n + 1])
                        last.then_inc(turned_kept[s].sem, 1)

                body(step, 0, before=False)
                with act.Fori(1, PAIRS) as i:
                    body(step, i)
                body(step, PAIRS, after=False)

            @block.vector
            def _(dve):
                def step(k, s, i):
                    link = Chain(dve, chains[s], i, started)
                    link.n = links_before[k]
                    if k == 1:
                        dve.wait_ge(*first[s].at(1, i))
                        link(dve.tensor_copy(u[s][:, 0, :], Bk[s][:, 0:2 * HID]))
                        dve.tensor_copy(gate[s][:], Bk[s][:, 2 * HID:2 * HID + GATES]).then_inc(gates_kept[s].sem, 1)
                        dve.wait_ge(*gate_exp[s].at(1, i))
                        link(dve.tensor_scalar(gate_e[s][:], gate_e[s][:], 1.0, None, ALU.add))
                        link(dve.reciprocal(gate[s][:], gate_e[s][:]))
                        link(dve.tensor_tensor(biased[s][:], gate[s][:, 1:GATES], exp_bias[:], ALU.add), True)
                        link(dve.max(best[s][:], biased[s][:]), True)
                        link(dve.max_index(best_i[s][:], best[s][:], biased[s][:]))
                        link(dve.tensor_copy(best_f[s][:], best_i[s][:]))
                        dve.tensor_scalar(onehot[s][:], iota[:, 0:E8], best_f[s][:, 0:1], None, ALU.is_equal).then_inc(
                            routed[s].sem, 1)
                        dve.wait_ge(*routed[s].at(1, i))
                        link(dve.tensor_tensor(chosen[s][:], gate[s][:, 1:GATES], onehot[s][:], ALU.mult))
                        link(dve.tensor_copy(pair[s][:, 0:1], gate[s][:, 0:1]))
                        link(dve.tensor_reduce(pair[s][:, 1:2], chosen[s][:], AX, ALU.add))
                        link(dve.tensor_reduce(pair_m[s][:], pair[s][:], AX, ALU.max))
                        dve.tensor_scalar(pair[s][:], pair[s][:], pair_m[s][:], None, ALU.subtract).then_inc(
                            pair_ready[s].sem, 1)
                    if k == 2:
                        dve.wait_ge(*rows_done[s].at(1, i))
                        link(dve.tensor_copy(ohT[s][:], Bk[s][0:E8, 3 * P:4 * P]))
                        for t in range(DT):
                            for half in range(2):
                                last = dve.tensor_tensor(xTe[s][:, t, 4 * half:4 * half + 4, :], R[s][:, half],
                                                         fT[s][:, t, :].unsqueeze(1).to_broadcast([P, 4, P]), ALU.mult)
                        last.then_inc(masked[s].sem, 1)
                        dve.wait_ge(*pair_exp[s].at(1, i))
                        link(dve.tensor_reduce(pair_m[s][:], pair[s][:], AX, ALU.add))
                        link(dve.reciprocal(pair_m[s][:], pair_m[s][:]))
                        link(dve.tensor_scalar(mix[s][:], pair[s][:], pair_m[s][:], None, ALU.mult))
                        link(dve.tensor_scalar(mix[s][:, 0:1], mix[s][:, 0:1], -1.0, None, ALU.add))
                        link(dve.tensor_tensor(mix[s][:], mix[s][:], hit[:, bass.ds(i * 2 + s, 1)].to_broadcast([P, 2]),
                                               ALU.mult))
                        link(dve.tensor_scalar(mix[s][:, 0:1], mix[s][:, 0:1], 1.0, None, ALU.add))
                    if k == 3:
                        dve.wait_ge(*hidden[s].at(1, i))
                        dve.tensor_copy(u[s][:, 1, :], A[s][:, 0:2 * HID]).then_inc(u_ready[s].sem, 1)
                        dve.wait_ge(*u_tanh[s].at(1, i))
                        link(dve.scalar_tensor_tensor(out=ue[s][:], in0=ue[s][:], scalar=1.0, in1=u[s][:, :, 0:HID],
                                                      op0=ALU.add, op1=ALU.mult))
                        link(dve.scalar_tensor_tensor(out=z[s][:], in0=ue[s][:], scalar=0.5, in1=u[s][:, :, HID:2 * HID],
                                                      op0=ALU.mult, op1=ALU.mult))
                        inner[s].vector(dve, link, lambda t: z[s][:, t, :], 1e-5)
                        for n in range(2):
                            last = dve.tensor_scalar(z[s][:, n, :], z[s][:, n, :], inner[s].mean(n), inner[s].r(n),
                                                     ALU.subtract, ALU.mult)
                        last.then_inc(z_ready[s].sem, 1)
                    if k == 4:
                        dve.wait_ge(*turned_kept[s].at(2, i))
                        for half in range(2):
                            last = dve.tensor_tensor(zTe[s][:, 4 * half:4 * half + 4, :], R[s][:, half],
                                                     zT[s][:, 1, :].unsqueeze(1).to_broadcast([P, 4, P]), ALU.mult)
                        last.then_inc(z_masked[s].sem, 1)
                    if k == 5:
                        dve.wait_ge(*outs[s].at(1, i))
                        dve.wait_ge(*stored[s].at(0, i))
                        link(dve.scalar_tensor_tensor(out=y[s][:], in0=Bk[s][:, 0:D], scalar=mix[s][:, 0:1],
                                                      in1=x[s][:], op0=ALU.mult, op1=ALU.add))
                        dve.scalar_tensor_tensor(out=y[s][:], in0=Bk[s][:, D:2 * D], scalar=mix[s][:, 1:2],
                                                 in1=y[s][:], op0=ALU.mult, op1=ALU.add).then_inc(x_read[s].sem, 1)
                        dve.wait_ge(*x_read[s].at(1, i))
                        outer[s].vector(dve, link, lambda t: y[s][:], 1e-5)
                        dve.tensor_scalar(y[s][:], y[s][:], outer[s].mean(0), outer[s].r(0), ALU.subtract,
                                          ALU.mult).then_inc(done[s].sem, 1)
                        link.close()
                    elif k + 1 < STEPS:
                        assert link.n == links_before[k + 1], (k, link.n)

                links_before = (0, 0, 11, 18, 33, 33)
                for s in SL:
                    x_read[s].open(dve)
                body(step, 0, before=False)
                with dve.Fori(1, PAIRS) as i:
                    body(step, i)
                body(step, PAIRS, after=False)


PF = 4
PB = D // PF
LH, LD = 16, 16
ROWS = P // B
LG = S // ROWS
HP = 32


def linear_constants():
    angle = np.pi / 2 * np.arange(1, B + 1, dtype=np.float32) / B
    s, c = np.sin(angle, dtype=np.float32), np.cos(angle, dtype=np.float32)
    pair = np.outer(s, s) + np.outer(c, c)
    return np.kron(pair, np.eye(ROWS)).astype(np.float32)


def linear_stage(nc, x_in, w, x_out):
    rows_in = x_in.rearrange("(l g r) d -> g l r d", l=B, r=ROWS)
    rows_out = x_out.rearrange("(l g r) d -> g l r d", l=B, r=ROWS)
    with ExitStack() as ctx:
        m = Room(nc, ctx, "lin")
        ident = m.sb("ident", [P, P])
        ones = m.sb("ones", [1, P])
        pair = m.sb("pair", [P, P])
        s2 = {n: m.sb("s2" + n, [P, PF, PB]) for n in "qkvo"}
        a2 = {n: m.sb("a2" + n, [P, DT, PF, PF]) for n in "qkvo"}
        term = m.sb("term", [P, PF, PB])
        weights = {n: m.sb("w" + n, [P, DT, PF, PB]) for n in "qkvo"}
        padded = {n: m.sb("wp" + n, [P, DT, PF, 4, HP]) for n in "qk"}
        row_bias = {n: m.sb("b" + n, [1, 4 * P]) for n in "qk"}
        row_bias.update({n: m.sb("b" + n, [1, D]) for n in "vo"})
        affine = {n: m.sb(n, [P, D]) for n in ("g1", "b1", "g2", "b2")}
        w_in = m.counter("w_in")
        b_in = m.counter("b_in")
        built = m.counter("built")

        with nc.Block() as block:
            @block.sync
            def _(sp):
                for n in "qkvo":
                    for half in range(2):
                        rows = slice(half * PB, (half + 1) * PB)
                        sp.dma_start(s2[n][rows], w[n + "S"].rearrange("n k l -> k n l")).then_inc(w_in.sem, 16)
                        sp.dma_start(a2[n][rows], w[n + "A_halves"][half].rearrange("k n j -> (k n j)").partition_broadcast(
                            PB).rearrange("p (k n j) -> p k n j", k=DT, n=PF)).then_inc(w_in.sem, 16)
                sp.dma_start(ident[:], w["ident"]).then_inc(b_in.sem, 16)
                sp.dma_start(pair[:], w["pair"]).then_inc(b_in.sem, 16)
                for n in "qkvo":
                    sp.dma_start(row_bias[n][:], w[n + "b_row"]).then_inc(b_in.sem, 16)
                for n in affine:
                    sp.dma_start(affine[n][:], w[n].partition_broadcast(P)).then_inc(b_in.sem, 16)
                sp.wait_ge(*b_in.at(16 * 10))

            @block.vector
            def _(dve):
                dve.memset(ones[:], 1.0)
                for n in "qk":
                    dve.memset(padded[n][:], 0.0)
                link = Chain(dve, built)
                dve.wait_ge(*w_in.at(64 * 4))
                for n in "qkvo":
                    for k in range(DT):
                        for c in range(PF):
                            out = weights[n][:, k] if c == 0 else term[:]
                            link(dve.tensor_tensor(out, a2[n][:, k, c, :].unsqueeze(2).to_broadcast([P, PF, PB]),
                                                   s2[n][:, c, :].unsqueeze(1).to_broadcast([P, PF, PB]), ALU.mult))
                            if c:
                                link(dve.tensor_tensor(weights[n][:, k], weights[n][:, k], term[:], ALU.add))
                    if n in "qk":
                        for k in range(DT):
                            for c in range(PF):
                                last = dve.tensor_copy(padded[n][:, k, c, :, 0:LD],
                                                       weights[n][:, k, c, :].rearrange("p (h m) -> p h m", m=LD))
                        link(last)

        SL = range(4)
        GO = LG // len(SL)
        x_next = [m.sb(f"x_next{s}", [P, D]) for s in SL]
        x = [m.sb(f"x{s}", [P, D]) for s in SL]
        qn = [m.sb(f"qn{s}", [P, D]) for s in SL]
        fT = [m.sb(f"fT{s}", [P, 2 * DT, P]) for s in SL]
        qT = [m.sb(f"qT{s}", [P, 4, P]) for s in SL]
        kT = [m.sb(f"kT{s}", [P, 4, P]) for s in SL]
        v = [m.sb(f"v{s}", [P, LH, LD + 1]) for s in SL]
        masked = [m.sb(f"masked{s}", [P, 4, 4, P]) for s in SL]
        z = [m.sb(f"z{s}", [P, LH]) for s in SL]
        o = [m.sb(f"o{s}", [P, D]) for s in SL]
        oT = [m.sb(f"oT{s}", [P, DT, P]) for s in SL]
        y = [m.sb(f"y{s}", [P, D]) for s in SL]
        X = [m.ps(f"X{s}", [P, 4, P]) for s in SL]
        Y = [m.ps(f"Y{s}", [P, 4, P]) for s in SL]
        flatX = [bank[:].rearrange("p g t -> p (g t)") for bank in X]
        flatY = [bank[:].rearrange("p g t -> p (g t)") for bank in Y]
        norms = [Norm(m, f"n{k}", len(SL)) for k in range(3)]
        started = m.counter("started", ahead=1)
        loaded = [m.counter(f"loaded{s}", 16 * B) for s in SL]
        stored = [m.counter(f"stored{s}", 16 * B, ahead=16 * B) for s in SL]
        x_copied = [m.counter(f"x_copied{s}", 1, ahead=1) for s in SL]
        q_normed = [m.counter(f"q_normed{s}", 1) for s in SL]
        turned = [m.counter(f"turned{s}", 2) for s in SL]
        turned_kept = [m.counter(f"turned_kept{s}", 2) for s in SL]
        projected = [m.counter(f"projected{s}", 3) for s in SL]
        qk_kept = [m.counter(f"qk_kept{s}", 2) for s in SL]
        v_kept = [m.counter(f"v_kept{s}", 1) for s in SL]
        scored = [m.counter(f"scored{s}", 4) for s in SL]
        mask_done = [m.counter(f"mask_done{s}", 4) for s in SL]
        weighed = [m.counter(f"weighed{s}", 1) for s in SL]
        o_normed = [m.counter(f"o_normed{s}", 1) for s in SL]
        final = [m.counter(f"final{s}", 1) for s in SL]
        x_read = [m.counter(f"x_read{s}", 1, ahead=1) for s in SL]
        done = [m.counter(f"done{s}", 1) for s in SL]
        chain = m.counter("chain", 3 * 13)
        steps = [m.counter(f"steps{s}", 9) for s in SL]

        with nc.Block() as block:
            @block.sync
            def _(sp):
                started.open(sp)
                for s in SL:
                    stored[s].open(sp)

                def load(i):
                    for s in SL:
                        sp.wait_ge(*x_copied[s].at(0, i))
                        for l in range(B):
                            sp.dma_start(x_next[s][l * ROWS:(l + 1) * ROWS, :],
                                         rows_in[bass.ds(i * len(SL) + s, 1)][0][l]).then_inc(loaded[s].sem, 16)

                def store(i):
                    for s in SL:
                        sp.wait_ge(*done[s].at(1, i))
                        for l in range(B):
                            sp.dma_start(rows_out[bass.ds(i * len(SL) + s, 1)][0][l],
                                         y[s][l * ROWS:(l + 1) * ROWS, :]).then_inc(stored[s].sem, 16)

                load(0)
                with sp.Fori(0, GO - 1) as i:
                    load(i + 1)
                    store(i)
                store(GO - 1)
                for s in SL:
                    sp.wait_ge(*stored[s].at(0, GO))

            @block.tensor
            def _(pe):
                with pe.Fori(0, GO) as i:
                    for s in SL:
                        pe.wait_ge(*q_normed[s].at(1, i))
                        for n, src in enumerate((x[s], qn[s])):
                            for k in range(DT):
                                last = pe.transpose(X[s][:, n * DT + k, :], src[:, k * P:(k + 1) * P], ident[:])
                        last.then_inc(turned[s].sem, 1)
                    for s in SL:
                        pe.wait_ge(*turned_kept[s].at(1, i))
                        for n, bank, first in (("q", Y[s], DT), ("k", X[s], 0)):
                            for g in range(4):
                                for k in range(DT):
                                    pe.matmul(bank[:, g, :], padded[n][:, k, g].rearrange("p h m -> p (h m)"),
                                              fT[s][:, first + k, :], start=(k == 0), stop=False)
                                last = pe.matmul(bank[:, g, :], row_bias[n][:, g * P:(g + 1) * P], ones[:],
                                                 start=False, stop=True)
                            last.then_inc(projected[s].sem, 1)
                    for s in SL:
                        pe.wait_ge(*qk_kept[s].at(1, i))
                        for k in range(DT):
                            pe.matmul(flatY[s][:, 0:D], fT[s][:, k, :], weights["v"][:, k].rearrange("p j l -> p (j l)"),
                                      start=(k == 0), stop=False)
                        pe.matmul(flatY[s][:, 0:D], ones[:], row_bias["v"][:], start=False, stop=True).then_inc(
                            projected[s].sem, 1)
                    for h in range(4):
                        for s in SL:
                            if h == 0:
                                pe.wait_ge(*qk_kept[s].at(2, i))
                            elif h == 1:
                                pe.wait_ge(*v_kept[s].at(1, i))
                            else:
                                pe.wait_ge(*mask_done[s].at(h - 1, i))
                            for g in range(4):
                                rows = slice(HP * h, HP * h + LD)
                                last = pe.matmul((X, Y)[h % 2][s][:, g, :], kT[s][rows, g, :], qT[s][rows, g, :],
                                                 start=True, stop=True)
                            last.then_inc(scored[s].sem, 1)
                    for s in SL:
                        pe.wait_ge(*mask_done[s].at(4, i))
                        for h in range(LH):
                            last = pe.matmul(flatX[s][:, h * (LD + 1):(h + 1) * (LD + 1)],
                                             masked[s][:, h % 4, h // 4, :], v[s][:, h, :], start=True, stop=True)
                        last.then_inc(weighed[s].sem, 1)
                    for s in SL:
                        pe.wait_ge(*o_normed[s].at(1, i))
                        for k in range(DT):
                            last = pe.transpose(Y[s][:, k, :], o[s][:, k * P:(k + 1) * P], ident[:])
                        last.then_inc(turned[s].sem, 1)
                    for s in SL:
                        pe.wait_ge(*turned_kept[s].at(2, i))
                        for k in range(DT):
                            pe.matmul(flatX[s][:, 0:D], oT[s][:, k, :], weights["o"][:, k].rearrange("p j l -> p (j l)"),
                                      start=(k == 0), stop=False)
                        pe.matmul(flatX[s][:, 0:D], ones[:], row_bias["o"][:], start=False, stop=True).then_inc(
                            final[s].sem, 1)

            @block.scalar
            def _(act):
                for s in SL:
                    x_copied[s].open(act)
                with act.Fori(0, GO) as i:
                    for s in SL:
                        act.wait_ge(*loaded[s].at(16 * B, i))
                        act.wait_ge(*x_read[s].at(0, i))
                        act.activation(x[s][:], x_next[s][:], ACT.Copy).then_inc(x_copied[s].sem, 1)
                    for s in SL:
                        act.wait_ge(*turned[s].at(1, i))
                        act.activation(fT[s][:], X[s][:], ACT.Copy).then_inc(turned_kept[s].sem, 1)
                    for s in SL:
                        for n, (dst, bank) in enumerate(((qT[s], Y[s]), (kT[s], X[s]))):
                            act.wait_ge(*projected[s].at(n + 1, i))
                            act.activation(dst[:], bank[:], ACT.Relu).then_inc(qk_kept[s].sem, 1)
                    for s in SL:
                        act.wait_ge(*turned[s].at(2, i))
                        act.activation(oT[s][:], Y[s][:, 0:DT, :], ACT.Copy).then_inc(turned_kept[s].sem, 1)

            @block.vector
            def _(dve):
                for s in SL:
                    x_read[s].open(dve)
                    dve.memset(v[s][:], 1.0)
                with dve.Fori(0, GO) as i:
                    link = Chain(dve, chain, i, started)
                    step = [Chain(dve, steps[s], i, started) for s in SL]

                    def scale(n, s, src, dst):
                        return dve.tensor_scalar(dst[s][:], src[s][:], norms[n].mean(s), norms[n].r(s),
                                                 ALU.subtract, ALU.mult)

                    for s in SL:
                        dve.wait_ge(*x_copied[s].at(1, i))
                        last = dve.bn_stats(norms[0].stats[:, s, :], x[s][:])
                    norms[0].finish(dve, link, last, 1e-5)
                    for s in SL:
                        step[s](scale(0, s, x, qn))
                    for s in SL:
                        step[s](dve.tensor_tensor(qn[s][:], qn[s][:], affine["g1"][:], ALU.mult))
                        dve.tensor_tensor(qn[s][:], qn[s][:], affine["b1"][:], ALU.add).then_inc(q_normed[s].sem, 1)
                    for s in SL:
                        dve.wait_ge(*projected[s].at(3, i))
                        dve.tensor_copy(v[s][:, :, 0:LD], flatY[s][:, 0:D].rearrange("p (h m) -> p h m", m=LD)).then_inc(
                            v_kept[s].sem, 1)
                    for h in range(4):
                        for s in SL:
                            dve.wait_ge(*scored[s].at(h + 1, i))
                            dve.tensor_tensor(masked[s][:, h], (X, Y)[h % 2][s][:],
                                              pair[:].unsqueeze(1).to_broadcast([P, 4, P]), ALU.mult).then_inc(
                                mask_done[s].sem, 1)
                    for s in SL:
                        dve.wait_ge(*weighed[s].at(1, i))
                        ov = flatX[s][:, 0:LH * (LD + 1)].rearrange("p (h m) -> p h m", m=LD + 1)
                        step[s](dve.tensor_scalar(z[s][:], ov[:, :, LD], 1e-6, None, ALU.max))
                        step[s](dve.reciprocal(z[s][:], z[s][:]))
                        step[s](dve.tensor_tensor(o[s][:].rearrange("p (h m) -> p h m", m=LD), ov[:, :, 0:LD],
                                                  z[s][:].unsqueeze(2).to_broadcast([P, LH, LD]), ALU.mult))
                        step[s](dve.tensor_tensor(o[s][:], o[s][:], qn[s][:], ALU.add), True)
                        last = dve.bn_stats(norms[1].stats[:, s, :], o[s][:])
                    norms[1].finish(dve, link, last, 1e-5)
                    for s in SL:
                        step[s](scale(1, s, o, o))
                    for s in SL:
                        step[s](dve.tensor_tensor(o[s][:], o[s][:], affine["g2"][:], ALU.mult))
                        dve.tensor_tensor(o[s][:], o[s][:], affine["b2"][:], ALU.add).then_inc(o_normed[s].sem, 1)
                    for s in SL:
                        dve.wait_ge(*o_normed[s].at(1, i))
                        dve.wait_ge(*stored[s].at(0, i))
                        dve.tensor_tensor(y[s][:], x[s][:], o[s][:], ALU.add).then_inc(x_read[s].sem, 1)
                    for s in SL:
                        dve.wait_ge(*final[s].at(1, i))
                        dve.wait_ge(*x_read[s].at(1, i))
                        step[s](dve.tensor_tensor(y[s][:], y[s][:], flatX[s][:, 0:D], ALU.add), True)
                        last = dve.bn_stats(norms[2].stats[:, s, :], y[s][:])
                    norms[2].finish(dve, link, last, 1e-5)
                    for s in SL:
                        scale(2, s, y, y).then_inc(done[s].sem, 1)
                    for s in SL:
                        step[s].close()
                    link.close()


LAYERS, HD = 4, 64
QW = 16 * HD
FF = 1024
FFT = FF // P


def decoder_stage(nc, x_in, bias_in, w, x_out):
    tiles_in = x_in.rearrange("(t p) d -> p t d", p=P)
    tiles_out = x_out.rearrange("(t p) d -> p t d", p=P)
    STEPS = LAYERS * B
    with ExitStack() as ctx:
        m = Room(nc, ctx, "dec")
        ident = m.sb("ident", [P, P])
        ones = m.sb("ones", [1, P])
        x = m.sb("x", [P, NT, D])
        xn = m.sb("xn", [P, 2, ST, D])
        xnT = m.sb("xnT", [P, 2, DT, S])
        ctxT = m.sb("ctxT", [P, DT, S])
        bias = m.sb("bias", [P, 2, ST, S])
        wq = m.sb("wq", [P, DT, QW])
        wk = m.sb("wk", [P, DT, QW])
        wv = m.sb("wv", [P, DT, QW])
        wo = m.sb("wo", [P, QW // P, D])
        wf1 = m.sb("wf1", [P, DT, FF])
        wf2 = m.sb("wf2", [P, FFT, D])
        bf1 = m.sb("bf1", [P, FFT])
        bf2 = m.sb("bf2", [1, D])
        hid = m.sb("hid", [P, FFT, S])
        at = Heads(m, HD, HD, HD, HD ** -0.5, True)
        norm = Norm(m, "norm", ST)
        started = m.counter("started", ahead=1)
        const_in = m.counter("const_in")
        qkv_loaded = m.counter("qkv_loaded", 16 * 3)
        wo_loaded = m.counter("wo_loaded", 16)
        ff_loaded = m.counter("ff_loaded", 16 * 4)
        ctx_loaded = m.counter("ctx_loaded", 16)
        bias_loaded = m.counter("bias_loaded", 16)
        chain = [m.counter(f"chain{n}", 17) for n in range(2)]
        added = m.counter("added", 1)
        normed = [m.counter(f"normed{n}", 1) for n in range(2)]
        n_turned = [m.counter(f"n_turned{n}", 1) for n in range(2)]
        nT_kept = [m.counter(f"nT_kept{n}", 1) for n in range(2)]
        up = m.counter("up", FFT // 2)
        up_kept_a = m.counter("up_kept_a", FFT // 4)
        up_kept_v = m.counter("up_kept_v", FFT // 4)
        down = m.counter("down", 1, ahead=1)
        step_done = m.counter("step_done", 1)

        with nc.Block() as block:
            @block.sync
            def _(sp):
                started.open(sp)

                def load_step(i):
                    sp.wait_ge(*at.projected.at(0, i))
                    sp.dma_start(ctxT[:], w["ctxT"].rearrange("b (k p) s -> b p k s", p=P)[
                        bass.ds(i % B, 1)][0]).then_inc(ctx_loaded.sem, 16)
                    sp.wait_ge(*at.bias_added.at(0, i - 1))
                    sp.dma_start(bias[:, bass.ds(i % 2, 1)][:, 0], bias_in.rearrange("n (t p) s -> n p t s", p=P)[
                        bass.ds(i, 1)][0]).then_inc(bias_loaded.sem, 16)

                def load(names, l, signal):
                    for dst, name in names:
                        src = w[name].rearrange("l (k p) n -> l p k n", p=P)
                        sp.dma_start(dst[:], src[bass.ds(l, 1)][0]).then_inc(signal.sem, 16)

                sp.dma_start(ident[:], w["ident"]).then_inc(const_in.sem, 16)
                sp.dma_start(x[:], tiles_in).then_inc(const_in.sem, 16)
                with sp.Fori(0, LAYERS) as l:
                    sp.wait_ge(*at.projected.at(0, l * B))
                    load(((wk, "wk"), (wq, "wq"), (wv, "wv")), l, qkv_loaded)
                    load_step(l * B)
                    sp.wait_ge(*at.projected_out.at(0, l * B))
                    load(((wo, "wo"),), l, wo_loaded)
                    load_step(l * B + 1)
                    sp.wait_ge(*down.at(0, l * B))
                    load(((wf1, "wf1"), (wf2, "wf2")), l, ff_loaded)
                    sp.dma_start(bf1[:], w["bf1_cols"][bass.ds(l, 1)][0]).then_inc(ff_loaded.sem, 16)
                    sp.dma_start(bf2[:], w["bf2"][bass.ds(l, 1)]).then_inc(ff_loaded.sem, 16)
                    with sp.Fori(2, B) as b:
                        load_step(l * B + b)

            @block.tensor
            def _(pe):
                def rows(weight, source):
                    def project(g, bank):
                        for mt in range(at.MT):
                            col = (g * at.MT + mt) * P
                            for k in range(DT):
                                last = pe.matmul(bank[:, mt, :], weight[:, k, col:col + P], source[:, k, :],
                                                 start=(k == 0), stop=(k == DT - 1))
                        return last
                    return project

                def values(g, bank):
                    for t in range(ST):
                        for k in range(DT):
                            last = pe.matmul(bank[:, t, :], ctxT[:, k, t * P:(t + 1) * P],
                                             wv[:, k, g * at.WIDTH:(g + 1) * at.WIDTH],
                                             start=(k == 0), stop=(k == DT - 1))
                    return last

                def project(g, i):
                    at.project(pe, g, rows(wk, ctxT), rows(wq, xnT[:, 0]), values, i)

                def turn_normed(n, bank, i):
                    pe.wait_ge(*normed[n].at(1, i))
                    for k in range(DT):
                        for t in range(ST):
                            last = pe.transpose(bank[:, k, t * P:(t + 1) * P], xn[:, n, t, k * P:(k + 1) * P], ident[:])
                    last.then_inc(n_turned[n].sem, 1)

                def first_projection(i):
                    pe.wait_ge(*qkv_loaded.at(16 * 3, i // B))
                    pe.wait_ge(*ctx_loaded.at(16, i))
                    pe.wait_ge(*nT_kept[0].at(1, i))
                    project(0, i)

                def up_rows(j, i):
                    for f in range(2):
                        for k in range(DT):
                            last = pe.matmul((at.psA, at.psB)[j % 2][:, f, :],
                                             wf1[:, k, (2 * j + f) * P:(2 * j + f + 1) * P], xnT[:, 1, k, :],
                                             start=(k == 0), stop=(k == DT - 1))
                    last.then_inc(up.sem, 1)

                def down_rows(i):
                    pe.wait_ge(*up_kept_a.at(FFT // 4, i))
                    pe.wait_ge(*up_kept_v.at(FFT // 4, i))
                    for t in range(ST):
                        for f in range(FFT):
                            pe.matmul(at.psA[:, t, :], hid[:, f, t * P:(t + 1) * P], wf2[:, f, :],
                                      start=(f == 0), stop=False)
                        last = pe.matmul(at.psA[:, t, :], ones[:], bf2[:], start=False, stop=True)
                    last.then_inc(down.sem, 1)

                def out_0(i):
                    pe.wait_ge(*at.o_kept.at(at.GROUPS, i))
                    at.turn_out(pe, ident, 0, i)
                    at.turn_out(pe, ident, 1, i)

                def out_1(i):
                    pe.wait_ge(*at.oT_kept.at(1, i))
                    at.turn_out(pe, ident, 2, i)
                    pe.wait_ge(*at.oT_kept.at(2, i))
                    at.turn_out(pe, ident, 3, i)

                def out_2(i):
                    pe.wait_ge(*wo_loaded.at(16, i // B))
                    at.project_out(pe, wo, i)

                def step(i, before, after):
                    p = i - 1

                    def e0():
                        pe.wait_ge(*at.v_kept.at(1, i))
                        out_0(p)

                    def e3():
                        if before:
                            pe.wait_ge(*added.at(1, p))
                        else:
                            pe.wait_ge(*at.v_kept.at(1, i))
                        project(1, i)

                    def e5():
                        pe.wait_ge(*at.q_kept.at(2, i))
                        turn_normed(1, at.psA, p)

                    def e6():
                        if before:
                            pe.wait_ge(*nT_kept[1].at(1, p))
                        pe.wait_ge(*at.v_kept.at(2, i))
                        pe.wait_ge(*at.q_kept.at(2, i))
                        project(2, i)

                    def e7():
                        pe.wait_ge(*ff_loaded.at(16 * 4, p // B))
                        pe.wait_ge(*at.q_kept.at(3, i))
                        up_rows(0, p)

                    def e8():
                        pe.wait_ge(*at.v_kept.at(3, i))
                        up_rows(1, p)

                    def e9():
                        pe.wait_ge(*up_kept_a.at(1, p))
                        up_rows(2, p)

                    def e10():
                        if before:
                            pe.wait_ge(*up_kept_a.at(2, p))
                            pe.wait_ge(*up_kept_v.at(1, p))
                        pe.wait_ge(*at.v_kept.at(3, i))
                        pe.wait_ge(*at.q_kept.at(3, i))
                        project(3, i)

                    def e11():
                        pe.wait_ge(*at.v_kept.at(4, i))
                        up_rows(3, p)

                    def e13():
                        pe.wait_ge(*at.q_kept.at(4, i))
                        down_rows(p)

                    def e14():
                        if before:
                            pe.wait_ge(*up_kept_v.at(2, p))
                        pe.wait_ge(*at.v_kept.at(4, i))
                        turn_normed(0, at.psB, i + 1)

                    def e17():
                        if before:
                            pe.wait_ge(*step_done.at(1, p))
                        pe.wait_ge(*at.q_kept.at(4, i))
                        first_projection(i + 1)

                    extra = {3: e3, 6: e6, 10: e10}
                    if before:
                        extra.update({0: e0, 1: lambda: out_1(p), 2: lambda: out_2(p), 5: e5, 7: e7, 8: e8, 9: e9,
                                      11: e11, 13: e13})
                    if after:
                        extra.update({14: e14, at.HEADS + 1: e17})
                    at.tensor(pe, ident, i, extra)

                pe.wait_ge(*const_in.at(32))
                down.open(pe)
                at.projected.open(pe)
                at.projected_out.open(pe)
                turn_normed(0, at.psB, 0)
                first_projection(0)
                step(0, False, True)
                with pe.Fori(1, STEPS - 1) as i:
                    step(i, True, True)
                step(STEPS - 1, True, False)
                last = STEPS - 1
                pe.wait_ge(*step_done.at(1, last - 1))
                pe.wait_ge(*at.v_kept.at(4, last))
                out_0(last)
                out_1(last)
                out_2(last)
                pe.wait_ge(*added.at(1, last))
                turn_normed(1, at.psA, last)
                pe.wait_ge(*nT_kept[1].at(1, last))
                up_rows(0, last)
                up_rows(1, last)
                pe.wait_ge(*up_kept_a.at(1, last))
                up_rows(2, last)
                pe.wait_ge(*up_kept_v.at(1, last))
                up_rows(3, last)
                down_rows(last)

            @block.scalar
            def _(act):
                def keep_normed(n, bank, i):
                    act.wait_ge(*n_turned[n].at(1, i))
                    act.activation(xnT[:, n], bank[:], ACT.Copy).then_inc(nT_kept[n].sem, 1)

                def keep_up(j, i):
                    act.wait_ge(*up.at(j + 1, i))
                    for f in range(2):
                        last = act.activation(hid[:, 2 * j + f, :], at.psA[:, f, :], ACT.Relu,
                                              bias=bf1[:, 2 * j + f:2 * j + f + 1])
                    last.then_inc(up_kept_a.sem, 1)

                def keep_out(j, i):
                    at.keep_turned_out(act, j, i)
                    at.keep_turned_out(act, j + 1, i)

                def step(i, before, after):
                    p = i - 1
                    extra = {3: lambda: at.keep_qk(act, 1, i), 6: lambda: at.keep_qk(act, 2, i),
                             10: lambda: at.keep_qk(act, 3, i)}
                    if before:
                        extra.update({0: lambda: keep_out(0, p), 1: lambda: keep_out(2, p),
                                      5: lambda: keep_normed(1, at.psA, p), 7: lambda: keep_up(0, p),
                                      9: lambda: keep_up(2, p)})
                    if after:
                        extra.update({14: lambda: keep_normed(0, at.psB, i + 1),
                                      at.HEADS + 1: lambda: at.keep_qk(act, 0, i + 1)})
                    at.scalar(act, i, extra)

                keep_normed(0, at.psB, 0)
                at.keep_qk(act, 0, 0)
                step(0, False, True)
                with act.Fori(1, STEPS - 1) as i:
                    step(i, True, True)
                step(STEPS - 1, True, False)
                last = STEPS - 1
                keep_out(0, last)
                keep_out(2, last)
                keep_normed(1, at.psA, last)
                keep_up(0, last)
                keep_up(2, last)

            @block.vector
            def _(dve):
                def rows(i):
                    return x[:, bass.ds(i % B * ST, ST)]

                def normalise(n, i):
                    link = Chain(dve, chain[n], i, started)
                    xb = rows(i)
                    norm.vector(dve, link, lambda t: xb[:, t, :], 0.0)
                    link(dve.tensor_tensor(norm.work[:], norm.mv[:, :, 1], norm.rstd[:], ALU.mult))
                    link(dve.tensor_scalar(norm.work[:], norm.work[:], 1e-6, None, ALU.add))
                    link(dve.reciprocal(norm.rstd[:], norm.work[:]))
                    for t in range(ST):
                        last = dve.tensor_scalar(xn[:, n, t, :], xb[:, t, :], norm.mean(t), norm.r(t),
                                                 ALU.subtract, ALU.mult)
                    last.then_inc(normed[n].sem, 1)
                    dve.wait_ge(*normed[n].at(1, i))
                    link(dve.tensor_copy(norm.work[:, 0:1], norm.rstd[:, 0:1]))
                    link.close()

                def add_out(i):
                    dve.wait_ge(*at.projected_out.at(1, i))
                    xb = rows(i)
                    dve.tensor_tensor(xb, xb, at.psA[:], ALU.add).then_inc(added.sem, 1)

                def add_down(i):
                    dve.wait_ge(*down.at(1, i))
                    xb = rows(i)
                    dve.tensor_tensor(xb, xb, at.psA[:], ALU.add).then_inc(step_done.sem, 1)

                def keep_up(j, i):
                    dve.wait_ge(*up.at(j + 1, i))
                    for f in range(2):
                        last = dve.tensor_scalar(hid[:, 2 * j + f, :], at.psB[:, f, :],
                                                 bf1[:, 2 * j + f:2 * j + f + 1], 0.0, ALU.add, ALU.max)
                    last.then_inc(up_kept_v.sem, 1)

                def norm_out(i):
                    alone(dve, *added.at(1, i), started)
                    normalise(1, i)

                def norm_next(i):
                    normalise(0, i)

                def step(i, before, after):
                    p = i - 1

                    def e3():
                        if before:
                            norm_out(p)
                        at.keep_v(dve, 1, i)

                    def e6():
                        at.normalise(dve, 0, i)
                        at.keep_v(dve, 2, i)

                    def e10():
                        at.normalise(dve, 1, i)
                        at.keep_v(dve, 3, i)

                    def e17():
                        at.normalise(dve, 3, i)
                        if after:
                            at.keep_v(dve, 0, i + 1)

                    extra = {3: e3, 6: e6, 10: e10, 14: lambda: at.normalise(dve, 2, i), at.HEADS + 1: e17}
                    if before:
                        extra.update({2: lambda: add_out(p), 8: lambda: keep_up(1, p), 11: lambda: keep_up(3, p),
                                      13: lambda: add_down(p)})
                    if after:
                        extra[12] = lambda: norm_next(i + 1)
                    dve.wait_ge(*bias_loaded.at(16, i))
                    at.vector(dve, bias[:, bass.ds(i % 2, 1)][:, 0], i, extra)

                at.bias_added.open(dve)
                dve.memset(ones[:], 1.0)
                dve.wait_ge(*const_in.at(32))
                normalise(0, 0)
                at.keep_v(dve, 0, 0)
                step(0, False, True)
                with dve.Fori(1, STEPS - 1) as i:
                    step(i, True, True)
                step(STEPS - 1, True, False)
                last = STEPS - 1
                add_out(last)
                norm_out(last)
                keep_up(1, last)
                keep_up(3, last)
                add_down(last)
                dve.wait_ge(*step_done.at(1, last))

        HALF = NT // 2
        xs = [t[:].rearrange("p t d -> p (t d)").rearrange("p (t d) -> p t d", d=D) for t in (at.o, at.oT)]
        again = [m.counter(f"again{h}") for h in range(2)]
        done = [m.counter(f"done{h}") for h in range(2)]
        stored = m.counter("stored")
        fin = m.counter("fin")
        norm1 = Norm(m, "norm1", HALF)
        norm2 = Norm(m, "norm2", HALF)
        tokens = [slice(h * HALF, (h + 1) * HALF) for h in range(2)]
        with nc.Block() as block:
            @block.sync
            def _(sp):
                for h in range(2):
                    sp.dma_start(xs[h], tiles_in[:, tokens[h]]).then_inc(again[h].sem, 16)
                for h in range(2):
                    sp.wait_ge(*done[h].at(1))
                    sp.dma_start(tiles_out[:, tokens[h]], x[:, tokens[h]]).then_inc(stored.sem, 16)
                sp.wait_ge(*stored.at(32))

            @block.vector
            def _(dve):
                link = Chain(dve, fin)
                for h in range(2):
                    xb = x[:, tokens[h]]
                    norm1.vector(dve, link, lambda t: xb[:, t, :], 0.0)
                    link(dve.tensor_tensor(norm1.work[:], norm1.mv[:, :, 1], norm1.rstd[:], ALU.mult))
                    link(dve.tensor_scalar(norm1.work[:], norm1.work[:], 1e-6, None, ALU.add))
                    link(dve.reciprocal(norm1.rstd[:], norm1.work[:]))
                    for t in range(HALF):
                        last = dve.tensor_scalar(xb[:, t, :], xb[:, t, :], norm1.mean(t), norm1.r(t),
                                                 ALU.subtract, ALU.mult)
                    link(last)
                    dve.wait_ge(*again[h].at(16))
                    link(dve.tensor_tensor(xb, xb, xs[h], ALU.add))
                    norm2.vector(dve, link, lambda t: xb[:, t, :], 1e-5)
                    for t in range(HALF):
                        last = dve.tensor_scalar(xb[:, t, :], xb[:, t, :], norm2.mean(t), norm2.r(t),
                                                 ALU.subtract, ALU.mult)
                    last.then_inc(done[h].sem, 1)
                    dve.wait_ge(*done[h].at(1))


E14, FE = 14, 512
FT = FE // P
CH = 512
NC4 = TOK // CH
CT = CH // P


def moe14_stage(nc, x_in, w, out):
    xin_c = x_in.rearrange("(c t p) d -> c p t d", p=P, t=CT)
    w1_e = w["w1"].rearrange("e (k p) f -> e p k f", p=P)
    w2_e = w["w2"].rearrange("e (k p) d -> e p k d", p=P)
    with ExitStack() as ctx:
        m = Room(nc, ctx, "m14")
        ident = m.sb("ident", [P, P])
        gate_w = m.sb("gate_w", [P, DT, E14])
        b2 = m.sb("b2", [E14, D])
        b1 = m.sb("b1", [P, E14, FT])
        iota = m.sb("iota", [P, E14])
        xT = [m.sb(f"xT_{half}", [P, DT, TOK], F32R) for half in ("high", "low")]
        acc = m.sb("acc", [P, NT, D])
        wt = m.sb("wt", [P, NT, E14])
        xTs = [m.sb(f"xTs{n}", [P, DT, CH]) for n in range(2)]
        top = m.sb("top", [P, NT, 1])
        prob = m.sb("prob", [P, NT, E14])
        psumr = m.sb("psumr", [P, NT, 1])
        best = m.sb("best", [P, NT, 8])
        best_i = m.sb("best_i", [P, NT, 8], U32)
        best_f = m.sb("best_f", [P, NT, 8])
        mask = m.sb("mask", [P, NT, E14])
        mask2 = m.sb("mask2", [P, NT, E14])
        den = m.sb("den", [P, NT, 1])
        wT = m.sb("wT", [E14, 2, CH])
        w1_raw = m.sb("w1_raw", [P, DT, FE])
        w2_raw = m.sb("w2_raw", [P, FT, D])
        w1s = [m.sb(f"w1_{half}", [P, 2, DT, FE], F32R) for half in ("high", "low")]
        w2s = [m.sb(f"w2_{half}", [P, 2, FT, D], F32R) for half in ("high", "low")]
        hid = m.sb("hid", [P, 2, FT, CH])
        hids = [m.sb(f"hid_{half}", [P, 2, FT, CH], F32R) for half in ("high", "low")]
        psT = m.ps("psT", [P, DT, CH])
        psL = m.ps("psL", [P, 512])
        psW = m.ps("psW", [P, 512])
        psB = m.ps("psB", [P, CT, D])
        started = m.counter("started", ahead=1)
        const_in = m.counter("const_in")
        x_loaded = [m.counter(f"x_loaded{c}") for c in range(NC4)]
        xT_done = m.counter("xT_done")
        xT_stored = m.counter("xT_stored")
        xT_high = m.counter("xT_high")
        logits = m.counter("logits")
        shifted = m.counter("shifted")
        exps = m.counter("exps")
        w_ready = m.counter("w_ready")
        wT_done = m.counter("wT_done")
        wT_stored = m.counter("wT_stored")
        bias_done = m.counter("bias_done")
        bias_added = m.counter("bias_added")
        chain = m.counter("chain")
        turn_bank = [psT, psB[:].rearrange("p t d -> p (t d)").rearrange("p (k c) -> p k c", k=DT)]
        bias_bank = [psT[:].rearrange("p k c -> p (k c)").rearrange("p (t d) -> p t d", d=D), psB]
        row_bank = [psW, psL]

        with nc.Block() as block:
            @block.sync
            def _(sp):
                started.open(sp)
                sp.dma_start(ident[:], w["ident"]).then_inc(const_in.sem, 16)
                for c in range(NC4):
                    sp.dma_start(acc[:, c * CT:(c + 1) * CT], xin_c[c]).then_inc(x_loaded[c].sem, 16)
                sp.dma_start(gate_w[:], w["gate_wT"].rearrange("(k p) e -> p k e", p=P)).then_inc(const_in.sem, 16)
                sp.dma_start(b2[:], w["b2"]).then_inc(const_in.sem, 16)
                sp.dma_start(b1[:], w["b1_cols"]).then_inc(const_in.sem, 16)
                sp.dma_start(iota[:], w["iota14"].partition_broadcast(P)).then_inc(const_in.sem, 16)

            @block.tensor
            def _(pe):
                def turn(c):
                    pe.wait_ge(*x_loaded[c].at(16))
                    if c >= 2:
                        pe.wait_ge(*xT_stored.at(c - 1))
                    for k in range(DT):
                        for t in range(CT):
                            last = pe.transpose(turn_bank[c % 2][:, k, t * P:(t + 1) * P],
                                                acc[:, c * CT + t, k * P:(k + 1) * P], ident[:])
                    last.then_inc(xT_done.sem, 1)

                def route(c):
                    pe.wait_ge(*xT_stored.at(c + 1))
                    for t in range(CT):
                        tile = c * CT + t
                        for k in range(DT):
                            last = pe.matmul(psL[:, tile * E14:(tile + 1) * E14], xTs[c % 2][:, k, t * P:(t + 1) * P],
                                             gate_w[:, k, :], start=(k == 0), stop=(k == DT - 1))
                    last.then_inc(logits.sem, 1)

                pe.wait_ge(*const_in.at(80))
                for c in range(NC4):
                    turn(c)
                    if c:
                        route(c - 1)
                route(NC4 - 1)
                pe.wait_ge(*w_ready.at(1))
                for c in range(NC4 + 1):
                    if c < NC4:
                        if c >= 2:
                            pe.wait_ge(*wT_stored.at(c - 1))
                        for t in range(CT):
                            last = pe.transpose(row_bank[c % 2][0:E14, t * P:(t + 1) * P], wt[:, c * CT + t, :], ident[:])
                        last.then_inc(wT_done.sem, 1)
                    if c:
                        pe.wait_ge(*wT_stored.at(c))
                        if c >= 3:
                            pe.wait_ge(*bias_added.at(c - 2))
                        for t in range(CT):
                            last = pe.matmul(bias_bank[(c - 1) % 2][:, t, :], wT[:, (c - 1) % 2, t * P:(t + 1) * P], b2[:],
                                             start=True, stop=True)
                        last.then_inc(bias_done.sem, 1)

            @block.scalar
            def _(act):
                for c in range(NC4):
                    act.wait_ge(*xT_stored.at(c + 1))
                    act.activation(xT[0][:, :, c * CH:(c + 1) * CH], xTs[c % 2][:], ACT.Copy).then_inc(xT_high.sem, 1)
                act.wait_ge(*shifted.at(1))
                act.activation(prob[:], prob[:], ACT.Exp).then_inc(exps.sem, 1)
                for c in range(NC4):
                    act.wait_ge(*wT_done.at(c + 1))
                    if c >= 2:
                        act.wait_ge(*bias_done.at(c - 1))
                    act.activation(wT[:, c % 2, :], row_bank[c % 2][0:E14, :], ACT.Copy).then_inc(wT_stored.sem, 1)

            @block.vector
            def _(dve):
                link = Chain(dve, chain)
                for c in range(NC4):
                    dve.wait_ge(*xT_done.at(c + 1))
                    if c >= 2:
                        dve.wait_ge(*logits.at(c - 1))
                    dve.tensor_copy(xTs[c % 2][:], turn_bank[c % 2][:]).then_inc(xT_stored.sem, 1)
                    dve.wait_ge(*xT_stored.at(c + 1))
                    dve.wait_ge(*xT_high.at(c + 1))
                    columns = slice(c * CH, (c + 1) * CH)
                    link(dve.tensor_tensor(xT[1][:, :, columns], xTs[c % 2][:], xT[0][:, :, columns].bitcast(F32),
                                           ALU.subtract))
                dve.wait_ge(*const_in.at(80))
                dve.wait_ge(*logits.at(NC4))
                lg = psL[:, 0:NT * E14].rearrange("p (t e) -> p t e", e=E14)
                link(dve.tensor_reduce(top[:, :, 0], lg, AX, ALU.max))
                dve.tensor_tensor(prob[:], lg, top[:].to_broadcast([P, NT, E14]), ALU.subtract).then_inc(shifted.sem, 1)
                dve.wait_ge(*exps.at(1))
                link(dve.tensor_reduce(psumr[:, :, 0], prob[:], AX, ALU.add))
                link(dve.reciprocal(psumr[:], psumr[:]))
                link(dve.tensor_tensor(prob[:], prob[:], psumr[:].to_broadcast([P, NT, E14]), ALU.mult))
                for t in range(NT):
                    last = dve.max(best[:, t, :], prob[:, t, :])
                link(last)
                for t in range(NT):
                    last = dve.max_index(best_i[:, t, :], best[:, t, :], prob[:, t, :])
                link(last)
                link(dve.tensor_copy(best_f[:], best_i[:]))
                places = iota[:].unsqueeze(1).to_broadcast([P, NT, E14])
                dve.tensor_tensor(mask[:], places, best_f[:, :, 0:1].to_broadcast([P, NT, E14]), ALU.is_equal)
                link(dve.tensor_tensor(mask2[:], places, best_f[:, :, 1:2].to_broadcast([P, NT, E14]), ALU.is_equal))
                link(dve.tensor_tensor(mask[:], mask[:], mask2[:], ALU.add))
                link(dve.tensor_tensor(den[:], best[:, :, 0:1], best[:, :, 1:2], ALU.add))
                link(dve.tensor_scalar(den[:], den[:], 1e-10, None, ALU.max))
                link(dve.reciprocal(den[:], den[:]))
                link(dve.tensor_tensor(mask[:], mask[:], prob[:], ALU.mult))
                dve.tensor_tensor(wt[:], mask[:], den[:].to_broadcast([P, NT, E14]), ALU.mult).then_inc(w_ready.sem, 1)
                for c in range(NC4):
                    dve.wait_ge(*bias_done.at(c + 1))
                    part = acc[:, c * CT:(c + 1) * CT]
                    dve.tensor_tensor(part, part, bias_bank[c % 2][:], ALU.add).then_inc(bias_added.sem, 1)

        UNITS = 2 * NC4
        PASSES = E14 // 2
        w_loaded = m.counter("w_loaded", 2 * 32)
        w_split = m.counter("w_split", 2)
        w_high = m.counter("w_high", 2)
        up = m.counter("up", UNITS * FT)
        gelu = m.counter("gelu", UNITS * FT, ahead=2)
        high_done = m.counter("high_done", UNITS)
        hid_split = m.counter("hid_split", UNITS, ahead=2)
        down = m.counter("down", UNITS * 2, ahead=UNITS * 2)
        summed = m.counter("summed", UNITS * 2, ahead=8)
        psU = [psL, psW]

        def down_bank(n):
            if n % 4 < 2:
                return psB[:, 2 * (n % 2):2 * (n % 2) + 2, :]
            return psT[:, n % 2, :].rearrange("p (t d) -> p t d", d=D)

        with nc.Block() as block:
            @block.sync
            def _(sp):
                def load(i, s):
                    if not (isinstance(i, int) and i * 2 + s == 0):
                        sp.wait_ge(*w_split.at(s, i))
                    sp.dma_start(w1_raw[:], w1_e[bass.ds(i * 2 + s, 1)][0]).then_inc(w_loaded.sem, 16)
                    sp.dma_start(w2_raw[:], w2_e[bass.ds(i * 2 + s, 1)][0]).then_inc(w_loaded.sem, 16)

                load(0, 0)
                with sp.Fori(0, PASSES - 1) as i:
                    load(i, 1)
                    load(i, 2)
                load(PASSES - 1, 1)

            @block.tensor
            def _(pe):
                down.open(pe)
                with pe.Fori(0, PASSES) as i:
                    for u in range(UNITS + 1):
                        if u < UNITS:
                            s, c = u // NC4, u % NC4
                            if c == 0:
                                pe.wait_ge(*w_split.at(s + 1, i))
                            for f in range(FT):
                                pe.wait_ge(*gelu.at(u * FT + f + 1 - 2, i))
                                for k in range(DT):
                                    last = split_product(pe, psU[f % 2][:], [x[:, s, k, f * P:(f + 1) * P] for x in w1s],
                                                         [x[:, k, c * CH:(c + 1) * CH] for x in xT],
                                                         k == 0, k == DT - 1)
                                last.then_inc(up.sem, 1)
                        if u > 0:
                            v = u - 1
                            s = v // NC4
                            pe.wait_ge(*hid_split.at(v + 1, i))
                            for h in range(2):
                                n = v * 2 + h
                                pe.wait_ge(*summed.at(n + 1 - 4, i))
                                for t in range(2):
                                    tokens = slice((2 * h + t) * P, (2 * h + t + 1) * P)
                                    for f in range(FT):
                                        last = split_product(pe, down_bank(n)[:, t, :],
                                                             [x[:, v % 2, f, tokens] for x in hids],
                                                             [x[:, s, f, :] for x in w2s], f == 0, f == FT - 1)
                                last.then_inc(down.sem, 1)

            @block.scalar
            def _(act):
                gelu.open(act)
                with act.Fori(0, PASSES) as i:
                    for u in range(UNITS):
                        act.wait_ge(*hid_split.at(u + 1 - 2, i))
                        for f in range(FT):
                            alone(act, *up.at(u * FT + f + 1, i), started)
                            act.activation(hid[:, u % 2, f, :], psU[f % 2][:], ACT.Gelu,
                                           bias=b1[:, bass.ds(i * 2 + u // NC4, 1), f]).then_inc(gelu.sem, 1)

            @block.vector
            def _(dve):
                def split_weights(i, s):
                    slot = s % 2
                    dve.wait_ge(*w_loaded.at(32 * (s + 1), i))
                    dve.tensor_copy(w1s[0][:, slot], w1_raw[:])
                    dve.tensor_copy(w2s[0][:, slot], w2_raw[:]).then_inc(w_high.sem, 1)
                    dve.wait_ge(*w_high.at(s + 1, i))
                    dve.tensor_tensor(w1s[1][:, slot], w1_raw[:], w1s[0][:, slot].bitcast(F32), ALU.subtract)
                    dve.tensor_tensor(w2s[1][:, slot], w2_raw[:], w2s[0][:, slot].bitcast(F32), ALU.subtract).then_inc(
                        w_split.sem, 1)

                def split_hidden(u, i):
                    slot = u % 2
                    dve.wait_ge(*gelu.at(u * FT + FT, i))
                    dve.wait_ge(*down.at(2 * (u + 1) - 4, i))
                    dve.tensor_copy(hids[0][:, slot], hid[:, slot]).then_inc(high_done.sem, 1)
                    dve.wait_ge(*high_done.at(u + 1, i))
                    dve.tensor_tensor(hids[1][:, slot], hid[:, slot], hids[0][:, slot].bitcast(F32),
                                      ALU.subtract).then_inc(hid_split.sem, 1)

                def add(u, i):
                    s, c = u // NC4, u % NC4
                    for h in range(2):
                        n = u * 2 + h
                        dve.wait_ge(*down.at(n + 1, i))
                        dve.wait_ge(*summed.at(n + 1 - 8, i))
                        for t in range(2):
                            tile = c * CT + 2 * h + t
                            last = dve.scalar_tensor_tensor(
                                out=acc[:, tile, :], in0=down_bank(n)[:, t, :],
                                scalar=wt[:, tile, bass.ds(i * 2 + s, 1)], in1=acc[:, tile, :],
                                op0=ALU.mult, op1=ALU.add)
                        last.then_inc(summed.sem, 1)

                def experts(i, more):
                    for u in range(UNITS + 1):
                        if u < UNITS:
                            split_hidden(u, i)
                        if u > 0:
                            add(u - 1, i)
                        if u == 1:
                            split_weights(i, 1)
                        if u == NC4 + 1 and more:
                            dve.wait_ge(*down.at(2 * NC4, i))
                            split_weights(i, 2)

                summed.open(dve)
                hid_split.open(dve)
                split_weights(0, 0)
                with dve.Fori(0, PASSES - 1) as i:
                    experts(i, True)
                experts(PASSES - 1, False)

        HALF = NT // 2
        xs = hid[:].rearrange("p u f c -> p (u f c)").rearrange("p (t d) -> p t d", d=D)
        x_again = [m.counter(f"x_again{h}") for h in range(2)]
        normed = [m.counter(f"normed{h}") for h in range(2)]
        stored = m.counter("stored")
        fin = m.counter("fin")
        norm = Norm(m, "norm", HALF)
        tokens = [slice(h * HALF, (h + 1) * HALF) for h in range(2)]
        tiles_in = x_in.rearrange("(t p) d -> p t d", p=P)
        tiles_out = out.rearrange("(t p) d -> p t d", p=P)

        with nc.Block() as block:
            @block.sync
            def _(sp):
                for h in range(2):
                    sp.dma_start(xs[:, tokens[h]], tiles_in[:, tokens[h]]).then_inc(x_again[h].sem, 16)
                for h in range(2):
                    sp.wait_ge(*normed[h].at(1))
                    sp.dma_start(tiles_out[:, tokens[h]], acc[:, tokens[h]]).then_inc(stored.sem, 16)
                sp.wait_ge(*stored.at(32))

            @block.vector
            def _(dve):
                link = Chain(dve, fin)
                for h in range(2):
                    part = acc[:, tokens[h]]
                    link(dve.tensor_scalar(part, part, 100.0, -100.0, ALU.min, ALU.max))
                    dve.wait_ge(*x_again[h].at(16))
                    link(dve.tensor_tensor(part, part, xs[:, tokens[h]], ALU.add))
                    norm.vector(dve, link, lambda t: part[:, t, :], 1e-5)
                    for t in range(HALF):
                        last = dve.tensor_scalar(part[:, t, :], part[:, t, :], norm.mean(t), norm.r(t),
                                                 ALU.subtract, ALU.mult)
                    last.then_inc(normed[h].sem, 1)
                    dve.wait_ge(*normed[h].at(1))


def build(nc, a, out):
    def of(stage):
        named = {k.split(".", 1)[1]: v for k, v in a.items() if k.startswith(stage + ".")}
        named.update(ident=a["ident"], ctxT=a["ctxT"])
        return named

    between = [nc.dram_tensor(f"x_after_{n}", (TOK, D), F32, kind="Internal").ap() for n in range(1, 6)]
    bias = nc.dram_tensor("distance_bias", (NL * B, S, S), F32, kind="Internal").ap()
    bias_stage(nc, of("bias"), bias)
    scan_stage(nc, a["x"], of("ssm"), between[0])
    cross_stage(nc, between[0], of("xat"), between[1])
    moe8_stage(nc, between[1], of("m8"), between[2])
    linear_stage(nc, between[2], of("lin"), between[3])
    decoder_stage(nc, between[3], bias, of("dec"), between[4])
    moe14_stage(nc, between[4], of("m14"), out)


def layouts(i):
    def turned(v):
        return np.swapaxes(v, -1, -2)

    def cols(v):
        return turned(v.reshape(*v.shape[:-1], -1, P))

    def padded_heads(v):
        wide = np.zeros((LH, HP), v.dtype)
        wide[:, :LD] = v.reshape(LH, LD)
        return wide.reshape(1, LH * HP)

    s, x0, f0 = (lambda n: i["L0_attn_" + n]), (lambda n: i["L0_xattn_" + n]), (lambda n: i["L0_ffn_" + n])
    l1, x1, f1 = (lambda n: i["L1_attn_" + n]), (lambda n: i["L1_xattn_" + n]), (lambda n: i["L1_ffn_" + n])
    dist = i["fside_BxSxS2_0"]
    a = {
        "ident": np.eye(P, dtype=np.float32),
        "x": i["x"].reshape(TOK, D),
        "ctxT": turned(i["ctx_1024"]),
        "bias.distT": turned(dist),
        "bias.dist": dist,
        "bias.mask": i["mask_Bx1x1xS2_ff0"].reshape(B, S),
        "bias.abw": np.stack([x1("Wth")[:, 0].T, x1("bth").T, x1("Wto")[:, :, 0].T], 1),
        "bias.bto": x1("bto")[:, 0],
        "ssm.ln_wb": np.stack([cols(s("ln_w")), cols(s("ln_b"))], -1),
        "ssm.in_wT": turned(s("in_w")),
        "ssm.in_b_cols": cols(s("in_b")),
        "ssm.taps": np.concatenate([s("conv_w")[:, 0], s("conv_b")[:, None]], 1).reshape(IT, P, TAPS + 1).transpose(1, 0, 2),
        "ssm.xp_wT": turned(s("xp_w")),
        "ssm.dtp_wT": turned(s("dtp_w")),
        "ssm.dtp_b_cols": cols(s("dtp_b")),
        "ssm.A_log": s("A_log"),
        "ssm.D_cols": cols(s("D")),
        "ssm.out_wT": turned(s("out_w")),
        "ssm.out_b": s("out_b"),
        "xat.bo": x0("bo"),
        "m8.iota_tok": np.arange(TOK, dtype=np.float32),
        "m8.gates_wT": np.concatenate([turned(f0("sg_w")), turned(f0("eg_w"))], 1),
        "m8.gates_b": np.concatenate([f0("sg_b"), f0("eg_b")]),
        "m8.gains": np.stack([f0("s_ln_g"), f0("sel_ln_g")], 1),
        "m8.shifts": np.stack([f0("s_ln_b"), f0("sel_ln_b")], 1),
        "lin.pair": linear_constants(),
        "lin.qb_row": padded_heads(l1("qb")),
        "lin.kb_row": padded_heads(l1("kb")),
        "lin.vb_row": l1("vb")[None],
        "lin.ob_row": l1("ob")[None],
        "dec.bf1_cols": cols(x1("bf1")),
        "m14.gate_wT": turned(f1("gate_w")),
        "m14.b1_cols": f1("b1").reshape(E14, FT, P).transpose(2, 0, 1),
        "m14.iota14": np.arange(E14, dtype=np.float32),
        "dec.bf2": x1("bf2"),
        "dec.wq": x1("Wq").reshape(LAYERS, D, QW),
        "dec.wk": x1("Wk").reshape(LAYERS, D, QW),
        "dec.wv": x1("Wv").reshape(LAYERS, D, QW),
        "dec.wo": x1("Wo").reshape(LAYERS, QW, D),
        "dec.wf1": x1("Wf1"),
        "dec.wf2": x1("Wf2"),
    }
    for n in ("Wq", "Wk", "Wv", "Wo"):
        a[f"xat.{n}T"] = turned(x0(n))
    for n in ("sw1", "sw2", "sw3", "ew1", "ew2", "ew3"):
        a[f"m8.{n}T"] = turned(f0(n))
    for n in ("index_b", "index_t", "sb1", "sb2", "sb3", "eb1", "eb2", "eb3", "exp_bias"):
        a[f"m8.{n}"] = f0(n)
    for n in ("g1", "b1", "g2", "b2"):
        a[f"lin.{n}"] = l1(n)
    for n in "qkvo":
        a[f"lin.{n}S"] = l1(n + "S")
        a[f"lin.{n}A_halves"] = l1(n + "A").reshape(PF, DT, 2, PF).transpose(2, 1, 0, 3)
    for n in ("w1", "w2", "b2"):
        a[f"m14.{n}"] = f1(n)
    return {k: np.ascontiguousarray(v) for k, v in a.items()}


def kernel(**inputs):
    import concourse.bacc as bacc
    from concourse.bass_utils import run_bass_kernel_spmd

    nc = bacc.Bacc("TRN2", target_bir_lowering=False, num_devices=1)
    arrays = layouts({k: np.asarray(v) for k, v in inputs.items()})
    dram = {k.replace(".", "_"): v for k, v in arrays.items()}
    aps = {k: nc.dram_tensor(k.replace(".", "_") + "_in", v.shape, mybir.dt.from_np(v.dtype), kind="ExternalInput").ap()
           for k, v in arrays.items()}
    out = nc.dram_tensor("out_0", (TOK, D), F32, kind="ExternalOutput").ap()
    build(nc, aps, out)
    r = run_bass_kernel_spmd(nc, [{k + "_in": v for k, v in dram.items()}], core_ids=[0])
    return r.results[0]["out_0"].reshape(B, S, D)
```
